# Optimizing a Trainium2 kernel written in Bass

```python
import numpy as np
import jax
import jax.numpy as jnp

def _softmax(x, axis=-1):
    return jax.nn.softmax(x, axis=axis)

def _gelu(x):
    return jax.nn.gelu(x, approximate=True)

def _silu(x):
    return jax.nn.silu(x)

def _sigmoid(x):
    return jax.nn.sigmoid(x)

def _layernorm(x, axis=-1, eps=1e-05):
    m = jnp.mean(x, axis=axis, keepdims=True)
    v = jnp.var(x, axis=axis, keepdims=True)
    return (x - m) / jnp.sqrt(v + eps)

def _scatter_add(tgt, idx, src, axis=0):
    return tgt.at[idx].add(src)

def _segment_sum(src, seg, n):
    return jax.ops.segment_sum(src, seg, n)
kernel_name = 'mk_decoder_postln_d4_seqx_r4_2deed3'

def setup_inputs(seed: int=0):
    np.random.seed(seed)
    _w = jnp.asarray

    def _rec_inputs():
        import jax
        import jax.numpy as jnp
        _rk = jax.random.key(seed)
        x = -0.0002928 + 1 * jax.random.normal(jax.random.fold_in(_rk, 1), (4, 1024, 256), jnp.float32)
        _lenS = 1024 - jax.random.randint(jax.random.fold_in(_rk, 7), (4,), 0, max(1, 1024 // 4) + 1, jnp.int32)
        _lenS2 = 77 - jax.random.randint(jax.random.fold_in(_rk, 8), (4,), 0, max(1, 77 // 4) + 1, jnp.int32)
        _ctx_1024P = jax.random.normal(jax.random.fold_in(_rk, 11), (4, 16, 256), jnp.float32)
        _ctx_1024c = jax.random.dirichlet(jax.random.fold_in(_rk, 511), 0.3 * jnp.ones((16,), jnp.float32), (4, 77))
        _ctx_1024t = jnp.einsum('bsk,bkd->bsd', _ctx_1024c, _ctx_1024P)
        _ctx_1024t = _ctx_1024t * jax.lax.rsqrt(jnp.mean(jnp.square(_ctx_1024t)) + 1e-12) * 0.953939
        ctx_1024 = -1.39393e-06 + 0.999914 * (_ctx_1024t + 0.3 * jax.random.normal(jax.random.fold_in(_rk, 611), (4, 77, 256), jnp.float32))
        fside_BxS2_0 = -0.00600047 + 0.990131 * jax.random.normal(jax.random.fold_in(_rk, 12), (4, 77), jnp.float32)
        return (x, ctx_1024, fside_BxS2_0)
    x, ctx_1024, fside_BxS2_0 = _rec_inputs()

    def _L0_attn_setup():
        import jax, jax.numpy as jnp
        import numpy as np
        QMAX = 255.0

        def fake_quant(x, scale, zero_point):
            q = x / scale + zero_point
            q = jnp.clip(q, 0.0, QMAX)
            q = q + jax.lax.stop_gradient(jnp.round(q) - q)
            return (q - zero_point) * scale
        key = jax.random.key(seed)
        ks = jax.random.split(key, 8)
        B, S, E, H = (4, 256, 256, 16)
        x = jax.random.normal(ks[0], (B, S, E), dtype=jnp.float32)
        W_qkv = jax.random.normal(ks[1], (3 * E, E), dtype=jnp.float32) * (1.0 / np.sqrt(E))
        b_qkv = jax.random.uniform(ks[2], (3 * E,), minval=-1.0 / np.sqrt(E), maxval=1.0 / np.sqrt(E))
        W_proj = jax.random.normal(ks[3], (E, E), dtype=jnp.float32) * (1.0 / np.sqrt(E))
        b_proj = jax.random.uniform(ks[4], (E,), minval=-1.0 / np.sqrt(E), maxval=1.0 / np.sqrt(E))

        def w_qparams(W):
            wmin, wmax = (W.min(axis=1), W.max(axis=1))
            s = (wmax - wmin) / QMAX
            zp = jnp.round(-wmin / s)
            return (s, zp)
        s_w_qkv, zp_w_qkv = w_qparams(W_qkv)
        s_w_proj, zp_w_proj = w_qparams(W_proj)
        s_act_qkv = jnp.float32(8.0 / QMAX)
        zp_act_qkv = jnp.float32(128.0)
        s_attn = jnp.float32(0.06)
        zp_attn = jnp.float32(128.0)
        s_act_proj = jnp.float32(0.02)
        zp_act_proj = jnp.float32(128.0)
        return dict(x=x, W_qkv=W_qkv, b_qkv=b_qkv, W_proj=W_proj, b_proj=b_proj, s_act_qkv=s_act_qkv, zp_act_qkv=zp_act_qkv, s_w_qkv=s_w_qkv, zp_w_qkv=zp_w_qkv, s_attn=s_attn, zp_attn=zp_attn, s_act_proj=s_act_proj, zp_act_proj=zp_act_proj, s_w_proj=s_w_proj, zp_w_proj=zp_w_proj)
    _L0_attn_all = _L0_attn_setup()
    _L0_attn_in = {k: v for k, v in _L0_attn_all.items() if k in ('W_qkv', 'b_qkv', 'W_proj', 'b_proj', 's_act_qkv', 'zp_act_qkv', 's_w_qkv', 'zp_w_qkv', 's_attn', 'zp_attn', 's_act_proj', 'zp_act_proj', 's_w_proj', 'zp_w_proj')}
    del _L0_attn_all

    def _L0_xattn_setup():
        import jax, jax.numpy as jnp
        import numpy as np
        EMBED = 256
        NHEAD = 16
        HEAD_DIM = EMBED // NHEAD
        key = jax.random.key(seed)
        ks = jax.random.split(key, 8)
        B, SQ, SKV = (2, 512, 512)
        scale = 1.0 / np.sqrt(EMBED)
        return {'query': jax.random.normal(ks[0], (B, SQ, EMBED), dtype=jnp.float32), 'key': jax.random.normal(ks[1], (B, SKV, EMBED), dtype=jnp.float32), 'value': jax.random.normal(ks[2], (B, SKV, EMBED), dtype=jnp.float32), 'attention_bias': jax.random.normal(ks[3], (B, SKV), dtype=jnp.float32), 'Wq': jax.random.normal(ks[4], (EMBED, EMBED), dtype=jnp.float32) * scale, 'Wk': jax.random.normal(ks[5], (EMBED, EMBED), dtype=jnp.float32) * scale, 'Wv': jax.random.normal(ks[6], (EMBED, EMBED), dtype=jnp.float32) * scale, 'Wo': jax.random.normal(ks[7], (EMBED, EMBED), dtype=jnp.float32) * scale}
    _L0_xattn_all = _L0_xattn_setup()
    _L0_xattn_in = {k: v for k, v in _L0_xattn_all.items() if k in ('Wq', 'Wk', 'Wv', 'Wo')}
    del _L0_xattn_all

    def _L0_ffn_setup():
        import jax, jax.numpy as jnp
        import numpy as np
        B, S, D, E, F = (4, 512, 256, 8, 1024)
        key = jax.random.key(seed)
        k0, k1, k2, k3 = jax.random.split(key, 4)
        x = jax.random.normal(k0, (B, S, D), dtype=jnp.float32)
        wg = jax.random.normal(k1, (D, E), dtype=jnp.float32) * 0.02
        w_gate = jax.random.normal(k2, (E, D, F), dtype=jnp.float32) * 0.02
        w_down = jax.random.normal(k3, (E, F, D), dtype=jnp.float32) * 0.02
        return {'x': x, 'wg': wg, 'w_gate': w_gate, 'w_down': w_down}
    _L0_ffn_all = _L0_ffn_setup()
    _L0_ffn_in = {k: v for k, v in _L0_ffn_all.items() if k in ('wg', 'w_gate', 'w_down')}
    del _L0_ffn_all

    def _L1_attn_setup():
        import jax, jax.numpy as jnp
        import numpy as np
        B, S, H, NH = (2, 512, 256, 16)
        HD = H // NH
        EPS = 1e-06

        def _layernorm(x, scale, bias):
            x32 = x.astype(jnp.float32)
            mean = jnp.mean(x32, axis=-1, keepdims=True)
            var = jnp.mean(jnp.square(x32 - mean), axis=-1, keepdims=True)
            return (x32 - mean) * jax.lax.rsqrt(var + EPS) * scale + bias
        key = jax.random.key(seed)
        ks = jax.random.split(key, 16)
        init = lambda k, shape, fan_in: jax.random.normal(k, shape, jnp.float32) / np.sqrt(fan_in)
        return {'x': jax.random.normal(ks[0], (B, S, H), jnp.float32), 'Wq': init(ks[1], (H, H), H), 'bq': jnp.zeros((H,), jnp.float32), 'Wk': init(ks[2], (H, H), H), 'bk': jnp.zeros((H,), jnp.float32), 'Wv': init(ks[3], (H, H), H), 'bv': jnp.zeros((H,), jnp.float32), 'q_scale': jnp.ones((HD,), jnp.float32), 'q_bias': jnp.zeros((HD,), jnp.float32), 'k_scale': jnp.ones((HD,), jnp.float32), 'k_bias': jnp.zeros((HD,), jnp.float32), 'v_scale': jnp.ones((HD,), jnp.float32), 'v_bias': jnp.zeros((HD,), jnp.float32), 'Wo': init(ks[4], (H, H), H), 'bo': jnp.zeros((H,), jnp.float32)}
    _L1_attn_all = _L1_attn_setup()
    _L1_attn_in = {k: v for k, v in _L1_attn_all.items() if k in ('Wq', 'bq', 'Wk', 'bk', 'Wv', 'bv', 'q_scale', 'q_bias', 'k_scale', 'k_bias', 'v_scale', 'v_bias', 'Wo', 'bo')}
    del _L1_attn_all

    def _L1_xattn_setup():
        import jax, jax.numpy as jnp
        import numpy as np
        E, T, H, F = (8, 256, 256, 1024)
        key = jax.random.key(seed)
        k1, k2, k3 = jax.random.split(key, 3)
        x = jax.random.normal(k1, (E, T, H), dtype=jnp.float32)
        w1 = jax.random.normal(k2, (E, F, H), dtype=jnp.float32) * (1.0 / np.sqrt(H))
        w2 = jax.random.normal(k3, (E, F, H), dtype=jnp.float32) * (1.0 / np.sqrt(F))
        return {'x': x, 'w1': w1, 'w2': w2}
    _L1_xattn_all = _L1_xattn_setup()
    _L1_xattn_in = {k: v for k, v in _L1_xattn_all.items() if k in ()}
    del _L1_xattn_all

    def _L1_ffn_setup():
        import jax, jax.numpy as jnp
        import numpy as np
        DIM = 256
        DEPTH = 2
        HEADS = 8
        DIM_HEAD = 64
        WINDOW = 128
        INNER = HEADS * DIM_HEAD
        HID = int(DIM * 4 * 2 / 3)
        B, N = (2, 2048)
        QK_SCALE = 8.0

        def shift_token(t):
            t1, t2 = jnp.split(t, 2, axis=-1)
            t2 = jnp.pad(t2, ((0, 0), (1, 0), (0, 0)))[:, :-1]
            return jnp.concatenate([t1, t2], axis=-1)

        def l2norm(t):
            return t / jnp.clip(jnp.linalg.norm(t, axis=-1, keepdims=True), 1e-12)

        def rotate_half(x):
            x1, x2 = jnp.split(x, 2, axis=-1)
            return jnp.concatenate([-x2, x1], axis=-1)

        def rotary_xpos(q, k):
            n = q.shape[-2]
            half_idx = jnp.arange(0, DIM_HEAD, 2, dtype=jnp.float32)
            inv_freq = 1.0 / 10000.0 ** (half_idx / DIM_HEAD)
            t = jnp.arange(n, dtype=jnp.float32)
            freqs = t[:, None] * inv_freq[None, :]
            freqs = jnp.concatenate([freqs, freqs], axis=-1)
            base = (half_idx + 0.4 * DIM_HEAD) / (1.4 * DIM_HEAD)
            power = (t - n // 2) / float(WINDOW // 2)
            scale = base[None, :] ** power[:, None]
            scale = jnp.concatenate([scale, scale], axis=-1)
            cos, sin = (jnp.cos(freqs), jnp.sin(freqs))
            q = q * cos * scale + rotate_half(q) * sin * scale
            k = k * cos / scale + rotate_half(k) * sin / scale
            return (q, k)

        def local_attention(q, k, v):
            b, h, n, d = q.shape
            w = n // WINDOW
            bq = q.reshape(b, h, w, WINDOW, d) * QK_SCALE
            bk = k.reshape(b, h, w, WINDOW, d)
            bv = v.reshape(b, h, w, WINDOW, d)

            def look_around(t):
                p = jnp.pad(t, ((0, 0), (0, 0), (1, 0), (0, 0), (0, 0)))
                return jnp.concatenate([p[:, :, :w], p[:, :, 1:]], axis=3)
            bk, bv = (look_around(bk), look_around(bv))
            bt = jnp.arange(n).reshape(w, WINDOW)
            btp = jnp.pad(bt, ((1, 0), (0, 0)), constant_values=-1)
            btk = jnp.concatenate([btp[:w], btp[1:]], axis=1)
            sim = jnp.einsum('bhwid,bhwjd->bhwij', bq, bk)
            i = bt[:, :, None]
            j = btk[:, None, :]
            mask = (i < j) | (i > j + WINDOW) | (j == -1)
            sim = jnp.where(mask, -jnp.finfo(sim.dtype).max, sim)
            attn = jax.nn.softmax(sim, axis=-1)
            out = jnp.einsum('bhwij,bhwjd->bhwid', attn, bv)
            return out.reshape(b, h, n, d)

        def _layer(x, wqkv, qs, ksc, wo, lg, lb, w1, b1, w2, b2):
            b, n, _ = x.shape
            h = shift_token(x)
            qkv = h @ wqkv
            q, k, v = jnp.split(qkv, 3, axis=-1)
            to_heads = lambda t: t.reshape(b, n, HEADS, DIM_HEAD).transpose(0, 2, 1, 3)
            q, k, v = (to_heads(q), to_heads(k), to_heads(v))
            q = l2norm(q) * qs
            k = l2norm(k) * ksc
            q, k = rotary_xpos(q, k)
            o = local_attention(q, k, v)
            o = o.transpose(0, 2, 1, 3).reshape(b, n, INNER)
            x = x + o @ wo
            h = shift_token(x)
            mu = h.mean(-1, keepdims=True)
            var = h.var(-1, keepdims=True)
            h = (h - mu) / jnp.sqrt(var + 1e-05) * lg + lb
            h = h @ w1 + b1
            a, g = jnp.split(h, 2, axis=-1)
            h = a * jax.nn.gelu(g, approximate=False)
            x = x + h @ w2 + b2
            return x
        key = jax.random.key(seed)
        ks = jax.random.split(key, 6)
        return {'x': jax.random.normal(ks[0], (B, N, DIM), jnp.float32), 'wqkv': jax.random.normal(ks[1], (DEPTH, DIM, 3 * INNER), jnp.float32) * 0.02, 'q_scale': jnp.ones((DEPTH, DIM_HEAD), jnp.float32), 'k_scale': jnp.ones((DEPTH, DIM_HEAD), jnp.float32), 'wo': jax.random.normal(ks[2], (DEPTH, INNER, DIM), jnp.float32) * 0.02, 'ln_g': jnp.ones((DEPTH, DIM), jnp.float32), 'ln_b': jnp.zeros((DEPTH, DIM), jnp.float32), 'w1': jax.random.normal(ks[3], (DEPTH, DIM, 2 * HID), jnp.float32) * 0.02, 'b1': jnp.zeros((DEPTH, 2 * HID), jnp.float32), 'w2': jax.random.normal(ks[4], (DEPTH, HID, DIM), jnp.float32) * 0.02, 'b2': jnp.zeros((DEPTH, DIM), jnp.float32)}
    _L1_ffn_all = _L1_ffn_setup()
    _L1_ffn_in = {k: v for k, v in _L1_ffn_all.items() if k in ('wqkv', 'q_scale', 'k_scale', 'wo', 'ln_g', 'ln_b', 'w1', 'b1', 'w2', 'b2')}
    del _L1_ffn_all

    def _L2_attn_setup():
        import jax, jax.numpy as jnp
        import numpy as np
        D_MODEL = 256
        D_INNER = 512
        D_STATE = 16
        D_CONV = 4
        DT_RANK = 64
        BATCH = 2
        SEQ = 256

        def _silu(v):
            return v * jax.nn.sigmoid(v)
        key = jax.random.key(seed)
        ks = jax.random.split(key, 8)
        s = 0.02
        return {'x': jax.random.normal(ks[0], (BATCH, SEQ, D_MODEL), jnp.float32), 'norm_w': jnp.ones((D_MODEL,), jnp.float32), 'in_proj_w': jax.random.normal(ks[1], (2 * D_INNER, D_MODEL), jnp.float32) * s, 'conv_w': jax.random.normal(ks[2], (D_INNER, 1, D_CONV), jnp.float32) * s, 'conv_b': jnp.zeros((D_INNER,), jnp.float32), 'x_proj_w': jax.random.normal(ks[3], (DT_RANK + 2 * D_STATE, D_INNER), jnp.float32) * s, 'dt_proj_w': jax.random.normal(ks[4], (D_INNER, DT_RANK), jnp.float32) * s, 'dt_proj_b': jnp.zeros((D_INNER,), jnp.float32), 'A_log': jnp.log(jnp.broadcast_to(jnp.arange(1, D_STATE + 1, dtype=jnp.float32), (D_INNER, D_STATE))), 'D': jnp.ones((D_INNER,), jnp.float32), 'out_proj_w': jax.random.normal(ks[5], (D_MODEL, D_INNER), jnp.float32) * s}
    _L2_attn_all = _L2_attn_setup()
    _L2_attn_in = {k: v for k, v in _L2_attn_all.items() if k in ('norm_w', 'in_proj_w', 'conv_w', 'conv_b', 'x_proj_w', 'dt_proj_w', 'dt_proj_b', 'A_log', 'D', 'out_proj_w')}
    del _L2_attn_all

    def _L2_xattn_setup():
        import jax, jax.numpy as jnp
        import numpy as np
        D1, D2, D3 = (256, 256, 256)
        key = jax.random.key(seed)
        k1, k2, kw, kb = jax.random.split(key, 4)
        x1 = jax.random.normal(k1, (8, 512, D1), dtype=jnp.float32)
        x2 = jax.random.normal(k2, (8, 512, D2), dtype=jnp.float32)
        bound = 1.0 / np.sqrt(D1 + D2)
        W = jax.random.uniform(kw, (D3, D1 + D2), minval=-bound, maxval=bound, dtype=jnp.float32)
        b = jax.random.uniform(kb, (D3,), minval=-bound, maxval=bound, dtype=jnp.float32)
        return {'x1': x1, 'x2': x2, 'W': W, 'b': b}
    _L2_xattn_all = _L2_xattn_setup()
    _L2_xattn_in = {k: v for k, v in _L2_xattn_all.items() if k in ('W', 'b')}
    del _L2_xattn_all

    def _L2_ffn_setup():
        import jax, jax.numpy as jnp
        import numpy as np
        import math
        BETA = 0.9
        THRESHOLD = 1.0
        NUM_STEPS = 5
        ALPHA = 2.0

        @jax.custom_vjp
        def spike_fn(u):
            return (u > 0).astype(u.dtype)

        def _spike_fwd(u):
            return (spike_fn(u), u)

        def _spike_bwd(u, g):
            s = jnp.pi / 2.0 * ALPHA * u
            return (g * (ALPHA / 2.0) / (1.0 + s * s),)
        spike_fn.defvjp(_spike_fwd, _spike_bwd)
        key = jax.random.key(seed)
        k1, k2, k3 = jax.random.split(key, 3)
        n_embd = 256
        x = jax.random.normal(k1, (4, 512, n_embd), dtype=jnp.float32)
        W_fc = jax.random.normal(k2, (4 * n_embd, n_embd), dtype=jnp.float32) / math.sqrt(n_embd)
        W_proj = jax.random.normal(k3, (n_embd, 4 * n_embd), dtype=jnp.float32) / math.sqrt(4 * n_embd)
        return {'x': x, 'W_fc': W_fc, 'W_proj': W_proj}
    _L2_ffn_all = _L2_ffn_setup()
    _L2_ffn_in = {k: v for k, v in _L2_ffn_all.items() if k in ('W_fc', 'W_proj')}
    del _L2_ffn_all

    def _L3_attn_setup():
        import jax, jax.numpy as jnp
        import numpy as np
        D = 256
        H = 16
        HKV = 4
        HD = D // H
        L = 64
        EPS = 1e-06
        LN_EPS = 1e-05
        B, S = (2, 256)

        def _feat(x):
            return jax.nn.elu(x) + 1.0
        key = jax.random.key(seed)
        ks = jax.random.split(key, 8)
        w = lambda k, shape: jax.random.normal(k, shape, jnp.float32) * 0.02
        return {'x': jax.random.normal(ks[0], (B, S, D), jnp.float32), 'Wq': w(ks[1], (D, D)), 'bq': jnp.zeros((D,), jnp.float32), 'Wk': w(ks[2], (D, HKV * HD)), 'bk': jnp.zeros((HKV * HD,), jnp.float32), 'Wv': w(ks[3], (D, HKV * HD)), 'bv': jnp.zeros((HKV * HD,), jnp.float32), 'Wc': w(ks[4], (HKV * HD, L)), 'We': w(ks[5], (L, HKV * HD)), 'Wo': w(ks[6], (D, D)), 'bo': jnp.zeros((D,), jnp.float32), 'gamma': jnp.ones((D,), jnp.float32), 'beta': jnp.zeros((D,), jnp.float32)}
    _L3_attn_all = _L3_attn_setup()
    _L3_attn_in = {k: v for k, v in _L3_attn_all.items() if k in ('Wq', 'bq', 'Wk', 'bk', 'Wv', 'bv', 'Wc', 'We', 'Wo', 'bo', 'gamma', 'beta')}
    del _L3_attn_all

    def _L3_xattn_setup():
        import jax, jax.numpy as jnp
        import numpy as np
        HEADS = 16
        key = jax.random.key(seed)
        ks = jax.random.split(key, 6)
        b, n, m, dim = (2, 512, 128, 256)
        s = dim ** (-0.5)
        return {'x': jax.random.normal(ks[0], (b, n, dim), jnp.float32), 'mem': jax.random.normal(ks[1], (b, m, dim), jnp.float32), 'Wq': jax.random.normal(ks[2], (dim, dim), jnp.float32) * s, 'Wkv': jax.random.normal(ks[3], (dim, 2 * dim), jnp.float32) * s, 'Wout': jax.random.normal(ks[4], (dim, dim), jnp.float32) * s, 'bout': jnp.zeros((dim,), jnp.float32)}
    _L3_xattn_all = _L3_xattn_setup()
    _L3_xattn_in = {k: v for k, v in _L3_xattn_all.items() if k in ('Wq', 'Wkv', 'Wout', 'bout')}
    del _L3_xattn_all

    def _L3_ffn_setup():
        import jax, jax.numpy as jnp
        import numpy as np
        NUM_KEYS = 128
        TOP_K = 8
        NUM_HEADS = 4
        key = jax.random.key(seed)
        ks = jax.random.split(key, 8)
        b, t, d = (1, 512, 256)
        inter = 512
        E, h, ret = (4096, NUM_HEADS, 64)
        s = 0.02
        return {'hidden_states': jax.random.normal(ks[0], (b, t, d), jnp.float32), 'w_queries': jax.random.normal(ks[1], (h * ret, d), jnp.float32) * s, 'keys': jax.random.normal(ks[2], (h, NUM_KEYS, 2, ret // 2), jnp.float32) * s, 'down_embed': jax.random.normal(ks[3], (E, d), jnp.float32) * s, 'up_embed': jax.random.normal(ks[4], (E, d), jnp.float32) * s, 'w_gate': jax.random.normal(ks[5], (inter, d), jnp.float32) * s, 'w_up': jax.random.normal(ks[6], (inter, d), jnp.float32) * s, 'w_down': jax.random.normal(ks[7], (d, inter), jnp.float32) * s}
    _L3_ffn_all = _L3_ffn_setup()
    _L3_ffn_in = {k: v for k, v in _L3_ffn_all.items() if k in ('w_queries', 'keys', 'down_embed', 'up_embed', 'w_gate', 'w_up', 'w_down')}
    del _L3_ffn_all
    return {'x': x, 'ctx_1024': ctx_1024, 'fside_BxS2_0': fside_BxS2_0, 'L0_attn_W_qkv': _L0_attn_in['W_qkv'], 'L0_attn_b_qkv': _L0_attn_in['b_qkv'], 'L0_attn_W_proj': _L0_attn_in['W_proj'], 'L0_attn_b_proj': _L0_attn_in['b_proj'], 'L0_attn_s_act_qkv': _L0_attn_in['s_act_qkv'], 'L0_attn_zp_act_qkv': _L0_attn_in['zp_act_qkv'], 'L0_attn_s_w_qkv': _L0_attn_in['s_w_qkv'], 'L0_attn_zp_w_qkv': _L0_attn_in['zp_w_qkv'], 'L0_attn_s_attn': _L0_attn_in['s_attn'], 'L0_attn_zp_attn': _L0_attn_in['zp_attn'], 'L0_attn_s_act_proj': _L0_attn_in['s_act_proj'], 'L0_attn_zp_act_proj': _L0_attn_in['zp_act_proj'], 'L0_attn_s_w_proj': _L0_attn_in['s_w_proj'], 'L0_attn_zp_w_proj': _L0_attn_in['zp_w_proj'], 'L0_xattn_Wq': _L0_xattn_in['Wq'], 'L0_xattn_Wk': _L0_xattn_in['Wk'], 'L0_xattn_Wv': _L0_xattn_in['Wv'], 'L0_xattn_Wo': _L0_xattn_in['Wo'], 'L0_ffn_wg': _L0_ffn_in['wg'], 'L0_ffn_w_gate': _L0_ffn_in['w_gate'], 'L0_ffn_w_down': _L0_ffn_in['w_down'], 'L1_attn_Wq': _L1_attn_in['Wq'], 'L1_attn_bq': _L1_attn_in['bq'], 'L1_attn_Wk': _L1_attn_in['Wk'], 'L1_attn_bk': _L1_attn_in['bk'], 'L1_attn_Wv': _L1_attn_in['Wv'], 'L1_attn_bv': _L1_attn_in['bv'], 'L1_attn_q_scale': _L1_attn_in['q_scale'], 'L1_attn_q_bias': _L1_attn_in['q_bias'], 'L1_attn_k_scale': _L1_attn_in['k_scale'], 'L1_attn_k_bias': _L1_attn_in['k_bias'], 'L1_attn_v_scale': _L1_attn_in['v_scale'], 'L1_attn_v_bias': _L1_attn_in['v_bias'], 'L1_attn_Wo': _L1_attn_in['Wo'], 'L1_attn_bo': _L1_attn_in['bo'], 'L1_ffn_wqkv': _L1_ffn_in['wqkv'], 'L1_ffn_q_scale': _L1_ffn_in['q_scale'], 'L1_ffn_k_scale': _L1_ffn_in['k_scale'], 'L1_ffn_wo': _L1_ffn_in['wo'], 'L1_ffn_ln_g': _L1_ffn_in['ln_g'], 'L1_ffn_ln_b': _L1_ffn_in['ln_b'], 'L1_ffn_w1': _L1_ffn_in['w1'], 'L1_ffn_b1': _L1_ffn_in['b1'], 'L1_ffn_w2': _L1_ffn_in['w2'], 'L1_ffn_b2': _L1_ffn_in['b2'], 'L2_attn_norm_w': _L2_attn_in['norm_w'], 'L2_attn_in_proj_w': _L2_attn_in['in_proj_w'], 'L2_attn_conv_w': _L2_attn_in['conv_w'], 'L2_attn_conv_b': _L2_attn_in['conv_b'], 'L2_attn_x_proj_w': _L2_attn_in['x_proj_w'], 'L2_attn_dt_proj_w': _L2_attn_in['dt_proj_w'], 'L2_attn_dt_proj_b': _L2_attn_in['dt_proj_b'], 'L2_attn_A_log': _L2_attn_in['A_log'], 'L2_attn_D': _L2_attn_in['D'], 'L2_attn_out_proj_w': _L2_attn_in['out_proj_w'], 'L2_xattn_W': _L2_xattn_in['W'], 'L2_xattn_b': _L2_xattn_in['b'], 'L2_ffn_W_fc': _L2_ffn_in['W_fc'], 'L2_ffn_W_proj': _L2_ffn_in['W_proj'], 'L3_attn_Wq': _L3_attn_in['Wq'], 'L3_attn_bq': _L3_attn_in['bq'], 'L3_attn_Wk': _L3_attn_in['Wk'], 'L3_attn_bk': _L3_attn_in['bk'], 'L3_attn_Wv': _L3_attn_in['Wv'], 'L3_attn_bv': _L3_attn_in['bv'], 'L3_attn_Wc': _L3_attn_in['Wc'], 'L3_attn_We': _L3_attn_in['We'], 'L3_attn_Wo': _L3_attn_in['Wo'], 'L3_attn_bo': _L3_attn_in['bo'], 'L3_attn_gamma': _L3_attn_in['gamma'], 'L3_attn_beta': _L3_attn_in['beta'], 'L3_xattn_Wq': _L3_xattn_in['Wq'], 'L3_xattn_Wkv': _L3_xattn_in['Wkv'], 'L3_xattn_Wout': _L3_xattn_in['Wout'], 'L3_xattn_bout': _L3_xattn_in['bout'], 'L3_ffn_w_queries': _L3_ffn_in['w_queries'], 'L3_ffn_keys': _L3_ffn_in['keys'], 'L3_ffn_down_embed': _L3_ffn_in['down_embed'], 'L3_ffn_up_embed': _L3_ffn_in['up_embed'], 'L3_ffn_w_gate': _L3_ffn_in['w_gate'], 'L3_ffn_w_up': _L3_ffn_in['w_up'], 'L3_ffn_w_down': _L3_ffn_in['w_down']}

def reference(x, ctx_1024, fside_BxS2_0, L0_attn_W_qkv, L0_attn_b_qkv, L0_attn_W_proj, L0_attn_b_proj, L0_attn_s_act_qkv, L0_attn_zp_act_qkv, L0_attn_s_w_qkv, L0_attn_zp_w_qkv, L0_attn_s_attn, L0_attn_zp_attn, L0_attn_s_act_proj, L0_attn_zp_act_proj, L0_attn_s_w_proj, L0_attn_zp_w_proj, L0_xattn_Wq, L0_xattn_Wk, L0_xattn_Wv, L0_xattn_Wo, L0_ffn_wg, L0_ffn_w_gate, L0_ffn_w_down, L1_attn_Wq, L1_attn_bq, L1_attn_Wk, L1_attn_bk, L1_attn_Wv, L1_attn_bv, L1_attn_q_scale, L1_attn_q_bias, L1_attn_k_scale, L1_attn_k_bias, L1_attn_v_scale, L1_attn_v_bias, L1_attn_Wo, L1_attn_bo, L1_ffn_wqkv, L1_ffn_q_scale, L1_ffn_k_scale, L1_ffn_wo, L1_ffn_ln_g, L1_ffn_ln_b, L1_ffn_w1, L1_ffn_b1, L1_ffn_w2, L1_ffn_b2, L2_attn_norm_w, L2_attn_in_proj_w, L2_attn_conv_w, L2_attn_conv_b, L2_attn_x_proj_w, L2_attn_dt_proj_w, L2_attn_dt_proj_b, L2_attn_A_log, L2_attn_D, L2_attn_out_proj_w, L2_xattn_W, L2_xattn_b, L2_ffn_W_fc, L2_ffn_W_proj, L3_attn_Wq, L3_attn_bq, L3_attn_Wk, L3_attn_bk, L3_attn_Wv, L3_attn_bv, L3_attn_Wc, L3_attn_We, L3_attn_Wo, L3_attn_bo, L3_attn_gamma, L3_attn_beta, L3_xattn_Wq, L3_xattn_Wkv, L3_xattn_Wout, L3_xattn_bout, L3_ffn_w_queries, L3_ffn_keys, L3_ffn_down_embed, L3_ffn_up_embed, L3_ffn_w_gate, L3_ffn_w_up, L3_ffn_w_down):
    import jax
    import jax.numpy as jnp

    def _L0_attn_ref(x, W_qkv, b_qkv, W_proj, b_proj, s_act_qkv, zp_act_qkv, s_w_qkv, zp_w_qkv, s_attn, zp_attn, s_act_proj, zp_act_proj, s_w_proj, zp_w_proj):
        import jax, jax.numpy as jnp
        import numpy as np
        QMAX = 255.0

        def fake_quant(x, scale, zero_point):
            q = x / scale + zero_point
            q = jnp.clip(q, 0.0, QMAX)
            q = q + jax.lax.stop_gradient(jnp.round(q) - q)
            return (q - zero_point) * scale
        B, S, E = x.shape
        H = 16
        D = E // H
        x_q = fake_quant(x, s_act_qkv, zp_act_qkv)
        Wq = fake_quant(W_qkv, s_w_qkv[:, None], zp_w_qkv[:, None])
        qkv = jnp.einsum('bse,fe->bsf', x_q, Wq) + b_qkv
        qkv = qkv.reshape(B, S, 3, H, D).transpose(2, 0, 3, 1, 4)
        q, k, v = (qkv[0], qkv[1], qkv[2])
        attn = jnp.einsum('bhsd,bhtd->bhst', q, k) / jnp.sqrt(jnp.float32(D))
        attn = fake_quant(attn, s_attn, zp_attn)
        attn = jax.nn.softmax(attn, axis=-1)
        out = jnp.einsum('bhst,bhtd->bhsd', attn, v)
        out = out.transpose(0, 2, 1, 3).reshape(B, S, E)
        out_q = fake_quant(out, s_act_proj, zp_act_proj)
        Wp = fake_quant(W_proj, s_w_proj[:, None], zp_w_proj[:, None])
        return jnp.einsum('bse,fe->bsf', out_q, Wp) + b_proj

    def _L0_xattn_ref(query, key, value, attention_bias, Wq, Wk, Wv, Wo):
        import jax, jax.numpy as jnp
        import numpy as np
        EMBED = 256
        NHEAD = 16
        HEAD_DIM = EMBED // NHEAD
        B, SQ, _ = query.shape
        SKV = key.shape[1]

        def proj(x, W, S):
            return (x @ W.T).reshape(B, S, NHEAD, HEAD_DIM).transpose(0, 2, 1, 3)
        q = proj(query, Wq, SQ)
        k = proj(key, Wk, SKV)
        v = proj(value, Wv, SKV)
        scores = jnp.einsum('bhqd,bhkd->bhqk', q, k) / np.sqrt(HEAD_DIM)
        scores = scores + attention_bias[:, None, None, :]
        probs = jax.nn.softmax(scores, axis=-1)
        out = jnp.einsum('bhqk,bhkd->bhqd', probs, v)
        out = out.transpose(0, 2, 1, 3).reshape(B, SQ, EMBED)
        return out @ Wo.T

    def _L0_ffn_ref(x, wg, w_gate, w_down):
        import jax, jax.numpy as jnp
        import numpy as np
        B, S, D, E, F = (4, 512, 256, 8, 1024)
        Bb, Ss, Dd = x.shape
        Ee = wg.shape[1]
        T = Bb * Ss
        C = 2 * T // Ee
        tokens = x.reshape(T, Dd)
        logits = tokens.astype(jnp.float32) @ wg.astype(jnp.float32)
        gates = jax.nn.softmax(logits, axis=-1)
        idx1 = jnp.argmax(gates, axis=-1)
        mask1 = jax.nn.one_hot(idx1, Ee, dtype=jnp.int32)
        logits_no1 = jnp.where(mask1 > 0, -jnp.inf, logits)
        idx2 = jnp.argmax(logits_no1, axis=-1)
        mask2 = jax.nn.one_hot(idx2, Ee, dtype=jnp.int32)
        g1 = jnp.take_along_axis(gates, idx1[:, None], axis=-1)[:, 0]
        g2 = jnp.take_along_axis(gates, idx2[:, None], axis=-1)[:, 0]
        denom = jnp.clip(g1 + g2, 1e-09, None)
        g1, g2 = (g1 / denom, g2 / denom)
        loc1 = jnp.cumsum(mask1, axis=0) - mask1
        loc2 = jnp.cumsum(mask2, axis=0) - mask2 + jnp.sum(mask1, axis=0, keepdims=True)
        loc1_s = jnp.sum(loc1 * mask1, axis=-1)
        loc2_s = jnp.sum(loc2 * mask2, axis=-1)
        keep1 = (loc1_s < C).astype(x.dtype)
        keep2 = (loc2_s < C).astype(x.dtype)
        f1 = idx1 * C + jnp.minimum(loc1_s, C - 1)
        f2 = idx2 * C + jnp.minimum(loc2_s, C - 1)
        disp = jnp.zeros((Ee * C, Dd), dtype=x.dtype)
        disp = disp.at[f1].add(tokens * keep1[:, None])
        disp = disp.at[f2].add(tokens * keep2[:, None])
        disp = disp.reshape(Ee, C, Dd)
        h = jax.nn.gelu(jnp.einsum('ecd,edf->ecf', disp, w_gate), approximate=False)
        eo = jnp.einsum('ecf,efd->ecd', h, w_down).reshape(Ee * C, Dd)
        out = (g1 * keep1)[:, None].astype(x.dtype) * eo[f1] + (g2 * keep2)[:, None].astype(x.dtype) * eo[f2]
        return out.reshape(Bb, Ss, Dd)

    def _L1_attn_ref(x, Wq, bq, Wk, bk, Wv, bv, q_scale, q_bias, k_scale, k_bias, v_scale, v_bias, Wo, bo):
        import jax, jax.numpy as jnp
        import numpy as np
        B, S, H, NH = (2, 512, 256, 16)
        HD = H // NH
        EPS = 1e-06

        def _layernorm(x, scale, bias):
            x32 = x.astype(jnp.float32)
            mean = jnp.mean(x32, axis=-1, keepdims=True)
            var = jnp.mean(jnp.square(x32 - mean), axis=-1, keepdims=True)
            return (x32 - mean) * jax.lax.rsqrt(var + EPS) * scale + bias
        b, s, _ = x.shape
        q = (x @ Wq + bq).reshape(b, s, NH, HD)
        k = (x @ Wk + bk).reshape(b, s, NH, HD)
        v = (x @ Wv + bv).reshape(b, s, NH, HD)
        q = _layernorm(q, q_scale, q_bias)
        k = _layernorm(k, k_scale, k_bias)
        v = _layernorm(v, v_scale, v_bias)
        scale = HD ** (-0.5)
        scores = jnp.einsum('bqhd,bkhd->bhqk', q, k) * scale
        probs = jax.nn.softmax(scores, axis=-1)
        out = jnp.einsum('bhqk,bkhd->bqhd', probs, v).reshape(b, s, NH * HD)
        return out @ Wo + bo

    def _L1_xattn_ref(x, w1, w2):
        import jax, jax.numpy as jnp
        import numpy as np
        E, T, H, F = (8, 256, 256, 1024)
        h = jnp.einsum('eth,efh->etf', x, w1)
        g = jax.nn.gelu(h, approximate=True)
        out = jnp.einsum('etf,efh->eth', g, w2)
        return out

    def _L1_ffn_ref(x, wqkv, q_scale, k_scale, wo, ln_g, ln_b, w1, b1, w2, b2):
        import jax, jax.numpy as jnp
        import numpy as np
        DIM = 256
        DEPTH = 2
        HEADS = 8
        DIM_HEAD = 64
        WINDOW = 128
        INNER = HEADS * DIM_HEAD
        HID = int(DIM * 4 * 2 / 3)
        B, N = (2, 2048)
        QK_SCALE = 8.0

        def shift_token(t):
            t1, t2 = jnp.split(t, 2, axis=-1)
            t2 = jnp.pad(t2, ((0, 0), (1, 0), (0, 0)))[:, :-1]
            return jnp.concatenate([t1, t2], axis=-1)

        def l2norm(t):
            return t / jnp.clip(jnp.linalg.norm(t, axis=-1, keepdims=True), 1e-12)

        def rotate_half(x):
            x1, x2 = jnp.split(x, 2, axis=-1)
            return jnp.concatenate([-x2, x1], axis=-1)

        def rotary_xpos(q, k):
            n = q.shape[-2]
            half_idx = jnp.arange(0, DIM_HEAD, 2, dtype=jnp.float32)
            inv_freq = 1.0 / 10000.0 ** (half_idx / DIM_HEAD)
            t = jnp.arange(n, dtype=jnp.float32)
            freqs = t[:, None] * inv_freq[None, :]
            freqs = jnp.concatenate([freqs, freqs], axis=-1)
            base = (half_idx + 0.4 * DIM_HEAD) / (1.4 * DIM_HEAD)
            power = (t - n // 2) / float(WINDOW // 2)
            scale = base[None, :] ** power[:, None]
            scale = jnp.concatenate([scale, scale], axis=-1)
            cos, sin = (jnp.cos(freqs), jnp.sin(freqs))
            q = q * cos * scale + rotate_half(q) * sin * scale
            k = k * cos / scale + rotate_half(k) * sin / scale
            return (q, k)

        def local_attention(q, k, v):
            b, h, n, d = q.shape
            w = n // WINDOW
            bq = q.reshape(b, h, w, WINDOW, d) * QK_SCALE
            bk = k.reshape(b, h, w, WINDOW, d)
            bv = v.reshape(b, h, w, WINDOW, d)

            def look_around(t):
                p = jnp.pad(t, ((0, 0), (0, 0), (1, 0), (0, 0), (0, 0)))
                return jnp.concatenate([p[:, :, :w], p[:, :, 1:]], axis=3)
            bk, bv = (look_around(bk), look_around(bv))
            bt = jnp.arange(n).reshape(w, WINDOW)
            btp = jnp.pad(bt, ((1, 0), (0, 0)), constant_values=-1)
            btk = jnp.concatenate([btp[:w], btp[1:]], axis=1)
            sim = jnp.einsum('bhwid,bhwjd->bhwij', bq, bk)
            i = bt[:, :, None]
            j = btk[:, None, :]
            mask = (i < j) | (i > j + WINDOW) | (j == -1)
            sim = jnp.where(mask, -jnp.finfo(sim.dtype).max, sim)
            attn = jax.nn.softmax(sim, axis=-1)
            out = jnp.einsum('bhwij,bhwjd->bhwid', attn, bv)
            return out.reshape(b, h, n, d)

        def _layer(x, wqkv, qs, ksc, wo, lg, lb, w1, b1, w2, b2):
            b, n, _ = x.shape
            h = shift_token(x)
            qkv = h @ wqkv
            q, k, v = jnp.split(qkv, 3, axis=-1)
            to_heads = lambda t: t.reshape(b, n, HEADS, DIM_HEAD).transpose(0, 2, 1, 3)
            q, k, v = (to_heads(q), to_heads(k), to_heads(v))
            q = l2norm(q) * qs
            k = l2norm(k) * ksc
            q, k = rotary_xpos(q, k)
            o = local_attention(q, k, v)
            o = o.transpose(0, 2, 1, 3).reshape(b, n, INNER)
            x = x + o @ wo
            h = shift_token(x)
            mu = h.mean(-1, keepdims=True)
            var = h.var(-1, keepdims=True)
            h = (h - mu) / jnp.sqrt(var + 1e-05) * lg + lb
            h = h @ w1 + b1
            a, g = jnp.split(h, 2, axis=-1)
            h = a * jax.nn.gelu(g, approximate=False)
            x = x + h @ w2 + b2
            return x
        for l in range(DEPTH):
            x = _layer(x, wqkv[l], q_scale[l], k_scale[l], wo[l], ln_g[l], ln_b[l], w1[l], b1[l], w2[l], b2[l])
        return x

    def _L2_attn_ref(x, norm_w, in_proj_w, conv_w, conv_b, x_proj_w, dt_proj_w, dt_proj_b, A_log, D, out_proj_w):
        import jax, jax.numpy as jnp
        import numpy as np
        D_MODEL = 256
        D_INNER = 512
        D_STATE = 16
        D_CONV = 4
        DT_RANK = 64
        BATCH = 2
        SEQ = 256

        def _silu(v):
            return v * jax.nn.sigmoid(v)
        b, l, d = x.shape
        x_copy = x
        h = x * jax.lax.rsqrt(jnp.mean(x * x, axis=-1, keepdims=True) + 1e-05) * norm_w
        x_and_res = h @ in_proj_w.T
        xs, res = jnp.split(x_and_res, 2, axis=-1)
        xc = jnp.transpose(xs, (0, 2, 1))
        xc = jax.lax.conv_general_dilated(xc, conv_w, window_strides=(1,), padding=[(D_CONV - 1, 0)], feature_group_count=D_INNER, dimension_numbers=('NCH', 'OIH', 'NCH'))
        xc = xc + conv_b[None, :, None]
        u = _silu(jnp.transpose(xc, (0, 2, 1)))
        A = -jnp.exp(A_log)
        x_dbl = u @ x_proj_w.T
        delta, Bm, Cm = jnp.split(x_dbl, [DT_RANK, DT_RANK + D_STATE], axis=-1)
        delta = jax.nn.softplus(delta @ dt_proj_w.T + dt_proj_b)
        deltaA = jnp.exp(jnp.einsum('bld,dn->bldn', delta, A))
        deltaB_u = (delta * u)[..., None] * Bm[:, :, None, :]

        def step(state, inp):
            dA, dBu, c = inp
            state = dA * state + dBu
            y = jnp.einsum('bdn,bn->bd', state, c)
            return (state, y)
        init = jnp.zeros((b, D_INNER, D_STATE), dtype=u.dtype)
        _, ys = jax.lax.scan(step, init, (jnp.transpose(deltaA, (1, 0, 2, 3)), jnp.transpose(deltaB_u, (1, 0, 2, 3)), jnp.transpose(Cm, (1, 0, 2))))
        y = jnp.transpose(ys, (1, 0, 2)) + u * D
        y = y * _silu(res)
        return y @ out_proj_w.T + x_copy

    def _L2_xattn_ref(x1, x2, W, b):
        import jax, jax.numpy as jnp
        import numpy as np
        D1, D2, D3 = (256, 256, 256)
        d1 = x1.shape[-1]
        W1 = W[:, :d1]
        W2 = W[:, d1:]
        part1 = jnp.einsum('bld,ed->ble', x1, W1)
        part2 = jnp.einsum('bld,ed->be', x2, W2) / x2.shape[1]
        return part1 + part2[:, None, :] + b

    def _L2_ffn_ref(x, W_fc, W_proj):
        import jax, jax.numpy as jnp
        import numpy as np
        import math
        BETA = 0.9
        THRESHOLD = 1.0
        NUM_STEPS = 5
        ALPHA = 2.0

        @jax.custom_vjp
        def spike_fn(u):
            return (u > 0).astype(u.dtype)

        def _spike_fwd(u):
            return (spike_fn(u), u)

        def _spike_bwd(u, g):
            s = jnp.pi / 2.0 * ALPHA * u
            return (g * (ALPHA / 2.0) / (1.0 + s * s),)
        spike_fn.defvjp(_spike_fwd, _spike_bwd)
        h = jnp.square(jax.nn.relu(jnp.einsum('bsd,fd->bsf', x, W_fc)))
        y = jnp.einsum('bsf,df->bsd', h, W_proj)

        def step(mem, _):
            reset = jax.lax.stop_gradient(spike_fn(mem - THRESHOLD))
            mem_new = BETA * mem + y - reset * THRESHOLD
            spk = spike_fn(mem_new - THRESHOLD)
            return (mem_new, spk)
        mem0 = jnp.zeros_like(y)
        _, spks = jax.lax.scan(step, mem0, None, length=NUM_STEPS)
        return jnp.sum(spks, axis=0) / NUM_STEPS

    def _L3_attn_ref(x, Wq, bq, Wk, bk, Wv, bv, Wc, We, Wo, bo, gamma, beta):
        import jax, jax.numpy as jnp
        import numpy as np
        D = 256
        H = 16
        HKV = 4
        HD = D // H
        L = 64
        EPS = 1e-06
        LN_EPS = 1e-05
        B, S = (2, 256)

        def _feat(x):
            return jax.nn.elu(x) + 1.0
        b, s, _ = x.shape
        residual = x
        q = x @ Wq + bq
        k = x @ Wk + bk
        v = x @ Wv + bv
        k = k @ Wc @ We
        v = v @ Wc @ We
        q = q.reshape(b, s, H, HD).transpose(0, 2, 1, 3)
        k = k.reshape(b, s, HKV, HD).transpose(0, 2, 1, 3)
        v = v.reshape(b, s, HKV, HD).transpose(0, 2, 1, 3)
        rep = H // HKV
        k = jnp.repeat(k, rep, axis=1)
        v = jnp.repeat(v, rep, axis=1)
        qf = _feat(q)
        kf = _feat(k)
        kv = jnp.einsum('bhsf,bhsd->bhsfd', kf, v)
        kv_cum = jnp.cumsum(kv, axis=2)
        num = jnp.einsum('bhsf,bhsfd->bhsd', qf, kv_cum)
        den = jnp.einsum('bhsf,bhsf->bhs', qf, jnp.cumsum(kf, axis=2))[..., None] + EPS
        o = num / den
        o = o.transpose(0, 2, 1, 3).reshape(b, s, D)
        o = o @ Wo + bo
        y = residual + o
        mu = jnp.mean(y, axis=-1, keepdims=True)
        var = jnp.var(y, axis=-1, keepdims=True)
        return (y - mu) / jnp.sqrt(var + LN_EPS) * gamma + beta

    def _L3_xattn_ref(x, mem, Wq, Wkv, Wout, bout):
        import jax, jax.numpy as jnp
        import numpy as np
        HEADS = 16
        b, n, dim = x.shape
        h = HEADS
        d = dim // h
        scale = d ** (-0.5)
        mem_len = mem.shape[1]
        q = x @ Wq
        xc = jnp.concatenate((mem, x), axis=1)
        kv = xc @ Wkv
        k, v = jnp.split(kv, 2, axis=-1)

        def to_heads(t):
            bb, nn, _ = t.shape
            return t.reshape(bb, nn, h, d).transpose(0, 2, 1, 3)
        q, k, v = (to_heads(q), to_heads(k), to_heads(v))
        dots = jnp.einsum('bhid,bhjd->bhij', q, k) * scale
        j = dots.shape[-1]
        i_idx = jnp.arange(n)[:, None]
        j_idx = jnp.arange(j)[None, :]
        mask = j_idx > i_idx + mem_len
        dots = jnp.where(mask[None, None], -jnp.inf, dots)
        attn = jax.nn.softmax(dots, axis=-1)
        out = jnp.einsum('bhij,bhjd->bhid', attn, v)
        out = out.transpose(0, 2, 1, 3).reshape(b, n, dim)
        return out @ Wout + bout

    def _L3_ffn_ref(hidden_states, w_queries, keys, down_embed, up_embed, w_gate, w_up, w_down):
        import jax, jax.numpy as jnp
        import numpy as np
        NUM_KEYS = 128
        TOP_K = 8
        NUM_HEADS = 4
        b, t, d = hidden_states.shape
        h, nk, _, n = keys.shape
        k = TOP_K
        q = (hidden_states @ w_queries.T).reshape(b, t, 2, h, n)
        sim = jnp.einsum('btphn,hkpn->pbthk', q, keys)
        sx, ix = jax.lax.top_k(sim[0], k)
        sy, iy = jax.lax.top_k(sim[1], k)
        all_scores = (sx[..., :, None] + sy[..., None, :]).reshape(b, t, h, k * k)
        all_idx = (ix[..., :, None] * nk + iy[..., None, :]).reshape(b, t, h, k * k)
        scores, pos = jax.lax.top_k(all_scores, k)
        indices = jnp.take_along_axis(all_idx, pos, axis=-1)
        de = down_embed[indices]
        ue = up_embed[indices]
        ew = jnp.einsum('btd,bthkd->bthk', hidden_states, de)
        ew = jax.nn.silu(ew) * jax.nn.softmax(scores, axis=-1)
        experts_states = jnp.einsum('bthk,bthkd->btd', ew, ue)
        mlp = jax.nn.silu(hidden_states @ w_gate.T) * (hidden_states @ w_up.T) @ w_down.T
        return mlp + experts_states
    x = _layernorm(x + _L0_attn_ref(x, L0_attn_W_qkv, L0_attn_b_qkv, L0_attn_W_proj, L0_attn_b_proj, L0_attn_s_act_qkv, L0_attn_zp_act_qkv, L0_attn_s_w_qkv, L0_attn_zp_w_qkv, L0_attn_s_attn, L0_attn_zp_attn, L0_attn_s_act_proj, L0_attn_zp_act_proj, L0_attn_s_w_proj, L0_attn_zp_w_proj), axis=-1)
    x = _layernorm(x + _L0_xattn_ref(x, ctx_1024, ctx_1024, fside_BxS2_0, L0_xattn_Wq, L0_xattn_Wk, L0_xattn_Wv, L0_xattn_Wo), axis=-1)
    x = _layernorm(x + _L0_ffn_ref(x, L0_ffn_wg, L0_ffn_w_gate, L0_ffn_w_down), axis=-1)
    x = _layernorm(x + _L1_attn_ref(x, L1_attn_Wq, L1_attn_bq, L1_attn_Wk, L1_attn_bk, L1_attn_Wv, L1_attn_bv, L1_attn_q_scale, L1_attn_q_bias, L1_attn_k_scale, L1_attn_k_bias, L1_attn_v_scale, L1_attn_v_bias, L1_attn_Wo, L1_attn_bo), axis=-1)
    x = _layernorm(x + _L1_xattn_ref(x, ctx_1024, ctx_1024), axis=-1)
    x = _layernorm(x + _L1_ffn_ref(x, L1_ffn_wqkv, L1_ffn_q_scale, L1_ffn_k_scale, L1_ffn_wo, L1_ffn_ln_g, L1_ffn_ln_b, L1_ffn_w1, L1_ffn_b1, L1_ffn_w2, L1_ffn_b2), axis=-1)
    x = _layernorm(x + _L2_attn_ref(x, L2_attn_norm_w, L2_attn_in_proj_w, L2_attn_conv_w, L2_attn_conv_b, L2_attn_x_proj_w, L2_attn_dt_proj_w, L2_attn_dt_proj_b, L2_attn_A_log, L2_attn_D, L2_attn_out_proj_w), axis=-1)
    x = _layernorm(x + _L2_xattn_ref(x, ctx_1024, L2_xattn_W, L2_xattn_b), axis=-1)
    x = _layernorm(x + _L2_ffn_ref(x, L2_ffn_W_fc, L2_ffn_W_proj), axis=-1)
    x = _layernorm(x + _L3_attn_ref(x, L3_attn_Wq, L3_attn_bq, L3_attn_Wk, L3_attn_bk, L3_attn_Wv, L3_attn_bv, L3_attn_Wc, L3_attn_We, L3_attn_Wo, L3_attn_bo, L3_attn_gamma, L3_attn_beta), axis=-1)
    x = _layernorm(x + _L3_xattn_ref(x, ctx_1024, L3_xattn_Wq, L3_xattn_Wkv, L3_xattn_Wout, L3_xattn_bout), axis=-1)
    x = _layernorm(x + _L3_ffn_ref(x, L3_ffn_w_queries, L3_ffn_keys, L3_ffn_down_embed, L3_ffn_up_embed, L3_ffn_w_gate, L3_ffn_w_up, L3_ffn_w_down), axis=-1)
    return x

_drawn_inputs = setup_inputs


def setup_inputs(seed=0):
    import zlib

    import numpy as np

    out = dict(_drawn_inputs(seed))
    spreads = {'L1_attn_bq': (0.0, 0.606),
     'L1_attn_bk': (0.0, 0.8),
     'L1_attn_bv': (0.0, 0.1),
     'L1_attn_q_scale': (1.0, 0.6),
     'L1_attn_q_bias': (0.0, 0.665),
     'L1_attn_k_scale': (1.0, 0.6),
     'L1_attn_k_bias': (0.0, 2.0),
     'L1_attn_v_scale': (1.0, 0.2),
     'L1_attn_v_bias': (0.0, 0.1),
     'L1_attn_bo': (0.0, 0.1),
     'L1_ffn_q_scale': (1.0, 0.6),
     'L1_ffn_k_scale': (1.0, 0.6),
     'L1_ffn_ln_g': (1.0, 0.6),
     'L1_ffn_ln_b': (0.0, 0.763),
     'L1_ffn_b1': (0.0, 0.405),
     'L1_ffn_b2': (0.0, 0.1),
     'L2_attn_norm_w': (1.0, 0.6),
     'L2_attn_conv_b': (0.0, 0.8),
     'L2_attn_dt_proj_b': (0.0, 0.8),
     'L2_attn_D': (1.0, 0.6),
     'L3_attn_bq': (0.0, 2.0),
     'L3_attn_bk': (0.0, 2.0),
     'L3_attn_bv': (0.0, 0.8),
     'L3_attn_bo': (0.0, 0.8),
     'L3_attn_gamma': (1.0, 0.2),
     'L3_attn_beta': (0.0, 0.1),
     'L3_xattn_bout': (0.0, 0.1)}
    factors = {'L0_attn_s_w_qkv': 15.298,
     'L0_attn_zp_w_qkv': 15.826,
     'L0_attn_s_w_proj': 8.0,
     'L0_attn_zp_w_proj': 8.0,
     'L2_attn_in_proj_w': 7.904,
     'L2_attn_conv_w': 8.0,
     'L2_attn_x_proj_w': 8.0,
     'L2_attn_dt_proj_w': 8.0,
     'L2_attn_A_log': 8.0,
     'L2_attn_out_proj_w': 7.9,
     'L3_attn_Wq': 8.0,
     'L3_attn_Wk': 8.0,
     'L3_attn_Wv': 8.0,
     'L3_attn_Wc': 8.0,
     'L3_attn_We': 8.0,
     'L3_attn_Wo': 8.0,
     'L3_ffn_w_queries': 8.0,
     'L3_ffn_keys': 8.0,
     'L3_ffn_down_embed': 3.523,
     'L3_ffn_up_embed': 4.562,
     'L0_attn_b_qkv': 3.754,
     'L0_attn_b_proj': 8.0}
    for name, (base, spread) in spreads.items():
        noise = np.random.default_rng([zlib.crc32(name.encode()), seed]).standard_normal(out[name].shape)
        drawn = base * np.exp(spread * noise) if base else spread * noise
        out[name] = jnp.asarray(drawn.astype(out[name].dtype))
    for name, factor in factors.items():
        out[name] = (out[name] * factor).astype(out[name].dtype)
    return out
```

```python
from contextlib import ExitStack, contextmanager

import concourse.bass as bass
from concourse import mybir

F32 = mybir.dt.float32
U32 = mybir.dt.uint32
ALU = mybir.AluOpType
ACT = mybir.ActivationFunctionType
AX = mybir.AxisListType

P = 128
BATCH, SEQ, DIM = 4, 1024, 256
TOKENS = BATCH * SEQ
CTX = 77
FC = DIM // P
GROUP = 512
GROUPS = TOKENS // GROUP
HEADS, HEAD = 16, 16
SLOT = 32
PACK = P // SLOT
HGS = HEADS // PACK
PADDED = HEADS * SLOT
ONE = HEAD
BIAS = HEAD + 1
TILES = SEQ // P
FAR = -float(2 ** 60)
ROUND = float(1.5 * 2 ** 23)
QMAX = 255.0
C_ID, C_MEAN, C_ONES, C_HEADMEAN, C_DEN, C_FART, C_FARN, C_KEEPT, C_BEFORE, C_BAND, C_SELF = (P * n for n in range(11))
C_IOTA = 11 * P
C_ROWS = C_IOTA + P
C_END = C_ROWS + 1


def sbuf(nc, name, shape, dtype):
    return nc.sbuf_tensor(name, shape, dtype, allow_name_mangling=True)


def banks(nc, name, shape, dtype):
    return nc.psum_tensor(name, shape, dtype, allow_name_mangling=True)


@contextmanager
def step(nc, names):
    with ExitStack() as ctx:
        sems = [ctx.enter_context(nc.semaphore(n)) for n in names.split()]
        with nc.Block() as block:
            yield (block, *sems)
        nums = sorted(s.num for s in sems)
        start = 0
        for n in range(len(nums)):
            if n + 1 == len(nums) or nums[n + 1] != nums[n] + 1:
                nc.sync.sem_clear(range(nums[start], nums[n] + 1))
                start = n + 1
        nc.all_engine_barrier(sem_only=True)


def in_order(eng, sem):
    count = [0]

    def then(instruction):
        count[0] += 1
        instruction.then_inc(sem, 1)
        eng.wait_ge(sem, count[0])

    return then


def load(nc, pairs):
    with step(nc, "loaded") as (block, loaded):
        @block.sync
        def _(sp):
            for dst, src in pairs:
                sp.dma_start(dst, src).then_inc(loaded, 16)
            sp.wait_ge(loaded, 16 * len(pairs))


class Chip:

    def __init__(self, nc, ctx, io):
        self.nc, self.io, self.ctx = nc, io, ctx
        self.xt = ctx.enter_context(sbuf(nc, "residual", [P, FC, TOKENS], F32))
        self.const = ctx.enter_context(sbuf(nc, "constants", [P, C_END], F32))
        self.eps = ctx.enter_context(sbuf(nc, "epsilons", [P, 4], F32))
        self.z = ctx.enter_context(sbuf(nc, "norm_sum", [P, FC, GROUP], F32))
        self.sq = ctx.enter_context(sbuf(nc, "norm_squares", [P, FC, GROUP], F32))
        self.rstd = ctx.enter_context(sbuf(nc, "norm_rstd", [P, GROUP], F32))

    def keep_semaphore(self, name):
        return self.ctx.enter_context(self.nc.semaphore(name))

    def c(self, start, n=P):
        return self.const[:, start:start + n]


def add_norm(chip, tok, psum, product=None, ready=None, bias=None, affine=None, keeps=1.0):
    nc, z, sq, rstd = chip.nc, chip.z, chip.sq, chip.rstd
    y_ps, mean_ps, var_ps = psum[:, 0:2, :], psum[:, 2, :], psum[:, 3, :]
    rounds = 2 if affine else 1
    x = lambda c: chip.xt[:, c, tok]
    with step(nc, "y_ready sum_ready mean_ready centred squares_ready var_ready rstd_ready dve_step") as (
            block, y_ready, sum_ready, mean_ready, centred, squares_ready, var_ready, rstd_ready, dve_step):
        @block.tensor
        def _(pe):
            if product:
                weights, inputs = product
                chunks = weights.shape[1]
                for c in range(FC):
                    for k in range(chunks):
                        last = nc.tensor.matmul(y_ps[:, c, :], weights[:, k, c * P:(c + 1) * P], inputs(k),
                                                start=(k == 0), stop=(k == chunks - 1))
                    last.then_inc(y_ready, 1)
            for r in range(rounds):
                pe.wait_ge(sum_ready, FC * (r + 1))
                for c in range(FC):
                    last = nc.tensor.matmul(mean_ps, chip.c(C_MEAN), z[:, c, :], start=(c == 0), stop=(c == FC - 1))
                last.then_inc(mean_ready, 1)
                pe.wait_ge(squares_ready, FC * (r + 1))
                for c in range(FC):
                    last = nc.tensor.matmul(var_ps, chip.c(C_MEAN), sq[:, c, :], start=(c == 0), stop=(c == FC - 1))
                last.then_inc(var_ready, 1)

        @block.scalar
        def _(act):
            for r in range(rounds):
                for c in range(FC):
                    act.wait_ge(centred, FC * r + c + 1)
                    nc.scalar.activation(sq[:, c, :], z[:, c, :], ACT.Square).then_inc(squares_ready, 1)
                act.wait_ge(var_ready, r + 1)
                nc.scalar.activation(rstd[:, :], var_ps, ACT.Sqrt, bias=chip.eps[:, 0:1]).then_inc(rstd_ready, 1)

        @block.vector
        def _(dve):
            then = in_order(dve, dve_step)
            for c in range(FC):
                if product:
                    dve.wait_ge(y_ready, c + 1)
                y = y_ps[:, c, :] if product else ready(c)
                if keeps != 1.0:
                    nc.vector.scalar_tensor_tensor(out=z[:, c, :], in0=x(c), scalar=keeps, in1=y,
                                                   op0=ALU.mult, op1=ALU.add).then_inc(sum_ready, 1)
                elif bias is None:
                    nc.vector.tensor_tensor(z[:, c, :], y, x(c), ALU.add).then_inc(sum_ready, 1)
                else:
                    nc.vector.scalar_tensor_tensor(out=z[:, c, :], in0=y, scalar=bias[:, c:c + 1], in1=x(c),
                                                   op0=ALU.add, op1=ALU.add).then_inc(sum_ready, 1)
            for r in range(rounds):
                dve.wait_ge(mean_ready, r + 1)
                for c in range(FC):
                    nc.vector.tensor_tensor(z[:, c, :], z[:, c, :], mean_ps, ALU.subtract).then_inc(centred, 1)
                dve.wait_ge(rstd_ready, r + 1)
                then(nc.vector.reciprocal(rstd[:, :], rstd[:, :]))
                dve.wait_ge(squares_ready, FC * (r + 1))
                for c in range(FC):
                    if r == rounds - 1:
                        nc.vector.tensor_tensor(x(c), z[:, c, :], rstd[:, :], ALU.mult)
                    else:
                        scale, shift = affine
                        then(nc.vector.tensor_tensor(z[:, c, :], z[:, c, :], rstd[:, :], ALU.mult))
                        then(nc.vector.tensor_scalar(z[:, c, :], z[:, c, :], scale[:, c:c + 1], shift[:, c:c + 1],
                                                     ALU.mult, ALU.add))
                        nc.vector.tensor_tensor(z[:, c, :], z[:, c, :], x(c), ALU.add).then_inc(sum_ready, 1)


def group_slice(g):
    return bass.ds(g * GROUP, GROUP)


def output_projection(chip, ot, weights, bias=None, affine=None):
    nc = chip.nc
    with banks(nc, "norm_psum", [P, 4, GROUP], F32) as psum, nc.Fori(0, GROUPS) as g:
        add_norm(chip, group_slice(g), psum, product=(weights, lambda k: ot[:, k, group_slice(g)]),
                 bias=bias, affine=affine)


def head_attention(chip, mode, weights, biases, sources, ot, ctx_source=None, ctx_bias=None, norm=None, quant=None):
    nc = chip.nc
    quantised, cross, normed, linear = mode == "quant", mode == "cross", mode == "heads_norm", mode == "linear"
    own = not cross
    causal = mode in ("causal", "linear")
    context = mode in ("cross", "causal")
    maxed = mode in ("cross", "causal", "heads_norm")
    chunks = weights.shape[2]
    scale = 1.0 if linear else HEAD ** -0.5
    halves = SEQ // GROUP
    per_half = GROUP // P
    with ExitStack() as ctx:
        sb = lambda name, shape: ctx.enter_context(sbuf(nc, name, shape, F32))
        w = sb("head_weights", [P, 3, chunks, P])
        bs = sb("head_biases", [P, 3])
        qkv = sb("head_qkv", [P, 3, SEQ])
        q_t, k_t, v_t = qkv[:, 0, :], qkv[:, 1, :], qkv[:, 2, :]
        v = sb("head_values", [P, TILES, P])
        probs = sb("probs", [P, 3, 2, GROUP])
        raw_out = sb("raw_out", [P, halves, GROUP])
        rden = sb("recip_den", [P, halves, GROUP])
        if context:
            kv_c = sb("context_kv", [P, 2, CTX])
            v_c = sb("context_values", [P, P])
        if maxed:
            row_max = sb("row_max", [P, TILES, P])
            row_max_c = sb("row_max_context", [P, TILES, PACK])
        if normed or linear:
            head_sq = sb("head_squares", [P, 2, GROUP])
            head_rstd = sb("head_rstd", [P, 2, GROUP])
        s_ps = ctx.enter_context(banks(nc, "scores", [P, 6, GROUP], F32))
        o_ps = ctx.enter_context(banks(nc, "outputs", [P, 2, GROUP], F32))
        if maxed:
            with step(nc, "cleared") as (block, cleared):
                @block.gpsimd
                def _(pool):
                    nc.gpsimd.memset(row_max[:, :, :], 0.0).then_inc(cleared, 1)
                    pool.wait_ge(cleared, 1)

        flat = lambda first, n: s_ps[:, first:first + 2, :].rearrange("p b n -> p (b n)")[:, 0:n]

        def items(half):
            out = [(None, 0)] if context else []
            if own:
                tiles = per_half * (half + 1) if causal else TILES
                out += [(kt, max(0, kt - per_half * half) * P if causal else 0) for kt in range(tiles)]
            return out

        plan = [(half, kt, off, pair) for half in range(halves) for kt, off in items(half) for pair in range(2)]
        diagonal = lambda half, kt: causal and kt is not None and kt >= per_half * half
        done_by = lambda n, by_dve: sum(1 for h, kt, _, _ in plan[:n + 1] if (linear and diagonal(h, kt)) == by_dve)

        with nc.Fori(0, HGS) as hg:
            with step(nc, "staged") as (block, staged):
                @block.scalar
                def _(act):
                    for t in range(3):
                        for c in range(chunks):
                            nc.scalar.activation(w[:, t, c, :], weights[:, t, c, bass.ds(hg * P, P)], ACT.Copy).then_inc(staged, 1)
                    nc.scalar.activation(bs[:, :], biases[:, :, bass.ds(hg, 1)].rearrange("p t o -> p (t o)"), ACT.Copy).then_inc(staged, 1)
                    act.wait_ge(staged, 3 * chunks + 1)
            with nc.Fori(0, BATCH) as b:
                with step(nc, "projected q_ready kv_ready context_ready squares_ready var_ready rstd_ready normed_ready "
                              "turned values_ready context_values_ready natural_ready rowmax_taken rowmax_ready max_turned "
                              "q_final scores_ready levels_ready probs_ready diagonal_ready outputs_added raw_ready "
                              "den_ready dve_step") as (
                        block, projected, q_ready, kv_ready, context_ready, squares_ready, var_ready, rstd_ready, normed_ready,
                        turned, values_ready, context_values_ready, natural_ready, rowmax_taken, rowmax_ready, max_turned,
                        q_final, scores_ready, levels_ready, probs_ready, diagonal_ready, outputs_added, raw_ready,
                        den_ready, dve_step):
                    own_jobs = [(t, j) for t in range(3 if own else 1) for j in range(halves)]
                    tok = lambda j: bass.ds(b * SEQ + j * GROUP, GROUP)

                    @block.tensor
                    def _(pe):
                        for n, (t, j) in enumerate(own_jobs):
                            for c in range(chunks):
                                last = nc.tensor.matmul(s_ps[:, n, :], w[:, t, c, :], sources[t](c, tok(j)),
                                                        start=(c == 0), stop=(c == chunks - 1))
                            last.then_inc(projected, 1)
                        if context:
                            for t in (1, 2):
                                biased = t == 1 and ctx_bias is not None
                                for c in range(chunks):
                                    last = nc.tensor.matmul(o_ps[:, t - 1, 0:CTX], w[:, t, c, :], ctx_source(c, b),
                                                            start=(c == 0), stop=(c == chunks - 1 and not biased))
                                if biased:
                                    last = nc.tensor.matmul(o_ps[:, 0, 0:CTX], ctx_bias[0], ctx_bias[1](b),
                                                            start=False, stop=True)
                                last.then_inc(projected, 1)
                        if normed:
                            for n in range(len(own_jobs)):
                                pe.wait_ge(squares_ready, n + 1)
                                if n >= 2:
                                    pe.wait_ge(rstd_ready, n - 1)
                                nc.tensor.matmul(o_ps[:, n % 2, :], chip.c(C_HEADMEAN), head_sq[:, n % 2, :],
                                                 start=True, stop=True).then_inc(var_ready, 1)
                        if own:
                            if normed:
                                pe.wait_ge(normed_ready, 3 * halves)
                            elif linear:
                                pe.wait_ge(normed_ready, 2 * halves)
                                pe.wait_ge(kv_ready, halves)
                            else:
                                pe.wait_ge(q_ready, halves)
                                pe.wait_ge(kv_ready, 2 * halves)
                            for kt in range(TILES):
                                last = nc.tensor.transpose(s_ps[:, kt // per_half, (kt % per_half) * P:(kt % per_half + 1) * P],
                                                           v_t[:, kt * P:(kt + 1) * P], chip.c(C_ID))
                            last.then_inc(turned, 1)
                        if context:
                            pe.wait_ge(context_ready, 2)
                            pe.wait_ge(q_ready, 2)
                            nc.tensor.transpose(s_ps[0:CTX, 2, 0:P], kv_c[:, 1, :], chip.c(C_ID)).then_inc(turned, 1)
                        if maxed:
                            if own:
                                pe.wait_ge(values_ready, 1)
                            if context:
                                pe.wait_ge(context_values_ready, 1)
                            for n in range(TILES * PACK):
                                qt, h = divmod(n, PACK)
                                ring = 3 * (n % 2)
                                hp = slice(SLOT * h, SLOT * (h + 1))
                                if n >= 2:
                                    pe.wait_ge(rowmax_taken, n - 1)
                                lhs = q_t[hp, qt * P:(qt + 1) * P]
                                seen = 0 if cross else (qt + 1) * P if causal else SEQ
                                for j in range((seen + GROUP - 1) // GROUP):
                                    cols = min(GROUP, seen - j * GROUP)
                                    edge = causal and j == qt // per_half
                                    last = nc.tensor.matmul(s_ps[:, ring + j, 0:cols], lhs, k_t[hp, j * GROUP:j * GROUP + cols],
                                                            start=True, stop=not edge)
                                    if edge:
                                        last = nc.tensor.matmul(s_ps[:, ring + j, cols - P:cols], chip.c(C_ID), chip.c(C_FARN),
                                                                start=False, stop=True)
                                if context:
                                    last = nc.tensor.matmul(s_ps[:, ring + 2, 0:CTX], lhs, kv_c[hp, 0, :], start=True, stop=True)
                                last.then_inc(natural_ready, 1)
                            if own and context:
                                pe.wait_ge(rowmax_ready, 1)
                            else:
                                pe.wait_ge(rowmax_taken, TILES * PACK)
                            for qt in range(TILES):
                                last = nc.tensor.transpose(s_ps[:, qt // per_half, (qt % per_half) * P:(qt % per_half + 1) * P],
                                                           row_max[:, qt, :], chip.c(C_ID))
                            last.then_inc(max_turned, 1)
                            pe.wait_ge(q_final, 1)
                        else:
                            pe.wait_ge(values_ready, 1)

                        def scores(n):
                            half, kt, off, pair = plan[n]
                            rows = CTX if kt is None else P
                            if n >= 3:
                                if quantised:
                                    pe.wait_ge(levels_ready, n - 2)
                                else:
                                    if done_by(n - 3, False):
                                        pe.wait_ge(probs_ready, done_by(n - 3, False))
                                    if linear and done_by(n - 3, True):
                                        pe.wait_ge(diagonal_ready, done_by(n - 3, True))
                            for i in range(2):
                                h = 2 * pair + i
                                kp = SLOT if not linear else HEAD
                                hp = slice(SLOT * h, SLOT * h + kp)
                                keys = kv_c[hp, 0, :] if kt is None else k_t[hp, kt * P:(kt + 1) * P]
                                out = s_ps[0:rows, 2 * (n % 3) + i, :]
                                edge = diagonal(half, kt) and not linear
                                last = nc.tensor.matmul(out[:, off:GROUP], keys, q_t[hp, half * GROUP + off:(half + 1) * GROUP],
                                                        start=True, stop=not edge)
                                if edge:
                                    last = nc.tensor.matmul(out[:, off:off + P], chip.c(C_ID), chip.c(C_FART),
                                                            start=False, stop=True)
                            last.then_inc(scores_ready, 1)

                        def outputs(n):
                            half, kt, off, pair = plan[n]
                            rows = CTX if kt is None else P
                            by_dve = linear and diagonal(half, kt)
                            pe.wait_ge(diagonal_ready if by_dve else probs_ready, done_by(n, by_dve))
                            first = (kt, off) == items(half)[0]
                            final = (kt, off) == items(half)[-1]
                            for i in range(2):
                                h = 2 * pair + i
                                hs = slice(SLOT * h, SLOT * (h + 1))
                                vals = v_c[0:CTX, hs] if kt is None else v[:, kt, hs]
                                last = nc.tensor.matmul(o_ps[hs, half, off:GROUP], vals, probs[0:rows, n % 3, i, off:GROUP],
                                                        start=first, stop=final)
                            last.then_inc(outputs_added, 1)

                        for n in range(len(plan) + 2):
                            if n < len(plan):
                                scores(n)
                            if n >= 2:
                                outputs(n - 2)
                        for half in range(halves):
                            pe.wait_ge(raw_ready, half + 1)
                            nc.tensor.matmul(s_ps[:, half, :], chip.c(C_DEN), raw_out[:, half, :],
                                             start=True, stop=True).then_inc(den_ready, 1)

                    @block.scalar
                    def _(act):
                        def root(n):
                            act.wait_ge(var_ready, n + 1)
                            if n >= 2:
                                act.wait_ge(normed_ready, n - 1)
                            nc.scalar.activation(head_rstd[:, n % 2, :], o_ps[:, n % 2, :], ACT.Sqrt,
                                                 bias=chip.eps[:, 1:2]).then_inc(rstd_ready, 1)

                        if normed:
                            for n, (t, j) in enumerate(own_jobs):
                                act.wait_ge(q_ready, n + 1)
                                if n >= 2:
                                    act.wait_ge(var_ready, n - 1)
                                nc.scalar.activation(head_sq[:, n % 2, :], qkv[:, t, j * GROUP:(j + 1) * GROUP],
                                                     ACT.Square).then_inc(squares_ready, 1)
                                if n >= 1:
                                    root(n - 1)
                            root(len(own_jobs) - 1)
                        elif own:
                            if linear:
                                for n in range(2 * halves):
                                    act.wait_ge(squares_ready, n + 1)
                                    if n >= 2:
                                        act.wait_ge(normed_ready, n - 1)
                                    nc.scalar.activation(head_rstd[:, n % 2, :], head_sq[:, n % 2, :], ACT.Exp).then_inc(rstd_ready, 1)
                            for n, (t, j) in list(enumerate(own_jobs))[2 * halves if linear else halves:]:
                                act.wait_ge(projected, n + 1)
                                nc.scalar.activation(qkv[:, t, j * GROUP:(j + 1) * GROUP], s_ps[:, n, :], ACT.Identity,
                                                     bias=bs[:, t:t + 1]).then_inc(kv_ready, 1)
                        if context:
                            for t in (1, 2):
                                act.wait_ge(projected, len(own_jobs) + t)
                                nc.scalar.activation(kv_c[:, t - 1, :], o_ps[:, t - 1, 0:CTX], ACT.Identity,
                                                     bias=bs[:, t:t + 1]).then_inc(context_ready, 1)
                        if own:
                            act.wait_ge(turned, 1)
                            nc.scalar.activation(v[:, :, :].rearrange("p t n -> p (t n)"), flat(0, SEQ), ACT.Copy).then_inc(values_ready, 1)
                        if context:
                            act.wait_ge(turned, 2 if own else 1)
                            nc.scalar.activation(v_c[0:CTX, :], s_ps[0:CTX, 2, 0:P], ACT.Copy).then_inc(context_values_ready, 1)

                        def raw(half):
                            act.wait_ge(outputs_added, sum(1 for p in plan if p[0] <= half))
                            nc.scalar.activation(raw_out[:, half, :], o_ps[:, half, :], ACT.Copy).then_inc(raw_ready, 1)

                        for n, (half, kt, off, pair) in enumerate(plan):
                            rows = CTX if kt is None else P
                            src = s_ps[0:rows, 2 * (n % 3):2 * (n % 3) + 2, off:GROUP]
                            dst = probs[0:rows, n % 3, :, off:GROUP]
                            if linear and diagonal(half, kt):
                                continue
                            act.wait_ge(levels_ready if quantised else scores_ready, n + 1)
                            if n >= 3:
                                act.wait_ge(outputs_added, n - 2)
                            if quantised:
                                nc.scalar.activation(dst, dst, ACT.Exp, bias=quant[:, 4:5],
                                                     scale=quant[:, 3:4]).then_inc(probs_ready, 1)
                            elif linear:
                                nc.scalar.activation(dst, src, ACT.Copy).then_inc(probs_ready, 1)
                            else:
                                nc.scalar.activation(dst, src, ACT.Exp, scale=scale).then_inc(probs_ready, 1)
                        for half in range(halves):
                            raw(half)

                    @block.vector
                    def _(dve):
                        then = in_order(dve, dve_step)
                        for n, (t, j) in enumerate(own_jobs):
                            if linear and t < 2:
                                part = qkv[:, t, j * GROUP:(j + 1) * GROUP]
                                dve.wait_ge(projected, n + 1)
                                if n >= 2:
                                    dve.wait_ge(rstd_ready, n - 1)
                                nc.vector.tensor_scalar(head_sq[:, n % 2, :], s_ps[:, n, :], bs[:, t:t + 1], 0.0,
                                                        ALU.add, ALU.min).then_inc(squares_ready, 1)
                                then(nc.vector.tensor_scalar(part, s_ps[:, n, :], bs[:, t:t + 1], 0.0, ALU.add, ALU.max))
                                dve.wait_ge(rstd_ready, n + 1)
                                nc.vector.tensor_tensor(part, part, head_rstd[:, n % 2, :], ALU.add).then_inc(normed_ready, 1)
                            elif (t == 0 and not linear) or normed:
                                dve.wait_ge(projected, n + 1)
                                nc.vector.tensor_scalar(qkv[:, t, j * GROUP:(j + 1) * GROUP], s_ps[:, n, :], bs[:, t:t + 1], None,
                                                        ALU.add).then_inc(q_ready, 1)
                        if normed:
                            dve.wait_ge(q_ready, len(own_jobs))
                            for n, (t, j) in enumerate(own_jobs):
                                part = qkv[:, t, j * GROUP:(j + 1) * GROUP]
                                dve.wait_ge(rstd_ready, n + 1)
                                then(nc.vector.reciprocal(head_rstd[:, n % 2, :], head_rstd[:, n % 2, :]))
                                then(nc.vector.tensor_tensor(part, part, head_rstd[:, n % 2, :], ALU.mult))
                                nc.vector.tensor_scalar(part, part, norm[:, t, 0:1], norm[:, t, 1:2],
                                                        ALU.mult, ALU.add).then_inc(normed_ready, 1)
                        if maxed:
                            for n in range(TILES * PACK):
                                qt, h = divmod(n, PACK)
                                ring = 3 * (n % 2)
                                seen = 0 if cross else (qt + 1) * P if causal else SEQ
                                dve.wait_ge(natural_ready, n + 1)
                                at = row_max[:, qt, SLOT * h + ONE:SLOT * h + ONE + 1]
                                if own:
                                    last = nc.vector.reduce_max(at, flat(ring, seen), AX.X)
                                if context:
                                    last = nc.vector.reduce_max(row_max_c[:, qt, h:h + 1] if own else at, s_ps[:, ring + 2, 0:CTX], AX.X)
                                last.then_inc(rowmax_taken, 1)
                            if own and context:
                                dve.wait_ge(rowmax_taken, TILES * PACK)
                                every = row_max[:, :, ONE:P:SLOT]
                                nc.vector.tensor_tensor(every, every, row_max_c[:, :, :], ALU.max).then_inc(rowmax_ready, 1)
                            dve.wait_ge(max_turned, 1)
                            nc.vector.tensor_tensor(q_t, q_t, flat(0, SEQ), ALU.subtract).then_inc(q_final, 1)
                        for n, (half, kt, off, pair) in enumerate(plan):
                            src = s_ps[:, 2 * (n % 3):2 * (n % 3) + 2, :]
                            if quantised:
                                lv = probs[:, n % 3, :, :]
                                dve.wait_ge(scores_ready, n + 1)
                                if n >= 3:
                                    dve.wait_ge(outputs_added, n - 2)
                                then(nc.vector.tensor_scalar(lv, src, quant[:, 1:2], quant[:, 2:3], ALU.mult, ALU.add))
                                then(nc.vector.tensor_scalar(lv, lv, ROUND, ROUND, ALU.add, ALU.max))
                                nc.vector.tensor_scalar(lv, lv, ROUND + QMAX, ROUND, ALU.min, ALU.subtract).then_inc(levels_ready, 1)
                            if linear and diagonal(half, kt):
                                dve.wait_ge(scores_ready, n + 1)
                                if n >= 3:
                                    dve.wait_ge(outputs_added, n - 2)
                                keep = chip.c(C_KEEPT).rearrange("p (o n) -> p o n", o=1).to_broadcast((P, 2, P))
                                last = nc.vector.tensor_tensor(probs[:, n % 3, :, off:off + P], src[:, :, off:off + P], keep, ALU.mult)
                                if off + P < GROUP:
                                    last = nc.vector.tensor_copy(probs[:, n % 3, :, off + P:GROUP], src[:, :, off + P:GROUP])
                                last.then_inc(diagonal_ready, 1)
                        for half in range(halves):
                            dve.wait_ge(den_ready, half + 1)
                            den = s_ps[:, half, :]
                            if linear:
                                then(nc.vector.tensor_scalar(rden[:, half, :], den, 1e-6, None, ALU.add))
                                den = rden[:, half, :]
                            then(nc.vector.reciprocal(rden[:, half, :], den))
                            out = ot[:, bass.ds(hg, 1), tok(half)].rearrange("p o n -> p (o n)")
                            if quantised:
                                then(nc.vector.tensor_tensor(rden[:, half, :], raw_out[:, half, :], rden[:, half, :], ALU.mult))
                                fake_quant(nc, then, rden[:, half, :], rden[:, half, :], quant[:, 5:8], out)
                            else:
                                nc.vector.tensor_tensor(out, raw_out[:, half, :], rden[:, half, :], ALU.mult)


def fake_quant(nc, then, tmp, src, scalars, out):
    inv, zero, scale = (scalars[:, n:n + 1] for n in range(3))
    then(nc.vector.tensor_scalar(tmp, src, inv, zero, ALU.mult, ALU.add))
    then(nc.vector.tensor_scalar(tmp, tmp, 0.0, QMAX, ALU.max, ALU.min))
    then(nc.vector.tensor_scalar(tmp, tmp, ROUND, ROUND, ALU.add, ALU.subtract))
    then(nc.vector.tensor_scalar(out, tmp, zero, scale, ALU.subtract, ALU.mult))


def load_heads(chip, ctx, layer, chunks=FC):
    nc, io = chip.nc, chip.io
    sb = lambda name, shape: ctx.enter_context(sbuf(nc, name, shape, F32))
    w = sb(layer + "_w", [P, 3, chunks, PADDED])
    wo = sb(layer + "_wo", [P, HGS, DIM])
    biases = sb(layer + "_b", [P, 3, HGS])
    bo = sb(layer + "_bo", [P, FC])
    load(nc, [(w[:, t, :, :], io[layer + "_w"][t].rearrange("(c p) m -> p c m", p=P)) for t in range(3)] + [
        (wo[:, :, :], io[layer + "_wo"].rearrange("(g p) n -> p g n", p=P)),
        (biases[:, :, :], io[layer + "_b"]), (bo[:, :], io[layer + "_bo"])])
    return w, wo, biases, bo


def quantised_attention(chip):
    nc, io = chip.nc, chip.io
    with ExitStack() as ctx:
        sb = lambda name, shape: ctx.enter_context(sbuf(nc, name, shape, F32))
        w, wo, biases, bo = load_heads(chip, ctx, "L0_attn")
        ot = sb("head_out", [P, HGS, TOKENS])
        ten = sb("scalars", [P, 8])
        quant = sb("quant", [P, 8])
        quant_x = sb("quant_x", [P, 3])
        xq = sb("x_quantised", [P, FC, TOKENS])
        with ExitStack() as early:
            eb = lambda name, shape: early.enter_context(sbuf(nc, name, shape, F32))
            sw = eb("weight_scales", [P, 2, 3, PADDED])
            sp_ = eb("proj_scales", [P, 2, DIM])
            inv = eb("weight_inverse", [P, 3, PADDED])
            inv_p = eb("proj_inverse", [P, DIM])
            load(nc, [(sw[:, n, :, :].rearrange("p t m -> p (t m)"), io["L0_attn_ws"][n:n + 1, :].partition_broadcast(P))
                      for n in range(2)]
                 + [(sp_[:, n, :], io["L0_attn_ps"][n:n + 1, :].partition_broadcast(P)) for n in range(2)]
                 + [(ten[:, 0:6], io["L0_attn_scalars"].partition_broadcast(P))])
            with step(nc, "dve_step") as (block, dve_step):
                @block.vector
                def _(dve):
                    then = in_order(dve, dve_step)
                    one = lambda t, n: t[:, n:n + 1]
                    then(nc.vector.reciprocal(one(quant_x, 0), one(ten, 0)))
                    then(nc.vector.tensor_copy(one(quant_x, 1), one(ten, 1)))
                    then(nc.vector.tensor_copy(one(quant_x, 2), one(ten, 0)))
                    then(nc.vector.tensor_scalar(one(quant, 0), one(ten, 2), HEAD ** 0.5, None, ALU.mult))
                    then(nc.vector.reciprocal(one(quant, 1), one(quant, 0)))
                    then(nc.vector.tensor_copy(one(quant, 2), one(ten, 3)))
                    then(nc.vector.tensor_copy(one(quant, 3), one(ten, 2)))
                    then(nc.vector.tensor_scalar(one(quant, 4), one(ten, 2), -QMAX, None, ALU.mult))
                    then(nc.vector.reciprocal(one(quant, 5), one(ten, 4)))
                    then(nc.vector.tensor_copy(one(quant, 6), one(ten, 5)))
                    then(nc.vector.tensor_copy(one(quant, 7), one(ten, 4)))
                    then(nc.vector.reciprocal(inv[:, :, :], sw[:, 0, :, :]))
                    then(nc.vector.reciprocal(inv_p[:, :], sp_[:, 0, :]))
                    jobs = [(w[:, t, c, :], inv[:, t, :], sw[:, 1, t, :], sw[:, 0, t, :]) for t in range(3) for c in range(FC)]
                    jobs += [(wo[:, g, :], inv_p[:, :], sp_[:, 1, :], sp_[:, 0, :]) for g in range(HGS)]
                    for weight, inverse, zero, scale in jobs:
                        then(nc.vector.tensor_tensor(weight, weight, inverse, ALU.mult))
                        then(nc.vector.tensor_tensor(weight, weight, zero, ALU.add))
                        then(nc.vector.tensor_scalar(weight, weight, 0.0, QMAX, ALU.max, ALU.min))
                        then(nc.vector.tensor_scalar(weight, weight, ROUND, ROUND, ALU.add, ALU.subtract))
                        then(nc.vector.tensor_tensor(weight, weight, zero, ALU.subtract))
                        then(nc.vector.tensor_tensor(weight, weight, scale, ALU.mult))
                    for g in range(HGS):
                        then(nc.vector.tensor_scalar(wo[:, g, :], wo[:, g, :], chip.c(C_ROWS, 1), None, ALU.mult))
        with sbuf(nc, "x_levels", [P, FC, GROUP], F32) as tmp, nc.Fori(0, GROUPS) as g:
            with step(nc, "dve_step") as (block, dve_step):
                @block.vector
                def _(dve):
                    fake_quant(nc, in_order(dve, dve_step), tmp[:, :, :], chip.xt[:, :, group_slice(g)], quant_x, xq[:, :, group_slice(g)])
        src = lambda c, tok: xq[:, c, tok]
        head_attention(chip, "quant", w, biases, (src, src, src), ot, quant=quant)
        output_projection(chip, ot, wo, bias=bo)


def context_slice(chip):
    return lambda c, b: chip.ctx_t[:, c, bass.ds(b * CTX, CTX)]


def cross_attention(chip):
    nc, io = chip.nc, chip.io
    with ExitStack() as ctx:
        sb = lambda name, shape: ctx.enter_context(sbuf(nc, name, shape, F32))
        w, wo, biases, bo = load_heads(chip, ctx, "L0_xattn")
        ot = sb("head_out", [P, HGS, TOKENS])
        key_bias = sb("key_bias", [1, BATCH * CTX])
        rows = sb("bias_rows", [1, P])
        load(nc, [(key_bias[:, :], io["key_bias"]), (rows[:, :], io["bias_rows"])])
        src = lambda c, tok: chip.xt[:, c, tok]
        head_attention(chip, "cross", w, biases, (src, None, None), ot, ctx_source=context_slice(chip),
                       ctx_bias=(rows[:, :], lambda b: key_bias[:, bass.ds(b * CTX, CTX)]))
        output_projection(chip, ot, wo, bias=bo)


def normed_attention(chip):
    nc, io = chip.nc, chip.io
    with ExitStack() as ctx:
        sb = lambda name, shape: ctx.enter_context(sbuf(nc, name, shape, F32))
        w, wo, biases, bo = load_heads(chip, ctx, "L1_attn")
        ot = sb("head_out", [P, HGS, TOKENS])
        norm = sb("head_norm", [P, 3, 2])
        means = sb("head_means", [P, 3 * FC * HEADS])
        load(nc, [(norm[:, :, :], io["L1_attn_norm"])])
        with banks(nc, "bias_means", [P, 3 * HGS], F32) as mean_ps, step(nc, "means_ready dve_step") as (block, means_ready, dve_step):
            @block.tensor
            def _(pe):
                nc.tensor.matmul(mean_ps[:, :], chip.c(C_HEADMEAN), biases[:, :, :].rearrange("p t g -> p (t g)"),
                                 start=True, stop=True).then_inc(means_ready, 1)

            @block.vector
            def _(dve):
                then = in_order(dve, dve_step)
                heads = w[:, :, :, :].rearrange("p t c (h d) -> p (t c h) d", d=SLOT)[:, :, 0:HEAD]
                then(nc.vector.reduce_sum(means[:, :], heads, AX.X))
                then(nc.vector.tensor_scalar(means[:, :], means[:, :], 1.0 / HEAD, None, ALU.mult))
                spread = means[:, :].rearrange("p (h o) -> p h o", o=1).to_broadcast((P, 3 * FC * HEADS, HEAD))
                then(nc.vector.tensor_tensor(heads, heads, spread, ALU.subtract))
                dve.wait_ge(means_ready, 1)
                every = biases[:, :, :].rearrange("p t g -> p (t g)")
                then(nc.vector.tensor_tensor(every, every, mean_ps[:, :], ALU.subtract))
        src = lambda c, tok: chip.xt[:, c, tok]
        head_attention(chip, "heads_norm", w, biases, (src, src, src), ot, norm=norm)
        output_projection(chip, ot, wo, bias=bo)


def causal_attention(chip):
    nc = chip.nc
    with ExitStack() as ctx:
        w, wo, biases, bo = load_heads(chip, ctx, "L3_xattn")
        ot = ctx.enter_context(sbuf(nc, "head_out", [P, HGS, TOKENS], F32))
        src = lambda c, tok: chip.xt[:, c, tok]
        head_attention(chip, "causal", w, biases, (src, src, src), ot, ctx_source=context_slice(chip))
        output_projection(chip, ot, wo, bias=bo)


def linear_attention(chip):
    nc, io = chip.nc, chip.io
    with ExitStack() as ctx:
        sb = lambda name, shape: ctx.enter_context(sbuf(nc, name, shape, F32))
        w, wo, biases, bo = load_heads(chip, ctx, "L3_attn")
        ot = sb("head_out", [P, HGS, TOKENS])
        latent = sb("latent", [P, TOKENS])
        wkv = sb("kv_down", [P, FC, P])
        bkv = sb("kv_bias", [P, 1])
        wc = sb("kv_compress", [P, P])
        affine = sb("affine", [P, 2, FC])
        load(nc, [(wkv[:, :, :], io["L3_attn_wkv"].rearrange("(c p) m -> p c m", p=P)), (bkv[:, :], io["L3_attn_bkv"]),
                  (wc[:, :], io["L3_attn_wc"]), (affine[:, :, :], io["L3_attn_affine"])])
        with sbuf(nc, "kv", [P, GROUP], F32) as kv, banks(nc, "kv_psum", [P, 2, GROUP], F32) as ps, nc.Fori(0, GROUPS) as g:
            with step(nc, "down_ready kv_ready latent_ready stored") as (block, down_ready, kv_ready, latent_ready, stored):
                @block.tensor
                def _(pe):
                    for c in range(FC):
                        last = nc.tensor.matmul(ps[:, 0, :], wkv[:, c, :], chip.xt[:, c, group_slice(g)], start=(c == 0), stop=(c == FC - 1))
                    last.then_inc(down_ready, 1)
                    pe.wait_ge(kv_ready, 1)
                    nc.tensor.matmul(ps[:, 1, :], wc[:, :], kv[:, :], start=True, stop=True).then_inc(latent_ready, 1)

                @block.scalar
                def _(act):
                    act.wait_ge(down_ready, 1)
                    nc.scalar.activation(kv[:, :], ps[:, 0, :], ACT.Identity, bias=bkv[:, 0:1]).then_inc(kv_ready, 1)
                    act.wait_ge(latent_ready, 1)
                    nc.scalar.activation(latent[:, group_slice(g)], ps[:, 1, :], ACT.Copy).then_inc(stored, 1)
        x_src = lambda c, tok: chip.xt[:, c, tok]
        kv_src = lambda c, tok: latent[:, tok]
        head_attention(chip, "linear", w, biases, (x_src, kv_src, kv_src), ot)
        output_projection(chip, ot, wo, bias=bo, affine=(affine[:, 0, :], affine[:, 1, :]))


def context_mlp(chip):
    nc, io = chip.nc, chip.io
    with ExitStack() as ctx:
        rows = ctx.enter_context(sbuf(nc, "context_rows", [CTX, BATCH, DIM], F32))
        stage = ctx.enter_context(sbuf(nc, "context_stage", [P, FC, CTX], F32))
        stage_rows = ctx.enter_context(sbuf(nc, "context_stage_rows", [CTX, 1, DIM], F32))
        h = ctx.enter_context(sbuf(nc, "hidden", [CTX, 2, GROUP], F32))
        ps = ctx.enter_context(banks(nc, "hidden_psum", [P, 2, GROUP], F32))
        norm_ps = ctx.enter_context(banks(nc, "norm_psum", [P, 4, GROUP], F32))
        load(nc, [(rows[:, :, :], io["ctx"].rearrange("(b s) d -> s b d", b=BATCH))])
        halves = SEQ // GROUP
        with nc.Fori(0, BATCH) as b:
            tok = lambda j: bass.ds(b * SEQ + j * GROUP, GROUP)
            with step(nc, "staged products_ready hidden_ready") as (block, staged, products_ready, hidden_ready):
                @block.vector
                def _(dve):
                    nc.vector.tensor_copy(stage[:, :, :], chip.ctx_t[:, :, bass.ds(b * CTX, CTX)]).then_inc(staged, 1)
                    nc.vector.tensor_copy(stage_rows[:, 0, :], rows[:, bass.ds(b, 1), :].rearrange("p o d -> p (o d)")).then_inc(staged, 1)
                    dve.wait_ge(staged, 2)

                @block.tensor
                def _(pe):
                    pe.wait_ge(staged, 2)
                    for j in range(halves):
                        for c in range(FC):
                            last = nc.tensor.matmul(ps[0:CTX, j, :], stage[:, c, :], chip.xt[:, c, tok(j)], start=(c == 0), stop=(c == FC - 1))
                        last.then_inc(products_ready, 1)

                @block.scalar
                def _(act):
                    for j in range(halves):
                        act.wait_ge(products_ready, j + 1)
                        nc.scalar.activation(h[:, j, :], ps[0:CTX, j, :], ACT.Gelu_apprx_tanh).then_inc(hidden_ready, 1)
            for j in range(halves):
                add_norm(chip, tok(j), norm_ps, product=(stage_rows, lambda k, j=j: h[:, j, :]))


def concat_context(chip):
    nc, io = chip.nc, chip.io
    with ExitStack() as ctx:
        sb = lambda name, shape: ctx.enter_context(sbuf(nc, name, shape, F32))
        w = sb("concat_w", [P, 2 * FC, DIM])
        bias = sb("concat_b", [P, FC])
        sums = sb("context_sums", [P, FC, BATCH])
        shift = sb("context_shift", [P, BATCH, FC])
        shift_b = sb("context_shift_now", [P, FC])
        load(nc, [(w[:, :, :], io["L2_xattn_w"].rearrange("(c p) n -> p c n", p=P)), (bias[:, :], io["L2_xattn_b"])])
        norm_ps = ctx.enter_context(banks(nc, "norm_psum", [P, 4, GROUP], F32))
        ps = ctx.enter_context(banks(nc, "shift_psum", [P, FC, BATCH], F32))
        with step(nc, "sums_ready shift_ready dve_step") as (block, sums_ready, shift_ready, dve_step):
            @block.vector
            def _(dve):
                nc.vector.reduce_sum(sums[:, :, :], chip.ctx_t[:, :, :].rearrange("p c (b s) -> p c b s", b=BATCH), AX.X).then_inc(sums_ready, 1)
                dve.wait_ge(shift_ready, FC)
                then = in_order(dve, dve_step)
                for c in range(FC):
                    then(nc.vector.tensor_scalar(shift[:, :, c], ps[:, c, :], 1.0 / CTX, bias[:, c:c + 1], ALU.mult, ALU.add))

            @block.tensor
            def _(pe):
                pe.wait_ge(sums_ready, 1)
                for c in range(FC):
                    for k in range(FC):
                        last = nc.tensor.matmul(ps[:, c, :], w[:, FC + k, c * P:(c + 1) * P], sums[:, k, :], start=(k == 0), stop=(k == FC - 1))
                    last.then_inc(shift_ready, 1)
        with nc.Fori(0, BATCH) as b:
            with step(nc, "staged") as (block, staged):
                @block.vector
                def _(dve):
                    nc.vector.tensor_copy(shift_b[:, :], shift[:, bass.ds(b, 1), :].rearrange("p o c -> p (o c)")).then_inc(staged, 1)
                    dve.wait_ge(staged, 1)
            for j in range(SEQ // GROUP):
                tok = bass.ds(b * SEQ + j * GROUP, GROUP)
                add_norm(chip, tok, norm_ps, product=(w[:, 0:FC, :], lambda k, tok=tok: chip.xt[:, k, tok]), bias=shift_b)


def spiking_ffn(chip):
    nc, io = chip.nc, chip.io
    inner = 4 * DIM
    ic = inner // P
    steps, beta, threshold = 5, 0.9, 1.0
    with ExitStack() as ctx:
        sb = lambda name, shape: ctx.enter_context(sbuf(nc, name, shape, F32))
        w1, w2 = sb("fc_w", [P, FC, inner]), sb("proj_w", [P, ic, DIM])
        h = sb("hidden", [P, ic, GROUP])
        y, mem, spike, total = (sb(n, [P, FC, GROUP]) for n in ("drive", "membrane", "spike", "spikes"))
        load(nc, [(w1[:, :, :], io["L2_ffn_w1"].rearrange("(c p) n -> p c n", p=P)), (w2[:, :, :], io["L2_ffn_w2"].rearrange("(c p) n -> p c n", p=P))])
        h_ps = ctx.enter_context(banks(nc, "hidden_psum", [P, 2, GROUP], F32))
        y_ps = ctx.enter_context(banks(nc, "drive_psum", [P, 2, GROUP], F32))
        norm_ps = ctx.enter_context(banks(nc, "norm_psum", [P, 4, GROUP], F32))
        with nc.Fori(0, GROUPS) as g:
            with step(nc, "h_ready relu_ready squared y_ready dve_step") as (block, h_ready, relu_ready, squared, y_ready, dve_step):
                @block.tensor
                def _(pe):
                    for n in range(ic):
                        if n >= 2:
                            pe.wait_ge(relu_ready, n - 1)
                        for c in range(FC):
                            last = nc.tensor.matmul(h_ps[:, n % 2, :], w1[:, c, n * P:(n + 1) * P], chip.xt[:, c, group_slice(g)],
                                                    start=(c == 0), stop=(c == FC - 1))
                        last.then_inc(h_ready, 1)
                    for c in range(FC):
                        for n in range(ic):
                            pe.wait_ge(squared, n + 1)
                            last = nc.tensor.matmul(y_ps[:, c, :], w2[:, n, c * P:(c + 1) * P], h[:, n, :], start=(n == 0), stop=(n == ic - 1))
                    last.then_inc(y_ready, 1)

                @block.scalar
                def _(act):
                    for n in range(ic):
                        act.wait_ge(h_ready, n + 1)
                        nc.scalar.activation(h[:, n, :], h_ps[:, n % 2, :], ACT.Relu).then_inc(relu_ready, 1)
                        act.wait_ge(relu_ready, n + 1)
                        nc.scalar.activation(h[:, n, :], h[:, n, :], ACT.Square).then_inc(squared, 1)

                @block.vector
                def _(dve):
                    then = in_order(dve, dve_step)
                    dve.wait_ge(y_ready, 1)
                    then(nc.vector.tensor_copy(y[:, :, :], y_ps[:, :, :]))
                    then(nc.vector.tensor_copy(mem[:, :, :], y[:, :, :]))
                    then(nc.vector.tensor_scalar(spike[:, :, :], mem[:, :, :], threshold, None, ALU.is_gt))
                    then(nc.vector.tensor_copy(total[:, :, :], spike[:, :, :]))
                    for s in range(1, steps):
                        then(nc.vector.scalar_tensor_tensor(out=mem[:, :, :], in0=mem[:, :, :], scalar=beta, in1=y[:, :, :], op0=ALU.mult, op1=ALU.add))
                        then(nc.vector.tensor_tensor(mem[:, :, :], mem[:, :, :], spike[:, :, :], ALU.subtract))
                        then(nc.vector.tensor_scalar(spike[:, :, :], mem[:, :, :], threshold, None, ALU.is_gt))
                        then(nc.vector.tensor_tensor(total[:, :, :], total[:, :, :], spike[:, :, :], ALU.add))
                    then(nc.vector.tensor_scalar(total[:, :, :], total[:, :, :], 1.0 / steps, None, ALU.mult))
            add_norm(chip, group_slice(g), norm_ps, ready=lambda c: total[:, c, :])


EXPERTS, EXPERT_INNER = 8, 1024
CAPACITY = 2 * TOKENS // EXPERTS
TOKEN_TILES = TOKENS // P


def token_rows(chip, rows, logits=None, gate_w=None):
    nc = chip.nc
    per = GROUP // P
    with ExitStack() as ctx:
        stage = ctx.enter_context(sbuf(nc, "token_stage", [P, FC, GROUP], F32))
        turn_ps = ctx.enter_context(banks(nc, "rows_psum", [P, per, DIM], F32))
        logit_ps = ctx.enter_context(banks(nc, "logits_psum", [P, per, EXPERTS], F32))
        with nc.Fori(0, GROUPS) as g, step(nc, "staged turned logits_ready copied") as (block, staged, turned, logits_ready, copied):
            @block.vector
            def _(dve):
                nc.vector.tensor_copy(stage[:, :, :], chip.xt[:, :, group_slice(g)]).then_inc(staged, 1)
                if logits is not None:
                    dve.wait_ge(logits_ready, 1)
                    nc.vector.tensor_copy(logits[:, bass.ds(g * per, per), :], logit_ps[:, :, :]).then_inc(copied, 1)

            @block.tensor
            def _(pe):
                pe.wait_ge(staged, 1)
                for t in range(per):
                    for c in range(FC):
                        last = nc.tensor.transpose(turn_ps[:, t, c * P:(c + 1) * P], stage[:, c, t * P:(t + 1) * P], chip.c(C_ID))
                last.then_inc(turned, 1)
                if logits is not None:
                    for t in range(per):
                        for c in range(FC):
                            last = nc.tensor.matmul(logit_ps[:, t, :], stage[:, c, t * P:(t + 1) * P], gate_w[:, c, :],
                                                    start=(c == 0), stop=(c == FC - 1))
                    last.then_inc(logits_ready, 1)

            @block.scalar
            def _(act):
                act.wait_ge(turned, 1)
                nc.scalar.activation(rows[:, bass.ds(g * per, per), :], turn_ps[:, :, :], ACT.Copy).then_inc(copied, 1)


def route(chip, logits, place, scatter_to, gates):
    nc = chip.nc
    E, N = EXPERTS, TOKEN_TILES
    with ExitStack() as ctx:
        sb = lambda name, shape: ctx.enter_context(sbuf(nc, name, shape, F32))
        best = sb("best", [P, 2, N])
        index = sb("expert_index", [P, 2, N])
        hot = sb("one_hot", [P, 2, N, E])
        work = sb("route_work", [P, N, E])
        rest = sb("route_rest", [P, N, E])
        total = sb("tile_totals", [P, 2, 2, N, E])
        slot = sb("slots", [P, 2, N])
        keep = sb("keep", [P, 2, N])
        ex = sb("gate_exps", [P, N, E])
        small = sb("gate_sums", [P, 4, N])
        ps = ctx.enter_context(banks(nc, "route_psum", [P, 2, 2, N, E], F32))
        wide = lambda t: t.rearrange("p (n o) -> p n o", o=1).to_broadcast((P, N, E))
        iota = chip.c(C_IOTA, E).rearrange("p (o e) -> p o e", o=1).to_broadcast((P, N, E))
        with step(nc, "hot_ready counts_ready shifted exps_ready dve_step") as (block, hot_ready, counts_ready, shifted, exps_ready, dve_step):
            @block.vector
            def _(dve):
                then = in_order(dve, dve_step)
                tt, ts = nc.vector.tensor_tensor, nc.vector.tensor_scalar
                for k in range(2):
                    src = logits[:, :, :] if k == 0 else rest[:, :, :]
                    then(nc.vector.reduce_max(best[:, k, :], src, AX.X))
                    then(tt(work[:, :, :], src, wide(best[:, k, :]), ALU.is_lt))
                    then(ts(work[:, :, :], work[:, :, :], float(E), None, ALU.mult))
                    then(tt(work[:, :, :], work[:, :, :], iota, ALU.add))
                    then(nc.vector.tensor_reduce(index[:, k, :], work[:, :, :], AX.X, ALU.min))
                    nc.vector.tensor_tensor(hot[:, k, :, :], wide(index[:, k, :]), iota, ALU.is_equal).then_inc(hot_ready, 1)
                    dve.wait_ge(hot_ready, k + 1)
                    if k == 0:
                        then(ts(rest[:, :, :], hot[:, 0, :, :], FAR, None, ALU.mult))
                        then(tt(rest[:, :, :], logits[:, :, :], rest[:, :, :], ALU.add))
                nc.vector.tensor_tensor(work[:, :, :], logits[:, :, :], wide(best[:, 0, :]), ALU.subtract).then_inc(shifted, 1)
                nc.vector.tensor_tensor(small[:, 1, :], best[:, 1, :], best[:, 0, :], ALU.subtract).then_inc(shifted, 1)
                dve.wait_ge(exps_ready, 2)
                then(nc.vector.reduce_sum(small[:, 0, :], ex[:, :, :], AX.X))
                then(nc.vector.reciprocal(small[:, 0, :], small[:, 0, :]))
                then(tt(small[:, 1, :], small[:, 2, :], small[:, 0, :], ALU.mult))
                then(tt(small[:, 3, :], small[:, 0, :], small[:, 1, :], ALU.add))
                then(ts(small[:, 3, :], small[:, 3, :], 1e-9, None, ALU.max))
                then(nc.vector.reciprocal(small[:, 3, :], small[:, 3, :]))
                dve.wait_ge(counts_ready, 1)
                for k in range(2):
                    then(nc.vector.memset(total[:, 0, k, 0, :], 0.0))
                    then(nc.vector.tensor_copy(total[:, 0, k, 1:N, :], ps[:, 1, k, 0:N - 1, :]))
                at = 0
                for shift in (1, 2, 4, 8, 16):
                    for k in range(2):
                        then(nc.vector.tensor_copy(total[:, 1 - at, k, 0:shift, :], total[:, at, k, 0:shift, :]))
                        then(tt(total[:, 1 - at, k, shift:N, :], total[:, at, k, shift:N, :], total[:, at, k, 0:N - shift, :], ALU.add))
                    at = 1 - at
                for k in range(2):
                    then(tt(work[:, :, :], ps[:, 0, k, :, :], total[:, at, k, :, :], ALU.add))
                    if k == 1:
                        then(tt(rest[:, 0, :], total[:, at, 0, N - 1, :], ps[:, 1, 0, N - 1, :], ALU.add))
                        then(tt(work[:, :, :], work[:, :, :], rest[:, 0:1, :].to_broadcast((P, N, E)), ALU.add))
                    then(tt(work[:, :, :], work[:, :, :], hot[:, k, :, :], ALU.mult))
                    then(nc.vector.reduce_sum(slot[:, k, :], work[:, :, :], AX.X))
                then(ts(keep[:, :, :], slot[:, :, :], float(CAPACITY), None, ALU.is_lt))
                then(ts(slot[:, :, :], slot[:, :, :], float(CAPACITY - 1), None, ALU.min))
                then(ts(index[:, :, :], index[:, :, :], float(CAPACITY), None, ALU.mult))
                then(tt(slot[:, :, :], slot[:, :, :], index[:, :, :], ALU.add))
                then(nc.vector.tensor_copy(place[:, :, :], slot[:, :, :]))
                then(ts(index[:, :, :], keep[:, :, :], -float(2 * EXPERTS * CAPACITY), float(2 * EXPERTS * CAPACITY), ALU.mult, ALU.add))
                then(tt(slot[:, :, :], slot[:, :, :], index[:, :, :], ALU.add))
                then(nc.vector.tensor_copy(scatter_to[:, :, :], slot[:, :, :]))
                for k in range(2):
                    then(tt(gates[:, k, :], small[:, k, :], small[:, 3, :], ALU.mult))
                    then(tt(gates[:, k, :], gates[:, k, :], keep[:, k, :], ALU.mult))

            @block.scalar
            def _(act):
                act.wait_ge(shifted, 2)
                nc.scalar.activation(ex[:, :, :], work[:, :, :], ACT.Exp).then_inc(exps_ready, 1)
                nc.scalar.activation(small[:, 2, :], small[:, 1, :], ACT.Exp).then_inc(exps_ready, 1)

            @block.tensor
            def _(pe):
                for k in range(2):
                    pe.wait_ge(hot_ready, k + 1)
                    nc.tensor.matmul(ps[:, 0, k, :, :], chip.c(C_BEFORE), hot[:, k, :, :], start=True, stop=True)
                    last = nc.tensor.matmul(ps[:, 1, k, :, :], chip.c(C_ONES), hot[:, k, :, :], start=True, stop=True)
                last.then_inc(counts_ready, 1)


def expert_ffn(chip):
    nc, io = chip.nc, chip.io
    slots = EXPERTS * CAPACITY
    ic, tiles = EXPERT_INNER // P, CAPACITY // P
    dispatched = nc.dram_tensor("dispatched", (slots, DIM), F32).ap()
    produced = nc.dram_tensor("produced", (slots, DIM), F32).ap()
    with ExitStack() as ctx:
        sb = lambda name, shape, dt=F32: ctx.enter_context(sbuf(nc, name, shape, dt))
        place, scatter_to = sb("place", [P, 2, TOKEN_TILES], U32), sb("scatter_to", [P, 2, TOKEN_TILES], U32)
        gates = sb("gates", [P, 2, TOKEN_TILES])
        with ExitStack() as early:
            rows = early.enter_context(sbuf(nc, "rows", [P, TOKEN_TILES, DIM], F32))
            logits = early.enter_context(sbuf(nc, "logits", [P, TOKEN_TILES, EXPERTS], F32))
            gate_w = early.enter_context(sbuf(nc, "gate_w", [P, FC, EXPERTS], F32))
            zeros = early.enter_context(sbuf(nc, "zeros", [P, 16 * DIM], F32))
            load(nc, [(gate_w[:, :, :], io["L0_ffn_wg"].rearrange("(c p) e -> p c e", p=P))])
            with step(nc, "cleared zeroed") as (block, cleared, zeroed):
                @block.gpsimd
                def _(pool):
                    nc.gpsimd.memset(zeros[:, :], 0.0).then_inc(cleared, 1)

                @block.sync
                def _(sp):
                    sp.wait_ge(cleared, 1)
                    whole = dispatched.rearrange("(n p r) d -> n p (r d)", p=P, r=16)
                    for n in range(whole.shape[0]):
                        sp.dma_start(whole[n], zeros[:, :]).then_inc(zeroed, 16)
                    sp.wait_ge(zeroed, 16 * whole.shape[0])
            token_rows(chip, rows, logits, gate_w)
            route(chip, logits, place, scatter_to, gates)
            scattered = chip.keep_semaphore("scattered")
            with nc.Block() as block:
                @block.gpsimd
                def _(pool):
                    for t in range(TOKEN_TILES):
                        for k in range(2):
                            nc.gpsimd.indirect_dma_start(
                                out=dispatched, out_offset=bass.IndirectOffsetOnAxis(ap=scatter_to[:, k, t:t + 1], axis=0),
                                in_=rows[:, t, :], in_offset=None, bounds_check=slots - 1, oob_is_err=False).then_inc(scattered, 16)
                    pool.wait_ge(scattered, 16 * 2 * TOKEN_TILES)
        with ExitStack() as mid:
            eb = lambda name, shape: mid.enter_context(sbuf(nc, name, shape, F32))
            w1, w2 = eb("expert_w1", [P, FC, EXPERT_INNER]), eb("expert_w2", [P, ic, DIM])
            taken = eb("taken", [P, tiles, DIM])
            taken_t = eb("taken_t", [P, FC, CAPACITY])
            h = eb("expert_hidden", [P, ic, GROUP])
            made = eb("made", [P, tiles, DIM])
            turn_ps = mid.enter_context(banks(nc, "taken_psum", [P, 2, GROUP], F32))
            h_ps = mid.enter_context(banks(nc, "expert_psum", [P, 2, GROUP], F32))
            y_ps = mid.enter_context(banks(nc, "made_psum", [P, 2, GROUP], F32))
            per = GROUP // P
            with nc.Fori(0, EXPERTS) as e, step(nc, "weights_loaded taken_loaded turned turned_copied h_ready hidden_ready y_ready made_ready stored") as (
                    block, weights_loaded, taken_loaded, turned, turned_copied, h_ready, hidden_ready, y_ready, made_ready, stored):
                @block.sync
                def _(sp):
                    own = bass.ds(e * CAPACITY, CAPACITY)
                    sp.dma_start(taken[:, :, :], dispatched[own, :].rearrange("(t p) d -> p t d", p=P)).then_inc(taken_loaded, 16)
                    sp.dma_start(w1[:, :, :], io["L0_ffn_w1"][bass.ds(e * DIM, DIM), :].rearrange("(c p) f -> p c f", p=P)).then_inc(weights_loaded, 16)
                    sp.dma_start(w2[:, :, :], io["L0_ffn_w2"][bass.ds(e * EXPERT_INNER, EXPERT_INNER), :].rearrange("(c p) d -> p c d", p=P)).then_inc(weights_loaded, 16)
                    sp.wait_ge(made_ready, tiles)
                    sp.dma_start(produced[own, :].rearrange("(t p) d -> p t d", p=P), made[:, :, :]).then_inc(stored, 16)
                    sp.wait_ge(stored, 16)

                @block.tensor
                def _(pe):
                    pe.wait_ge(taken_loaded, 16)
                    for c in range(FC):
                        for j in range(CAPACITY // GROUP):
                            n = c * (CAPACITY // GROUP) + j
                            if n >= 2:
                                pe.wait_ge(turned_copied, n - 1)
                            for t in range(per):
                                last = nc.tensor.transpose(turn_ps[:, n % 2, t * P:(t + 1) * P], taken[:, j * per + t, c * P:(c + 1) * P], chip.c(C_ID))
                            last.then_inc(turned, 1)
                    pe.wait_ge(turned_copied, FC * (CAPACITY // GROUP))
                    pe.wait_ge(weights_loaded, 32)
                    for j in range(CAPACITY // GROUP):
                        for n in range(ic):
                            m = j * ic + n
                            if m >= 2:
                                pe.wait_ge(hidden_ready, m - 1)
                            for c in range(FC):
                                last = nc.tensor.matmul(h_ps[:, m % 2, :], w1[:, c, n * P:(n + 1) * P], taken_t[:, c, j * GROUP:(j + 1) * GROUP],
                                                        start=(c == 0), stop=(c == FC - 1))
                            last.then_inc(h_ready, 1)
                        pe.wait_ge(hidden_ready, (j + 1) * ic)
                        for t in range(per):
                            m = j * per + t
                            if m >= 2:
                                pe.wait_ge(made_ready, m - 1)
                            for n in range(ic):
                                last = nc.tensor.matmul(y_ps[:, m % 2, 0:DIM], h[:, n, t * P:(t + 1) * P], w2[:, n, :], start=(n == 0), stop=(n == ic - 1))
                            last.then_inc(y_ready, 1)

                @block.scalar
                def _(act):
                    for j in range(CAPACITY // GROUP):
                        if j:
                            act.wait_ge(y_ready, j * per)
                        for n in range(ic):
                            m = j * ic + n
                            act.wait_ge(h_ready, m + 1)
                            nc.scalar.activation(h[:, n, :], h_ps[:, m % 2, :], ACT.Gelu).then_inc(hidden_ready, 1)

                @block.vector
                def _(dve):
                    for c in range(FC):
                        for j in range(CAPACITY // GROUP):
                            n = c * (CAPACITY // GROUP) + j
                            dve.wait_ge(turned, n + 1)
                            nc.vector.tensor_copy(taken_t[:, c, j * GROUP:(j + 1) * GROUP], turn_ps[:, n % 2, :]).then_inc(turned_copied, 1)
                    for m in range(tiles):
                        dve.wait_ge(y_ready, m + 1)
                        nc.vector.tensor_copy(made[:, m, :], y_ps[:, m % 2, 0:DIM]).then_inc(made_ready, 1)
        combine(chip, ctx, produced, place, gates)


def combine(chip, ctx, produced, place, gates):
    nc = chip.nc
    per = GROUP // P
    sb = lambda name, shape, dt=F32: ctx.enter_context(sbuf(nc, name, shape, dt))
    gathered = [chip.keep_semaphore(f"gathered_{t}") for t in range(per)]
    got = sb("got", [P, per, 2, DIM])
    at = sb("place_now", [P, per, 2], U32)
    gate = sb("gate_now", [P, 2, per])
    mixed = sb("mixed", [P, per, DIM])
    turn_ps = ctx.enter_context(banks(nc, "mixed_psum", [P, FC, GROUP], F32))
    norm_ps = ctx.enter_context(banks(nc, "norm_psum", [P, 4, GROUP], F32))
    with nc.Fori(0, GROUPS) as g:
        with step(nc, "staged mixed_ready turned dve_step") as (block, staged, mixed_ready, turned, dve_step):
            @block.vector
            def _(dve):
                then = in_order(dve, dve_step)
                tiles = bass.ds(g * per, per)
                nc.vector.tensor_copy(at[:, :, :].rearrange("p t k -> p k t"), place[:, :, tiles]).then_inc(staged, 1)
                then(nc.vector.tensor_copy(gate[:, :, :], gates[:, :, tiles]))
                for t in range(per):
                    dve.wait_ge(gathered[t], 32 * g + 32)
                    then(nc.vector.tensor_scalar(mixed[:, t, :], got[:, t, 0, :], gate[:, 0, t:t + 1], None, ALU.mult))
                    nc.vector.scalar_tensor_tensor(out=mixed[:, t, :], in0=got[:, t, 1, :], scalar=gate[:, 1, t:t + 1], in1=mixed[:, t, :],
                                                   op0=ALU.mult, op1=ALU.add).then_inc(mixed_ready, 1)

            @block.gpsimd
            def _(pool):
                pool.wait_ge(staged, 1)
                for t in range(per):
                    for k in range(2):
                        nc.gpsimd.indirect_dma_start(out=got[:, t, k, :], out_offset=None, in_=produced,
                                                     in_offset=bass.IndirectOffsetOnAxis(ap=at[:, t, k:k + 1], axis=0)).then_inc(gathered[t], 16)
                for t in range(per):
                    pool.wait_ge(gathered[t], 32 * g + 32)

            @block.tensor
            def _(pe):
                for t in range(per):
                    pe.wait_ge(mixed_ready, t + 1)
                    for c in range(FC):
                        last = nc.tensor.transpose(turn_ps[:, c, t * P:(t + 1) * P], mixed[:, t, c * P:(c + 1) * P], chip.c(C_ID))
                last.then_inc(turned, 1)
        add_norm(chip, group_slice(g), norm_ps, ready=lambda c: turn_ps[:, c, :])


WIDE_HEADS, WIDE = 8, 64
INNER = WIDE_HEADS * WIDE
DEPTH = 2
HIDDEN = DIM * 4 * 2 // 3
HC = -(-HIDDEN // P)


def local_transformer(chip):
    nc, io = chip.nc, chip.io
    H2 = 2 * WIDE_HEADS
    with ExitStack() as ctx:
        sb = lambda name, shape: ctx.enter_context(sbuf(nc, name, shape, F32))
        inner = sb("inner", [P, FC, TOKENS])
        rope = sb("rope", [P, 2, TILES, 2, WIDE])
        norm_ps_name = "norm_psum"
        load(nc, [(rope[:, :, :, :, :], io["rope"])])
        with step(nc, "copied") as (block, copied):
            @block.scalar
            def _(act):
                nc.scalar.activation(inner[:, :, :], chip.xt[:, :, :], ACT.Copy).then_inc(copied, 1)
                act.wait_ge(copied, 1)
        with nc.Fori(0, DEPTH) as layer:
            window_attention(chip, layer, inner, rope)
            gated_ffn(chip, layer, inner)
        with banks(nc, norm_ps_name, [P, 4, GROUP], F32) as ps, nc.Fori(0, GROUPS) as g:
            add_norm(chip, group_slice(g), ps, ready=lambda c: inner[:, c, group_slice(g)])


def window_attention(chip, layer, inner, rope):
    nc, io = chip.nc, chip.io
    H2, HP = 2 * WIDE_HEADS, WIDE_HEADS // 2
    with ExitStack() as ctx:
        sb = lambda name, shape: ctx.enter_context(sbuf(nc, name, shape, F32))
        wqkv = sb("wide_w", [P, FC, 3 * INNER])
        wo = sb("wide_wo", [P, INNER // P, DIM])
        scales = sb("wide_scales", [P, 2, WIDE])
        load(nc, [(wqkv[:, :, :], io["L1_ffn_wqkv"][bass.ds(layer * DIM, DIM), :].rearrange("(c p) n -> p c n", p=P)),
                  (wo[:, :, :], io["L1_ffn_wo"][bass.ds(layer * INNER, INNER), :].rearrange("(c p) n -> p c n", p=P)),
                  (scales[:, :, :].rearrange("p a d -> p (a d)"), io["L1_ffn_scales"][bass.ds(layer, 1), :].partition_broadcast(P))])
        shifted = sb("shifted", [P, FC, P])
        squares = sb("qk_squares", [P, H2, WIDE])
        sums = sb("qk_sums", [P, H2])
        qk = sb("qk", [P, H2, WIDE])
        turned_qk = sb("qk_rotated", [P, H2, WIDE])
        tables = sb("rope_now", [P, 2, 2, WIDE])
        qk_t = sb("qk_t", [P, 2, HP, P])
        before_k = sb("before_k", [P, HP, P])
        values, before_v = sb("wide_values", [P, INNER]), sb("before_v", [P, INNER])
        probs = sb("wide_probs", [P, WIDE_HEADS, 2 * P])
        probs_t = sb("wide_probs_t", [P, WIDE_HEADS, 2, P])
        top = sb("wide_max", [P, WIDE_HEADS])
        den = sb("wide_den", [P, WIDE_HEADS])
        out = sb("wide_out", [P, INNER])
        out_t = sb("wide_out_t", [P, INNER // P, SEQ])
        pa = ctx.enter_context(banks(nc, "wide_psum_a", [P, 4, GROUP], F32))
        pb = ctx.enter_context(banks(nc, "wide_psum_b", [P, 4, GROUP], F32))
        spot = lambda h: (h % 2) * HP + h // 2

        def tile_step(b, w, first):
            tok = b * SEQ + w * P
            span = P if first else 2 * P
            with step(nc, "shift_ready products_ready squares_ready sums_ready root_ready values_ready qk_ready turned qk_turned scores_ready "
                          "masked exps_ready probs_turned probs_copied out_ready out_scaled out_turned kept dve_step") as (
                    block, shift_ready, products_ready, squares_ready, sums_ready, root_ready, values_ready, qk_ready, turned, qk_turned, scores_ready,
                    masked, exps_ready, probs_turned, probs_copied, out_ready, out_scaled, out_turned, kept, dve_step):
                scores_of = lambda h: pb[:, spot(h) // 2, (spot(h) % 2) * 2 * P:(spot(h) % 2) * 2 * P + 2 * P]
                score_all = pb[:, :, :].rearrange("p b (s n) -> p (b s) n", n=2 * P)

                def copy_probs(engine_copy, p):
                    src = pa[:, p, :].rearrange("p (h s n) -> p h s n", h=2, s=2)[:, :, 0:span // P, :]
                    engine_copy(probs_t[:, 2 * p:2 * p + 2, 0:span // P, :], src).then_inc(probs_copied, 1)

                @block.tensor
                def _(pe):
                    pe.wait_ge(shift_ready, 2)
                    for n in range(3):
                        for c in range(FC):
                            last = nc.tensor.matmul(pa[:, n, :], shifted[:, c, :], wqkv[:, c, n * INNER:(n + 1) * INNER], start=(c == 0), stop=(c == FC - 1))
                        last.then_inc(products_ready, 1)
                    pe.wait_ge(qk_ready, 1)
                    for t in range(2):
                        for p in range(HP):
                            last = nc.tensor.transpose(pa[:, t, p * P:(p + 1) * P],
                                                       qk[:, t * WIDE_HEADS + 2 * p:t * WIDE_HEADS + 2 * p + 2, :].rearrange("p h d -> p (h d)"), chip.c(C_ID))
                    last.then_inc(turned, 1)
                    pe.wait_ge(qk_turned, 1)
                    for h in range(WIDE_HEADS):
                        rows = slice(WIDE * (h % 2), WIDE * (h % 2) + WIDE)
                        q = qk_t[rows, 0, h // 2, :]
                        if not first:
                            nc.tensor.matmul(scores_of(h)[:, P:2 * P], q, before_k[rows, h // 2, :], start=True, stop=True)
                        last = nc.tensor.matmul(scores_of(h)[:, 0:P], q, qk_t[rows, 1, h // 2, :], start=True, stop=True)
                    last.then_inc(scores_ready, 1)
                    pe.wait_ge(exps_ready, WIDE_HEADS)
                    pe.wait_ge(values_ready, 1)
                    for h in range(WIDE_HEADS):
                        for s in range(span // P):
                            last = nc.tensor.transpose(pa[:, h // 2, ((h % 2) * 2 + s) * P:((h % 2) * 2 + s + 1) * P],
                                                       probs[:, spot(h), s * P:(s + 1) * P], chip.c(C_ID))
                        if h % 2:
                            last.then_inc(probs_turned, 1)
                    pe.wait_ge(probs_copied, HP)
                    for h in range(WIDE_HEADS):
                        for s in range(span // P):
                            vals = (values, before_v)[s]
                            last = nc.tensor.matmul(pb[:, 0, h * WIDE:(h + 1) * WIDE], probs_t[:, h, s, :], vals[:, h * WIDE:(h + 1) * WIDE],
                                                    start=(s == 0), stop=(s == span // P - 1))
                    last.then_inc(out_ready, 1)
                    pe.wait_ge(out_scaled, 1)
                    for c in range(INNER // P):
                        last = nc.tensor.transpose(pb[:, 1, c * P:(c + 1) * P], out[:, c * P:(c + 1) * P], chip.c(C_ID))
                    last.then_inc(out_turned, 1)

                @block.scalar
                def _(act):
                    act.wait_ge(products_ready, 2)
                    nc.scalar.activation(squares[:, :, :].rearrange("p h d -> p (h d)"), pa[:, 0:2, :].rearrange("p b n -> p (b n)"), ACT.Square).then_inc(squares_ready, 1)
                    act.wait_ge(products_ready, 3)
                    nc.scalar.activation(values[:, :], pa[:, 2, :], ACT.Copy).then_inc(values_ready, 1)
                    act.wait_ge(sums_ready, 1)
                    nc.scalar.activation(sums[:, :], sums[:, :], ACT.Sqrt).then_inc(root_ready, 1)
                    act.wait_ge(masked, 1)
                    for h in range(WIDE_HEADS):
                        nc.scalar.activation(probs[:, spot(h), 0:span], probs[:, spot(h), 0:span], ACT.Exp, scale=WIDE ** 0.5,
                                             bias=top[:, spot(h):spot(h) + 1], accum_out=den[:, spot(h):spot(h) + 1]).then_inc(exps_ready, 1)
                    for p in range(0, HP, 2):
                        act.wait_ge(probs_turned, p + 1)
                        copy_probs(lambda o, i: nc.scalar.activation(o, i, ACT.Copy), p)
                    act.wait_ge(scores_ready, 1)
                    act.wait_ge(out_ready, 1)
                    nc.scalar.activation(before_k[:, :, :], qk_t[:, 1, :, :], ACT.Copy).then_inc(kept, 1)
                    nc.scalar.activation(before_v[:, :], values[:, :], ACT.Copy).then_inc(kept, 1)

                @block.vector
                def _(dve):
                    then = in_order(dve, dve_step)
                    tt = nc.vector.tensor_tensor
                    nc.vector.tensor_copy(shifted[:, 0, :], inner[:, 0, bass.ds(tok, P)]).then_inc(shift_ready, 1)
                    if first:
                        then(nc.vector.memset(shifted[:, 1, 0:1], 0.0))
                        nc.vector.tensor_copy(shifted[:, 1, 1:P], inner[:, 1, bass.ds(tok, P - 1)]).then_inc(shift_ready, 1)
                    else:
                        nc.vector.tensor_copy(shifted[:, 1, :], inner[:, 1, bass.ds(tok - 1, P)]).then_inc(shift_ready, 1)
                    for a in range(2):
                        then(nc.vector.tensor_copy(tables[:, a, :, :], rope[:, a, bass.ds(w, 1), :, :].rearrange("p o q d -> p (o q) d")))
                    dve.wait_ge(squares_ready, 1)
                    nc.vector.reduce_sum(sums[:, :], squares[:, :, :], AX.X).then_inc(sums_ready, 1)
                    dve.wait_ge(root_ready, 1)
                    then(nc.vector.tensor_scalar(sums[:, :], sums[:, :], 1e-12, None, ALU.max))
                    then(nc.vector.reciprocal(sums[:, :], sums[:, :]))
                    raw = pa[:, 0:2, :].rearrange("p b (h d) -> p (b h) d", d=WIDE)
                    then(tt(qk[:, :, :], raw, sums[:, :].rearrange("p (h o) -> p h o", o=1).to_broadcast((P, H2, WIDE)), ALU.mult))
                    half = WIDE // 2
                    for t in range(2):
                        own = slice(t * WIDE_HEADS, (t + 1) * WIDE_HEADS)
                        wide = lambda table, d0, n: table[:, d0:d0 + n].rearrange("p (o d) -> p o d", o=1).to_broadcast((P, WIDE_HEADS, n))
                        then(tt(qk[:, own, :], qk[:, own, :], wide(scales[:, t, :], 0, WIDE), ALU.mult))
                        then(tt(turned_qk[:, own, 0:half], qk[:, own, half:WIDE], wide(tables[:, 1, t, :], 0, half), ALU.mult))
                        then(tt(turned_qk[:, own, half:WIDE], qk[:, own, 0:half], wide(tables[:, 1, t, :], half, half), ALU.mult))
                        then(tt(qk[:, own, :], qk[:, own, :], wide(tables[:, 0, t, :], 0, WIDE), ALU.mult))
                    nc.vector.tensor_tensor(qk[:, :, :], qk[:, :, :], turned_qk[:, :, :], ALU.add).then_inc(qk_ready, 1)
                    dve.wait_ge(turned, 1)
                    nc.vector.tensor_copy(qk_t[:, :, :, :].rearrange("p t h n -> p (t h n)"), pa[:, 0:2, :].rearrange("p b n -> p (b n)")).then_inc(qk_turned, 1)
                    dve.wait_ge(scores_ready, 1)
                    mask = lambda at: chip.c(at).rearrange("p (o n) -> p o n", o=1).to_broadcast((P, WIDE_HEADS, P))
                    then(tt(probs[:, :, 0:P], score_all[:, :, 0:P], mask(C_SELF), ALU.add))
                    if not first:
                        then(tt(probs[:, :, P:2 * P], score_all[:, :, P:2 * P], mask(C_BAND), ALU.add))
                    then(nc.vector.reduce_max(top[:, :], probs[:, :, 0:span], AX.X))
                    nc.vector.tensor_scalar(top[:, :], top[:, :], -WIDE ** 0.5, None, ALU.mult).then_inc(masked, 1)
                    for p in range(1, HP, 2):
                        dve.wait_ge(probs_turned, p + 1)
                        copy_probs(nc.vector.tensor_copy, p)
                    dve.wait_ge(exps_ready, WIDE_HEADS)
                    then(nc.vector.reciprocal(den[:, :], den[:, :]))
                    dve.wait_ge(out_ready, 1)
                    inv = den[:, :].rearrange("p (a c o) -> p c a o", a=2, o=1).to_broadcast((P, HP, 2, WIDE))
                    nc.vector.tensor_tensor(out[:, :].rearrange("p (c a d) -> p c a d", a=2, d=WIDE),
                                            pb[:, 0, :].rearrange("p (c a d) -> p c a d", a=2, d=WIDE), inv, ALU.mult).then_inc(out_scaled, 1)
                    dve.wait_ge(out_turned, 1)
                    nc.vector.tensor_copy(out_t[:, :, bass.ds(w * P, P)], pb[:, 1, :].rearrange("p (c n) -> p c n", n=P))

        with nc.Fori(0, BATCH) as b:
            tile_step(b, 0, True)
            with nc.Fori(1, TILES) as w:
                tile_step(b, w, False)
            for j in range(SEQ // GROUP):
                at = bass.ds(b * SEQ + j * GROUP, GROUP)
                with step(nc, "y_ready added") as (block, y_ready, added):
                    @block.tensor
                    def _(pe):
                        for c in range(FC):
                            for k in range(INNER // P):
                                last = nc.tensor.matmul(pa[:, c, :], wo[:, k, c * P:(c + 1) * P], out_t[:, k, j * GROUP:(j + 1) * GROUP],
                                                        start=(k == 0), stop=(k == INNER // P - 1))
                            last.then_inc(y_ready, 1)

                    @block.vector
                    def _(dve):
                        for c in range(FC):
                            dve.wait_ge(y_ready, c + 1)
                            nc.vector.tensor_tensor(inner[:, c, at], pa[:, c, :], inner[:, c, at], ALU.add).then_inc(added, 1)


def gated_ffn(chip, layer, inner):
    nc, io = chip.nc, chip.io
    with ExitStack() as ctx:
        sb = lambda name, shape: ctx.enter_context(sbuf(nc, name, shape, F32))
        w1, w2 = sb("gated_w1", [P, FC, 2 * HC * P]), sb("gated_w2", [P, HC, DIM])
        b1, b2, affine = sb("gated_b1", [P, 2 * HC]), sb("gated_b2", [P, FC]), sb("gated_norm", [P, 2 * FC])
        load(nc, [(w1[:, :, :], io["L1_ffn_w1"][bass.ds(layer * DIM, DIM), :].rearrange("(c p) n -> p c n", p=P)),
                  (w2[:, :, :], io["L1_ffn_w2"][bass.ds(layer * HC * P, HC * P), :].rearrange("(c p) n -> p c n", p=P)),
                  (b1[:, :], io["L1_ffn_b1"][bass.ds(layer * P, P), :]), (b2[:, :], io["L1_ffn_b2"][bass.ds(layer * P, P), :]),
                  (affine[:, :], io["L1_ffn_ln"][bass.ds(layer * P, P), :])])
        h = sb("gated_in", [P, FC, GROUP])
        sq = sb("gated_squares", [P, FC, GROUP])
        rstd = sb("gated_rstd", [P, GROUP])
        gate = sb("gate", [P, 2, GROUP])
        hidden = sb("gated_hidden", [P, HC, GROUP])
        after = sb("gated_after", [P, FC, TOKENS])
        st_ps = ctx.enter_context(banks(nc, "gated_stats", [P, 2, GROUP], F32))
        h_ps = ctx.enter_context(banks(nc, "gated_psum", [P, 4, GROUP], F32))
        y_ps = ctx.enter_context(banks(nc, "gated_out", [P, 2, GROUP], F32))
        with nc.Fori(0, BATCH) as b:
            for j in range(SEQ // GROUP):
                at = b * SEQ + j * GROUP
                with step(nc, "shift_ready mean_ready centred squares_ready var_ready rstd_ready normed pair_ready gate_ready hidden_ready y_ready dve_step") as (
                        block, shift_ready, mean_ready, centred, squares_ready, var_ready, rstd_ready, normed, pair_ready, gate_ready, hidden_ready, y_ready, dve_step):
                    @block.tensor
                    def _(pe):
                        pe.wait_ge(shift_ready, FC)
                        for c in range(FC):
                            last = nc.tensor.matmul(st_ps[:, 0, :], chip.c(C_MEAN), h[:, c, :], start=(c == 0), stop=(c == FC - 1))
                        last.then_inc(mean_ready, 1)
                        pe.wait_ge(squares_ready, FC)
                        for c in range(FC):
                            last = nc.tensor.matmul(st_ps[:, 1, :], chip.c(C_MEAN), sq[:, c, :], start=(c == 0), stop=(c == FC - 1))
                        last.then_inc(var_ready, 1)
                        pe.wait_ge(normed, FC)
                        for n in range(HC):
                            if n >= 2:
                                pe.wait_ge(hidden_ready, n - 1)
                            for part in range(2):
                                for c in range(FC):
                                    m = part * HC + n
                                    last = nc.tensor.matmul(h_ps[:, 2 * (n % 2) + part, :], w1[:, c, m * P:(m + 1) * P], h[:, c, :], start=(c == 0), stop=(c == FC - 1))
                            last.then_inc(pair_ready, 1)
                        for c in range(FC):
                            for n in range(HC):
                                pe.wait_ge(hidden_ready, n + 1)
                                last = nc.tensor.matmul(y_ps[:, c, :], w2[:, n, c * P:(c + 1) * P], hidden[:, n, :], start=(n == 0), stop=(n == HC - 1))
                            last.then_inc(y_ready, 1)

                    @block.scalar
                    def _(act):
                        for c in range(FC):
                            act.wait_ge(centred, c + 1)
                            nc.scalar.activation(sq[:, c, :], h[:, c, :], ACT.Square).then_inc(squares_ready, 1)
                        act.wait_ge(var_ready, 1)
                        nc.scalar.activation(rstd[:, :], st_ps[:, 1, :], ACT.Sqrt, bias=chip.eps[:, 0:1]).then_inc(rstd_ready, 1)
                        for n in range(HC):
                            act.wait_ge(pair_ready, n + 1)
                            if n >= 2:
                                act.wait_ge(hidden_ready, n - 1)
                            nc.scalar.activation(gate[:, n % 2, :], h_ps[:, 2 * (n % 2) + 1, :], ACT.Gelu, bias=b1[:, HC + n:HC + n + 1]).then_inc(gate_ready, 1)

                    @block.vector
                    def _(dve):
                        then = in_order(dve, dve_step)
                        nc.vector.tensor_copy(h[:, 0, :], inner[:, 0, bass.ds(at, GROUP)]).then_inc(shift_ready, 1)
                        if j == 0:
                            then(nc.vector.memset(h[:, 1, 0:1], 0.0))
                            nc.vector.tensor_copy(h[:, 1, 1:GROUP], inner[:, 1, bass.ds(at, GROUP - 1)]).then_inc(shift_ready, 1)
                        else:
                            nc.vector.tensor_copy(h[:, 1, :], inner[:, 1, bass.ds(at - 1, GROUP)]).then_inc(shift_ready, 1)
                        dve.wait_ge(mean_ready, 1)
                        for c in range(FC):
                            nc.vector.tensor_tensor(h[:, c, :], h[:, c, :], st_ps[:, 0, :], ALU.subtract).then_inc(centred, 1)
                        dve.wait_ge(rstd_ready, 1)
                        then(nc.vector.reciprocal(rstd[:, :], rstd[:, :]))
                        for c in range(FC):
                            then(nc.vector.tensor_tensor(h[:, c, :], h[:, c, :], rstd[:, :], ALU.mult))
                            nc.vector.tensor_scalar(h[:, c, :], h[:, c, :], affine[:, c:c + 1], affine[:, FC + c:FC + c + 1], ALU.mult, ALU.add).then_inc(normed, 1)
                        for n in range(HC):
                            dve.wait_ge(gate_ready, n + 1)
                            nc.vector.scalar_tensor_tensor(out=hidden[:, n, :], in0=h_ps[:, 2 * (n % 2), :], scalar=b1[:, n:n + 1], in1=gate[:, n % 2, :],
                                                           op0=ALU.add, op1=ALU.mult).then_inc(hidden_ready, 1)
                        for c in range(FC):
                            dve.wait_ge(y_ready, c + 1)
                            nc.vector.scalar_tensor_tensor(out=after[:, c, bass.ds(at, GROUP)], in0=y_ps[:, c, :], scalar=b2[:, c:c + 1],
                                                           in1=inner[:, c, bass.ds(at, GROUP)], op0=ALU.add, op1=ALU.add)
        with step(nc, "copied") as (block, copied):
            @block.scalar
            def _(act):
                nc.scalar.activation(inner[:, 0, :], after[:, 0, :], ACT.Copy).then_inc(copied, 1)

            @block.vector
            def _(dve):
                nc.vector.tensor_copy(inner[:, 1, :], after[:, 1, :]).then_inc(copied, 1)


STATES, TAPS, RANK = 16, 4, 64
SC = 2 * DIM // P


def state_space(chip):
    nc, io = chip.nc, chip.io
    halves = SEQ // GROUP
    width = SC * P
    with ExitStack() as ctx:
        sb = lambda name, shape: ctx.enter_context(sbuf(nc, name, shape, F32))
        w_in, w_out = sb("in_w", [P, FC, 2 * width]), sb("out_w", [P, SC, DIM])
        w_x, w_dt = sb("x_w", [P, SC, RANK + 2 * STATES]), sb("dt_w", [RANK, width])
        conv = sb("conv_w", [P, SC, TAPS])
        per_feature = sb("ssm_vectors", [P, 3, SC])
        norm_w = sb("ssm_norm", [P, FC])
        a_log = sb("a_log", [P, SC, STATES])
        pick = sb("pick", [2 * STATES, 2 * STATES * P])
        load(nc, [(w_in[:, :, :], io["L2_attn_win"].rearrange("(c p) n -> p c n", p=P)),
                  (w_out[:, :, :], io["L2_attn_wout"].rearrange("(c p) n -> p c n", p=P)),
                  (w_x[:, :, :], io["L2_attn_wx"].rearrange("(c p) n -> p c n", p=P)), (w_dt[:, :], io["L2_attn_wdt"]),
                  (conv[:, :, :], io["L2_attn_conv"].rearrange("(c p) k -> p c k", p=P)), (per_feature[:, :, :], io["L2_attn_vec"]),
                  (norm_w[:, :], io["L2_attn_norm"]), (a_log[:, :, :], io["L2_attn_alog"].rearrange("(c p) n -> p c n", p=P)),
                  (pick[:, :], io["pick"])])
        xs = sb("ssm_x", [P, SC, TAPS - 1 + SEQ])
        gate = sb("ssm_gate", [P, SC, SEQ])
        chip.ssm_states = sb("ssm_states", [2 * STATES, SEQ])
        u, dt, du = sb("ssm_u", [P, SC, SEQ]), sb("ssm_dt", [P, SC, SEQ]), sb("ssm_du", [P, SC, SEQ])
        with step(nc, "exp_ready dve_step") as (block, exp_ready, dve_step):
            @block.scalar
            def _(act):
                nc.scalar.activation(a_log[:, :, :], a_log[:, :, :], ACT.Exp).then_inc(exp_ready, 1)

            @block.vector
            def _(dve):
                dve.wait_ge(exp_ready, 1)
                then = in_order(dve, dve_step)
                then(nc.vector.tensor_scalar(a_log[:, :, :], a_log[:, :, :], -1.0, None, ALU.mult))
                then(nc.vector.memset(xs[:, :, 0:TAPS - 1], 0.0))
        with nc.Fori(0, BATCH) as b:
            ssm_inputs(chip, b, w_in, norm_w, xs, gate)
            ssm_steps(chip, conv, per_feature, w_x, w_dt, xs, u, dt, du)
            ssm_scan(chip, a_log, pick, u, dt, du, gate, per_feature, xs)
            with banks(nc, "norm_psum", [P, 4, GROUP], F32) as norm_ps:
                for j in range(halves):
                    add_norm(chip, bass.ds(b * SEQ + j * GROUP, GROUP), norm_ps, keeps=2.0,
                             product=(w_out, lambda k, j=j: u[:, k, j * GROUP:(j + 1) * GROUP]))


def ssm_inputs(chip, b, w_in, norm_w, xs, gate):
    nc = chip.nc
    halves = SEQ // GROUP
    with ExitStack() as ctx:
        h = ctx.enter_context(sbuf(nc, "ssm_in", [P, FC, SEQ], F32))
        sq, rms = chip.sq, chip.rstd
        mean_ps = ctx.enter_context(banks(nc, "ssm_mean", [P, 2, GROUP], F32))
        in_ps = ctx.enter_context(banks(nc, "ssm_in_psum", [P, 4, GROUP], F32))
        with step(nc, "squares_ready mean_ready rms_ready h_ready in_ready in_copied dve_step") as (
                block, squares_ready, mean_ready, rms_ready, h_ready, in_ready, in_copied, dve_step):
            jobs = [(m, j) for m in range(2 * SC) for j in range(halves)]
            x = lambda c, j: chip.xt[:, c, bass.ds(b * SEQ + j * GROUP, GROUP)]

            @block.scalar
            def _(act):
                for j in range(halves):
                    if j:
                        act.wait_ge(mean_ready, j)
                    for c in range(FC):
                        nc.scalar.activation(sq[:, c, :], x(c, j), ACT.Square).then_inc(squares_ready, 1)
                    act.wait_ge(mean_ready, j + 1)
                    if j:
                        act.wait_ge(h_ready, j)
                    nc.scalar.activation(rms[:, :], mean_ps[:, j, :], ACT.Sqrt, bias=chip.eps[:, 0:1]).then_inc(rms_ready, 1)
                for n, (m, j) in enumerate(jobs):
                    act.wait_ge(in_ready, n + 1)
                    part = slice(j * GROUP, (j + 1) * GROUP)
                    if m < SC:
                        dst = xs[:, m, TAPS - 1 + j * GROUP:TAPS - 1 + (j + 1) * GROUP]
                        nc.scalar.activation(dst, in_ps[:, n % 4, :], ACT.Copy).then_inc(in_copied, 1)
                    else:
                        nc.scalar.activation(gate[:, m - SC, part], in_ps[:, n % 4, :], ACT.Silu).then_inc(in_copied, 1)

            @block.tensor
            def _(pe):
                for j in range(halves):
                    pe.wait_ge(squares_ready, FC * (j + 1))
                    for c in range(FC):
                        last = nc.tensor.matmul(mean_ps[:, j, :], chip.c(C_MEAN), sq[:, c, :], start=(c == 0), stop=(c == FC - 1))
                    last.then_inc(mean_ready, 1)
                pe.wait_ge(h_ready, halves)
                for n, (m, j) in enumerate(jobs):
                    if n >= 4:
                        pe.wait_ge(in_copied, n - 3)
                    for c in range(FC):
                        last = nc.tensor.matmul(in_ps[:, n % 4, :], w_in[:, c, m * P:(m + 1) * P], h[:, c, j * GROUP:(j + 1) * GROUP],
                                                start=(c == 0), stop=(c == FC - 1))
                    last.then_inc(in_ready, 1)

            @block.vector
            def _(dve):
                then = in_order(dve, dve_step)
                for j in range(halves):
                    dve.wait_ge(rms_ready, j + 1)
                    then(nc.vector.reciprocal(rms[:, :], rms[:, :]))
                    for c in range(FC):
                        last = nc.vector.scalar_tensor_tensor(out=h[:, c, j * GROUP:(j + 1) * GROUP], in0=x(c, j), scalar=norm_w[:, c:c + 1],
                                                              in1=rms[:, :], op0=ALU.mult, op1=ALU.mult)
                    last.then_inc(h_ready, 1)


def ssm_steps(chip, conv, per_feature, w_x, w_dt, xs, u, dt, du):
    nc = chip.nc
    halves = SEQ // GROUP
    with ExitStack() as ctx:
        pre = ctx.enter_context(sbuf(nc, "ssm_pre", [P, 2, SEQ], F32))
        logs = ctx.enter_context(sbuf(nc, "ssm_logs", [P, 2, SEQ], F32))
        series = ctx.enter_context(sbuf(nc, "ssm_series", [P, SEQ], F32))
        low = ctx.enter_context(sbuf(nc, "ssm_low", [RANK, SEQ], F32))
        states = chip.ssm_states
        low_ps = ctx.enter_context(banks(nc, "ssm_low_psum", [P, 2, GROUP], F32))
        dt_ps = ctx.enter_context(banks(nc, "ssm_dt_psum", [P, 2, GROUP], F32))
        st_ps = ctx.enter_context(banks(nc, "ssm_states_psum", [P, 2, GROUP], F32))
        with step(nc, "conv_ready u_ready low_ready low_copied dt_ready shifted_ready size_ready exp_ready log_ready dt_done dve_step") as (
                block, conv_ready, u_ready, low_ready, low_copied, dt_ready, shifted_ready, size_ready, exp_ready, log_ready, dt_done, dve_step):
            flat = lambda t: t[:, :, :].rearrange("p b n -> p (b n)")

            @block.vector
            def _(dve):
                then = in_order(dve, dve_step)
                for c in range(SC):
                    acc = pre[:, c % 2, :]
                    if c >= 2:
                        dve.wait_ge(u_ready, c - 1)
                    for k in range(TAPS):
                        tap = xs[:, c, k:k + SEQ]
                        if k == 0:
                            then(nc.vector.tensor_scalar(acc, tap, conv[:, c, 0:1], per_feature[:, 0, c:c + 1], ALU.mult, ALU.add))
                        else:
                            last = nc.vector.scalar_tensor_tensor(out=acc, in0=tap, scalar=conv[:, c, k:k + 1], in1=acc, op0=ALU.mult, op1=ALU.add)
                            if k < TAPS - 1:
                                then(last)
                    last.then_inc(conv_ready, 1)
                edge = 2.0 ** -6
                for c in range(SC):
                    dve.wait_ge(dt_ready, c + 1)
                    bias = per_feature[:, 1, c:c + 1]
                    nc.vector.tensor_scalar(dt[:, c, :], flat(dt_ps), bias, 0.0, ALU.add, ALU.max).then_inc(shifted_ready, 1)
                    dve.wait_ge(exp_ready, c + 1)
                    e, log, stt = pre[:, c % 2, :], logs[:, c % 2, :], nc.vector.scalar_tensor_tensor
                    then(nc.vector.tensor_scalar(series[:, :], e, -1 / 4, 1 / 3, ALU.mult, ALU.add))
                    then(nc.vector.tensor_tensor(series[:, :], series[:, :], e, ALU.mult))
                    then(stt(out=series[:, :], in0=series[:, :], scalar=-0.5, in1=e, op0=ALU.add, op1=ALU.mult))
                    then(stt(out=series[:, :], in0=series[:, :], scalar=1.0, in1=e, op0=ALU.add, op1=ALU.mult))
                    dve.wait_ge(log_ready, c + 1)
                    then(stt(out=log, in0=e, scalar=edge, in1=log, op0=ALU.is_lt, op1=ALU.subtract))
                    then(stt(out=series[:, :], in0=log, scalar=-1.0, in1=series[:, :], op0=ALU.mult, op1=ALU.max))
                    dve.wait_ge(shifted_ready, c + 1)
                    then(nc.vector.tensor_tensor(dt[:, c, :], dt[:, c, :], series[:, :], ALU.add))
                    nc.vector.tensor_tensor(du[:, c, :], dt[:, c, :], u[:, c, :], ALU.mult).then_inc(dt_done, 1)

            @block.scalar
            def _(act):
                for c in range(SC):
                    act.wait_ge(conv_ready, c + 1)
                    nc.scalar.activation(u[:, c, :], pre[:, c % 2, :], ACT.Silu).then_inc(u_ready, 1)
                act.wait_ge(low_ready, 1)
                nc.scalar.activation(low[:, :], flat(low_ps)[0:RANK, :], ACT.Copy).then_inc(low_copied, 1)
                nc.scalar.activation(states[:, :], flat(st_ps)[0:2 * STATES, :], ACT.Copy).then_inc(low_copied, 1)
                for c in range(SC):
                    act.wait_ge(dt_ready, c + 1)
                    act.wait_ge(shifted_ready, c + 1)
                    if c >= 2:
                        act.wait_ge(dt_done, c - 1)
                    part = pre[:, c % 2, :]
                    nc.scalar.activation(part, flat(dt_ps), ACT.Abs, bias=per_feature[:, 1, c:c + 1]).then_inc(size_ready, 1)
                    act.wait_ge(size_ready, c + 1)
                    nc.scalar.activation(part, part, ACT.Exp, scale=-1.0).then_inc(exp_ready, 1)
                    act.wait_ge(exp_ready, c + 1)
                    nc.scalar.activation(logs[:, c % 2, :], part, ACT.Ln, bias=chip.eps[:, 2:3]).then_inc(log_ready, 1)

            @block.tensor
            def _(pe):
                for j in range(halves):
                    for c in range(SC):
                        pe.wait_ge(u_ready, c + 1)
                        nc.tensor.matmul(low_ps[0:RANK, j, :], w_x[:, c, 0:RANK], u[:, c, j * GROUP:(j + 1) * GROUP], start=(c == 0), stop=(c == SC - 1))
                        last = nc.tensor.matmul(st_ps[0:2 * STATES, j, :], w_x[:, c, RANK:RANK + 2 * STATES], u[:, c, j * GROUP:(j + 1) * GROUP],
                                                start=(c == 0), stop=(c == SC - 1))
                last.then_inc(low_ready, 1)
                pe.wait_ge(low_copied, 1)
                for c in range(SC):
                    if c:
                        pe.wait_ge(shifted_ready, c)
                        pe.wait_ge(size_ready, c)
                    for j in range(halves):
                        last = nc.tensor.matmul(dt_ps[:, j, :], w_dt[:, c * P:(c + 1) * P], low[:, j * GROUP:(j + 1) * GROUP], start=True, stop=True)
                    last.then_inc(dt_ready, 1)


def ssm_scan(chip, a, pick, u, dt, du, gate, per_feature, y):
    nc = chip.nc
    halves = SEQ // GROUP
    with ExitStack() as ctx:
        sb = lambda name, shape: ctx.enter_context(sbuf(nc, name, shape, F32))
        decay, added, state, term = (sb(n, [P, 2, SEQ]) for n in ("decay", "added", "state", "term"))
        b_ps = ctx.enter_context(banks(nc, "state_in", [P, 2, SEQ], F32))
        c_ps = ctx.enter_context(banks(nc, "state_out", [P, 2, SEQ], F32))
        sums = lambda c: y[:, c, TAPS - 1:TAPS - 1 + SEQ]
        total = STATES * SC
        with step(nc, "spread_ready decay_ready added_ready state_ready term_ready summed dve_step") as (
                block, spread_ready, decay_ready, added_ready, state_ready, term_ready, summed, dve_step):
            @block.tensor
            def _(pe):
                for n in range(STATES):
                    if n >= 2:
                        pe.wait_ge(term_ready, SC * (n - 1))
                    for which, ps in ((0, b_ps), (1, c_ps)):
                        row = which * STATES + n
                        for j in range(halves):
                            last = nc.tensor.matmul(ps[:, n % 2, j * GROUP:(j + 1) * GROUP], pick[:, row * P:(row + 1) * P],
                                                    chip.ssm_states[:, j * GROUP:(j + 1) * GROUP], start=True, stop=True)
                    last.then_inc(spread_ready, 1)

            @block.scalar
            def _(act):
                for i in range(total):
                    n, c = divmod(i, SC)
                    if i >= 2:
                        act.wait_ge(state_ready, i - 1)
                    nc.scalar.activation(decay[:, i % 2, :], dt[:, c, :], ACT.Exp, scale=a[:, c, n:n + 1]).then_inc(decay_ready, 1)

            @block.vector
            def _(dve):
                then = in_order(dve, dve_step)
                for i in range(total):
                    n, c = divmod(i, SC)
                    dve.wait_ge(spread_ready, n + 1)
                    nc.vector.tensor_tensor(added[:, i % 2, :], du[:, c, :], b_ps[:, n % 2, :], ALU.mult).then_inc(added_ready, 1)
                    dve.wait_ge(added_ready, i + 1)
                    dve.wait_ge(decay_ready, i + 1)
                    nc.vector.tensor_tensor_scan(state[:, i % 2, :], decay[:, i % 2, :], added[:, i % 2, :], 0.0, ALU.mult, ALU.add).then_inc(state_ready, 1)
                    dve.wait_ge(state_ready, i + 1)
                    if i >= 2:
                        dve.wait_ge(summed, i - 1)
                    nc.vector.tensor_tensor(term[:, i % 2, :], state[:, i % 2, :], c_ps[:, n % 2, :], ALU.mult).then_inc(term_ready, 1)
                for c in range(SC):
                    dve.wait_ge(summed, total)
                    then(nc.vector.scalar_tensor_tensor(out=u[:, c, :], in0=u[:, c, :], scalar=per_feature[:, 2, c:c + 1], in1=sums(c), op0=ALU.mult, op1=ALU.add))
                    then(nc.vector.tensor_tensor(u[:, c, :], u[:, c, :], gate[:, c, :], ALU.mult))

            @block.gpsimd
            def _(pool):
                for i in range(total):
                    n, c = divmod(i, SC)
                    pool.wait_ge(term_ready, i + 1)
                    if n == 0:
                        nc.gpsimd.tensor_copy(sums(c), term[:, i % 2, :]).then_inc(summed, 1)
                    else:
                        pool.wait_ge(summed, i - SC + 1)
                        nc.gpsimd.tensor_tensor(sums(c), sums(c), term[:, i % 2, :], ALU.add).then_inc(summed, 1)


KEYS, TOP, SIDES, RHEADS, RDIM = 128, 8, 2, 4, 32
EMBEDS, RINNER = 4096, 512
PICKS = RHEADS * TOP


def retrieval_ffn(chip):
    nc, io = chip.nc, chip.io
    per = GROUP // P
    rc = RINNER // P
    with ExitStack() as ctx:
        sb = lambda name, shape, dt=F32: ctx.enter_context(sbuf(nc, name, shape, dt))
        wq, keys = sb("query_w", [P, FC, SIDES * P]), sb("product_keys", [P, SIDES, RHEADS * KEYS])
        wg, wu, wd = sb("r_gate_w", [P, FC, RINNER]), sb("r_up_w", [P, FC, RINNER]), sb("r_down_w", [P, rc, DIM])
        load(nc, [(wq[:, :, :], io["L3_ffn_wq"].rearrange("(c p) n -> p c n", p=P)), (keys[:, :, :], io["L3_ffn_keys"]),
                  (wg[:, :, :], io["L3_ffn_wg"].rearrange("(c p) n -> p c n", p=P)), (wu[:, :, :], io["L3_ffn_wu"].rearrange("(c p) n -> p c n", p=P)),
                  (wd[:, :, :], io["L3_ffn_wd"].rearrange("(c p) n -> p c n", p=P))])
        stage = sb("r_stage", [P, FC, GROUP])
        q_t = sb("r_queries", [P, SIDES, GROUP])
        rows = sb("r_rows", [P, per, DIM])
        sims = sb("r_sims", [P, SIDES, RHEADS * KEYS])
        best = sb("r_best", [P, SIDES, RHEADS, TOP])
        best_at = sb("r_best_at", [P, SIDES, RHEADS, TOP], U32)
        at_f = sb("r_at", [P, SIDES, RHEADS, TOP])
        sums, codes = sb("r_sums", [P, RHEADS, TOP, TOP]), sb("r_codes", [P, RHEADS, TOP, TOP])
        score, pos, pos_f = sb("r_score", [P, RHEADS, TOP]), sb("r_pos", [P, RHEADS, TOP], U32), sb("r_pos_f", [P, RHEADS, TOP])
        hot = sb("r_hot", [P, TOP, TOP * TOP])
        code = sb("r_code", [P, RHEADS, TOP])
        pick = sb("r_pick", [P, per, PICKS], U32)
        weight = sb("r_weight", [P, per, RHEADS, TOP])
        total = sb("r_total", [P, RHEADS])
        dots, act_dots = sb("r_dots", [P, PICKS]), sb("r_act", [P, PICKS])
        ring = 16
        down, up = sb("r_down", [P, ring, DIM]), sb("r_up", [P, ring, DIM])
        scratch = sb("r_scratch", [P, DIM])
        mixed = sb("r_mixed", [P, per, DIM])
        hidden, gate = sb("r_hidden", [P, rc, GROUP]), sb("r_gate", [P, 2, GROUP])
        arrived = [[chip.keep_semaphore(f"{side}_arrived_{n}") for side in ("down", "up")] for n in range(ring)]
        q_ps = ctx.enter_context(banks(nc, "r_psum_q", [P, 2, GROUP], F32))
        a_ps = ctx.enter_context(banks(nc, "r_psum_a", [P, 2, GROUP], F32))
        norm_ps = ctx.enter_context(banks(nc, "norm_psum", [P, 4, GROUP], F32))
        with nc.Fori(0, GROUPS) as g:
            retrieval_scores(chip, g, wq, keys, stage, q_t, rows, sims, best, best_at, at_f, sums, codes, score, pos, pos_f, hot, code,
                             pick, weight, total, q_ps, a_ps, norm_ps[:, 0:2, :])
            for t in range(per):
                retrieval_rows(chip, g * per + t, t, rows, pick, weight, dots, act_dots, down, up, scratch, mixed, arrived)
            with step(nc, "pair_ready gate_ready hidden_ready y_ready y_copied") as (block, pair_ready, gate_ready, hidden_ready, y_ready, y_copied):
                @block.tensor
                def _(pe):
                    for n in range(rc):
                        if n >= 1:
                            pe.wait_ge(hidden_ready, n)
                        for k, w in enumerate((wg, wu)):
                            for c in range(FC):
                                last = nc.tensor.matmul(a_ps[:, k, :], w[:, c, n * P:(n + 1) * P], stage[:, c, :], start=(c == 0), stop=(c == FC - 1))
                        last.then_inc(pair_ready, 1)
                    for c in range(FC):
                        for n in range(rc):
                            pe.wait_ge(hidden_ready, n + 1)
                            last = nc.tensor.matmul(q_ps[:, c, :], wd[:, n, c * P:(c + 1) * P], hidden[:, n, :], start=(n == 0), stop=False)
                        for t in range(per):
                            last = nc.tensor.matmul(q_ps[:, c, t * P:(t + 1) * P], mixed[:, t, c * P:(c + 1) * P], chip.c(C_ID), start=False, stop=(t == per - 1))
                    last.then_inc(y_ready, 1)

                @block.scalar
                def _(act):
                    for n in range(rc):
                        act.wait_ge(pair_ready, n + 1)
                        if n >= 2:
                            act.wait_ge(hidden_ready, n - 1)
                        nc.scalar.activation(gate[:, n % 2, :], a_ps[:, 0, :], ACT.Silu).then_inc(gate_ready, 1)

                @block.vector
                def _(dve):
                    for n in range(rc):
                        dve.wait_ge(gate_ready, n + 1)
                        nc.vector.tensor_tensor(hidden[:, n, :], gate[:, n % 2, :], a_ps[:, 1, :], ALU.mult).then_inc(hidden_ready, 1)
            add_norm(chip, group_slice(g), norm_ps, ready=lambda c: q_ps[:, c, :])


def retrieval_scores(chip, g, wq, keys, stage, q_t, rows, sims, best, best_at, at_f, sums, codes, score, pos, pos_f, hot, code,
                     pick, weight, total, q_ps, a_ps, rows_ps):
    nc = chip.nc
    per = GROUP // P
    with step(
            nc, "staged q_ready q_copied sims_ready sims_copied sims_used turned rows_ready shifted exps_ready dve_step") as (
            block, staged, q_ready, q_copied, sims_ready, sims_copied, sims_used, turned, rows_ready, shifted, exps_ready, dve_step):
        @block.tensor
        def _(pe):
            pe.wait_ge(staged, 1)
            for s in range(SIDES):
                for c in range(FC):
                    last = nc.tensor.matmul(q_ps[:, s, :], wq[:, c, s * P:(s + 1) * P], stage[:, c, :], start=(c == 0), stop=(c == FC - 1))
                last.then_inc(q_ready, 1)
            for t in range(per):
                for c in range(FC):
                    last = nc.tensor.transpose(rows_ps[:, t // 2, (t % 2) * DIM + c * P:(t % 2) * DIM + (c + 1) * P],
                                               stage[:, c, t * P:(t + 1) * P], chip.c(C_ID))
            last.then_inc(turned, 1)
            pe.wait_ge(q_copied, SIDES)
            for t in range(per):
                if t:
                    pe.wait_ge(sims_copied, t)
                for s in range(SIDES):
                    last = nc.tensor.matmul(a_ps[:, s, :], q_t[:, s, t * P:(t + 1) * P], keys[:, s, :], start=True, stop=True)
                last.then_inc(sims_ready, 1)

        @block.scalar
        def _(act):
            for s in range(SIDES):
                act.wait_ge(q_ready, s + 1)
                nc.scalar.activation(q_t[:, s, :], q_ps[:, s, :], ACT.Copy).then_inc(q_copied, 1)
            act.wait_ge(turned, 1)
            nc.scalar.activation(rows[:, :, :], rows_ps[:, :, :].rearrange("p b (t n) -> p (b t) n", n=DIM), ACT.Copy).then_inc(rows_ready, 1)
            for t in range(per):
                act.wait_ge(sims_ready, t + 1)
                if t:
                    act.wait_ge(sims_used, t)
                nc.scalar.activation(sims[:, :, :], a_ps[:, :, :], ACT.Copy).then_inc(sims_copied, 1)
            for t in range(per):
                act.wait_ge(shifted, t + 1)
                nc.scalar.activation(weight[:, t, :, :], weight[:, t, :, :], ACT.Exp).then_inc(exps_ready, 1)

        @block.vector
        def _(dve):
            then = in_order(dve, dve_step)
            nc.vector.tensor_copy(stage[:, :, :], chip.xt[:, :, group_slice(g)]).then_inc(staged, 1)
            tt = nc.vector.tensor_tensor
            for t in range(per):
                dve.wait_ge(sims_copied, t + 1)
                for s in range(SIDES):
                    for h in range(RHEADS):
                        own = sims[:, s, h * KEYS:(h + 1) * KEYS]
                        then(nc.vector.max(best[:, s, h, :], own))
                        last = nc.vector.max_index(best_at[:, s, h, :], best[:, s, h, :], own)
                        if (s, h) != (SIDES - 1, RHEADS - 1):
                            then(last)
                last.then_inc(sims_used, 1)
                dve.wait_ge(sims_used, t + 1)
                then(nc.vector.tensor_copy(at_f[:, :, :, :], best_at[:, :, :, :]))
                down_k = lambda v: v.rearrange("p (hk o) -> p hk o", o=1).to_broadcast((P, PICKS, TOP))
                first = lambda v: down_k(v[:, 0, :, :].rearrange("p h k -> p (h k)"))
                pairs = lambda v: v[:, :, :, :].rearrange("p h a b -> p (h a) b")
                then(nc.vector.tensor_scalar(at_f[:, 0, :, :], at_f[:, 0, :, :], float(KEYS), None, ALU.mult))
                for h in range(RHEADS):
                    second = lambda v: v[:, 1, h, :].rearrange("p (o k) -> p o k", o=1).to_broadcast((P, TOP, TOP))
                    mine = lambda v: v[:, 0, h, :].rearrange("p (k o) -> p k o", o=1).to_broadcast((P, TOP, TOP))
                    then(tt(sums[:, h, :, :], mine(best), second(best), ALU.add))
                    then(tt(codes[:, h, :, :], mine(at_f), second(at_f), ALU.add))
                for h in range(RHEADS):
                    flat = sums[:, h, :, :].rearrange("p a b -> p (a b)")
                    then(nc.vector.max(score[:, h, :], flat))
                    then(nc.vector.max_index(pos[:, h, :], score[:, h, :], flat))
                then(nc.vector.tensor_copy(pos_f[:, :, :], pos[:, :, :]))
                for h in range(RHEADS):
                    wide = pos_f[:, h, :].rearrange("p (k o) -> p k o", o=1).to_broadcast((P, TOP, TOP * TOP))
                    iota = chip.c(C_IOTA, TOP * TOP).rearrange("p (o n) -> p o n", o=1).to_broadcast((P, TOP, TOP * TOP))
                    flat = codes[:, h, :, :].rearrange("p a b -> p (a b)").rearrange("p (o n) -> p o n", o=1).to_broadcast((P, TOP, TOP * TOP))
                    then(tt(hot[:, :, :], wide, iota, ALU.is_equal))
                    then(tt(hot[:, :, :], hot[:, :, :], flat, ALU.mult))
                    then(nc.vector.reduce_sum(code[:, h, :], hot[:, :, :], AX.X))
                then(nc.vector.tensor_scalar(code[:, :, :], code[:, :, :], float(EMBEDS - 1), None, ALU.min))
                then(nc.vector.tensor_copy(pick[:, t, :], code[:, :, :].rearrange("p h k -> p (h k)")))
                top = score[:, :, 0:1].to_broadcast((P, RHEADS, TOP))
                nc.vector.tensor_tensor(weight[:, t, :, :], score[:, :, :], top, ALU.subtract).then_inc(shifted, 1)
            for t in range(per):
                dve.wait_ge(exps_ready, t + 1)
                then(nc.vector.reduce_sum(total[:, :], weight[:, t, :, :], AX.X))
                then(nc.vector.reciprocal(total[:, :], total[:, :]))
                then(tt(weight[:, t, :, :], weight[:, t, :, :], total[:, :].rearrange("p (h o) -> p h o", o=1).to_broadcast((P, RHEADS, TOP)), ALU.mult))


def retrieval_rows(chip, tile, t, rows, pick, weight, dots, act_dots, down, up, scratch, mixed, arrived):
    nc, io = chip.nc, chip.io
    ring = len(arrived)
    rounds = PICKS // ring
    come = lambda n: 16 * rounds * tile + 16 * (n // ring + 1)
    with step(nc, "dot_ready dots_active weighted added dve_step") as (block, dot_ready, dots_active, weighted, added, dve_step):
        @block.gpsimd
        def _(pool):
            def gather(table, to, n, sem):
                nc.gpsimd.indirect_dma_start(out=to[:, n % ring, :], out_offset=None, in_=io[table],
                                             in_offset=bass.IndirectOffsetOnAxis(ap=pick[:, t, n:n + 1], axis=0)).then_inc(sem, 16)

            for n in range(PICKS):
                if n >= ring:
                    pool.wait_ge(dot_ready, n - ring + 1)
                gather("L3_ffn_down", down, n, arrived[n % ring][0])
            for n in range(PICKS):
                if n >= ring:
                    pool.wait_ge(added, n - ring + 1)
                gather("L3_ffn_up", up, n, arrived[n % ring][1])
            pool.wait_ge(added, PICKS)

        @block.vector
        def _(dve):
            then = in_order(dve, dve_step)
            for n in range(PICKS):
                dve.wait_ge(arrived[n % ring][0], come(n))
                nc.vector.tensor_tensor_reduce(scratch[:, :], down[:, n % ring, :], rows[:, t, :], 1.0, 0.0, ALU.mult, ALU.add,
                                               dots[:, n:n + 1]).then_inc(dot_ready, 1)
                dve.wait_ge(dot_ready, n + 1)
            dve.wait_ge(dots_active, 1)
            nc.vector.tensor_tensor(act_dots[:, :], act_dots[:, :], weight[:, t, :, :].rearrange("p h k -> p (h k)"), ALU.mult).then_inc(weighted, 1)
            dve.wait_ge(weighted, 1)
            for n in range(PICKS):
                dve.wait_ge(arrived[n % ring][1], come(n))
                if n:
                    nc.vector.scalar_tensor_tensor(out=mixed[:, t, :], in0=up[:, n % ring, :], scalar=act_dots[:, n:n + 1], in1=mixed[:, t, :],
                                                   op0=ALU.mult, op1=ALU.add).then_inc(added, 1)
                else:
                    nc.vector.tensor_scalar(mixed[:, t, :], up[:, 0, :], act_dots[:, 0:1], None, ALU.mult).then_inc(added, 1)
                dve.wait_ge(added, n + 1)

        @block.scalar
        def _(act):
            act.wait_ge(dot_ready, PICKS)
            nc.scalar.activation(act_dots[:, :], dots[:, :], ACT.Silu).then_inc(dots_active, 1)


def rope_tables():
    import numpy as np
    f = np.float32
    half = np.arange(0, WIDE, 2, dtype=f)
    inv_freq = (f(1.0) / f(10000.0) ** (half / f(WIDE))).astype(f)
    t = np.arange(SEQ, dtype=f)
    freqs = (t[:, None] * inv_freq[None, :]).astype(f)
    base = ((half + f(0.4 * WIDE)) / f(1.4 * WIDE)).astype(f)
    power = ((t - SEQ // 2) / f(P // 2)).astype(f)
    scale = (base[None, :] ** power[:, None]).astype(f)
    twice = lambda v: np.concatenate([v, v], axis=-1)
    sign = np.where(np.arange(WIDE) < WIDE // 2, f(-1), f(1))
    out = np.zeros((2, SEQ, 2, WIDE), f)
    cos, sin, scale = twice(np.cos(freqs)), twice(np.sin(freqs)) * sign, twice(scale)
    out[0, :, 0], out[0, :, 1] = cos * scale, cos / scale
    out[1, :, 0], out[1, :, 1] = sin * scale, sin / scale
    return np.ascontiguousarray(out.reshape(2, TILES, P, 2, WIDE).transpose(2, 0, 1, 3, 4))


def layout_more(a, io, cols):
    import numpy as np
    f = np.float32
    io["L0_ffn_wg"] = a["L0_ffn_wg"]
    io["L0_ffn_w1"] = a["L0_ffn_w_gate"].reshape(EXPERTS * DIM, EXPERT_INNER)
    io["L0_ffn_w2"] = a["L0_ffn_w_down"].reshape(EXPERTS * EXPERT_INNER, DIM)
    io["rope"] = rope_tables()
    io["L1_ffn_wqkv"] = a["L1_ffn_wqkv"].reshape(DEPTH * DIM, 3 * INNER)
    io["L1_ffn_wo"] = a["L1_ffn_wo"].reshape(DEPTH * INNER, DIM)
    io["L1_ffn_scales"] = np.concatenate([a["L1_ffn_q_scale"], a["L1_ffn_k_scale"]], axis=1)
    w1, b1 = np.zeros((DEPTH, DIM, 2, HC * P), f), np.zeros((DEPTH, 2, HC * P), f)
    w1[..., :HIDDEN] = a["L1_ffn_w1"].reshape(DEPTH, DIM, 2, HIDDEN)
    b1[..., :HIDDEN] = a["L1_ffn_b1"].reshape(DEPTH, 2, HIDDEN)
    w2 = np.zeros((DEPTH, HC * P, DIM), f)
    w2[:, :HIDDEN] = a["L1_ffn_w2"]
    io["L1_ffn_w1"], io["L1_ffn_w2"] = w1.reshape(DEPTH * DIM, 2 * HC * P), w2.reshape(DEPTH * HC * P, DIM)
    io["L1_ffn_b1"] = np.concatenate([cols(b1[n].ravel()) for n in range(DEPTH)])
    io["L1_ffn_b2"] = np.concatenate([cols(a["L1_ffn_b2"][n]) for n in range(DEPTH)])
    io["L1_ffn_ln"] = np.concatenate([np.concatenate([cols(a["L1_ffn_ln_g"][n]), cols(a["L1_ffn_ln_b"][n])], axis=1) for n in range(DEPTH)])
    io["L2_attn_win"] = np.ascontiguousarray(a["L2_attn_in_proj_w"].T)
    io["L2_attn_wout"] = np.ascontiguousarray(a["L2_attn_out_proj_w"].T)
    io["L2_attn_wx"] = np.ascontiguousarray(a["L2_attn_x_proj_w"].T)
    io["L2_attn_wdt"] = np.ascontiguousarray(a["L2_attn_dt_proj_w"].T)
    io["L2_attn_conv"] = a["L2_attn_conv_w"].reshape(-1, TAPS)
    io["L2_attn_vec"] = np.ascontiguousarray(np.stack([cols(a["L2_attn_" + n]) for n in ("conv_b", "dt_proj_b", "D")], axis=1))
    io["L2_attn_norm"] = cols(a["L2_attn_norm_w"])
    io["L2_attn_alog"] = a["L2_attn_A_log"]
    pick = np.zeros((2 * STATES, 2 * STATES, P), f)
    pick[np.arange(2 * STATES), np.arange(2 * STATES)] = 1.0
    io["pick"] = pick.reshape(2 * STATES, -1)
    io["L3_ffn_wq"] = np.ascontiguousarray(a["L3_ffn_w_queries"].T)
    keys = np.zeros((RHEADS, RDIM, SIDES, RHEADS, KEYS), f)
    for h in range(RHEADS):
        keys[h, :, :, h, :] = a["L3_ffn_keys"][h].transpose(2, 1, 0)
    io["L3_ffn_keys"] = keys.reshape(P, SIDES, RHEADS * KEYS)
    io["L3_ffn_down"], io["L3_ffn_up"] = a["L3_ffn_down_embed"], a["L3_ffn_up_embed"]
    io["L3_ffn_wg"], io["L3_ffn_wu"], io["L3_ffn_wd"] = (np.ascontiguousarray(a["L3_ffn_w_" + n].T) for n in ("gate", "up", "down"))


LAYERS = [quantised_attention, cross_attention, expert_ffn, normed_attention, context_mlp, local_transformer,
          state_space, concat_context, spiking_ffn, linear_attention, causal_attention, retrieval_ffn]


def decoder(nc, io, out, layers):
    with ExitStack() as ctx:
        chip = Chip(nc, ctx, io)
        chip.ctx_t = ctx.enter_context(sbuf(nc, "context", [P, FC, BATCH * CTX], F32))
        load(nc, [(chip.xt[:, :, :], io["x"].rearrange("(c p) t -> p c t", p=P)), (chip.const[:, :], io["constants"]),
                  (chip.ctx_t[:, :, :], io["ctx_t"].rearrange("(c p) t -> p c t", p=P)), (chip.eps[:, :], io["epsilons"])])
        for layer in layers:
            layer(chip)
        with step(nc, "stored") as (block, stored):
            @block.sync
            def _(sp):
                sp.dma_start(out.rearrange("(c p) t -> p c t", p=P), chip.xt[:, :, :]).then_inc(stored, 16)
                sp.wait_ge(stored, 16)


def constants():
    import numpy as np
    row, col = np.arange(P)[:, None], np.arange(P)[None, :]
    c = np.zeros((P, C_END), np.float32)
    c[:, C_ID:C_ID + P] = row == col
    c[:, C_MEAN:C_MEAN + P] = 1.0 / DIM
    c[:, C_ONES:C_ONES + P] = 1.0
    c[:, C_HEADMEAN:C_HEADMEAN + P] = ((row // SLOT == col // SLOT) & (row % SLOT < HEAD) & (col % SLOT < HEAD)) / HEAD
    c[:, C_DEN:C_DEN + P] = (row // SLOT == col // SLOT) & (row % SLOT == ONE)
    c[:, C_FART:C_FART + P] = np.where(row > col, FAR, 0.0)
    c[:, C_FARN:C_FARN + P] = np.where(col > row, FAR, 0.0)
    c[:, C_KEEPT:C_KEEPT + P] = row <= col
    c[:, C_BEFORE:C_BEFORE + P] = row < col
    c[:, C_BAND:C_BAND + P] = np.where(col < row, FAR, 0.0)
    c[:, C_SELF:C_SELF + P] = np.where(col > row, FAR, 0.0)
    c[:, C_IOTA:C_IOTA + P] = col
    c[:, C_ROWS] = np.arange(P) % SLOT < HEAD
    return c


def layout(a):
    import numpy as np
    f = np.float32
    cols = lambda v: np.ascontiguousarray(v.reshape(-1, P).T)

    def pad_cols(w, pad=0.0):
        out = np.full((w.shape[0], HEADS, SLOT), pad, f)
        out[:, :, :HEAD] = w.reshape(w.shape[0], HEADS, HEAD)
        return out.reshape(w.shape[0], PADDED)

    def pad_rows(w):
        out = np.zeros((HEADS, SLOT, w.shape[1]), f)
        out[:, :HEAD] = w.reshape(HEADS, HEAD, w.shape[1])
        return out.reshape(PADDED, w.shape[1])

    def pad_bias(bq, bk, bv, key_bias=False):
        out = np.zeros((3, HEADS, SLOT), f)
        for t, v in enumerate((bq, bk, bv)):
            if v is not None:
                out[t, :, :HEAD] = v.reshape(HEADS, HEAD)
        out[1:, :, ONE] = 1.0
        if key_bias:
            out[0, :, BIAS] = 1.0
        return np.ascontiguousarray(out.reshape(3, HGS, P).transpose(2, 0, 1))

    none = np.zeros(DIM, f)
    io = {"x": np.ascontiguousarray(a["x"].reshape(TOKENS, DIM).T), "constants": constants(),
          "ctx_t": np.ascontiguousarray(a["ctx_1024"].reshape(-1, DIM).T), "ctx": a["ctx_1024"].reshape(-1, DIM),
          "epsilons": np.tile(np.array([1e-5, 1e-6, 1.0, 0.0], f), (P, 1))}
    w = a["L0_attn_W_qkv"]
    io["L0_attn_w"] = np.stack([pad_cols(w[t * DIM:(t + 1) * DIM].T) for t in range(3)])
    bqkv = a["L0_attn_b_qkv"].reshape(3, DIM)
    io["L0_attn_b"] = pad_bias(*bqkv)
    io["L0_attn_wo"] = pad_rows(a["L0_attn_W_proj"].T)
    io["L0_attn_bo"] = cols(a["L0_attn_b_proj"])
    io["L0_attn_ws"] = np.stack([pad_cols(a["L0_attn_s_w_qkv"].reshape(3, DIM), 1.0).ravel(),
                                 pad_cols(a["L0_attn_zp_w_qkv"].reshape(3, DIM)).ravel()])
    io["L0_attn_ps"] = np.stack([a["L0_attn_s_w_proj"], a["L0_attn_zp_w_proj"]])
    io["L0_attn_scalars"] = np.stack([a["L0_attn_" + n] for n in (
        "s_act_qkv", "zp_act_qkv", "s_attn", "zp_attn", "s_act_proj", "zp_act_proj")]).reshape(1, 6)
    io["L0_xattn_w"] = np.stack([pad_cols(a["L0_xattn_W" + n].T) for n in "qkv"])
    io["L0_xattn_b"] = pad_bias(None, None, None, key_bias=True)
    io["L0_xattn_wo"] = pad_rows(a["L0_xattn_Wo"].T)
    io["L0_xattn_bo"] = cols(none)
    io["key_bias"] = a["fside_BxS2_0"].reshape(1, -1)
    rows = np.zeros((1, P), f)
    rows[0, BIAS::SLOT] = HEAD ** 0.5
    io["bias_rows"] = rows
    io["L1_attn_w"] = np.stack([pad_cols(a["L1_attn_W" + n]) for n in "qkv"])
    plain = pad_bias(a["L1_attn_bq"], a["L1_attn_bk"], a["L1_attn_bv"])
    plain[ONE::SLOT] = 0.0
    io["L1_attn_b"] = plain
    norm = np.zeros((3, 2, PACK, SLOT), f)
    for t, n in enumerate("qkv"):
        norm[t, 0, :, :HEAD] = a[f"L1_attn_{n}_scale"]
        norm[t, 1, :, :HEAD] = a[f"L1_attn_{n}_bias"]
    norm[1:, 1, :, ONE] = 1.0
    io["L1_attn_norm"] = np.ascontiguousarray(norm.reshape(3, 2, P).transpose(2, 0, 1))
    io["L1_attn_wo"] = pad_rows(a["L1_attn_Wo"])
    io["L1_attn_bo"] = cols(a["L1_attn_bo"])
    io["L2_xattn_w"] = np.ascontiguousarray(a["L2_xattn_W"].T)
    io["L2_xattn_b"] = cols(a["L2_xattn_b"])
    io["L2_ffn_w1"] = np.ascontiguousarray(a["L2_ffn_W_fc"].T)
    io["L2_ffn_w2"] = np.ascontiguousarray(a["L2_ffn_W_proj"].T)
    half = DIM // 4
    wkv = np.concatenate([a["L3_attn_Wk"], a["L3_attn_Wv"]], axis=1)
    io["L3_attn_wkv"] = np.ascontiguousarray(wkv)
    io["L3_attn_bkv"] = np.concatenate([a["L3_attn_bk"], a["L3_attn_bv"]]).reshape(P, 1)
    wc = np.zeros((P, P), f)
    wc[:half, :half] = wc[half:, half:] = a["L3_attn_Wc"]
    io["L3_attn_wc"] = wc
    repeated = np.repeat(a["L3_attn_We"].reshape(half, HEADS // PACK, HEAD), PACK, axis=1).reshape(half, DIM)
    up = np.zeros((2, DIM, PADDED), f)
    up[0, :half] = up[1, half:2 * half] = pad_cols(repeated)
    io["L3_attn_w"] = np.stack([pad_cols(a["L3_attn_Wq"]), up[0], up[1]])
    io["L3_attn_b"] = pad_bias(a["L3_attn_bq"], None, None)
    io["L3_attn_wo"] = pad_rows(a["L3_attn_Wo"])
    io["L3_attn_bo"] = cols(a["L3_attn_bo"])
    io["L3_attn_affine"] = np.ascontiguousarray(np.stack([cols(a["L3_attn_gamma"]), cols(a["L3_attn_beta"])], axis=1))
    wkv = a["L3_xattn_Wkv"]
    io["L3_xattn_w"] = np.stack([pad_cols(a["L3_xattn_Wq"]), pad_cols(wkv[:, :DIM]), pad_cols(wkv[:, DIM:])])
    io["L3_xattn_b"] = pad_bias(None, None, None)
    io["L3_xattn_wo"] = pad_rows(a["L3_xattn_Wout"])
    io["L3_xattn_bo"] = cols(a["L3_xattn_bout"])
    layout_more(a, io, cols)
    return io


def kernel(**inputs):
    import numpy as np
    import concourse.bacc as bacc
    from concourse.bass_utils import run_bass_kernel_spmd

    arrays = layout({k: np.asarray(v) for k, v in inputs.items()})
    nc = bacc.Bacc("TRN2", target_bir_lowering=False, num_devices=1)
    io = {k: nc.dram_tensor("in_" + k, v.shape, mybir.dt.from_np(v.dtype), kind="ExternalInput").ap() for k, v in arrays.items()}
    out = nc.dram_tensor("out_t", (DIM, TOKENS), F32, kind="ExternalOutput").ap()
    decoder(nc, io, out, LAYERS)
    result = run_bass_kernel_spmd(nc, [{"in_" + k: v for k, v in arrays.items()}], core_ids=[0])
    return np.ascontiguousarray(result.results[0]["out_t"].T).reshape(BATCH, SEQ, DIM)
```

```python
from contextlib import ExitStack, contextmanager

import concourse.bass as bass
from concourse import mybir

F32 = mybir.dt.float32
BF16 = mybir.dt.bfloat16
U32 = mybir.dt.uint32
ALU = mybir.AluOpType
ACT = mybir.ActivationFunctionType
AX = mybir.AxisListType

P = 128
BATCH, SEQ, DIM = 4, 1024, 256
TOKENS = BATCH * SEQ
CTX = 77
FC = DIM // P
GROUP = 512
GROUPS = TOKENS // GROUP
HEADS, HEAD = 16, 16
SLOT = 32
PACK = P // SLOT
HGS = HEADS // PACK
PADDED = HEADS * SLOT
TILES = SEQ // P
FAR = -float(2 ** 60)
ROUND = float(1.5 * 2 ** 23)
QMAX = 255.0
C_ID, C_MEAN, C_ONES, C_HEADMEAN, C_DEN, C_FART, C_FARN, C_KEEPT, C_BEFORE, C_BAND, C_SELF = (P * n for n in range(11))
C_IOTA = 11 * P
C_SLOTS = C_IOTA + P
C_ROWS = C_SLOTS + P
C_PARTROW = C_ROWS + 1
C_END = C_PARTROW + 3


def sbuf(nc, name, shape, dtype):
    return nc.sbuf_tensor(name, shape, dtype, allow_name_mangling=True)


def banks(nc, name, shape, dtype):
    return nc.psum_tensor(name, shape, dtype, allow_name_mangling=True)


@contextmanager
def step(nc, names):
    with ExitStack() as ctx:
        sems = [ctx.enter_context(nc.semaphore(n)) for n in names.split()]
        with nc.Block() as block:
            yield (block, *sems)
        nums = sorted(s.num for s in sems)
        start = 0
        for n in range(len(nums)):
            if n + 1 == len(nums) or nums[n + 1] != nums[n] + 1:
                nc.sync.sem_clear(range(nums[start], nums[n] + 1))
                start = n + 1
        nc.all_engine_barrier(sem_only=True)


def in_order(eng, sem):
    count = [0]

    def then(instruction):
        count[0] += 1
        instruction.then_inc(sem, 1)
        eng.wait_ge(sem, count[0])

    return then


def load(nc, pairs):
    with step(nc, "loaded") as (block, loaded):
        @block.sync
        def _(sp):
            for dst, src in pairs:
                sp.dma_start(dst, src).then_inc(loaded, 16)
            sp.wait_ge(loaded, 16 * len(pairs))


class Chip:

    def __init__(self, nc, ctx, io):
        self.nc, self.io, self.ctx = nc, io, ctx
        self.xt = ctx.enter_context(sbuf(nc, "residual", [P, FC, TOKENS], F32))
        self.const = ctx.enter_context(sbuf(nc, "constants", [P, C_END], F32))
        self.id_bf, self.far_t, self.far_n = (ctx.enter_context(sbuf(nc, n, [P, P], BF16)) for n in ("identity_bf16", "far_t_bf16", "far_n_bf16"))
        self.eps = ctx.enter_context(sbuf(nc, "epsilons", [P, 4], F32))
        self.z = ctx.enter_context(sbuf(nc, "norm_sum", [P, 2, FC, GROUP], F32))
        self.sq = ctx.enter_context(sbuf(nc, "norm_squares", [P, 2, FC, GROUP], F32))
        self.root = ctx.enter_context(sbuf(nc, "norm_root", [P, 2, GROUP // P], F32))

    def keep_semaphore(self, name):
        return self.ctx.enter_context(self.nc.semaphore(name))

    def c(self, start, n=P):
        return self.const[:, start:start + n]


def add_norm(chip, toks, psum, product=None, ready=None, bias=None, affine=None, keeps=1.0):
    nc, z, sq, root = chip.nc, chip.z, chip.sq, chip.root
    n, per = len(toks), GROUP // P
    y_ps = lambda g, c: psum[:, 4 * g + c, :]
    mean_ps = lambda g: psum[:, 4 * g + 2, :]
    rstd_ps = lambda g: psum[:, 4 * g + 3, :]
    rounds = 2 if affine else 1
    x = lambda g, c: chip.xt[:, c, toks[g]]
    with step(nc, "y_ready sum_ready mean_ready centred squares_ready var_ready root_ready inverse_ready rstd_ready dve_step") as (
            block, y_ready, sum_ready, mean_ready, centred, squares_ready, var_ready, root_ready, inverse_ready, rstd_ready, dve_step):
        @block.tensor
        def _(pe):
            if product:
                weights, inputs = product
                chunks = weights.shape[1]
                for g in range(n):
                    for c in range(FC):
                        for k in range(chunks):
                            last = nc.tensor.matmul(y_ps(g, c), weights[:, k, c * P:(c + 1) * P], inputs(g, k),
                                                    start=(k == 0), stop=(k == chunks - 1))
                        last.then_inc(y_ready, 1)
            for r in range(rounds):
                for g in range(n):
                    pe.wait_ge(sum_ready, FC * (r * n + g + 1))
                    for c in range(FC):
                        last = nc.tensor.matmul(mean_ps(g), chip.c(C_MEAN), z[:, g, c, :], start=(c == 0), stop=(c == FC - 1))
                    last.then_inc(mean_ready, 1)
                for g in range(n):
                    pe.wait_ge(squares_ready, FC * (r * n + g + 1))
                    for t in range(per):
                        for c in range(FC):
                            last = nc.tensor.matmul(rstd_ps(g)[:, t:t + 1], sq[:, g, c, t * P:(t + 1) * P], chip.c(C_MEAN, 1),
                                                    start=(c == 0), stop=(c == FC - 1))
                    last.then_inc(var_ready, 1)
                for g in range(n):
                    pe.wait_ge(inverse_ready, r * n + g + 1)
                    for t in range(per):
                        last = nc.tensor.matmul(rstd_ps(g)[:, t * P:(t + 1) * P], root[:, g, t:t + 1].to_broadcast((P, P)),
                                                chip.c(C_ID), start=True, stop=True)
                    last.then_inc(rstd_ready, 1)

        @block.scalar
        def _(act):
            for r in range(rounds):
                for g in range(n):
                    for c in range(FC):
                        act.wait_ge(centred, FC * (r * n + g) + c + 1)
                        nc.scalar.activation(sq[:, g, c, :], z[:, g, c, :], ACT.Square).then_inc(squares_ready, 1)
                for g in range(n):
                    act.wait_ge(var_ready, r * n + g + 1)
                    nc.scalar.activation(root[:, g, :], rstd_ps(g)[:, 0:per], ACT.Sqrt, bias=chip.eps[:, 0:1]).then_inc(root_ready, 1)

        @block.vector
        def _(dve):
            then = in_order(dve, dve_step)
            for g in range(n):
                for c in range(FC):
                    if product:
                        dve.wait_ge(y_ready, FC * g + c + 1)
                    y = y_ps(g, c) if product else ready(g, c)
                    if keeps != 1.0:
                        nc.vector.scalar_tensor_tensor(out=z[:, g, c, :], in0=x(g, c), scalar=keeps, in1=y,
                                                       op0=ALU.mult, op1=ALU.add).then_inc(sum_ready, 1)
                    elif bias is None:
                        nc.vector.tensor_tensor(z[:, g, c, :], y, x(g, c), ALU.add).then_inc(sum_ready, 1)
                    else:
                        nc.vector.scalar_tensor_tensor(out=z[:, g, c, :], in0=y, scalar=bias[:, c:c + 1], in1=x(g, c),
                                                       op0=ALU.add, op1=ALU.add).then_inc(sum_ready, 1)
            for r in range(rounds):
                for g in range(n):
                    dve.wait_ge(mean_ready, r * n + g + 1)
                    for c in range(FC):
                        nc.vector.tensor_tensor(z[:, g, c, :], z[:, g, c, :], mean_ps(g), ALU.subtract).then_inc(centred, 1)
                for g in range(n):
                    dve.wait_ge(root_ready, r * n + g + 1)
                    nc.vector.reciprocal(root[:, g, :], root[:, g, :]).then_inc(inverse_ready, 1)
                for g in range(n):
                    dve.wait_ge(rstd_ready, r * n + g + 1)
                    for c in range(FC):
                        if r == rounds - 1:
                            nc.vector.tensor_tensor(x(g, c), z[:, g, c, :], rstd_ps(g), ALU.mult)
                        else:
                            scale, shift = affine
                            then(nc.vector.tensor_tensor(z[:, g, c, :], z[:, g, c, :], rstd_ps(g), ALU.mult))
                            then(nc.vector.tensor_scalar(z[:, g, c, :], z[:, g, c, :], scale[:, c:c + 1], shift[:, c:c + 1],
                                                         ALU.mult, ALU.add))
                            nc.vector.tensor_tensor(z[:, g, c, :], z[:, g, c, :], x(g, c), ALU.add).then_inc(sum_ready, 1)


def group_slice(g):
    return bass.ds(g * GROUP, GROUP)


def fake_quant(nc, then, tmp, src, scalars, out):
    inv, zero, scale = (scalars[:, n:n + 1] for n in range(3))
    then(nc.vector.tensor_scalar(tmp, src, inv, zero, ALU.mult, ALU.add))
    then(nc.vector.tensor_scalar(tmp, tmp, 0.0, QMAX, ALU.max, ALU.min))
    then(nc.vector.tensor_scalar(tmp, tmp, ROUND, ROUND, ALU.add, ALU.subtract))
    return nc.vector.tensor_scalar(out, tmp, zero, scale, ALU.subtract, ALU.mult)


PARTS = 3
PAIRS = [(0, 0), (0, 1), (0, 2), (1, 0), (1, 1), (2, 0)]
STACK = len(PAIRS) * HEAD
HALF_HEADS = P // HEAD
HALVES = SEQ // GROUP
PER_HALF = GROUP // P


def stack_parts(nc, sp, scratch, parts, stack, tokens, which, m, written, stacked, at):
    for p in range(PARTS):
        sp.dma_start(scratch[p, m * P:(m + 1) * P, 0:tokens], parts[:, p, :]).then_inc(written, 16)
    sp.wait_ge(written, at + 16 * PARTS)
    for n, pair in enumerate(PAIRS):
        sp.dma_start(stack[n * HEAD:(n + 1) * HEAD, m * HALF_HEADS:(m + 1) * HALF_HEADS, 0:tokens],
                     scratch[pair[which], m * P:(m + 1) * P, 0:tokens].rearrange("(h r) t -> r h t", r=HEAD)).then_inc(stacked, 16)


def split_attention(chip, mode, params, key_bias=None, norm=None, quant=None):
    nc, io = chip.nc, chip.io
    w, wo, b_qk, v_bias, bo = params
    quantised, normed, causal, cross = (mode == m for m in ("quant", "normed", "causal", "cross"))
    own, context, maxed = not cross, cross or causal, not quantised
    extra = PARTS if cross or quantised else 0
    max_row = STACK + extra
    rows = max_row + (PARTS if maxed else 0)
    scale = quant[:, 3:4] if quantised else HEAD ** -0.5
    sides = 2 if own else 1
    blocks = [(t, m) for m in range(2) for t in range(sides)]
    kinds = (1 if context else 0) + (HALVES if own else 0)

    def items(half):
        out = [(None, 0)] if context else []
        if own:
            tiles = PER_HALF * (half + 1) if causal else TILES
            out += [(kt, max(0, kt - PER_HALF * half) * P if causal else 0) for kt in range(tiles)]
        return out

    slots = [(g, half, kt, off) for g in range(HGS) for half in range(HALVES) for kt, off in items(half)]
    last_slot = {(g, half): n for n, (g, half, _, _) in enumerate(slots)}
    diagonal = lambda half, kt: causal and kt is not None and kt >= PER_HALF * half

    def first_pass(g):
        out = []
        for qt in range(TILES):
            if context:
                out.append((qt, None, None))
            if own:
                out += [(qt, i, j) for i in range(PACK) for j in range(1 + qt // PER_HALF if causal else HALVES)]
        return out

    order = []

    def maxima(g, jobs):
        order.extend(("max", g) + job for job in jobs)

    if maxed:
        maxima(0, first_pass(0))
        order.append(("turn", 0))
    per_group = len(slots) // HGS
    due = {}
    for n, (g, half, kt, off) in enumerate(slots):
        s = n % per_group
        jobs = first_pass(g + 1) if maxed and g + 1 < HGS else []
        spread = max(1, per_group - 3)
        share = jobs[len(jobs) * s // spread:len(jobs) * (s + 1) // spread] if s < spread else []
        order.extend(due.pop(n, []))
        order.append(("scores", n, 0))
        cuts = [len(share) // 5, 3 * len(share) // 5]
        maxima(g + 1, share[:cuts[0]])
        order.append(("scores", n, 1))
        maxima(g + 1, share[cuts[0]:cuts[1]])
        if n:
            order.append(("values", n - 1))
            if last_slot[slots[n - 1][:2]] == n - 1:
                order.append(("raw",) + slots[n - 1][:2])
                due.setdefault(n + 1, []).append(("sums",) + slots[n - 1][:2])
                due.setdefault(n + 2, []).append(("normal",) + slots[n - 1][:2])
        maxima(g + 1, share[cuts[1]:])
        if jobs and s == min(spread, per_group - 1):
            order.append(("turn", g + 1))
    for n in sorted(due):
        order.extend(due[n])
    order += [("values", len(slots) - 1), ("raw",) + slots[-1][:2]]
    order += [("sums",) + slots[-1][:2], ("normal",) + slots[-1][:2]]
    ring = {step_: r for r, step_ in enumerate(s for s in order if s[0] in ("max", "turn", "sums", "normal"))}

    with ExitStack() as ctx:
        sb = lambda name, shape, dt=F32: ctx.enter_context(sbuf(nc, name, shape, dt))
        q_stack = sb("query_stack", [rows, HEADS, SEQ], BF16)
        f = sb("features", [P, HGS, SEQ])
        ot = f
        probs = sb("probs", [P, 2, 2, 2, GROUP])
        parts = probs[:, :, :, :, :].rearrange("p a b c n -> p (a b c n)").bitcast(BF16)[:, 0:2 * PARTS * SEQ].rearrange(
            "p (n a t) -> p n a t", n=2, a=PARTS)
        raw_out = sb("raw_out", [P, HALVES, GROUP])
        inverse = sb("inverse", [P, HALVES, PER_HALF * PACK])
        wide_inverse = sb("wide_inverse", [P, HALVES, PER_HALF * PACK, SLOT])
        stage, sq = chip.z, chip.sq
        scratch = [nc.dram_tensor(f"{mode}_parts_{t}", (PARTS, DIM, SEQ), BF16).ap() for t in range(2)]
        if own:
            k_stack = sb("key_stack", [rows, HEADS, SEQ], BF16)
            v = sb("head_values", [P, TILES, HEADS, SLOT])
        if maxed:
            row_max = sb("row_max", [P, PACK, TILES, kinds])
            top = sb("top", [P, PACK, TILES])
            top_parts = sb("top_parts", [P, PARTS, PACK, TILES], BF16)
            top_rows = sb("top_rows", [PARTS * PACK * TILES, P], BF16)
            top_dram = nc.dram_tensor(f"{mode}_top", (PARTS, PACK, SEQ), BF16).ap()
        if context:
            keys_c = sb("context_keys", [rows, HEADS, BATCH * CTX], BF16)
            keys_now = sb("context_keys_now", [rows, HEADS, CTX], BF16)
            values_c = sb("context_values", [CTX, BATCH, HEADS, HEAD])
            values_now = sb("context_values_now", [CTX, HEADS, SLOT])
        if normed:
            head_root = sb("head_root", [P, len(blocks), TILES, HALF_HEADS])
            wide_root = sb("wide_root", [P, len(blocks), TILES, P])
            value_root = sb("value_root", [P, TILES * HEADS])

        with step(nc, "set dve_step") as (block, set_, dve_step):
            @block.vector
            def _(dve):
                fills = [(q_stack[STACK:rows, :, :], 1.0)]
                fills += [(k_stack[STACK:rows, :, :], 1.0), (v[:, :, :, HEAD + 1:], 0.0), (v[:, :, :, HEAD:HEAD + 1], 1.0)] if own else []
                fills += [(keys_c[STACK:rows, :, :], 1.0), (values_now[:, :, HEAD + 1:], 0.0),
                          (values_now[:, :, HEAD:HEAD + 1], 1.0)] if context else []
                fills += [(row_max[:, :, :, :], FAR)] if maxed else []
                for buffer, value in fills:
                    nc.vector.memset(buffer, value).then_inc(set_, 1)
                dve.wait_ge(set_, len(fills))
                if quantised:
                    then = in_order(dve, dve_step)
                    zero, zero_bf, row = inverse[:, 0, 0:1], parts[:, 0, 0, 0:1], inverse[:, 0, 1:2]
                    then(nc.vector.tensor_copy(zero, quant[:, 2:3]))
                    then(nc.vector.memset(row, 0.0))
                    for p in range(PARTS):
                        then(nc.vector.tensor_copy(zero_bf, zero))
                        then(nc.vector.tensor_tensor(zero, zero, zero_bf, ALU.subtract))
                        then(nc.vector.scalar_tensor_tensor(out=row, in0=zero_bf, scalar=chip.c(C_PARTROW + p, 1), in1=row,
                                                            op0=ALU.mult, op1=ALU.add))
                    then(nc.vector.tensor_scalar(k_stack[STACK:rows, :, :], k_stack[STACK:rows, :, :], row[STACK:rows, :], None, ALU.mult))
        if context:
            context_stacks(chip, mode, params, key_bias, f, parts, scratch[1], keys_c, values_c)

        def project_and_attend(b, s_ps, r_ps, o_ps):
            with step(nc, "staged now_ready projected f_ready squares_ready var_ready root_ready inverse_ready spread_ready "
                          "normed_ready part_ready parts_ready written stacked_0 stacked_1 v_projected v_ready v_squares v_roots v_scaled "
                          "ring_ready ring_read top_ready top_copied top_written top_loaded "
                          "scores_ready scores_read probs_ready outputs_added raw_ready wide_ready root_wide dve_step pool_step") as (
                    block, staged, now_ready, projected, f_ready, squares_ready, var_ready, root_ready, inverse_ready, spread_ready,
                    normed_ready, part_ready, parts_ready, written, stacked_0, stacked_1, v_projected, v_ready, v_squares, v_roots, v_scaled,
                    ring_ready, ring_read, top_ready, top_copied, top_written, top_loaded,
                    scores_ready, scores_read, probs_ready, outputs_added, raw_ready, wide_ready, root_wide, dve_step, pool_step):
                stacked = (stacked_0, stacked_1)
                jobs = [(n, j) for n in range(len(blocks)) for j in range(HALVES)]
                x = lambda c, j: stage[:, j, c, :]
                flat_x = chip.xt[:, :, bass.ds(b * SEQ, SEQ)].rearrange("p c (j t) -> p j c t", j=HALVES)
                block_out = lambda n: f[:, n, :]
                v_jobs = TILES // 2 if own else 0
                v_heads = v[:, :, :, 0:HEAD] if own else None

                @block.tensor
                def _(pe):
                    pe.wait_ge(staged, 1)
                    for k, (n, j) in enumerate(jobs):
                        t, m = blocks[n]
                        if k >= 4:
                            pe.wait_ge(f_ready, k - 3)
                        for c in range(FC):
                            last = nc.tensor.matmul(s_ps[:, k % 4, :], w[:, t, c, m * P:(m + 1) * P], x(c, j), start=(c == 0), stop=(c == FC - 1))
                        last.then_inc(projected, 1)
                    for k in range(v_jobs):
                        pe.wait_ge(f_ready, len(jobs) - 3 + k)
                        for i in range(2):
                            kt = 2 * k + i
                            for c in range(FC):
                                last = nc.tensor.matmul(s_ps[:, k, i * DIM:(i + 1) * DIM],
                                                        x(c, kt // PER_HALF)[:, (kt % PER_HALF) * P:(kt % PER_HALF + 1) * P], w[:, 2, c, :],
                                                        start=(c == 0), stop=(c == FC - 1))
                        last.then_inc(v_projected, 1)
                    if normed:
                        for n in range(len(blocks)):
                            pe.wait_ge(squares_ready, n + 1)
                            for kt in range(TILES):
                                at = (n * TILES + kt) * HALF_HEADS
                                last = nc.tensor.matmul(r_ps[:, 0, at:at + HALF_HEADS],
                                                        sq[:, n % 2, :, :].rearrange("p c t -> p (c t)")[:, kt * P:(kt + 1) * P],
                                                        chip.c(C_HEADMEAN)[:, 0:P:HEAD], start=True, stop=True)
                            last.then_inc(var_ready, 1)
                        for k, (n, j) in enumerate(jobs):
                            pe.wait_ge(root_wide, n + 1)
                            if k >= 2:
                                pe.wait_ge(normed_ready, k - 1)
                            for i in range(PER_HALF):
                                spread = wide_root[:, n, j * PER_HALF + i, :]
                                last = nc.tensor.matmul(o_ps[:, k % 2, i * P:(i + 1) * P], spread, chip.c(C_ID), start=True, stop=True)
                            last.then_inc(spread_ready, 1)

                    def ring_bank(step_):
                        r = ring[step_]
                        if r >= 2:
                            pe.wait_ge(ring_read, r - 1)
                        return r_ps[:, r % 2, :]

                    for step_ in order:
                        kind = step_[0]
                        if kind == "max":
                            _, g, qt, i, j = step_
                            if step_[2:] == first_pass(g)[0]:
                                pe.wait_ge(stacked[g // 2], 16 * len(PAIRS) * sides)
                                if context:
                                    pe.wait_ge(now_ready, 2)
                                if normed and g == 0:
                                    pe.wait_ge(inverse_ready, len(blocks))
                            out = ring_bank(step_)
                            heads = range(PACK) if i is None else [i]
                            for i_ in heads:
                                h = PACK * g + i_
                                lhs = q_stack[0:max_row, h, qt * P:(qt + 1) * P]
                                if i is None:
                                    last = nc.tensor.matmul(out[:, i_ * CTX:(i_ + 1) * CTX], lhs, keys_now[0:max_row, h, :], start=True, stop=True)
                                else:
                                    cols = min(GROUP, (qt + 1) * P - j * GROUP) if causal else GROUP
                                    edge = causal and j == qt // PER_HALF
                                    last = nc.tensor.matmul(out[:, 0:cols], lhs, k_stack[0:max_row, h, j * GROUP:j * GROUP + cols],
                                                            start=True, stop=not edge)
                                    if edge:
                                        last = nc.tensor.matmul(out[:, cols - P:cols], chip.id_bf[:, :], chip.far_n[:, :], start=False, stop=True)
                            last.then_inc(ring_ready, 1)
                        elif kind == "turn":
                            g = step_[1]
                            out = ring_bank(step_)
                            pe.wait_ge(top_ready, g + 1)
                            nc.tensor.matmul(out[0:PARTS * PACK * TILES, 0:P], top_parts[:, :, :, :].rearrange("p a i q -> p (a i q)"),
                                             chip.id_bf[:, :], start=True, stop=True).then_inc(ring_ready, 1)
                        elif kind == "scores":
                            _, n, pair = step_
                            g, half, kt, off = slots[n]
                            e = 2 * n + pair
                            if n % per_group == 0 and pair == 0:
                                pe.wait_ge(stacked[g // 2], 16 * len(PAIRS) * sides)
                                if maxed:
                                    pe.wait_ge(top_loaded, 16 * (g + 1))
                                if n == 0:
                                    pe.wait_ge(f_ready, len(jobs))
                                    if own:
                                        pe.wait_ge(v_ready, v_jobs)
                            if e >= 2:
                                pe.wait_ge(scores_read if quantised else probs_ready, e - 1)
                            for i in range(2):
                                h = PACK * g + 2 * pair + i
                                k_rows = CTX if kt is None else P
                                keys = keys_now[0:rows, h, :] if kt is None else k_stack[0:rows, h, kt * P:(kt + 1) * P]
                                out = s_ps[0:k_rows, 2 * (e % 2) + i, :]
                                edge = diagonal(half, kt)
                                last = nc.tensor.matmul(out[:, off:GROUP], keys, q_stack[0:rows, h, half * GROUP + off:(half + 1) * GROUP],
                                                        start=True, stop=not edge)
                                if edge:
                                    last = nc.tensor.matmul(out[:, off:off + P], chip.id_bf[:, :], chip.far_t[:, :], start=False, stop=True)
                            last.then_inc(scores_ready, 1)
                        elif kind == "values":
                            n = step_[1]
                            g, half, kt, off = slots[n]
                            k_rows = CTX if kt is None else P
                            first, final = (kt, off) == items(half)[0], (kt, off) == items(half)[-1]
                            pe.wait_ge(probs_ready, 2 * n + 2)
                            if n == 0 and normed:
                                pe.wait_ge(v_scaled, 1)
                            if first and g:
                                pe.wait_ge(raw_ready, HALVES * (g - 1) + half + 1)
                            for i in range(PACK):
                                h = PACK * g + i
                                vals = values_now[:, h, :] if kt is None else v[:, kt, h, :]
                                last = nc.tensor.matmul(o_ps[SLOT * i:SLOT * (i + 1), half, off:GROUP], vals,
                                                        probs[0:k_rows, n % 2, i // 2, i % 2, off:GROUP], start=first, stop=final)
                            last.then_inc(outputs_added, 1)
                        elif kind == "sums":
                            _, g, half = step_
                            out = ring_bank(step_)
                            pe.wait_ge(raw_ready, HALVES * g + half + 1)
                            for t in range(PER_HALF):
                                last = nc.tensor.matmul(out[:, t * PACK:(t + 1) * PACK], raw_out[:, half, t * P:(t + 1) * P],
                                                        chip.c(C_DEN)[:, 0:P:SLOT], start=True, stop=True)
                            last.then_inc(ring_ready, 1)
                        elif kind == "normal":
                            _, g, half = step_
                            out = ring_bank(step_)
                            pe.wait_ge(wide_ready, HALVES * g + half + 1)
                            for t in range(PER_HALF):
                                spread = wide_inverse[:, half, t * PACK:(t + 1) * PACK, :].rearrange("p h r -> p (h r)")
                                last = nc.tensor.matmul(out[:, t * P:(t + 1) * P], spread, chip.c(C_ID), start=True, stop=True)
                            last.then_inc(ring_ready, 1)

                @block.scalar
                def _(act):
                    for k, (n, j) in enumerate(jobs):
                        t, m = blocks[n]
                        act.wait_ge(projected, k + 1)
                        factor = quant[:, 1:2] if quantised and t == 0 else 1.0
                        nc.scalar.activation(f[:, n, j * GROUP:(j + 1) * GROUP], s_ps[:, k % 4, :], ACT.Identity,
                                             bias=b_qk[:, t, m:m + 1], scale=factor).then_inc(f_ready, 1)
                    if normed:
                        for n in range(len(blocks)):
                            act.wait_ge(f_ready, HALVES * (n + 1))
                            if n >= 2:
                                act.wait_ge(var_ready, n - 1)
                            nc.scalar.activation(sq[:, n % 2, :, :].rearrange("p c t -> p (c t)"), f[:, n, :], ACT.Square).then_inc(squares_ready, 1)
                        for n in range(len(blocks)):
                            act.wait_ge(var_ready, n + 1)
                            if n == 0:
                                act.wait_ge(var_ready, len(blocks))
                            at = n * TILES * HALF_HEADS
                            nc.scalar.activation(head_root[:, n, :, :].rearrange("p t h -> p (t h)"), r_ps[:, 0, at:at + TILES * HALF_HEADS],
                                                 ACT.Sqrt, bias=chip.eps[:, 1:2]).then_inc(root_ready, 1)
                        for n in range(len(blocks)):
                            act.wait_ge(inverse_ready, n + 1)
                            nc.scalar.activation(wide_root[:, n, :, :].rearrange("p t (h d) -> p (t h) d", d=HEAD),
                                                 head_root[:, n, :, :].rearrange("p t (h o) -> p (t h) o", o=1).to_broadcast((P, TILES * HALF_HEADS, HEAD)),
                                                 ACT.Copy).then_inc(root_wide, 1)
                        act.wait_ge(v_ready, v_jobs)
                        squares = sq[:, :, :, :].rearrange("p n c t -> p (n c t)").rearrange("p (t h d) -> p t h d", h=HEADS, d=HEAD)
                        nc.scalar.activation(squares, v_heads, ACT.Square).then_inc(v_squares, 1)
                        act.wait_ge(v_roots, 1)
                        nc.scalar.activation(value_root[:, :], value_root[:, :], ACT.Sqrt, bias=chip.eps[:, 1:2], scale=1.0 / HEAD).then_inc(v_roots, 1)
                    elif own:
                        for k in range(v_jobs):
                            if v_bias is None:
                                act.wait_ge(v_projected, k + 1)
                                nc.scalar.activation(v[:, 2 * k:2 * k + 2, :, 0:HEAD], s_ps[:, k, :].rearrange("p (t h d) -> p t h d", t=2, d=HEAD),
                                                     ACT.Copy).then_inc(v_ready, 1)
                    act.wait_ge(written, 16 * PARTS * len(blocks))
                    for step_ in order:
                        kind = step_[0]
                        if kind == "scores":
                            _, n, pair = step_
                            g, half, kt, off = slots[n]
                            e = 2 * n + pair
                            k_rows = CTX if kt is None else P
                            if n >= 2:
                                act.wait_ge(outputs_added, n - 1)
                            dst = probs[0:k_rows, n % 2, pair, :, off:GROUP]
                            if quantised:
                                act.wait_ge(scores_read, e + 1)
                                nc.scalar.activation(dst, dst, ACT.Exp, bias=quant[:, 4:5], scale=scale).then_inc(probs_ready, 1)
                            else:
                                act.wait_ge(scores_ready, e + 1)
                                nc.scalar.activation(dst, s_ps[0:k_rows, 2 * (e % 2):2 * (e % 2) + 2, off:GROUP], ACT.Exp,
                                                     scale=scale).then_inc(probs_ready, 1)
                        elif kind == "raw":
                            _, g, half = step_
                            act.wait_ge(outputs_added, last_slot[(g, half)] + 1)
                            if g:
                                act.wait_ge(ring_read, ring[("normal", g - 1, half)] + 1)
                            nc.scalar.activation(raw_out[:, half, :], o_ps[:, half, :], ACT.Copy).then_inc(raw_ready, 1)
                        elif kind == "normal":
                            _, g, half = step_
                            act.wait_ge(ring_read, ring[("sums", g, half)] + 1)
                            nc.scalar.activation(wide_inverse[:, half, :, :], inverse[:, half, :].rearrange("p (n o) -> p n o", o=1)
                                                 .to_broadcast((P, PER_HALF * PACK, SLOT)), ACT.Copy).then_inc(wide_ready, 1)

                @block.vector
                def _(dve):
                    then = in_order(dve, dve_step)
                    tt, ts, copy = nc.vector.tensor_tensor, nc.vector.tensor_scalar, nc.vector.tensor_copy
                    if quantised:
                        fake_quant(nc, then, stage[:, :, :, :], flat_x, quant[:, 8:11], stage[:, :, :, :]).then_inc(staged, 1)
                    else:
                        copy(stage[:, :, :, :], flat_x).then_inc(staged, 1)

                    def split(n):
                        dst = parts[:, n % 2, :, :]
                        if n >= 2:
                            dve.wait_ge(written, 16 * PARTS * (n - 1))
                        then(copy(dst[:, 0, :], f[:, n, :]))
                        then(tt(f[:, n, :], f[:, n, :], dst[:, 0, :], ALU.subtract))
                        copy(dst[:, 1, :], f[:, n, :]).then_inc(part_ready, 1)

                    def values(k):
                        dve.wait_ge(v_projected, k + 1)
                        bias = v_bias[:, :].rearrange("p (o h d) -> p o h d", o=1, d=HEAD).to_broadcast((P, 2, HEADS, HEAD))
                        tt(v[:, 2 * k:2 * k + 2, :, 0:HEAD], s_ps[:, k, :].rearrange("p (t h d) -> p t h d", t=2, d=HEAD), bias,
                           ALU.add).then_inc(v_ready, 1)

                    if normed:
                        for k in range(v_jobs):
                            values(k)
                        for n in range(len(blocks)):
                            dve.wait_ge(root_ready, n + 1)
                            nc.vector.reciprocal(head_root[:, n, :, :], head_root[:, n, :, :]).then_inc(inverse_ready, 1)
                        for k, (n, j) in enumerate(jobs):
                            t, m = blocks[n]
                            part = f[:, n, j * GROUP:(j + 1) * GROUP]
                            dve.wait_ge(spread_ready, k + 1)
                            tt(part, part, o_ps[:, k % 2, :], ALU.mult).then_inc(normed_ready, 1)
                            dve.wait_ge(normed_ready, k + 1)
                            then(ts(part, part, norm[0][:, t, 0:1], norm[0][:, t, 1:2], ALU.mult, ALU.add))
                            if j == HALVES - 1:
                                split(n)
                        squares = sq[:, :, :, :].rearrange("p n c t -> p (n c t)").rearrange("p (m d) -> p m d", d=HEAD)
                        dve.wait_ge(v_squares, 1)
                        nc.vector.reduce_sum(value_root[:, :], squares, AX.X).then_inc(v_roots, 1)
                        dve.wait_ge(v_roots, 2)
                        then(nc.vector.reciprocal(value_root[:, :], value_root[:, :]))
                        every = v_heads.rearrange("p t h d -> p (t h) d")
                        tt(every, every, value_root[:, :].rearrange("p (m o) -> p m o", o=1).to_broadcast((P, TILES * HEADS, HEAD)),
                           ALU.mult).then_inc(v_roots, 1)
                    else:
                        for n in range(len(blocks)):
                            dve.wait_ge(f_ready, HALVES * (n + 1))
                            split(n)
                        if own and v_bias is not None:
                            for k in range(v_jobs):
                                values(k)

                    dve.wait_ge(parts_ready, len(blocks))
                    dve.wait_ge(written, 16 * PARTS * len(blocks))
                    for step_ in order:
                        kind = step_[0]
                        if step_ in ring:
                            r = ring[step_]
                            src = r_ps[:, r % 2, :]
                            if kind != "turn":
                                dve.wait_ge(ring_ready, r + 1)
                        if kind == "max":
                            _, g, qt, i, j = step_
                            if i is None:
                                nc.vector.reduce_max(row_max[:, :, qt, 0], src[:, 0:PACK * CTX].rearrange("p (i n) -> p i n", i=PACK),
                                                     AX.X).then_inc(ring_read, 1)
                            else:
                                cols = min(GROUP, (qt + 1) * P - j * GROUP) if causal else GROUP
                                at = j + kinds - HALVES
                                nc.vector.reduce_max(row_max[:, i, qt, at:at + 1], src[:, 0:cols], AX.X).then_inc(ring_read, 1)
                        elif kind == "turn":
                            g = step_[1]
                            if r:
                                dve.wait_ge(ring_read, r)
                            then(nc.vector.reduce_max(top[:, :, :], row_max[:, :, :, :], AX.X))
                            then(ts(top[:, :, :], top[:, :, :], -1.0, None, ALU.mult))
                            for p in range(PARTS):
                                last = copy(top_parts[:, p, :, :], top[:, :, :])
                                if p < PARTS - 1:
                                    then(last)
                                    then(tt(top[:, :, :], top[:, :, :], top_parts[:, p, :, :], ALU.subtract))
                            last.then_inc(top_ready, 1)
                            dve.wait_ge(ring_ready, r + 1)
                            if g:
                                dve.wait_ge(top_written, 16 * g)
                            copy(top_rows[:, :], src[0:PARTS * PACK * TILES, 0:P]).then_inc(ring_read, 1)
                        elif kind == "scores" and quantised:
                            _, n, pair = step_
                            e = 2 * n + pair
                            lv = probs[:, n % 2, pair, :, :]
                            dve.wait_ge(scores_ready, e + 1)
                            if n >= 2:
                                dve.wait_ge(outputs_added, n - 1)
                            then(ts(lv, s_ps[:, 2 * (e % 2):2 * (e % 2) + 2, :], ROUND, ROUND, ALU.add, ALU.max))
                            ts(lv, lv, ROUND + QMAX, ROUND, ALU.min, ALU.subtract).then_inc(scores_read, 1)
                        elif kind == "sums":
                            _, g, half = step_
                            nc.vector.reciprocal(inverse[:, half, :], src[:, 0:PER_HALF * PACK]).then_inc(ring_read, 1)
                        elif kind == "normal":
                            _, g, half = step_
                            out = ot[:, g, half * GROUP:(half + 1) * GROUP]
                            tt(out, raw_out[:, half, :], src, ALU.mult).then_inc(ring_read, 1)
                            if quantised:
                                dve.wait_ge(ring_read, r + 1)
                                then(fake_quant(nc, then, out, out, quant[:, 5:8], out))

                @block.gpsimd
                def _(pool):
                    if context:
                        nc.gpsimd.tensor_copy(keys_now[:, :, :], keys_c[:, :, bass.ds(b * CTX, CTX)]).then_inc(now_ready, 1)
                        nc.gpsimd.tensor_copy(values_now[:, :, 0:HEAD], values_c[:, bass.ds(b, 1), :, :].rearrange("p o h d -> p (o h) d")).then_inc(now_ready, 1)
                    for n in range(len(blocks)):
                        pool.wait_ge(part_ready, n + 1)
                        nc.gpsimd.tensor_tensor(parts[:, n % 2, 2, :], f[:, n, :], parts[:, n % 2, 1, :], ALU.subtract).then_inc(parts_ready, 1)
                    if normed:
                        pool.wait_ge(v_roots, 3)
                        then = in_order(pool, pool_step)
                        every = v_heads.rearrange("p t h d -> p (t h) d")
                        wide = lambda n: norm[1][:, n, :].rearrange("p (o d) -> p o d", o=1).to_broadcast((P, TILES * HEADS, HEAD))
                        then(nc.gpsimd.tensor_tensor(every, every, wide(0), ALU.mult))
                        nc.gpsimd.tensor_tensor(every, every, wide(1), ALU.add).then_inc(v_scaled, 1)

                @block.sync
                def _(sp):
                    for n, (t, m) in enumerate(blocks):
                        sp.wait_ge(parts_ready, n + 1)
                        stack_parts(nc, sp, scratch[t], parts[:, n % 2, :, :], k_stack if t else q_stack, SEQ, t, m, written, stacked[m], 16 * PARTS * n)
                    if maxed:
                        for g in range(HGS):
                            sp.wait_ge(ring_read, ring[("turn", g)] + 1)
                            sp.dma_start(top_dram.rearrange("p i (q n) -> (p i q) n", n=P), top_rows[:, :]).then_inc(top_written, 16)
                            sp.wait_ge(top_written, 16 * (g + 1))
                            sp.dma_start(q_stack[max_row:rows, PACK * g:PACK * (g + 1), :], top_dram).then_inc(top_loaded, 16)

        with nc.Fori(0, BATCH) as b:
            with banks(nc, "scores", [P, 4, GROUP], F32) as s_ps, banks(nc, "ring", [P, 2, GROUP], F32) as r_ps, \
                    banks(nc, "outputs", [P, 2, GROUP], F32) as o_ps:
                project_and_attend(b, s_ps, r_ps, o_ps)
            with banks(nc, "norm_psum", [P, 8, GROUP], F32) as norm_ps:
                add_norm(chip, [bass.ds(b * SEQ + j * GROUP, GROUP) for j in range(HALVES)], norm_ps,
                         product=(wo, lambda j, k: ot[:, k, j * GROUP:(j + 1) * GROUP]), bias=bo)


def context_stacks(chip, mode, params, key_bias, f, parts, scratch, keys_c, values_c):
    nc = chip.nc
    w = params[0]
    width = BATCH * CTX
    with banks(nc, "context_psum", [P, 2 + BATCH, GROUP], F32) as ps, step(
            nc, "projected features_ready parts_ready bias_parts written bias_written stacked values_ready dve_step") as (
            block, projected, features_ready, parts_ready, bias_parts, written, bias_written, stacked, values_ready, dve_step):
        bias_at = 2 * width
        @block.tensor
        def _(pe):
            for m in range(FC):
                for c in range(FC):
                    last = nc.tensor.matmul(ps[:, m, 0:width], w[:, 1, c, m * P:(m + 1) * P], chip.ctx_t[:, c, :], start=(c == 0), stop=(c == FC - 1))
                last.then_inc(projected, 1)
            for b in range(BATCH):
                for c in range(FC):
                    last = nc.tensor.matmul(ps[0:CTX, 2 + b, 0:DIM], chip.ctx_t[:, c, b * CTX:(b + 1) * CTX], w[:, 2, c, :], start=(c == 0), stop=(c == FC - 1))
                last.then_inc(projected, 1)

        @block.scalar
        def _(act):
            for m in range(FC):
                act.wait_ge(projected, m + 1)
                nc.scalar.activation(f[:, m, 0:width], ps[:, m, 0:width], ACT.Copy).then_inc(features_ready, 1)
            for b in range(BATCH):
                act.wait_ge(projected, FC + b + 1)
                nc.scalar.activation(values_c[:, b, :, :], ps[0:CTX, 2 + b, 0:DIM].rearrange("p (h d) -> p h d", d=HEAD), ACT.Copy).then_inc(values_ready, 1)
            act.wait_ge(values_ready, BATCH)

        @block.vector
        def _(dve):
            then = in_order(dve, dve_step)
            jobs = []
            if key_bias is not None:
                then(nc.vector.tensor_scalar(key_bias, key_bias, HEAD ** 0.5, None, ALU.mult))
                jobs.append((key_bias, parts[0:1, 0, :, bias_at:bias_at + width], bias_parts))
            jobs += [(f[:, m, 0:width], parts[:, m, :, 0:width], parts_ready) for m in range(FC)]
            for n, (src, dst, ready) in enumerate(jobs):
                m = n - len(jobs) + FC
                if m >= 0:
                    dve.wait_ge(features_ready, m + 1)
                for p in range(PARTS):
                    last = nc.vector.tensor_copy(dst[:, p, :], src)
                    if p < PARTS - 1:
                        then(last)
                        then(nc.vector.tensor_tensor(src, src, dst[:, p, :], ALU.subtract))
                last.then_inc(ready, 1)

        @block.sync
        def _(sp):
            if key_bias is not None:
                sp.wait_ge(bias_parts, 1)
                at = nc.dram_tensor(f"{mode}_bias_parts", (PARTS, width), BF16).ap()
                sp.dma_start(at.rearrange("(o p) t -> o p t", o=1), parts[0:1, 0, :, bias_at:bias_at + width]).then_inc(bias_written, 16)
                sp.wait_ge(bias_written, 16)
                for h in range(HEADS):
                    sp.dma_start(keys_c[STACK:STACK + PARTS, h, :], at).then_inc(stacked, 16)
            for m in range(FC):
                sp.wait_ge(parts_ready, m + 1)
                stack_parts(nc, sp, scratch, parts[:, m, :, 0:width], keys_c, width, 1, m, written, stacked, 16 * PARTS * m)
            sp.wait_ge(stacked, 16 * (len(PAIRS) * FC + (HEADS if key_bias is not None else 0)))


def load_split(chip, ctx, layer, v_bias=True):
    nc, io = chip.nc, chip.io
    sb = lambda name, shape: ctx.enter_context(sbuf(nc, name, shape, F32))
    w = sb("split_w", [P, 3, FC, DIM])
    wo = sb("split_wo", [P, HGS, DIM])
    b_qk = sb("split_b", [P, 2, FC])
    bo = sb("split_bo", [P, FC])
    vb = sb("split_vb", [P, DIM]) if v_bias else None
    load(nc, [(w[:, t, :, :], io[layer + "_w"][t].rearrange("(c p) m -> p c m", p=P)) for t in range(3)] + [
        (wo[:, :, :], io[layer + "_wo"].rearrange("(g p) n -> p g n", p=P)),
        (b_qk[:, :, :], io[layer + "_b"]), (bo[:, :], io[layer + "_bo"])]
        + ([(vb[:, :], io[layer + "_vb"].partition_broadcast(P))] if v_bias else []))
    return w, wo, b_qk, vb, bo


def quantised_attention(chip):
    nc, io = chip.nc, chip.io
    with ExitStack() as ctx:
        sb = lambda name, shape: ctx.enter_context(sbuf(nc, name, shape, F32))
        params = load_split(chip, ctx, "L0_attn")
        w, wo, b_qk, _, _ = params
        ten = sb("scalars", [P, 8])
        quant = sb("quant", [P, 11])
        quant_x = quant[:, 8:11]
        with ExitStack() as early:
            eb = lambda name, shape: early.enter_context(sbuf(nc, name, shape, F32))
            sw = eb("weight_scales", [P, 2, 3, DIM])
            sp_ = eb("proj_scales", [P, 2, DIM])
            inv = eb("weight_inverse", [P, 3, DIM])
            inv_p = eb("proj_inverse", [P, DIM])
            load(nc, [(sw[:, n, :, :].rearrange("p t m -> p (t m)"), io["L0_attn_ws"][n:n + 1, :].partition_broadcast(P))
                      for n in range(2)]
                 + [(sp_[:, n, :], io["L0_attn_ps"][n:n + 1, :].partition_broadcast(P)) for n in range(2)]
                 + [(ten[:, 0:6], io["L0_attn_scalars"].partition_broadcast(P))])
            with step(nc, "dve_step") as (block, dve_step):
                @block.vector
                def _(dve):
                    then = in_order(dve, dve_step)
                    one = lambda t, n: t[:, n:n + 1]
                    then(nc.vector.reciprocal(one(quant_x, 0), one(ten, 0)))
                    then(nc.vector.tensor_copy(one(quant_x, 1), one(ten, 1)))
                    then(nc.vector.tensor_copy(one(quant_x, 2), one(ten, 0)))
                    then(nc.vector.tensor_scalar(one(quant, 0), one(ten, 2), HEAD ** 0.5, None, ALU.mult))
                    then(nc.vector.reciprocal(one(quant, 1), one(quant, 0)))
                    then(nc.vector.tensor_copy(one(quant, 2), one(ten, 3)))
                    then(nc.vector.tensor_copy(one(quant, 3), one(ten, 2)))
                    then(nc.vector.tensor_scalar(one(quant, 4), one(ten, 2), -QMAX, None, ALU.mult))
                    then(nc.vector.reciprocal(one(quant, 5), one(ten, 4)))
                    then(nc.vector.tensor_copy(one(quant, 6), one(ten, 5)))
                    then(nc.vector.tensor_copy(one(quant, 7), one(ten, 4)))
                    then(nc.vector.reciprocal(inv[:, :, :], sw[:, 0, :, :]))
                    then(nc.vector.reciprocal(inv_p[:, :], sp_[:, 0, :]))
                    jobs = [(w[:, t, c, :], inv[:, t, :], sw[:, 1, t, :], sw[:, 0, t, :]) for t in range(3) for c in range(FC)]
                    jobs += [(wo[:, g, :], inv_p[:, :], sp_[:, 1, :], sp_[:, 0, :]) for g in range(HGS)]
                    for weight, inverse, zero, scale in jobs:
                        then(nc.vector.tensor_tensor(weight, weight, inverse, ALU.mult))
                        then(nc.vector.tensor_tensor(weight, weight, zero, ALU.add))
                        then(nc.vector.tensor_scalar(weight, weight, 0.0, QMAX, ALU.max, ALU.min))
                        then(nc.vector.tensor_scalar(weight, weight, ROUND, ROUND, ALU.add, ALU.subtract))
                        then(nc.vector.tensor_tensor(weight, weight, zero, ALU.subtract))
                        then(nc.vector.tensor_tensor(weight, weight, scale, ALU.mult))
                    then(nc.vector.tensor_scalar(b_qk[:, 0, :], b_qk[:, 0, :], one(quant, 1), None, ALU.mult))
                    for g in range(HGS):
                        then(nc.vector.tensor_scalar(wo[:, g, :], wo[:, g, :], chip.c(C_ROWS, 1), None, ALU.mult))
        split_attention(chip, "quant", params, quant=quant)


def cross_attention(chip):
    nc, io = chip.nc, chip.io
    with ExitStack() as ctx:
        params = load_split(chip, ctx, "L0_xattn", v_bias=False)
        key_bias = ctx.enter_context(sbuf(nc, "key_bias", [1, BATCH * CTX], F32))
        load(nc, [(key_bias[:, :], io["key_bias"])])
        split_attention(chip, "cross", params, key_bias=key_bias[:, :])


def normed_attention(chip):
    nc, io = chip.nc, chip.io
    with ExitStack() as ctx:
        sb = lambda name, shape: ctx.enter_context(sbuf(nc, name, shape, F32))
        params = load_split(chip, ctx, "L1_attn")
        w, _, b_qk, v_bias, _ = params
        norm = sb("head_norm", [P, 2, 2])
        norm_v = sb("value_norm", [P, 2, HEAD])
        means = sb("head_means", [P, (3 * FC + 1) * HEADS])
        load(nc, [(norm[:, :, :], io["L1_attn_norm"]), (norm_v[:, :, :].rearrange("p n d -> p (n d)"), io["L1_attn_norm_v"].partition_broadcast(P))])
        with banks(nc, "bias_means", [P, 2 * FC], F32) as mean_ps, step(nc, "means_ready dve_step") as (block, means_ready, dve_step):
            @block.tensor
            def _(pe):
                nc.tensor.matmul(mean_ps[:, :], chip.c(C_HEADMEAN), b_qk[:, :, :].rearrange("p t m -> p (t m)"),
                                 start=True, stop=True).then_inc(means_ready, 1)

            @block.vector
            def _(dve):
                then = in_order(dve, dve_step)
                heads = [w[:, :, :, :].rearrange("p t c (h d) -> p (t c h) d", d=HEAD), v_bias[:, :].rearrange("p (h d) -> p h d", d=HEAD)]
                at = 0
                for part in heads:
                    n = part.shape[1]
                    mean = means[:, at:at + n]
                    then(nc.vector.reduce_sum(mean, part, AX.X))
                    then(nc.vector.tensor_scalar(mean, mean, 1.0 / HEAD, None, ALU.mult))
                    then(nc.vector.tensor_tensor(part, part, mean.rearrange("p (h o) -> p h o", o=1).to_broadcast((P, n, HEAD)), ALU.subtract))
                    at += n
                dve.wait_ge(means_ready, 1)
                every = b_qk[:, :, :].rearrange("p t m -> p (t m)")
                then(nc.vector.tensor_tensor(every, every, mean_ps[:, :], ALU.subtract))
        split_attention(chip, "normed", params, norm=(norm, norm_v))


def causal_attention(chip):
    with ExitStack() as ctx:
        params = load_split(chip, ctx, "L3_xattn", v_bias=False)
        split_attention(chip, "causal", params)


KV_HEADS = 4
REPEAT = HEADS // KV_HEADS


def linear_attention(chip):
    nc, io = chip.nc, chip.io
    with ExitStack() as ctx:
        sb = lambda name, shape: ctx.enter_context(sbuf(nc, name, shape, F32))
        wq, bq = sb("linear_wq", [P, FC, REPEAT, P]), sb("linear_bq", [P, 2, REPEAT])
        wkv, bkv = sb("kv_down", [P, FC, P]), sb("kv_bias", [P, 1])
        wc, wk, wkv_up = sb("kv_compress", [P, P]), sb("k_up", [P, P]), sb("kv_up", [P, P])
        wo, bo = sb("linear_wo", [P, REPEAT, DIM]), sb("linear_bo", [P, FC])
        affine = sb("affine", [P, 2, FC])
        load(nc, [(wq[:, c, :, :], io["L3_attn_wq"][c * P:(c + 1) * P]) for c in range(FC)]
             + [(bq[:, 0, :], io["L3_attn_bq"]), (wkv[:, :, :], io["L3_attn_wkv"].rearrange("(c p) m -> p c m", p=P)),
                (bkv[:, :], io["L3_attn_bkv"]), (wc[:, :], io["L3_attn_wc"]), (wk[:, :], io["L3_attn_wk"]), (wkv_up[:, :], io["L3_attn_wkv_up"]),
                (wo[:, :, :], io["L3_attn_wo"].rearrange("(r p) n -> p r n", p=P)), (bo[:, :], io["L3_attn_bo"]), (affine[:, :, :], io["L3_attn_affine"])])
        q_f, k_f = sb("query_features", [P, REPEAT, SEQ]), sb("key_features", [P, SEQ])
        k_rows, v_rows = sb("key_rows", [P, TILES, KV_HEADS, SLOT]), sb("value_rows", [P, TILES, KV_HEADS, SLOT])
        ot = sb("linear_out", [P, REPEAT, SEQ])
        with step(nc, "set_") as (block, set_):
            @block.vector
            def _(dve):
                nc.vector.tensor_scalar(bq[:, 1, :], bq[:, 0, :], 1.0, None, ALU.add).then_inc(set_, 1)
                nc.vector.memset(k_rows[:, :, :, :], 0.0).then_inc(set_, 1)
                nc.vector.memset(v_rows[:, :, :, HEAD + 1:], 0.0).then_inc(set_, 1)
                nc.vector.memset(v_rows[:, :, :, HEAD:HEAD + 1], 1.0).then_inc(set_, 1)
                dve.wait_ge(set_, 4)
        with nc.Fori(0, BATCH) as b:
            linear_features(chip, b, wq, bq, wkv, bkv, wc, wk, wkv_up, q_f, k_f, k_rows, v_rows)
            linear_chunks(chip, q_f, k_f, k_rows, v_rows, ot)
            with banks(nc, "norm_psum", [P, 8, GROUP], F32) as norm_ps:
                add_norm(chip, [bass.ds(b * SEQ + j * GROUP, GROUP) for j in range(HALVES)], norm_ps, bias=bo,
                         product=(wo, lambda j, r: ot[:, r, j * GROUP:(j + 1) * GROUP]), affine=(affine[:, 0, :], affine[:, 1, :]))


def linear_features(chip, b, wq, bq, wkv, bkv, wc, wk, wkv_up, q_f, k_f, k_rows, v_rows):
    nc = chip.nc
    part = lambda j: slice(j * GROUP, (j + 1) * GROUP)
    queries = [(4 + n % 4, q_f[:, n // HALVES, part(n % HALVES)], bq[:, 0, n // HALVES:n // HALVES + 1], bq[:, 1, n // HALVES:n // HALVES + 1])
               for n in range(REPEAT * HALVES)]
    keys = [(j, k_f[:, part(j)], 0.0, 1.0) for j in range(HALVES)]
    rows = [(2 + j, k_rows[:, PER_HALF * j:PER_HALF * (j + 1), :, 0:HEAD], 0.0, 1.0) for j in range(HALVES)]
    jobs = queries[:4] + keys + rows + queries[4:]
    with ExitStack() as ctx:
        kv = ctx.enter_context(sbuf(nc, "kv", [P, SEQ], F32))
        latent = ctx.enter_context(sbuf(nc, "latent", [P, SEQ], F32))
        low = ctx.enter_context(sbuf(nc, "feature_low", [P, 3, GROUP], F32))
        ps = ctx.enter_context(banks(nc, "linear_psum", [P, 8, GROUP], F32))

        def source(n):
            bank = ps[:, jobs[n][0], :]
            if jobs[n] in rows:
                return bank.rearrange("p (t s h d) -> p t s h d", t=PER_HALF, s=2, h=KV_HEADS)[:, :, 0, :, :]
            return bank

        def lower(n):
            buf = low[:, n % 3, :]
            if jobs[n] in rows:
                return buf[:, 0:GROUP // 2].rearrange("p (t h d) -> p t h d", t=PER_HALF, h=KV_HEADS)
            return buf

        with step(nc, "down_ready kv_ready latents_ready latents_copied projected rows_copied low_ready exps_ready features_ready") as (
                block, down_ready, kv_ready, latents_ready, latents_copied, projected, rows_copied, low_ready, exps_ready, features_ready):
            @block.tensor
            def _(pe):
                tok = lambda j: bass.ds(b * SEQ + j * GROUP, GROUP)

                def query(n):
                    for c in range(FC):
                        last = nc.tensor.matmul(ps[:, queries[n][0], :], wq[:, c, n // HALVES, :], chip.xt[:, c, tok(n % HALVES)], start=(c == 0), stop=(c == FC - 1))
                    last.then_inc(projected, 1)

                for j in range(HALVES):
                    for c in range(FC):
                        last = nc.tensor.matmul(ps[:, j, :], wkv[:, c, :], chip.xt[:, c, tok(j)], start=(c == 0), stop=(c == FC - 1))
                    last.then_inc(down_ready, 1)
                for n in range(4):
                    query(n)
                for j in range(HALVES):
                    pe.wait_ge(kv_ready, j + 1)
                    nc.tensor.matmul(ps[:, 2 + j, :], wc[:, :], kv[:, part(j)], start=True, stop=True).then_inc(latents_ready, 1)
                for j in range(HALVES):
                    pe.wait_ge(latents_copied, j + 1)
                    nc.tensor.matmul(ps[:, j, :], wk[:, :], latent[:, part(j)], start=True, stop=True).then_inc(projected, 1)
                for j in range(HALVES):
                    for t in range(PER_HALF):
                        last = nc.tensor.matmul(ps[:, 2 + j, t * P:(t + 1) * P], latent[:, (PER_HALF * j + t) * P:(PER_HALF * j + t + 1) * P], wkv_up[:, :],
                                                start=True, stop=True)
                    last.then_inc(projected, 1)
                for n in range(4, len(queries)):
                    pe.wait_ge(features_ready, n - 3)
                    query(n)

            @block.scalar
            def _(act):
                for j in range(HALVES):
                    act.wait_ge(down_ready, j + 1)
                    nc.scalar.activation(kv[:, part(j)], ps[:, j, :], ACT.Identity, bias=bkv[:, 0:1]).then_inc(kv_ready, 1)
                for j in range(HALVES):
                    act.wait_ge(latents_ready, j + 1)
                    nc.scalar.activation(latent[:, part(j)], ps[:, 2 + j, :], ACT.Copy).then_inc(latents_copied, 1)
                for n in range(len(jobs)):
                    act.wait_ge(low_ready, n + 1)
                    nc.scalar.activation(lower(n), lower(n), ACT.Exp).then_inc(exps_ready, 1)
                for j in range(HALVES):
                    act.wait_ge(features_ready, jobs.index(rows[j]) + 1)
                    nc.scalar.activation(v_rows[:, PER_HALF * j:PER_HALF * (j + 1), :, 0:HEAD],
                                         ps[:, 2 + j, :].rearrange("p (t s h d) -> p t s h d", t=PER_HALF, s=2, h=KV_HEADS)[:, :, 1, :, :],
                                         ACT.Copy).then_inc(rows_copied, 1)

            @block.vector
            def _(dve):
                def low_part(n):
                    dve.wait_ge(projected, n + 1)
                    if n >= 3:
                        dve.wait_ge(features_ready, n - 2)
                    nc.vector.tensor_scalar(lower(n), source(n), jobs[n][2], 0.0, ALU.add, ALU.min).then_inc(low_ready, 1)

                low_part(0)
                for n in range(len(jobs)):
                    if n + 1 < len(jobs):
                        low_part(n + 1)
                    dve.wait_ge(exps_ready, n + 1)
                    nc.vector.scalar_tensor_tensor(out=jobs[n][1], in0=source(n), scalar=jobs[n][3], in1=lower(n),
                                                   op0=ALU.add, op1=ALU.max).then_inc(features_ready, 1)


def linear_chunks(chip, q_f, k_f, k_rows, v_rows, ot):
    nc = chip.nc
    with ExitStack() as ctx:
        sb = lambda name, shape: ctx.enter_context(sbuf(nc, name, shape, F32))
        masked = sb("masked_products", [P, 2, KV_HEADS, GROUP])
        state = sb("linear_state", [P, 2, P])
        raw = sb("linear_raw", [P, 2, GROUP])
        inverse, wide = sb("linear_inverse", [P, 2, KV_HEADS * REPEAT]), sb("linear_inverse_wide", [P, 2, KV_HEADS * REPEAT, SLOT])
        product_ps = ctx.enter_context(banks(nc, "linear_products", [P, 3, GROUP], F32))
        out_ps = ctx.enter_context(banks(nc, "linear_outputs", [P, 2, GROUP], F32))
        state_ps = ctx.enter_context(banks(nc, "linear_sum", [P, P], F32))
        spread_ps = ctx.enter_context(banks(nc, "linear_spread", [P, 2, GROUP], F32))
        chunk = lambda c: slice(c * P, (c + 1) * P)
        own = lambda g: slice(SLOT * g, SLOT * g + HEAD)
        with step(nc, "products_ready masked_ready state_summed state_ready out_ready raw_ready sums_ready inverse_ready wide_ready spread_ready out_done dve_step") as (
                block, products_ready, masked_ready, state_summed, state_ready, out_ready, raw_ready, sums_ready, inverse_ready, wide_ready, spread_ready,
                out_done, dve_step):
            @block.tensor
            def _(pe):
                def products(c):
                    for g in range(KV_HEADS):
                        n = KV_HEADS * c + g
                        if n >= 3:
                            pe.wait_ge(masked_ready, n - 2)
                        nc.tensor.matmul(product_ps[:, n % 3, :].rearrange("p (r t) -> p r t", r=REPEAT), k_f[own(g), chunk(c)], q_f[own(g), :, chunk(c)],
                                         start=True, stop=True).then_inc(products_ready, 1)

                def outputs(c):
                    if c >= 2:
                        pe.wait_ge(raw_ready, c - 1)
                    out = out_ps[:, c % 2, :].rearrange("p (r t) -> p r t", r=REPEAT)
                    if c:
                        pe.wait_ge(state_ready, c)
                        nc.tensor.matmul(out, state[:, c % 2, :], q_f[:, :, chunk(c)], start=True, stop=False)
                    pe.wait_ge(masked_ready, KV_HEADS * (c + 1))
                    for g in range(KV_HEADS):
                        last = nc.tensor.matmul(out_ps[SLOT * g:SLOT * (g + 1), c % 2, :], v_rows[:, c, g, :], masked[:, c % 2, g, :], start=(c == 0), stop=True)
                    last.then_inc(out_ready, 1)

                def add_state(c):
                    if c:
                        pe.wait_ge(state_ready, c)
                    nc.tensor.matmul(state_ps[:, :], k_rows[:, c, :, :].rearrange("p h r -> p (h r)"), v_rows[:, c, :, :].rearrange("p h r -> p (h r)"),
                                     start=True, stop=True).then_inc(state_summed, 1)

                def sums(c):
                    pe.wait_ge(raw_ready, c + 1)
                    if c >= 2:
                        pe.wait_ge(out_done, c - 1)
                    for r in range(REPEAT):
                        last = nc.tensor.matmul(spread_ps[:, c % 2, r * KV_HEADS:(r + 1) * KV_HEADS], raw[:, c % 2, r * P:(r + 1) * P],
                                                chip.c(C_DEN)[:, 0:P:SLOT], start=True, stop=True)
                    last.then_inc(sums_ready, 1)

                def spread(c):
                    pe.wait_ge(wide_ready, c + 1)
                    for r in range(REPEAT):
                        last = nc.tensor.matmul(spread_ps[:, c % 2, r * P:(r + 1) * P],
                                                wide[:, c % 2, r * KV_HEADS:(r + 1) * KV_HEADS, :].rearrange("p h r -> p (h r)"), chip.c(C_ID), start=True, stop=True)
                    last.then_inc(spread_ready, 1)

                for c in range(TILES + 3):
                    if c < TILES:
                        products(c)
                        if c < TILES - 1:
                            add_state(c)
                    if 1 <= c <= TILES:
                        outputs(c - 1)
                    if 2 <= c <= TILES + 1:
                        sums(c - 2)
                    if c >= 3:
                        spread(c - 3)

            @block.vector
            def _(dve):
                then = in_order(dve, dve_step)
                keep = chip.c(C_KEEPT).rearrange("p (o n) -> p o n", o=1).to_broadcast((P, REPEAT, P))
                for c in range(TILES + 3):
                    if c < TILES:
                        for g in range(KV_HEADS):
                            n = KV_HEADS * c + g
                            dve.wait_ge(products_ready, n + 1)
                            if c >= 2:
                                dve.wait_ge(out_ready, c - 1)
                            nc.vector.tensor_tensor(masked[:, c % 2, g, :].rearrange("p (r t) -> p r t", r=REPEAT),
                                                    product_ps[:, n % 3, :].rearrange("p (r t) -> p r t", r=REPEAT), keep, ALU.mult).then_inc(masked_ready, 1)
                        if c < TILES - 1:
                            dve.wait_ge(state_summed, c + 1)
                            if c >= 1:
                                dve.wait_ge(out_ready, c)
                            last = nc.vector.tensor_tensor(state[:, (c + 1) % 2, :], state_ps[:, :], chip.c(C_SLOTS), ALU.mult)
                            if c:
                                then(last)
                                dve.wait_ge(state_ready, c)
                                last = nc.vector.tensor_tensor(state[:, (c + 1) % 2, :], state[:, (c + 1) % 2, :], state[:, c % 2, :], ALU.add)
                            last.then_inc(state_ready, 1)
                    if 2 <= c <= TILES + 1:
                        i = c - 2
                        dve.wait_ge(sums_ready, i + 1)
                        if i >= 2:
                            dve.wait_ge(wide_ready, i - 1)
                        then(nc.vector.tensor_scalar(inverse[:, i % 2, :], spread_ps[:, i % 2, 0:KV_HEADS * REPEAT], 1e-6, None, ALU.add))
                        nc.vector.reciprocal(inverse[:, i % 2, :], inverse[:, i % 2, :]).then_inc(inverse_ready, 1)
                    if c >= 3:
                        i = c - 3
                        dve.wait_ge(spread_ready, i + 1)
                        nc.vector.tensor_tensor(ot[:, :, chunk(i)], raw[:, i % 2, :].rearrange("p (r t) -> p r t", r=REPEAT),
                                                spread_ps[:, i % 2, :].rearrange("p (r t) -> p r t", r=REPEAT), ALU.mult).then_inc(out_done, 1)

            @block.scalar
            def _(act):
                for c in range(TILES + 2):
                    if c < TILES:
                        act.wait_ge(out_ready, c + 1)
                        if c >= 2:
                            act.wait_ge(out_done, c - 1)
                        nc.scalar.activation(raw[:, c % 2, :], out_ps[:, c % 2, :], ACT.Copy).then_inc(raw_ready, 1)
                    if 1 <= c <= TILES:
                        i = c - 1
                        act.wait_ge(inverse_ready, i + 1)
                        nc.scalar.activation(wide[:, i % 2, :, :], inverse[:, i % 2, :].rearrange("p (n o) -> p n o", o=1)
                                             .to_broadcast((P, KV_HEADS * REPEAT, SLOT)), ACT.Copy).then_inc(wide_ready, 1)


def context_mlp(chip):
    nc, io = chip.nc, chip.io
    with ExitStack() as ctx:
        rows = ctx.enter_context(sbuf(nc, "context_rows", [CTX, BATCH, DIM], F32))
        stage = ctx.enter_context(sbuf(nc, "context_stage", [P, FC, CTX], F32))
        stage_rows = ctx.enter_context(sbuf(nc, "context_stage_rows", [CTX, 1, DIM], F32))
        h = ctx.enter_context(sbuf(nc, "hidden", [CTX, 2, GROUP], F32))
        load(nc, [(rows[:, :, :], io["ctx"].rearrange("(b s) d -> s b d", b=BATCH))])
        halves = SEQ // GROUP
        with nc.Fori(0, BATCH) as b:
            tok = lambda j: bass.ds(b * SEQ + j * GROUP, GROUP)
            with banks(nc, "hidden_psum", [P, 2, GROUP], F32) as ps, step(nc, "staged products_ready hidden_ready") as (
                    block, staged, products_ready, hidden_ready):
                @block.vector
                def _(dve):
                    nc.vector.tensor_copy(stage[:, :, :], chip.ctx_t[:, :, bass.ds(b * CTX, CTX)]).then_inc(staged, 1)
                    nc.vector.tensor_copy(stage_rows[:, 0, :], rows[:, bass.ds(b, 1), :].rearrange("p o d -> p (o d)")).then_inc(staged, 1)
                    dve.wait_ge(staged, 2)

                @block.tensor
                def _(pe):
                    pe.wait_ge(staged, 2)
                    for j in range(halves):
                        for c in range(FC):
                            last = nc.tensor.matmul(ps[0:CTX, j, :], stage[:, c, :], chip.xt[:, c, tok(j)], start=(c == 0), stop=(c == FC - 1))
                        last.then_inc(products_ready, 1)

                @block.scalar
                def _(act):
                    for j in range(halves):
                        act.wait_ge(products_ready, j + 1)
                        nc.scalar.activation(h[:, j, :], ps[0:CTX, j, :], ACT.Gelu_apprx_tanh).then_inc(hidden_ready, 1)
            with banks(nc, "norm_psum", [P, 8, GROUP], F32) as norm_ps:
                add_norm(chip, [tok(j) for j in range(halves)], norm_ps, product=(stage_rows, lambda j, k: h[:, j, :]))


def concat_context(chip):
    nc, io = chip.nc, chip.io
    with ExitStack() as ctx:
        sb = lambda name, shape: ctx.enter_context(sbuf(nc, name, shape, F32))
        w = sb("concat_w", [P, 2 * FC, DIM])
        bias = sb("concat_b", [P, FC])
        sums = sb("context_sums", [P, FC, BATCH])
        shift = sb("context_shift", [P, BATCH, FC])
        shift_b = sb("context_shift_now", [P, FC])
        load(nc, [(w[:, :, :], io["L2_xattn_w"].rearrange("(c p) n -> p c n", p=P)), (bias[:, :], io["L2_xattn_b"])])
        with banks(nc, "shift_psum", [P, FC, BATCH], F32) as ps, step(nc, "sums_ready shift_ready dve_step") as (block, sums_ready, shift_ready, dve_step):
            @block.vector
            def _(dve):
                nc.vector.reduce_sum(sums[:, :, :], chip.ctx_t[:, :, :].rearrange("p c (b s) -> p c b s", b=BATCH), AX.X).then_inc(sums_ready, 1)
                dve.wait_ge(shift_ready, FC)
                then = in_order(dve, dve_step)
                for c in range(FC):
                    then(nc.vector.tensor_scalar(shift[:, :, c], ps[:, c, :], 1.0 / CTX, bias[:, c:c + 1], ALU.mult, ALU.add))

            @block.tensor
            def _(pe):
                pe.wait_ge(sums_ready, 1)
                for c in range(FC):
                    for k in range(FC):
                        last = nc.tensor.matmul(ps[:, c, :], w[:, FC + k, c * P:(c + 1) * P], sums[:, k, :], start=(k == 0), stop=(k == FC - 1))
                    last.then_inc(shift_ready, 1)
        with nc.Fori(0, BATCH) as b:
            with step(nc, "staged") as (block, staged):
                @block.vector
                def _(dve):
                    nc.vector.tensor_copy(shift_b[:, :], shift[:, bass.ds(b, 1), :].rearrange("p o c -> p (o c)")).then_inc(staged, 1)
                    dve.wait_ge(staged, 1)
            tok = lambda j: bass.ds(b * SEQ + j * GROUP, GROUP)
            with banks(nc, "norm_psum", [P, 8, GROUP], F32) as norm_ps:
                add_norm(chip, [tok(0), tok(1)], norm_ps, product=(w[:, 0:FC, :], lambda j, k: chip.xt[:, k, tok(j)]), bias=shift_b)


def spiking_ffn(chip):
    nc, io = chip.nc, chip.io
    inner = 4 * DIM
    ic = inner // P
    steps, beta, threshold = 5, 0.9, 1.0
    with ExitStack() as ctx:
        sb = lambda name, shape: ctx.enter_context(sbuf(nc, name, shape, F32))
        w1, w2 = sb("fc_w", [P, FC, inner]), sb("proj_w", [P, ic, DIM])
        h = sb("hidden", [P, ic, GROUP])
        y, mem, spike, total = (sb(n, [P, FC, GROUP]) for n in ("drive", "membrane", "spike", "spikes"))
        load(nc, [(w1[:, :, :], io["L2_ffn_w1"].rearrange("(c p) n -> p c n", p=P)), (w2[:, :, :], io["L2_ffn_w2"].rearrange("(c p) n -> p c n", p=P))])
        h_ps = ctx.enter_context(banks(nc, "hidden_psum", [P, 2, GROUP], F32))
        y_ps = ctx.enter_context(banks(nc, "drive_psum", [P, 2, GROUP], F32))
        norm_ps = ctx.enter_context(banks(nc, "norm_psum", [P, 4, GROUP], F32))
        with nc.Fori(0, GROUPS) as g:
            with step(nc, "h_ready relu_ready squared y_ready dve_step") as (block, h_ready, relu_ready, squared, y_ready, dve_step):
                @block.tensor
                def _(pe):
                    for n in range(ic):
                        if n >= 2:
                            pe.wait_ge(relu_ready, n - 1)
                        for c in range(FC):
                            last = nc.tensor.matmul(h_ps[:, n % 2, :], w1[:, c, n * P:(n + 1) * P], chip.xt[:, c, group_slice(g)],
                                                    start=(c == 0), stop=(c == FC - 1))
                        last.then_inc(h_ready, 1)
                    for c in range(FC):
                        for n in range(ic):
                            pe.wait_ge(squared, n + 1)
                            last = nc.tensor.matmul(y_ps[:, c, :], w2[:, n, c * P:(c + 1) * P], h[:, n, :], start=(n == 0), stop=(n == ic - 1))
                    last.then_inc(y_ready, 1)

                @block.scalar
                def _(act):
                    for n in range(ic):
                        act.wait_ge(h_ready, n + 1)
                        nc.scalar.activation(h[:, n, :], h_ps[:, n % 2, :], ACT.Relu).then_inc(relu_ready, 1)
                        act.wait_ge(relu_ready, n + 1)
                        nc.scalar.activation(h[:, n, :], h[:, n, :], ACT.Square).then_inc(squared, 1)

                @block.vector
                def _(dve):
                    then = in_order(dve, dve_step)
                    dve.wait_ge(y_ready, 1)
                    then(nc.vector.tensor_copy(y[:, :, :], y_ps[:, :, :]))
                    then(nc.vector.tensor_copy(mem[:, :, :], y[:, :, :]))
                    then(nc.vector.tensor_scalar(spike[:, :, :], mem[:, :, :], threshold, None, ALU.is_gt))
                    then(nc.vector.tensor_copy(total[:, :, :], spike[:, :, :]))
                    for s in range(1, steps):
                        then(nc.vector.scalar_tensor_tensor(out=mem[:, :, :], in0=mem[:, :, :], scalar=beta, in1=y[:, :, :], op0=ALU.mult, op1=ALU.add))
                        then(nc.vector.tensor_tensor(mem[:, :, :], mem[:, :, :], spike[:, :, :], ALU.subtract))
                        then(nc.vector.tensor_scalar(spike[:, :, :], mem[:, :, :], threshold, None, ALU.is_gt))
                        then(nc.vector.tensor_tensor(total[:, :, :], total[:, :, :], spike[:, :, :], ALU.add))
                    then(nc.vector.tensor_scalar(total[:, :, :], total[:, :, :], 1.0 / steps, None, ALU.mult))
            add_norm(chip, [group_slice(g)], norm_ps, ready=lambda _, c: total[:, c, :])


EXPERTS, EXPERT_INNER = 8, 1024
CAPACITY = 2 * TOKENS // EXPERTS
TOKEN_TILES = TOKENS // P


def token_rows(chip, rows, logits=None, gate_w=None):
    nc = chip.nc
    per = GROUP // P
    with ExitStack() as ctx:
        stage = ctx.enter_context(sbuf(nc, "token_stage", [P, FC, GROUP], F32))
        turn_ps = ctx.enter_context(banks(nc, "rows_psum", [P, per, DIM], F32))
        logit_ps = ctx.enter_context(banks(nc, "logits_psum", [P, per, EXPERTS], F32))
        with nc.Fori(0, GROUPS) as g, step(nc, "staged turned logits_ready copied") as (block, staged, turned, logits_ready, copied):
            @block.vector
            def _(dve):
                nc.vector.tensor_copy(stage[:, :, :], chip.xt[:, :, group_slice(g)]).then_inc(staged, 1)
                if logits is not None:
                    dve.wait_ge(logits_ready, 1)
                    nc.vector.tensor_copy(logits[:, bass.ds(g * per, per), :], logit_ps[:, :, :]).then_inc(copied, 1)

            @block.tensor
            def _(pe):
                pe.wait_ge(staged, 1)
                for t in range(per):
                    for c in range(FC):
                        last = nc.tensor.transpose(turn_ps[:, t, c * P:(c + 1) * P], stage[:, c, t * P:(t + 1) * P], chip.c(C_ID))
                last.then_inc(turned, 1)
                if logits is not None:
                    for t in range(per):
                        for c in range(FC):
                            last = nc.tensor.matmul(logit_ps[:, t, :], stage[:, c, t * P:(t + 1) * P], gate_w[:, c, :],
                                                    start=(c == 0), stop=(c == FC - 1))
                    last.then_inc(logits_ready, 1)

            @block.scalar
            def _(act):
                act.wait_ge(turned, 1)
                nc.scalar.activation(rows[:, bass.ds(g * per, per), :], turn_ps[:, :, :], ACT.Copy).then_inc(copied, 1)


def route(chip, logits, place, scatter_to, gates):
    nc = chip.nc
    E, N = EXPERTS, TOKEN_TILES
    with ExitStack() as ctx:
        sb = lambda name, shape: ctx.enter_context(sbuf(nc, name, shape, F32))
        best = sb("best", [P, 2, N])
        index = sb("expert_index", [P, 2, N])
        hot = sb("one_hot", [P, 2, N, E])
        work = sb("route_work", [P, N, E])
        rest = sb("route_rest", [P, N, E])
        total = sb("tile_totals", [P, 2, 2, N, E])
        slot = sb("slots", [P, 2, N])
        keep = sb("keep", [P, 2, N])
        ex = sb("gate_exps", [P, N, E])
        small = sb("gate_sums", [P, 4, N])
        ps = ctx.enter_context(banks(nc, "route_psum", [P, 2, 2, N, E], F32))
        wide = lambda t: t.rearrange("p (n o) -> p n o", o=1).to_broadcast((P, N, E))
        iota = chip.c(C_IOTA, E).rearrange("p (o e) -> p o e", o=1).to_broadcast((P, N, E))
        with step(nc, "hot_ready counts_ready shifted exps_ready dve_step") as (block, hot_ready, counts_ready, shifted, exps_ready, dve_step):
            @block.vector
            def _(dve):
                then = in_order(dve, dve_step)
                tt, ts = nc.vector.tensor_tensor, nc.vector.tensor_scalar
                for k in range(2):
                    src = logits[:, :, :] if k == 0 else rest[:, :, :]
                    then(nc.vector.reduce_max(best[:, k, :], src, AX.X))
                    then(tt(work[:, :, :], src, wide(best[:, k, :]), ALU.is_lt))
                    then(ts(work[:, :, :], work[:, :, :], float(E), None, ALU.mult))
                    then(tt(work[:, :, :], work[:, :, :], iota, ALU.add))
                    then(nc.vector.tensor_reduce(index[:, k, :], work[:, :, :], AX.X, ALU.min))
                    nc.vector.tensor_tensor(hot[:, k, :, :], wide(index[:, k, :]), iota, ALU.is_equal).then_inc(hot_ready, 1)
                    dve.wait_ge(hot_ready, k + 1)
                    if k == 0:
                        then(ts(rest[:, :, :], hot[:, 0, :, :], FAR, None, ALU.mult))
                        then(tt(rest[:, :, :], logits[:, :, :], rest[:, :, :], ALU.add))
                nc.vector.tensor_tensor(work[:, :, :], logits[:, :, :], wide(best[:, 0, :]), ALU.subtract).then_inc(shifted, 1)
                nc.vector.tensor_tensor(small[:, 1, :], best[:, 1, :], best[:, 0, :], ALU.subtract).then_inc(shifted, 1)
                dve.wait_ge(exps_ready, 2)
                then(nc.vector.reduce_sum(small[:, 0, :], ex[:, :, :], AX.X))
                then(nc.vector.reciprocal(small[:, 0, :], small[:, 0, :]))
                then(tt(small[:, 1, :], small[:, 2, :], small[:, 0, :], ALU.mult))
                then(tt(small[:, 3, :], small[:, 0, :], small[:, 1, :], ALU.add))
                then(ts(small[:, 3, :], small[:, 3, :], 1e-9, None, ALU.max))
                then(nc.vector.reciprocal(small[:, 3, :], small[:, 3, :]))
                dve.wait_ge(counts_ready, 1)
                for k in range(2):
                    then(nc.vector.memset(total[:, 0, k, 0, :], 0.0))
                    then(nc.vector.tensor_copy(total[:, 0, k, 1:N, :], ps[:, 1, k, 0:N - 1, :]))
                at = 0
                for shift in (1, 2, 4, 8, 16):
                    for k in range(2):
                        then(nc.vector.tensor_copy(total[:, 1 - at, k, 0:shift, :], total[:, at, k, 0:shift, :]))
                        then(tt(total[:, 1 - at, k, shift:N, :], total[:, at, k, shift:N, :], total[:, at, k, 0:N - shift, :], ALU.add))
                    at = 1 - at
                for k in range(2):
                    then(tt(work[:, :, :], ps[:, 0, k, :, :], total[:, at, k, :, :], ALU.add))
                    if k == 1:
                        then(tt(rest[:, 0, :], total[:, at, 0, N - 1, :], ps[:, 1, 0, N - 1, :], ALU.add))
                        then(tt(work[:, :, :], work[:, :, :], rest[:, 0:1, :].to_broadcast((P, N, E)), ALU.add))
                    then(tt(work[:, :, :], work[:, :, :], hot[:, k, :, :], ALU.mult))
                    then(nc.vector.reduce_sum(slot[:, k, :], work[:, :, :], AX.X))
                then(ts(keep[:, :, :], slot[:, :, :], float(CAPACITY), None, ALU.is_lt))
                then(ts(slot[:, :, :], slot[:, :, :], float(CAPACITY - 1), None, ALU.min))
                then(ts(index[:, :, :], index[:, :, :], float(CAPACITY), None, ALU.mult))
                then(tt(slot[:, :, :], slot[:, :, :], index[:, :, :], ALU.add))
                then(nc.vector.tensor_copy(place[:, :, :], slot[:, :, :]))
                then(ts(index[:, :, :], keep[:, :, :], -float(2 * EXPERTS * CAPACITY), float(2 * EXPERTS * CAPACITY), ALU.mult, ALU.add))
                then(tt(slot[:, :, :], slot[:, :, :], index[:, :, :], ALU.add))
                then(nc.vector.tensor_copy(scatter_to[:, :, :], slot[:, :, :]))
                for k in range(2):
                    then(tt(gates[:, k, :], small[:, k, :], small[:, 3, :], ALU.mult))
                    then(tt(gates[:, k, :], gates[:, k, :], keep[:, k, :], ALU.mult))

            @block.scalar
            def _(act):
                act.wait_ge(shifted, 2)
                nc.scalar.activation(ex[:, :, :], work[:, :, :], ACT.Exp).then_inc(exps_ready, 1)
                nc.scalar.activation(small[:, 2, :], small[:, 1, :], ACT.Exp).then_inc(exps_ready, 1)

            @block.tensor
            def _(pe):
                for k in range(2):
                    pe.wait_ge(hot_ready, k + 1)
                    nc.tensor.matmul(ps[:, 0, k, :, :], chip.c(C_BEFORE), hot[:, k, :, :], start=True, stop=True)
                    last = nc.tensor.matmul(ps[:, 1, k, :, :], chip.c(C_ONES), hot[:, k, :, :], start=True, stop=True)
                last.then_inc(counts_ready, 1)


def expert_ffn(chip):
    nc, io = chip.nc, chip.io
    slots = EXPERTS * CAPACITY
    ic, tiles = EXPERT_INNER // P, CAPACITY // P
    dispatched = nc.dram_tensor("dispatched", (slots, DIM), F32).ap()
    produced = nc.dram_tensor("produced", (slots, DIM), F32).ap()
    with ExitStack() as ctx:
        sb = lambda name, shape, dt=F32: ctx.enter_context(sbuf(nc, name, shape, dt))
        place, scatter_to = sb("place", [P, 2, TOKEN_TILES], U32), sb("scatter_to", [P, 2, TOKEN_TILES], U32)
        gates = sb("gates", [P, 2, TOKEN_TILES])
        with ExitStack() as early:
            rows = early.enter_context(sbuf(nc, "rows", [P, TOKEN_TILES, DIM], F32))
            logits = early.enter_context(sbuf(nc, "logits", [P, TOKEN_TILES, EXPERTS], F32))
            gate_w = early.enter_context(sbuf(nc, "gate_w", [P, FC, EXPERTS], F32))
            zeros = early.enter_context(sbuf(nc, "zeros", [P, 16 * DIM], F32))
            load(nc, [(gate_w[:, :, :], io["L0_ffn_wg"].rearrange("(c p) e -> p c e", p=P))])
            with step(nc, "cleared zeroed") as (block, cleared, zeroed):
                @block.gpsimd
                def _(pool):
                    nc.gpsimd.memset(zeros[:, :], 0.0).then_inc(cleared, 1)

                @block.sync
                def _(sp):
                    sp.wait_ge(cleared, 1)
                    whole = dispatched.rearrange("(n p r) d -> n p (r d)", p=P, r=16)
                    for n in range(whole.shape[0]):
                        sp.dma_start(whole[n], zeros[:, :]).then_inc(zeroed, 16)
                    sp.wait_ge(zeroed, 16 * whole.shape[0])
            token_rows(chip, rows, logits, gate_w)
            route(chip, logits, place, scatter_to, gates)
            scattered = chip.keep_semaphore("scattered")
            with nc.Block() as block:
                @block.gpsimd
                def _(pool):
                    for t in range(TOKEN_TILES):
                        for k in range(2):
                            nc.gpsimd.indirect_dma_start(
                                out=dispatched, out_offset=bass.IndirectOffsetOnAxis(ap=scatter_to[:, k, t:t + 1], axis=0),
                                in_=rows[:, t, :], in_offset=None, bounds_check=slots - 1, oob_is_err=False).then_inc(scattered, 16)
                    pool.wait_ge(scattered, 16 * 2 * TOKEN_TILES)
        with ExitStack() as mid:
            eb = lambda name, shape: mid.enter_context(sbuf(nc, name, shape, F32))
            w1, w2 = eb("expert_w1", [P, FC, EXPERT_INNER]), eb("expert_w2", [P, ic, DIM])
            taken = eb("taken", [P, tiles, DIM])
            taken_t = eb("taken_t", [P, FC, CAPACITY])
            h = eb("expert_hidden", [P, ic, GROUP])
            made = eb("made", [P, tiles, DIM])
            turn_ps = mid.enter_context(banks(nc, "taken_psum", [P, 2, GROUP], F32))
            h_ps = mid.enter_context(banks(nc, "expert_psum", [P, 2, GROUP], F32))
            y_ps = mid.enter_context(banks(nc, "made_psum", [P, 2, GROUP], F32))
            per = GROUP // P
            with nc.Fori(0, EXPERTS) as e, step(nc, "weights_loaded taken_loaded turned turned_copied h_ready hidden_ready y_ready made_ready stored") as (
                    block, weights_loaded, taken_loaded, turned, turned_copied, h_ready, hidden_ready, y_ready, made_ready, stored):
                @block.sync
                def _(sp):
                    own = bass.ds(e * CAPACITY, CAPACITY)
                    sp.dma_start(taken[:, :, :], dispatched[own, :].rearrange("(t p) d -> p t d", p=P)).then_inc(taken_loaded, 16)
                    sp.dma_start(w1[:, :, :], io["L0_ffn_w1"][bass.ds(e * DIM, DIM), :].rearrange("(c p) f -> p c f", p=P)).then_inc(weights_loaded, 16)
                    sp.dma_start(w2[:, :, :], io["L0_ffn_w2"][bass.ds(e * EXPERT_INNER, EXPERT_INNER), :].rearrange("(c p) d -> p c d", p=P)).then_inc(weights_loaded, 16)
                    sp.wait_ge(made_ready, tiles)
                    sp.dma_start(produced[own, :].rearrange("(t p) d -> p t d", p=P), made[:, :, :]).then_inc(stored, 16)
                    sp.wait_ge(stored, 16)

                @block.tensor
                def _(pe):
                    pe.wait_ge(taken_loaded, 16)
                    for c in range(FC):
                        for j in range(CAPACITY // GROUP):
                            n = c * (CAPACITY // GROUP) + j
                            if n >= 2:
                                pe.wait_ge(turned_copied, n - 1)
                            for t in range(per):
                                last = nc.tensor.transpose(turn_ps[:, n % 2, t * P:(t + 1) * P], taken[:, j * per + t, c * P:(c + 1) * P], chip.c(C_ID))
                            last.then_inc(turned, 1)
                    pe.wait_ge(turned_copied, FC * (CAPACITY // GROUP))
                    pe.wait_ge(weights_loaded, 32)
                    for j in range(CAPACITY // GROUP):
                        for n in range(ic):
                            m = j * ic + n
                            if m >= 2:
                                pe.wait_ge(hidden_ready, m - 1)
                            for c in range(FC):
                                last = nc.tensor.matmul(h_ps[:, m % 2, :], w1[:, c, n * P:(n + 1) * P], taken_t[:, c, j * GROUP:(j + 1) * GROUP],
                                                        start=(c == 0), stop=(c == FC - 1))
                            last.then_inc(h_ready, 1)
                        pe.wait_ge(hidden_ready, (j + 1) * ic)
                        for t in range(per):
                            m = j * per + t
                            if m >= 2:
                                pe.wait_ge(made_ready, m - 1)
                            for n in range(ic):
                                last = nc.tensor.matmul(y_ps[:, m % 2, 0:DIM], h[:, n, t * P:(t + 1) * P], w2[:, n, :], start=(n == 0), stop=(n == ic - 1))
                            last.then_inc(y_ready, 1)

                @block.scalar
                def _(act):
                    for j in range(CAPACITY // GROUP):
                        if j:
                            act.wait_ge(y_ready, j * per)
                        for n in range(ic):
                            m = j * ic + n
                            act.wait_ge(h_ready, m + 1)
                            nc.scalar.activation(h[:, n, :], h_ps[:, m % 2, :], ACT.Gelu).then_inc(hidden_ready, 1)

                @block.vector
                def _(dve):
                    for c in range(FC):
                        for j in range(CAPACITY // GROUP):
                            n = c * (CAPACITY // GROUP) + j
                            dve.wait_ge(turned, n + 1)
                            nc.vector.tensor_copy(taken_t[:, c, j * GROUP:(j + 1) * GROUP], turn_ps[:, n % 2, :]).then_inc(turned_copied, 1)
                    for m in range(tiles):
                        dve.wait_ge(y_ready, m + 1)
                        nc.vector.tensor_copy(made[:, m, :], y_ps[:, m % 2, 0:DIM]).then_inc(made_ready, 1)
        combine(chip, ctx, produced, place, gates)


def combine(chip, ctx, produced, place, gates):
    nc = chip.nc
    per = GROUP // P
    sb = lambda name, shape, dt=F32: ctx.enter_context(sbuf(nc, name, shape, dt))
    gathered = [chip.keep_semaphore(f"gathered_{t}") for t in range(per)]
    got = sb("got", [P, per, 2, DIM])
    at = sb("place_now", [P, per, 2], U32)
    gate = sb("gate_now", [P, 2, per])
    mixed = sb("mixed", [P, per, DIM])
    turn_ps = ctx.enter_context(banks(nc, "mixed_psum", [P, FC, GROUP], F32))
    norm_ps = ctx.enter_context(banks(nc, "norm_psum", [P, 4, GROUP], F32))
    with nc.Fori(0, GROUPS) as g:
        with step(nc, "staged mixed_ready turned dve_step") as (block, staged, mixed_ready, turned, dve_step):
            @block.vector
            def _(dve):
                then = in_order(dve, dve_step)
                tiles = bass.ds(g * per, per)
                nc.vector.tensor_copy(at[:, :, :].rearrange("p t k -> p k t"), place[:, :, tiles]).then_inc(staged, 1)
                then(nc.vector.tensor_copy(gate[:, :, :], gates[:, :, tiles]))
                for t in range(per):
                    dve.wait_ge(gathered[t], 32 * g + 32)
                    then(nc.vector.tensor_scalar(mixed[:, t, :], got[:, t, 0, :], gate[:, 0, t:t + 1], None, ALU.mult))
                    nc.vector.scalar_tensor_tensor(out=mixed[:, t, :], in0=got[:, t, 1, :], scalar=gate[:, 1, t:t + 1], in1=mixed[:, t, :],
                                                   op0=ALU.mult, op1=ALU.add).then_inc(mixed_ready, 1)

            @block.gpsimd
            def _(pool):
                pool.wait_ge(staged, 1)
                for t in range(per):
                    for k in range(2):
                        nc.gpsimd.indirect_dma_start(out=got[:, t, k, :], out_offset=None, in_=produced,
                                                     in_offset=bass.IndirectOffsetOnAxis(ap=at[:, t, k:k + 1], axis=0)).then_inc(gathered[t], 16)
                for t in range(per):
                    pool.wait_ge(gathered[t], 32 * g + 32)

            @block.tensor
            def _(pe):
                for t in range(per):
                    pe.wait_ge(mixed_ready, t + 1)
                    for c in range(FC):
                        last = nc.tensor.transpose(turn_ps[:, c, t * P:(t + 1) * P], mixed[:, t, c * P:(c + 1) * P], chip.c(C_ID))
                last.then_inc(turned, 1)
        add_norm(chip, [group_slice(g)], norm_ps, ready=lambda _, c: turn_ps[:, c, :])


WIDE_HEADS, WIDE = 8, 64
INNER = WIDE_HEADS * WIDE
DEPTH = 2
HIDDEN = DIM * 4 * 2 // 3
HC = -(-HIDDEN // P)


def local_transformer(chip):
    nc, io = chip.nc, chip.io
    with ExitStack() as ctx:
        sb = lambda name, shape: ctx.enter_context(sbuf(nc, name, shape, F32))
        inner = sb("inner", [P, FC, TOKENS])
        with step(nc, "copied") as (block, copied):
            @block.scalar
            def _(act):
                nc.scalar.activation(inner[:, :, :], chip.xt[:, :, :], ACT.Copy).then_inc(copied, 1)
                act.wait_ge(copied, 1)
        with nc.Fori(0, DEPTH) as layer:
            window_attention(chip, layer, inner)
            gated_ffn(chip, layer, inner)
        with banks(nc, "norm_psum", [P, 8, GROUP], F32) as ps, nc.Fori(0, GROUPS // 2) as pair:
            tok = lambda g: bass.ds((pair * 2 + g) * GROUP, GROUP)
            add_norm(chip, [tok(0), tok(1)], ps, ready=lambda g, c: inner[:, c, tok(g)])


def window_attention(chip, layer, inner):
    nc, io = chip.nc, chip.io
    H2, HP, half = 2 * WIDE_HEADS, WIDE_HEADS // 2, WIDE // 2
    stages, apart = 7, 3.5
    order = sorted(((s, i) for i in range(TILES) for s in range(stages)), key=lambda si: si[0] + apart * si[1])
    with ExitStack() as ctx:
        sb = lambda name, shape, dt=F32: ctx.enter_context(sbuf(nc, name, shape, dt))
        wqkv = sb("wide_w", [P, FC, 3 * INNER])
        wo = sb("wide_wo", [P, INNER // P, DIM])
        scales = sb("wide_scales", [P, 2, WIDE])
        tables = sb("rope", [P, 2, TILES, 2, WIDE])
        load(nc, [(tables[:, :, :, :, :], io["rope"]), (wqkv[:, :, :], io["L1_ffn_wqkv"][bass.ds(layer * DIM, DIM), :].rearrange("(c p) n -> p c n", p=P)),
                  (wo[:, :, :], io["L1_ffn_wo"][bass.ds(layer * INNER, INNER), :].rearrange("(c p) n -> p c n", p=P)),
                  (scales[:, :, :].rearrange("p a d -> p (a d)"), io["L1_ffn_scales"][bass.ds(layer, 1), :].partition_broadcast(P))])
        shifted = sb("shifted", [P, 2, FC, P])
        root = sb("qk_root", [P, 2, H2])
        qk, qk_cos = (sb(n, [P, 2, H2, WIDE]) for n in ("qk", "qk_cos"))
        squares, qk_sin = (t[:, :, :, :].rearrange("p n c t -> p n (c t)").rearrange("p n (h d) -> p n h d", d=WIDE) for t in (chip.z, chip.sq))
        qk_t = sb("qk_t", [P, 3, 2, HP, P])
        values = sb("wide_values", [P, 3, INNER])
        probs = sb("wide_probs", [P, 2, WIDE_HEADS, 2 * P])
        probs_t = sb("wide_probs_t", [P, 2, WIDE_HEADS, 2, P])
        top, den = sb("wide_max", [P, 2, WIDE_HEADS]), sb("wide_den", [P, 2, WIDE_HEADS])
        out = sb("wide_out", [P, 2, INNER])
        out_t = sb("wide_out_t", [P, INNER // P, SEQ])
        masks = sb("window_masks", [P, 2, P], BF16)
        ps = ctx.enter_context(banks(nc, "wide_psum", [P, 8, GROUP], F32))
        with step(nc, "set_") as (block, set_):
            @block.vector
            def _(dve):
                nc.vector.tensor_copy(masks[:, 0, :], chip.c(C_SELF)).then_inc(set_, 1)
                nc.vector.tensor_copy(masks[:, 1, :], chip.c(C_BAND)).then_inc(set_, 1)
                wide = lambda t, d0: scales[:, t, d0:d0 + half].rearrange("p (o d) -> p o d", o=1).to_broadcast((P, TILES, half))
                for t in range(2):
                    for a in range(2):
                        for d0 in (0, half):
                            nc.vector.tensor_tensor(tables[:, a, :, t, d0:d0 + half], tables[:, a, :, t, d0:d0 + half], wide(t, d0 if a == 0 else half - d0),
                                                    ALU.mult).then_inc(set_, 1)
                dve.wait_ge(set_, 10)

        spot = lambda h: (h % 2) * HP + h // 2
        bank = lambda i, n: ps[:, 4 * (i % 2) + n, :]
        four = lambda i: ps[:, 4 * (i % 2):4 * (i % 2) + 4, :]
        span = lambda i: P if i == 0 else 2 * P
        scores_of = lambda i, h: bank(i, spot(h) // 2)[:, (spot(h) % 2) * 2 * P:(spot(h) % 2) * 2 * P + 2 * P]
        all_scores = lambda i: four(i).rearrange("p b (s n) -> p (b s) n", n=2 * P)[:, :, 0:span(i)]

        def batch_step(b):
            with step(nc, "shift_ready products_ready squares_ready sums_ready root_ready values_ready normed sin_ready qk_ready turned qk_turned scores_ready "
                          "top_ready exps_ready probs_turned probs_copied out_ready out_scaled out_turned out_copied dve_step") as (
                    block, shift_ready, products_ready, squares_ready, sums_ready, root_ready, values_ready, normed, sin_ready, qk_ready, turned, qk_turned, scores_ready,
                    top_ready, exps_ready, probs_turned, probs_copied, out_ready, out_scaled, out_turned, out_copied, dve_step):
                def copy_probs(i, p, copy):
                    src = bank(i, p).rearrange("p (h s n) -> p h s n", h=2, s=2)[:, :, 0:span(i) // P, :]
                    copy(probs_t[:, i % 2, 2 * p:2 * p + 2, 0:span(i) // P, :], src).then_inc(probs_copied, 1)

                @block.tensor
                def _(pe):
                    for s, i in order:
                        if s == 0:
                            pe.wait_ge(shift_ready, FC * (i + 1))
                            if i >= 2:
                                pe.wait_ge(out_copied, i - 1)
                            for n in range(3):
                                for c in range(FC):
                                    last = nc.tensor.matmul(bank(i, n), shifted[:, i % 2, c, :], wqkv[:, c, n * INNER:(n + 1) * INNER], start=(c == 0), stop=(c == FC - 1))
                                last.then_inc(products_ready, 1)
                        elif s == 2:
                            pe.wait_ge(qk_ready, i + 1)
                            for t in range(2):
                                for p in range(HP):
                                    pair = t * WIDE_HEADS + 2 * p
                                    last = nc.tensor.transpose(bank(i, t)[:, p * P:(p + 1) * P], qk[:, i % 2, pair:pair + 2, :].rearrange("p h d -> p (h d)"), chip.c(C_ID))
                            last.then_inc(turned, 1)
                        elif s == 3:
                            pe.wait_ge(qk_turned, i + 1)
                            pe.wait_ge(values_ready, i + 1)
                            for h in range(WIDE_HEADS):
                                rows = slice(WIDE * (h % 2), WIDE * (h % 2) + WIDE)
                                for which in range(span(i) // P):
                                    to = scores_of(i, h)[:, which * P:(which + 1) * P]
                                    nc.tensor.matmul(to, qk_t[rows, i % 3, 0, h // 2, :], qk_t[rows, (i - which) % 3, 1, h // 2, :], start=True, stop=False)
                                    last = nc.tensor.matmul(to, chip.id_bf[:, :], masks[:, which, :], start=False, stop=True)
                            last.then_inc(scores_ready, 1)
                        elif s == 4:
                            pe.wait_ge(exps_ready, WIDE_HEADS * (i + 1))
                            for h in range(WIDE_HEADS):
                                for which in range(span(i) // P):
                                    at = ((h % 2) * 2 + which) * P
                                    last = nc.tensor.transpose(bank(i, h // 2)[:, at:at + P], probs[:, i % 2, spot(h), which * P:(which + 1) * P], chip.c(C_ID))
                                if h % 2:
                                    last.then_inc(probs_turned, 1)
                        elif s == 5:
                            pe.wait_ge(probs_copied, HP * (i + 1))
                            for h in range(WIDE_HEADS):
                                for which in range(span(i) // P):
                                    last = nc.tensor.matmul(bank(i, 0)[:, h * WIDE:(h + 1) * WIDE], probs_t[:, i % 2, h, which, :],
                                                            values[:, (i - which) % 3, h * WIDE:(h + 1) * WIDE], start=(which == 0), stop=(which == span(i) // P - 1))
                            last.then_inc(out_ready, 1)
                        elif s == 6:
                            pe.wait_ge(out_scaled, i + 1)
                            for c in range(INNER // P):
                                last = nc.tensor.transpose(bank(i, 1)[:, c * P:(c + 1) * P], out[:, i % 2, c * P:(c + 1) * P], chip.c(C_ID))
                            last.then_inc(out_turned, 1)

                @block.scalar
                def _(act):
                    for s, i in order:
                        if s == 0:
                            act.wait_ge(products_ready, 3 * i + 2)
                            if i >= 2:
                                act.wait_ge(sums_ready, i - 1)
                                act.wait_ge(out_ready, i - 1)
                            nc.scalar.activation(squares[:, i % 2, :, :].rearrange("p h d -> p (h d)"), four(i)[:, 0:2, :].rearrange("p b n -> p (b n)"),
                                                 ACT.Square).then_inc(squares_ready, 1)
                            act.wait_ge(products_ready, 3 * i + 3)
                            nc.scalar.activation(values[:, i % 3, :], bank(i, 2), ACT.Copy).then_inc(values_ready, 1)
                        elif s == 1:
                            act.wait_ge(sums_ready, i + 1)
                            nc.scalar.activation(root[:, i % 2, :], root[:, i % 2, :], ACT.Sqrt).then_inc(root_ready, 1)
                        elif s == 2:
                            act.wait_ge(turned, i + 1)
                            if i >= 2:
                                act.wait_ge(scores_ready, i - 1)
                            nc.scalar.activation(qk_t[:, i % 3, :, :, :].rearrange("p t h n -> p (t h n)"), four(i)[:, 0:2, :].rearrange("p b n -> p (b n)"),
                                                 ACT.Copy).then_inc(qk_turned, 1)
                        elif s == 3:
                            act.wait_ge(top_ready, i + 1)
                            if i >= 2:
                                act.wait_ge(probs_turned, HP * (i - 1))
                            for h in range(WIDE_HEADS):
                                n = spot(h)
                                nc.scalar.activation(probs[:, i % 2, n, 0:span(i)], all_scores(i)[:, n, :], ACT.Exp, scale=WIDE ** 0.5,
                                                     bias=top[:, i % 2, n:n + 1], accum_out=den[:, i % 2, n:n + 1]).then_inc(exps_ready, 1)
                        elif s == 4:
                            for p in range(0, HP, 2):
                                act.wait_ge(probs_turned, HP * i + p + 1)
                                copy_probs(i, p, lambda o, src: nc.scalar.activation(o, src, ACT.Copy))

                @block.vector
                def _(dve):
                    then = in_order(dve, dve_step)
                    tt = nc.vector.tensor_tensor
                    for s, i in order:
                        if s == 0:
                            tok = b * SEQ + i * P
                            if i >= 2:
                                dve.wait_ge(products_ready, 3 * (i - 1))
                            nc.vector.tensor_copy(shifted[:, i % 2, 0, :], inner[:, 0, bass.ds(tok, P)]).then_inc(shift_ready, 1)
                            if i == 0:
                                then(nc.vector.memset(shifted[:, 0, 1, 0:1], 0.0))
                                nc.vector.tensor_copy(shifted[:, 0, 1, 1:P], inner[:, 1, bass.ds(tok, P - 1)]).then_inc(shift_ready, 1)
                            else:
                                nc.vector.tensor_copy(shifted[:, i % 2, 1, :], inner[:, 1, bass.ds(tok - 1, P)]).then_inc(shift_ready, 1)
                            dve.wait_ge(squares_ready, i + 1)
                            nc.vector.reduce_sum(root[:, i % 2, :], squares[:, i % 2, :, :], AX.X).then_inc(sums_ready, 1)
                        elif s == 1:
                            dve.wait_ge(root_ready, i + 1)
                            then(nc.vector.tensor_scalar(root[:, i % 2, :], root[:, i % 2, :], 1e-12, None, ALU.max))
                            then(nc.vector.reciprocal(root[:, i % 2, :], root[:, i % 2, :]))
                            if i >= 2:
                                dve.wait_ge(turned, i - 1)
                            raw = four(i)[:, 0:2, :].rearrange("p b (h d) -> p (b h) d", d=WIDE)
                            tt(qk[:, i % 2, :, :], raw, root[:, i % 2, :].rearrange("p (h o) -> p h o", o=1).to_broadcast((P, H2, WIDE)), ALU.mult).then_inc(normed, 1)
                            dve.wait_ge(normed, i + 1)
                            for t in range(2):
                                own = slice(t * WIDE_HEADS, (t + 1) * WIDE_HEADS)
                                table = tables[:, 0, i, t, :].rearrange("p (o d) -> p o d", o=1).to_broadcast((P, WIDE_HEADS, WIDE))
                                then(tt(qk_cos[:, i % 2, own, :], qk[:, i % 2, own, :], table, ALU.mult))
                            dve.wait_ge(sin_ready, 4 * (i + 1))
                            tt(qk[:, i % 2, :, :], qk_cos[:, i % 2, :, :], qk_sin[:, i % 2, :, :], ALU.add).then_inc(qk_ready, 1)
                        elif s == 3:
                            dve.wait_ge(scores_ready, i + 1)
                            if i >= 2:
                                dve.wait_ge(exps_ready, WIDE_HEADS * (i - 1))
                            then(nc.vector.reduce_max(top[:, i % 2, :], all_scores(i), AX.X))
                            nc.vector.tensor_scalar(top[:, i % 2, :], top[:, i % 2, :], -WIDE ** 0.5, None, ALU.mult).then_inc(top_ready, 1)
                        elif s == 4:
                            for p in range(1, HP, 2):
                                dve.wait_ge(probs_turned, HP * i + p + 1)
                                copy_probs(i, p, nc.vector.tensor_copy)
                        elif s == 5:
                            then(nc.vector.reciprocal(den[:, i % 2, :], den[:, i % 2, :]))
                            dve.wait_ge(out_ready, i + 1)
                            inv = den[:, i % 2, :].rearrange("p (a c o) -> p c a o", a=2, o=1).to_broadcast((P, HP, 2, WIDE))
                            tt(out[:, i % 2, :].rearrange("p (c a d) -> p c a d", a=2, d=WIDE), bank(i, 0).rearrange("p (c a d) -> p c a d", a=2, d=WIDE), inv,
                               ALU.mult).then_inc(out_scaled, 1)
                        elif s == 6:
                            dve.wait_ge(out_turned, i + 1)
                            nc.vector.tensor_copy(out_t[:, :, i * P:(i + 1) * P], bank(i, 1).rearrange("p (c n) -> p c n", n=P)).then_inc(out_copied, 1)

                @block.gpsimd
                def _(pool):
                    for s, i in order:
                        if s == 1:
                            pool.wait_ge(normed, i + 1)
                            for t in range(2):
                                own = slice(t * WIDE_HEADS, (t + 1) * WIDE_HEADS)
                                for d0 in (0, half):
                                    table = tables[:, 1, i, t, d0:d0 + half].rearrange("p (o d) -> p o d", o=1).to_broadcast((P, WIDE_HEADS, half))
                                    nc.gpsimd.tensor_tensor(qk_sin[:, i % 2, own, d0:d0 + half], qk[:, i % 2, own, half - d0:WIDE - d0], table, ALU.mult).then_inc(sin_ready, 1)

        with nc.Fori(0, BATCH) as b:
            batch_step(b)
            with step(nc, "y_ready added") as (block, y_ready, added):
                at = lambda j: bass.ds(b * SEQ + j * GROUP, GROUP)

                @block.tensor
                def _(pe):
                    for j in range(HALVES):
                        for c in range(FC):
                            for k in range(INNER // P):
                                last = nc.tensor.matmul(ps[:, FC * j + c, :], wo[:, k, c * P:(c + 1) * P], out_t[:, k, j * GROUP:(j + 1) * GROUP],
                                                        start=(k == 0), stop=(k == INNER // P - 1))
                            last.then_inc(y_ready, 1)

                @block.vector
                def _(dve):
                    for j in range(HALVES):
                        for c in range(FC):
                            dve.wait_ge(y_ready, FC * j + c + 1)
                            nc.vector.tensor_tensor(inner[:, c, at(j)], ps[:, FC * j + c, :], inner[:, c, at(j)], ALU.add).then_inc(added, 1)


def gated_ffn(chip, layer, inner):
    nc, io = chip.nc, chip.io
    with ExitStack() as ctx:
        sb = lambda name, shape: ctx.enter_context(sbuf(nc, name, shape, F32))
        w1, w2 = sb("gated_w1", [P, FC, 2 * HC * P]), sb("gated_w2", [P, HC, DIM])
        b1, b2, affine = sb("gated_b1", [P, 2 * HC]), sb("gated_b2", [P, FC]), sb("gated_norm", [P, 2 * FC])
        load(nc, [(w1[:, :, :], io["L1_ffn_w1"][bass.ds(layer * DIM, DIM), :].rearrange("(c p) n -> p c n", p=P)),
                  (w2[:, :, :], io["L1_ffn_w2"][bass.ds(layer * HC * P, HC * P), :].rearrange("(c p) n -> p c n", p=P)),
                  (b1[:, :], io["L1_ffn_b1"][bass.ds(layer * P, P), :]), (b2[:, :], io["L1_ffn_b2"][bass.ds(layer * P, P), :]),
                  (affine[:, :], io["L1_ffn_ln"][bass.ds(layer * P, P), :])])
        h, sq, root = chip.z, chip.sq, chip.root
        gate = sb("gate", [P, 2, GROUP])
        hidden = sb("gated_hidden", [P, 2, HC, GROUP])
        after = sb("gated_after", [P, FC, TOKENS])
        st_ps = ctx.enter_context(banks(nc, "gated_stats", [P, 2, GROUP], F32))
        h_ps = ctx.enter_context(banks(nc, "gated_psum", [P, 4, GROUP], F32))
        y_ps = ctx.enter_context(banks(nc, "gated_out", [P, 2, GROUP], F32))
        with nc.Fori(0, BATCH) as b, step(
                nc, "shift_ready mean_ready centred squares_ready var_ready root_ready inverse_ready rstd_ready normed pair_ready gate_ready hidden_ready y_ready y_added dve_step") as (
                block, shift_ready, mean_ready, centred, squares_ready, var_ready, root_ready, inverse_ready, rstd_ready, normed, pair_ready, gate_ready, hidden_ready,
                y_ready, y_added, dve_step):
            at = lambda j: b * SEQ + j * GROUP
            pairs = [(j, n) for j in range(HALVES) for n in range(HC)]

            @block.tensor
            def _(pe):
                for j in range(HALVES):
                    pe.wait_ge(shift_ready, FC * (j + 1))
                    for c in range(FC):
                        last = nc.tensor.matmul(st_ps[:, j, :], chip.c(C_MEAN), h[:, j, c, :], start=(c == 0), stop=(c == FC - 1))
                    last.then_inc(mean_ready, 1)
                for j in range(HALVES):
                    pe.wait_ge(squares_ready, FC * (j + 1))
                    for t in range(PER_HALF):
                        for c in range(FC):
                            last = nc.tensor.matmul(st_ps[:, j, t:t + 1], sq[:, j, c, t * P:(t + 1) * P], chip.c(C_MEAN, 1), start=(c == 0), stop=(c == FC - 1))
                    last.then_inc(var_ready, 1)
                for j in range(HALVES):
                    pe.wait_ge(inverse_ready, j + 1)
                    for t in range(PER_HALF):
                        last = nc.tensor.matmul(st_ps[:, j, t * P:(t + 1) * P], root[:, j, t:t + 1].to_broadcast((P, P)), chip.c(C_ID), start=True, stop=True)
                    last.then_inc(rstd_ready, 1)
                for k, (j, n) in enumerate(pairs):
                    pe.wait_ge(normed, FC * (j + 1))
                    if k >= 2:
                        pe.wait_ge(hidden_ready, k - 1)
                    for part in range(2):
                        for c in range(FC):
                            m = part * HC + n
                            last = nc.tensor.matmul(h_ps[:, 2 * (k % 2) + part, :], w1[:, c, m * P:(m + 1) * P], h[:, j, c, :], start=(c == 0), stop=(c == FC - 1))
                    last.then_inc(pair_ready, 1)
                for j in range(HALVES):
                    for c in range(FC):
                        if j:
                            pe.wait_ge(y_added, c + 1)
                        for n in range(HC):
                            pe.wait_ge(hidden_ready, HC * j + n + 1)
                            last = nc.tensor.matmul(y_ps[:, c, :], w2[:, n, c * P:(c + 1) * P], hidden[:, j, n, :], start=(n == 0), stop=(n == HC - 1))
                        last.then_inc(y_ready, 1)

            @block.scalar
            def _(act):
                for j in range(HALVES):
                    for c in range(FC):
                        act.wait_ge(centred, FC * j + c + 1)
                        nc.scalar.activation(sq[:, j, c, :], h[:, j, c, :], ACT.Square).then_inc(squares_ready, 1)
                for j in range(HALVES):
                    act.wait_ge(var_ready, j + 1)
                    nc.scalar.activation(root[:, j, :], st_ps[:, j, 0:PER_HALF], ACT.Sqrt, bias=chip.eps[:, 0:1]).then_inc(root_ready, 1)
                for k, (j, n) in enumerate(pairs):
                    act.wait_ge(pair_ready, k + 1)
                    if k >= 2:
                        act.wait_ge(hidden_ready, k - 1)
                    nc.scalar.activation(gate[:, k % 2, :], h_ps[:, 2 * (k % 2) + 1, :], ACT.Gelu, bias=b1[:, HC + n:HC + n + 1]).then_inc(gate_ready, 1)

            @block.vector
            def _(dve):
                then = in_order(dve, dve_step)
                for j in range(HALVES):
                    nc.vector.tensor_copy(h[:, j, 0, :], inner[:, 0, bass.ds(at(j), GROUP)]).then_inc(shift_ready, 1)
                    if j == 0:
                        then(nc.vector.memset(h[:, 0, 1, 0:1], 0.0))
                        nc.vector.tensor_copy(h[:, 0, 1, 1:GROUP], inner[:, 1, bass.ds(at(0), GROUP - 1)]).then_inc(shift_ready, 1)
                    else:
                        nc.vector.tensor_copy(h[:, j, 1, :], inner[:, 1, bass.ds(at(j) - 1, GROUP)]).then_inc(shift_ready, 1)
                for j in range(HALVES):
                    dve.wait_ge(mean_ready, j + 1)
                    for c in range(FC):
                        nc.vector.tensor_tensor(h[:, j, c, :], h[:, j, c, :], st_ps[:, j, :], ALU.subtract).then_inc(centred, 1)
                for j in range(HALVES):
                    dve.wait_ge(root_ready, j + 1)
                    nc.vector.reciprocal(root[:, j, :], root[:, j, :]).then_inc(inverse_ready, 1)
                for j in range(HALVES):
                    dve.wait_ge(rstd_ready, j + 1)
                    for c in range(FC):
                        then(nc.vector.tensor_tensor(h[:, j, c, :], h[:, j, c, :], st_ps[:, j, :], ALU.mult))
                        nc.vector.tensor_scalar(h[:, j, c, :], h[:, j, c, :], affine[:, c:c + 1], affine[:, FC + c:FC + c + 1], ALU.mult, ALU.add).then_inc(normed, 1)
                for k, (j, n) in enumerate(pairs):
                    dve.wait_ge(gate_ready, k + 1)
                    nc.vector.scalar_tensor_tensor(out=hidden[:, j, n, :], in0=h_ps[:, 2 * (k % 2), :], scalar=b1[:, n:n + 1], in1=gate[:, k % 2, :],
                                                   op0=ALU.add, op1=ALU.mult).then_inc(hidden_ready, 1)
                for j in range(HALVES):
                    for c in range(FC):
                        dve.wait_ge(y_ready, FC * j + c + 1)
                        nc.vector.scalar_tensor_tensor(out=after[:, c, bass.ds(at(j), GROUP)], in0=y_ps[:, c, :], scalar=b2[:, c:c + 1],
                                                       in1=inner[:, c, bass.ds(at(j), GROUP)], op0=ALU.add, op1=ALU.add).then_inc(y_added, 1)
        with step(nc, "copied") as (block, copied):
            @block.scalar
            def _(act):
                nc.scalar.activation(inner[:, 0, :], after[:, 0, :], ACT.Copy).then_inc(copied, 1)

            @block.vector
            def _(dve):
                nc.vector.tensor_copy(inner[:, 1, :], after[:, 1, :]).then_inc(copied, 1)


STATES, TAPS, RANK = 16, 4, 64
SC = 2 * DIM // P


def state_space(chip):
    nc, io = chip.nc, chip.io
    halves = SEQ // GROUP
    width = SC * P
    with ExitStack() as ctx:
        sb = lambda name, shape: ctx.enter_context(sbuf(nc, name, shape, F32))
        w_in, w_out = sb("in_w", [P, FC, 2 * width]), sb("out_w", [P, SC, DIM])
        w_x, w_dt = sb("x_w", [P, SC, RANK + 2 * STATES]), sb("dt_w", [RANK, width])
        conv = sb("conv_w", [P, SC, TAPS])
        per_feature = sb("ssm_vectors", [P, 3, SC])
        norm_w = sb("ssm_norm", [P, FC])
        a_log = sb("a_log", [P, SC, STATES])
        pick = sb("pick", [2 * STATES, 2 * STATES * P])
        load(nc, [(w_in[:, :, :], io["L2_attn_win"].rearrange("(c p) n -> p c n", p=P)),
                  (w_out[:, :, :], io["L2_attn_wout"].rearrange("(c p) n -> p c n", p=P)),
                  (w_x[:, :, :], io["L2_attn_wx"].rearrange("(c p) n -> p c n", p=P)), (w_dt[:, :], io["L2_attn_wdt"]),
                  (conv[:, :, :], io["L2_attn_conv"].rearrange("(c p) k -> p c k", p=P)), (per_feature[:, :, :], io["L2_attn_vec"]),
                  (norm_w[:, :], io["L2_attn_norm"]), (a_log[:, :, :], io["L2_attn_alog"].rearrange("(c p) n -> p c n", p=P)),
                  (pick[:, :], io["pick"])])
        xs = sb("ssm_x", [P, SC, TAPS - 1 + SEQ])
        gate = sb("ssm_gate", [P, SC, SEQ])
        chip.ssm_states = sb("ssm_states", [2 * STATES, SEQ])
        u, dt, du = sb("ssm_u", [P, SC, SEQ]), sb("ssm_dt", [P, SC, SEQ]), sb("ssm_du", [P, SC, SEQ])
        with step(nc, "exp_ready dve_step") as (block, exp_ready, dve_step):
            @block.scalar
            def _(act):
                nc.scalar.activation(a_log[:, :, :], a_log[:, :, :], ACT.Exp).then_inc(exp_ready, 1)

            @block.vector
            def _(dve):
                dve.wait_ge(exp_ready, 1)
                then = in_order(dve, dve_step)
                then(nc.vector.tensor_scalar(a_log[:, :, :], a_log[:, :, :], -1.0, None, ALU.mult))
                then(nc.vector.memset(xs[:, :, 0:TAPS - 1], 0.0))
        with nc.Fori(0, BATCH) as b:
            ssm_inputs(chip, b, w_in, norm_w, xs, gate)
            ssm_steps(chip, conv, per_feature, w_x, w_dt, xs, u, dt, du)
            ssm_scan(chip, a_log, pick, u, dt, du, gate, per_feature, xs)
            with banks(nc, "norm_psum", [P, 8, GROUP], F32) as norm_ps:
                add_norm(chip, [bass.ds(b * SEQ + j * GROUP, GROUP) for j in range(halves)], norm_ps, keeps=2.0,
                         product=(w_out, lambda j, k: u[:, k, j * GROUP:(j + 1) * GROUP]))


def ssm_inputs(chip, b, w_in, norm_w, xs, gate):
    nc = chip.nc
    halves = SEQ // GROUP
    with ExitStack() as ctx:
        h = ctx.enter_context(sbuf(nc, "ssm_in", [P, FC, SEQ], F32))
        sq, rms = chip.sq[:, 0, :, :], chip.z[:, 0, 0, :]
        mean_ps = ctx.enter_context(banks(nc, "ssm_mean", [P, 2, GROUP], F32))
        in_ps = ctx.enter_context(banks(nc, "ssm_in_psum", [P, 4, GROUP], F32))
        with step(nc, "squares_ready mean_ready rms_ready h_ready in_ready in_copied dve_step") as (
                block, squares_ready, mean_ready, rms_ready, h_ready, in_ready, in_copied, dve_step):
            jobs = [(m, j) for m in range(2 * SC) for j in range(halves)]
            x = lambda c, j: chip.xt[:, c, bass.ds(b * SEQ + j * GROUP, GROUP)]

            @block.scalar
            def _(act):
                for j in range(halves):
                    if j:
                        act.wait_ge(mean_ready, j)
                    for c in range(FC):
                        nc.scalar.activation(sq[:, c, :], x(c, j), ACT.Square).then_inc(squares_ready, 1)
                    act.wait_ge(mean_ready, j + 1)
                    if j:
                        act.wait_ge(h_ready, j)
                    nc.scalar.activation(rms[:, :], mean_ps[:, j, :], ACT.Sqrt, bias=chip.eps[:, 0:1]).then_inc(rms_ready, 1)
                for n, (m, j) in enumerate(jobs):
                    act.wait_ge(in_ready, n + 1)
                    part = slice(j * GROUP, (j + 1) * GROUP)
                    if m < SC:
                        dst = xs[:, m, TAPS - 1 + j * GROUP:TAPS - 1 + (j + 1) * GROUP]
                        nc.scalar.activation(dst, in_ps[:, n % 4, :], ACT.Copy).then_inc(in_copied, 1)
                    else:
                        nc.scalar.activation(gate[:, m - SC, part], in_ps[:, n % 4, :], ACT.Silu).then_inc(in_copied, 1)

            @block.tensor
            def _(pe):
                for j in range(halves):
                    pe.wait_ge(squares_ready, FC * (j + 1))
                    for c in range(FC):
                        last = nc.tensor.matmul(mean_ps[:, j, :], chip.c(C_MEAN), sq[:, c, :], start=(c == 0), stop=(c == FC - 1))
                    last.then_inc(mean_ready, 1)
                pe.wait_ge(h_ready, halves)
                for n, (m, j) in enumerate(jobs):
                    if n >= 4:
                        pe.wait_ge(in_copied, n - 3)
                    for c in range(FC):
                        last = nc.tensor.matmul(in_ps[:, n % 4, :], w_in[:, c, m * P:(m + 1) * P], h[:, c, j * GROUP:(j + 1) * GROUP],
                                                start=(c == 0), stop=(c == FC - 1))
                    last.then_inc(in_ready, 1)

            @block.vector
            def _(dve):
                then = in_order(dve, dve_step)
                for j in range(halves):
                    dve.wait_ge(rms_ready, j + 1)
                    then(nc.vector.reciprocal(rms[:, :], rms[:, :]))
                    for c in range(FC):
                        last = nc.vector.scalar_tensor_tensor(out=h[:, c, j * GROUP:(j + 1) * GROUP], in0=x(c, j), scalar=norm_w[:, c:c + 1],
                                                              in1=rms[:, :], op0=ALU.mult, op1=ALU.mult)
                    last.then_inc(h_ready, 1)


def ssm_steps(chip, conv, per_feature, w_x, w_dt, xs, u, dt, du):
    nc = chip.nc
    halves = SEQ // GROUP
    with ExitStack() as ctx:
        pre = ctx.enter_context(sbuf(nc, "ssm_pre", [P, 2, SEQ], F32))
        logs = ctx.enter_context(sbuf(nc, "ssm_logs", [P, 2, SEQ], F32))
        series = ctx.enter_context(sbuf(nc, "ssm_series", [P, SEQ], F32))
        low = ctx.enter_context(sbuf(nc, "ssm_low", [RANK, SEQ], F32))
        states = chip.ssm_states
        low_ps = ctx.enter_context(banks(nc, "ssm_low_psum", [P, 2, GROUP], F32))
        dt_ps = ctx.enter_context(banks(nc, "ssm_dt_psum", [P, 2, GROUP], F32))
        st_ps = ctx.enter_context(banks(nc, "ssm_states_psum", [P, 2, GROUP], F32))
        with step(nc, "conv_ready u_ready low_ready low_copied dt_ready shifted_ready size_ready exp_ready log_ready dt_done dve_step") as (
                block, conv_ready, u_ready, low_ready, low_copied, dt_ready, shifted_ready, size_ready, exp_ready, log_ready, dt_done, dve_step):
            flat = lambda t: t[:, :, :].rearrange("p b n -> p (b n)")

            @block.vector
            def _(dve):
                then = in_order(dve, dve_step)
                for c in range(SC):
                    acc = pre[:, c % 2, :]
                    if c >= 2:
                        dve.wait_ge(u_ready, c - 1)
                    for k in range(TAPS):
                        tap = xs[:, c, k:k + SEQ]
                        if k == 0:
                            then(nc.vector.tensor_scalar(acc, tap, conv[:, c, 0:1], per_feature[:, 0, c:c + 1], ALU.mult, ALU.add))
                        else:
                            last = nc.vector.scalar_tensor_tensor(out=acc, in0=tap, scalar=conv[:, c, k:k + 1], in1=acc, op0=ALU.mult, op1=ALU.add)
                            if k < TAPS - 1:
                                then(last)
                    last.then_inc(conv_ready, 1)
                edge = 2.0 ** -6
                for c in range(SC):
                    dve.wait_ge(dt_ready, c + 1)
                    bias = per_feature[:, 1, c:c + 1]
                    nc.vector.tensor_scalar(dt[:, c, :], flat(dt_ps), bias, 0.0, ALU.add, ALU.max).then_inc(shifted_ready, 1)
                    dve.wait_ge(exp_ready, c + 1)
                    e, log, stt = pre[:, c % 2, :], logs[:, c % 2, :], nc.vector.scalar_tensor_tensor
                    then(nc.vector.tensor_scalar(series[:, :], e, -1 / 4, 1 / 3, ALU.mult, ALU.add))
                    then(nc.vector.tensor_tensor(series[:, :], series[:, :], e, ALU.mult))
                    then(stt(out=series[:, :], in0=series[:, :], scalar=-0.5, in1=e, op0=ALU.add, op1=ALU.mult))
                    then(stt(out=series[:, :], in0=series[:, :], scalar=1.0, in1=e, op0=ALU.add, op1=ALU.mult))
                    dve.wait_ge(log_ready, c + 1)
                    then(stt(out=log, in0=e, scalar=edge, in1=log, op0=ALU.is_lt, op1=ALU.subtract))
                    then(stt(out=series[:, :], in0=log, scalar=-1.0, in1=series[:, :], op0=ALU.mult, op1=ALU.max))
                    dve.wait_ge(shifted_ready, c + 1)
                    then(nc.vector.tensor_tensor(dt[:, c, :], dt[:, c, :], series[:, :], ALU.add))
                    nc.vector.tensor_tensor(du[:, c, :], dt[:, c, :], u[:, c, :], ALU.mult).then_inc(dt_done, 1)

            @block.scalar
            def _(act):
                for c in range(SC):
                    act.wait_ge(conv_ready, c + 1)
                    nc.scalar.activation(u[:, c, :], pre[:, c % 2, :], ACT.Silu).then_inc(u_ready, 1)
                act.wait_ge(low_ready, 1)
                nc.scalar.activation(low[:, :], flat(low_ps)[0:RANK, :], ACT.Copy).then_inc(low_copied, 1)
                nc.scalar.activation(states[:, :], flat(st_ps)[0:2 * STATES, :], ACT.Copy).then_inc(low_copied, 1)
                for c in range(SC):
                    act.wait_ge(dt_ready, c + 1)
                    act.wait_ge(shifted_ready, c + 1)
                    if c >= 2:
                        act.wait_ge(dt_done, c - 1)
                    part = pre[:, c % 2, :]
                    nc.scalar.activation(part, flat(dt_ps), ACT.Abs, bias=per_feature[:, 1, c:c + 1]).then_inc(size_ready, 1)
                    act.wait_ge(size_ready, c + 1)
                    nc.scalar.activation(part, part, ACT.Exp, scale=-1.0).then_inc(exp_ready, 1)
                    act.wait_ge(exp_ready, c + 1)
                    nc.scalar.activation(logs[:, c % 2, :], part, ACT.Ln, bias=chip.eps[:, 2:3]).then_inc(log_ready, 1)

            @block.tensor
            def _(pe):
                for j in range(halves):
                    for c in range(SC):
                        pe.wait_ge(u_ready, c + 1)
                        nc.tensor.matmul(low_ps[0:RANK, j, :], w_x[:, c, 0:RANK], u[:, c, j * GROUP:(j + 1) * GROUP], start=(c == 0), stop=(c == SC - 1))
                        last = nc.tensor.matmul(st_ps[0:2 * STATES, j, :], w_x[:, c, RANK:RANK + 2 * STATES], u[:, c, j * GROUP:(j + 1) * GROUP],
                                                start=(c == 0), stop=(c == SC - 1))
                last.then_inc(low_ready, 1)
                pe.wait_ge(low_copied, 1)
                for c in range(SC):
                    if c:
                        pe.wait_ge(shifted_ready, c)
                        pe.wait_ge(size_ready, c)
                    for j in range(halves):
                        last = nc.tensor.matmul(dt_ps[:, j, :], w_dt[:, c * P:(c + 1) * P], low[:, j * GROUP:(j + 1) * GROUP], start=True, stop=True)
                    last.then_inc(dt_ready, 1)


def ssm_scan(chip, a, pick, u, dt, du, gate, per_feature, y):
    nc = chip.nc
    halves = SEQ // GROUP
    with ExitStack() as ctx:
        sb = lambda name, shape: ctx.enter_context(sbuf(nc, name, shape, F32))
        decay, added, state, term = (sb(n, [P, 2, SEQ]) for n in ("decay", "added", "state", "term"))
        b_ps = ctx.enter_context(banks(nc, "state_in", [P, 2, SEQ], F32))
        c_ps = ctx.enter_context(banks(nc, "state_out", [P, 2, SEQ], F32))
        sums = lambda c: y[:, c, TAPS - 1:TAPS - 1 + SEQ]
        total = STATES * SC
        with step(nc, "spread_ready decay_ready added_ready state_ready term_ready summed dve_step") as (
                block, spread_ready, decay_ready, added_ready, state_ready, term_ready, summed, dve_step):
            @block.tensor
            def _(pe):
                for n in range(STATES):
                    if n >= 2:
                        pe.wait_ge(term_ready, SC * (n - 1))
                    for which, ps in ((0, b_ps), (1, c_ps)):
                        row = which * STATES + n
                        for j in range(halves):
                            last = nc.tensor.matmul(ps[:, n % 2, j * GROUP:(j + 1) * GROUP], pick[:, row * P:(row + 1) * P],
                                                    chip.ssm_states[:, j * GROUP:(j + 1) * GROUP], start=True, stop=True)
                    last.then_inc(spread_ready, 1)

            @block.scalar
            def _(act):
                for i in range(total):
                    n, c = divmod(i, SC)
                    if i >= 2:
                        act.wait_ge(state_ready, i - 1)
                    nc.scalar.activation(decay[:, i % 2, :], dt[:, c, :], ACT.Exp, scale=a[:, c, n:n + 1]).then_inc(decay_ready, 1)

            @block.vector
            def _(dve):
                then = in_order(dve, dve_step)
                for i in range(total):
                    n, c = divmod(i, SC)
                    dve.wait_ge(spread_ready, n + 1)
                    nc.vector.tensor_tensor(added[:, i % 2, :], du[:, c, :], b_ps[:, n % 2, :], ALU.mult).then_inc(added_ready, 1)
                    dve.wait_ge(added_ready, i + 1)
                    dve.wait_ge(decay_ready, i + 1)
                    nc.vector.tensor_tensor_scan(state[:, i % 2, :], decay[:, i % 2, :], added[:, i % 2, :], 0.0, ALU.mult, ALU.add).then_inc(state_ready, 1)
                    dve.wait_ge(state_ready, i + 1)
                    if i >= 2:
                        dve.wait_ge(summed, i - 1)
                    nc.vector.tensor_tensor(term[:, i % 2, :], state[:, i % 2, :], c_ps[:, n % 2, :], ALU.mult).then_inc(term_ready, 1)
                for c in range(SC):
                    dve.wait_ge(summed, total)
                    then(nc.vector.scalar_tensor_tensor(out=u[:, c, :], in0=u[:, c, :], scalar=per_feature[:, 2, c:c + 1], in1=sums(c), op0=ALU.mult, op1=ALU.add))
                    then(nc.vector.tensor_tensor(u[:, c, :], u[:, c, :], gate[:, c, :], ALU.mult))

            @block.gpsimd
            def _(pool):
                for i in range(total):
                    n, c = divmod(i, SC)
                    pool.wait_ge(term_ready, i + 1)
                    if n == 0:
                        nc.gpsimd.tensor_copy(sums(c), term[:, i % 2, :]).then_inc(summed, 1)
                    else:
                        pool.wait_ge(summed, i - SC + 1)
                        nc.gpsimd.tensor_tensor(sums(c), sums(c), term[:, i % 2, :], ALU.add).then_inc(summed, 1)


KEYS, TOP, SIDES, RHEADS, RDIM = 128, 8, 2, 4, 32
EMBEDS, RINNER = 4096, 512
PICKS = RHEADS * TOP


def retrieval_ffn(chip):
    nc, io = chip.nc, chip.io
    rc = RINNER // P
    with ExitStack() as ctx:
        sb = lambda name, shape, dt=F32: ctx.enter_context(sbuf(nc, name, shape, dt))
        b = {}
        b["wq"], b["keys"] = sb("query_w", [P, FC, SIDES * P]), sb("product_keys", [P, SIDES, RHEADS * KEYS])
        b["wg"], b["wu"], b["wd"] = sb("r_gate_w", [P, FC, RINNER]), sb("r_up_w", [P, FC, RINNER]), sb("r_down_w", [P, rc, DIM])
        load(nc, [(b["wq"][:, :, :], io["L3_ffn_wq"].rearrange("(c p) n -> p c n", p=P)), (b["keys"][:, :, :], io["L3_ffn_keys"]),
                  (b["wg"][:, :, :], io["L3_ffn_wg"].rearrange("(c p) n -> p c n", p=P)), (b["wu"][:, :, :], io["L3_ffn_wu"].rearrange("(c p) n -> p c n", p=P)),
                  (b["wd"][:, :, :], io["L3_ffn_wd"].rearrange("(c p) n -> p c n", p=P))])
        for when in ("now", "next"):
            b["rows_" + when] = sb("r_rows_" + when, [P, PER_HALF, DIM])
            b["pick_" + when] = sb("r_pick_" + when, [P, PER_HALF, PICKS], U32)
            b["weight_" + when] = sb("r_weight_" + when, [P, PER_HALF, RHEADS, TOP])
        b["stage"], b["q_t"] = sb("r_stage", [P, FC, GROUP]), sb("r_queries", [P, SIDES, GROUP])
        b["sims"] = sb("r_sims", [P, SIDES, RHEADS * KEYS])
        b["best"], b["at_f"] = sb("r_best", [P, SIDES, RHEADS, TOP]), sb("r_at", [P, SIDES, RHEADS, TOP])
        b["best_at"] = sb("r_best_at", [P, SIDES, RHEADS, TOP], U32)
        b["sums"], b["codes"] = sb("r_sums", [P, RHEADS, TOP, TOP]), sb("r_codes", [P, RHEADS, TOP, TOP])
        b["score"], b["pos"], b["pos_f"] = sb("r_score", [P, RHEADS, TOP]), sb("r_pos", [P, RHEADS, TOP], U32), sb("r_pos_f", [P, RHEADS, TOP])
        b["hot"], b["code"], b["total"] = sb("r_hot", [P, TOP, TOP * TOP]), sb("r_code", [P, RHEADS, TOP]), sb("r_total", [P, RHEADS])
        b["got"] = sb("r_got", [P, PICKS, 2 * DIM])
        b["scratch"] = sb("r_scratch", [P, 2, DIM])
        b["dots"], b["act"] = sb("r_dots", [P, PER_HALF, PICKS]), sb("r_act", [P, PER_HALF, PICKS])
        b["diagonal"] = sb("r_diagonal", [P, 2, TOP, P])
        b["hidden"], b["gate"] = sb("r_hidden", [P, rc, GROUP]), sb("r_gate", [P, 2, GROUP])
        arrived = [chip.keep_semaphore(f"row_arrived_{n}") for n in range(PICKS)]
        y_ps = ctx.enter_context(banks(nc, "r_psum_y", [P, FC, GROUP], F32))

        def group(now, following):
            retrieval_step(chip, b, arrived, y_ps, now, following)
            if now is not None:
                with banks(nc, "norm_psum", [P, 4, GROUP], F32) as norm_ps:
                    add_norm(chip, [group_slice(now)], norm_ps, ready=lambda _, c: y_ps[:, c, :])

        group(None, 0)
        with nc.Fori(0, GROUPS - 1) as g:
            group(g, g + 1)
        group(GROUPS - 1, None)


def retrieval_step(chip, b, arrived, y_ps, now, following):
    nc, io = chip.nc, chip.io
    per, rc = PER_HALF, RINNER // P
    current, ahead = now is not None, following is not None
    order = []
    for t in range(per):
        order.append(("search", t, 0))
        for h in range(RHEADS):
            order.append(("dots", t, h))
            if h:
                order.append(("mix", t, h - 1))
            if h < RHEADS - 1:
                order.append(("search", t, h + 1))
        order += [("mix", t, RHEADS - 1), ("search", t, RHEADS)]
    order = [s for s in order if (ahead if s[0] == "search" else current)]
    with ExitStack() as ctx:
        pair_ps = ctx.enter_context(banks(nc, "r_psum_pair", [P, 2, GROUP], F32))
        q_ps = ctx.enter_context(banks(nc, "r_psum_q", [P, SIDES, GROUP], F32))
        rows_ps = ctx.enter_context(banks(nc, "r_psum_rows", [P, 2, GROUP], F32))
        with step(nc, "taken pair_ready gate_ready hidden_ready staged q_ready q_copied turned rows_ready sims_ready sims_copied sims_used "
                      "shifted exps_ready dot_ready dots_active weighted diagonal_ready summed dve_step") as (
                block, taken, pair_ready, gate_ready, hidden_ready, staged, q_ready, q_copied, turned, rows_ready, sims_ready, sims_copied, sims_used,
                shifted, exps_ready, dot_ready, dots_active, weighted, diagonal_ready, summed, dve_step):
            if current:
                @block.gpsimd
                def _(pool):
                    pool.wait_ge(taken, 3)
                    for t in range(per):
                        for n in range(PICKS):
                            if t and n % TOP == 0:
                                pool.wait_ge(summed, RHEADS * (t - 1) + n // TOP + 1)
                            nc.gpsimd.indirect_dma_start(out=b["got"][:, n, :], out_offset=None, in_=io["L3_ffn_tables"],
                                                         in_offset=bass.IndirectOffsetOnAxis(ap=b["pick_now"][:, t, n:n + 1], axis=0)).then_inc(arrived[n], 16)

            @block.tensor
            def _(pe):
                if current:
                    x = lambda c: chip.xt[:, c, group_slice(now)]
                    for n in range(rc):
                        if n >= 1:
                            pe.wait_ge(hidden_ready, n)
                        for k, w in enumerate((b["wg"], b["wu"])):
                            for c in range(FC):
                                last = nc.tensor.matmul(pair_ps[:, k, :], w[:, c, n * P:(n + 1) * P], x(c), start=(c == 0), stop=(c == FC - 1))
                        last.then_inc(pair_ready, 1)
                if ahead:
                    for s in range(SIDES):
                        for c in range(FC):
                            last = nc.tensor.matmul(q_ps[:, s, :], b["wq"][:, c, s * P:(s + 1) * P], chip.xt[:, c, group_slice(following)],
                                                    start=(c == 0), stop=(c == FC - 1))
                        last.then_inc(q_ready, 1)
                    pe.wait_ge(staged, 1)
                    for t in range(per):
                        for c in range(FC):
                            at = (t % 2) * DIM + c * P
                            last = nc.tensor.transpose(rows_ps[:, t // 2, at:at + P], b["stage"][:, c, t * P:(t + 1) * P], chip.c(C_ID))
                    last.then_inc(turned, 1)
                if current:
                    for c in range(FC):
                        for n in range(rc):
                            pe.wait_ge(hidden_ready, n + 1)
                            nc.tensor.matmul(y_ps[:, c, :], b["wd"][:, n, c * P:(c + 1) * P], b["hidden"][:, n, :], start=(n == 0), stop=False)
                for kind, t, h in order:
                    if kind == "search" and h == 0:
                        pe.wait_ge(q_copied, SIDES)
                        if t:
                            pe.wait_ge(sims_copied, t)
                        for s in range(SIDES):
                            last = nc.tensor.matmul(pair_ps[:, s, :], b["q_t"][:, s, t * P:(t + 1) * P], b["keys"][:, s, :], start=True, stop=True)
                        last.then_inc(sims_ready, 1)
                    elif kind == "mix":
                        k = RHEADS * t + h
                        pe.wait_ge(diagonal_ready, TOP * (k + 1))
                        for n in range(TOP):
                            for c in range(FC):
                                row = b["got"][:, TOP * h + n, DIM + c * P:DIM + (c + 1) * P]
                                last = nc.tensor.matmul(y_ps[:, c, t * P:(t + 1) * P], row, b["diagonal"][:, k % 2, n, :],
                                                        start=False, stop=(k == RHEADS * per - 1 and n == TOP - 1))
                        last.then_inc(summed, 1)

            @block.scalar
            def _(act):
                if current:
                    nc.scalar.activation(b["rows_now"][:, :, :], b["rows_next"][:, :, :], ACT.Copy).then_inc(taken, 1)
                if ahead:
                    nc.scalar.activation(b["stage"][:, :, :], chip.xt[:, :, group_slice(following)], ACT.Copy).then_inc(staged, 1)
                if current:
                    for n in range(rc):
                        act.wait_ge(pair_ready, n + 1)
                        if n >= 2:
                            act.wait_ge(hidden_ready, n - 1)
                        nc.scalar.activation(b["gate"][:, n % 2, :], pair_ps[:, 0, :], ACT.Silu).then_inc(gate_ready, 1)
                if ahead:
                    for s in range(SIDES):
                        act.wait_ge(q_ready, s + 1)
                        nc.scalar.activation(b["q_t"][:, s, :], q_ps[:, s, :], ACT.Copy).then_inc(q_copied, 1)
                    act.wait_ge(turned, 1)
                    if current:
                        act.wait_ge(taken, 3)
                    nc.scalar.activation(b["rows_next"][:, :, :], rows_ps[:, :, :].rearrange("p b (t n) -> p (b t) n", n=DIM), ACT.Copy).then_inc(rows_ready, 1)
                for kind, t, h in order:
                    if kind == "search" and h == 0:
                        act.wait_ge(sims_ready, t + 1)
                        if t:
                            act.wait_ge(sims_used, t)
                        nc.scalar.activation(b["sims"][:, :, :], pair_ps[:, :, :], ACT.Copy).then_inc(sims_copied, 1)
                    elif kind == "search" and h == RHEADS:
                        weight = b["weight_next"][:, t, :, :]
                        act.wait_ge(shifted, t + 1)
                        nc.scalar.activation(weight, weight, ACT.Exp).then_inc(exps_ready, 1)
                    elif kind == "dots":
                        act.wait_ge(dot_ready, PICKS * t + TOP * (h + 1))
                        own = slice(TOP * h, TOP * (h + 1))
                        nc.scalar.activation(b["act"][:, t, own], b["dots"][:, t, own], ACT.Silu).then_inc(dots_active, 1)
                    elif kind == "mix":
                        k = RHEADS * t + h
                        act.wait_ge(weighted, k + 1)
                        if k >= 2:
                            act.wait_ge(summed, k - 1)
                        for n in range(TOP):
                            nc.scalar.activation(b["diagonal"][:, k % 2, n, :], chip.c(C_ID), ACT.Copy,
                                                 scale=b["act"][:, t, TOP * h + n:TOP * h + n + 1]).then_inc(diagonal_ready, 1)

            @block.vector
            def _(dve):
                then = in_order(dve, dve_step)
                tt, ts, copy = nc.vector.tensor_tensor, nc.vector.tensor_scalar, nc.vector.tensor_copy
                if current:
                    copy(b["pick_now"][:, :, :], b["pick_next"][:, :, :]).then_inc(taken, 1)
                    copy(b["weight_now"][:, :, :, :], b["weight_next"][:, :, :, :]).then_inc(taken, 1)
                    for n in range(rc):
                        dve.wait_ge(gate_ready, n + 1)
                        tt(b["hidden"][:, n, :], b["gate"][:, n % 2, :], pair_ps[:, 1, :], ALU.mult).then_inc(hidden_ready, 1)
                    dve.wait_ge(taken, 3)

                def best_keys(t, s):
                    dve.wait_ge(sims_copied, t + 1)
                    for h in range(RHEADS):
                        own = b["sims"][:, s, h * KEYS:(h + 1) * KEYS]
                        then(nc.vector.max(b["best"][:, s, h, :], own))
                        last = nc.vector.max_index(b["best_at"][:, s, h, :], b["best"][:, s, h, :], own)
                        if (s, h) != (SIDES - 1, RHEADS - 1):
                            then(last)
                    if s == SIDES - 1:
                        last.then_inc(sims_used, 1)
                        dve.wait_ge(sims_used, t + 1)

                def best_pairs():
                    best, at_f = b["best"], b["at_f"]
                    then(copy(at_f[:, :, :, :], b["best_at"][:, :, :, :]))
                    then(ts(at_f[:, 0, :, :], at_f[:, 0, :, :], float(KEYS), None, ALU.mult))
                    for h in range(RHEADS):
                        second = lambda v: v[:, 1, h, :].rearrange("p (o k) -> p o k", o=1).to_broadcast((P, TOP, TOP))
                        mine = lambda v: v[:, 0, h, :].rearrange("p (k o) -> p k o", o=1).to_broadcast((P, TOP, TOP))
                        then(tt(b["sums"][:, h, :, :], mine(best), second(best), ALU.add))
                        then(tt(b["codes"][:, h, :, :], mine(at_f), second(at_f), ALU.add))
                    for h in range(RHEADS):
                        flat = b["sums"][:, h, :, :].rearrange("p a b -> p (a b)")
                        then(nc.vector.max(b["score"][:, h, :], flat))
                        then(nc.vector.max_index(b["pos"][:, h, :], b["score"][:, h, :], flat))
                    then(copy(b["pos_f"][:, :, :], b["pos"][:, :, :]))

                def picked(t):
                    hot = b["hot"][:, :, :]
                    for h in range(RHEADS):
                        wide = b["pos_f"][:, h, :].rearrange("p (k o) -> p k o", o=1).to_broadcast((P, TOP, TOP * TOP))
                        iota = chip.c(C_IOTA, TOP * TOP).rearrange("p (o n) -> p o n", o=1).to_broadcast((P, TOP, TOP * TOP))
                        flat = b["codes"][:, h, :, :].rearrange("p a b -> p (a b)").rearrange("p (o n) -> p o n", o=1).to_broadcast((P, TOP, TOP * TOP))
                        then(tt(hot, wide, iota, ALU.is_equal))
                        then(tt(hot, hot, flat, ALU.mult))
                        then(nc.vector.reduce_sum(b["code"][:, h, :], hot, AX.X))
                    then(ts(b["code"][:, :, :], b["code"][:, :, :], float(EMBEDS - 1), None, ALU.min))
                    then(copy(b["pick_next"][:, t, :], b["code"][:, :, :].rearrange("p h k -> p (h k)")))
                    top = b["score"][:, :, 0:1].to_broadcast((P, RHEADS, TOP))
                    tt(b["weight_next"][:, t, :, :], b["score"][:, :, :], top, ALU.subtract).then_inc(shifted, 1)
                    dve.wait_ge(shifted, t + 1)

                def weights(t):
                    weight, total = b["weight_next"][:, t, :, :], b["total"][:, :]
                    dve.wait_ge(exps_ready, t + 1)
                    then(nc.vector.reduce_sum(total, weight, AX.X))
                    then(nc.vector.reciprocal(total, total))
                    then(tt(weight, weight, total.rearrange("p (h o) -> p h o", o=1).to_broadcast((P, RHEADS, TOP)), ALU.mult))

                for kind, t, h in order:
                    if kind == "search":
                        if h < SIDES:
                            if h == 1 and t:
                                weights(t - 1)
                            best_keys(t, h)
                        elif h == 2:
                            best_pairs()
                        elif h == 3:
                            picked(t)
                    elif kind == "dots":
                        for n in range(TOP * h, TOP * (h + 1)):
                            k = PICKS * t + n
                            dve.wait_ge(arrived[n], 16 * per * now + 16 * (t + 1))
                            if k >= 2:
                                dve.wait_ge(dot_ready, k - 1)
                            nc.vector.tensor_tensor_reduce(b["scratch"][:, k % 2, :], b["got"][:, n, 0:DIM], b["rows_now"][:, t, :], 1.0, 0.0, ALU.mult, ALU.add,
                                                           b["dots"][:, t, n:n + 1]).then_inc(dot_ready, 1)
                    elif kind == "mix":
                        own = slice(TOP * h, TOP * (h + 1))
                        dve.wait_ge(dots_active, RHEADS * t + h + 1)
                        tt(b["act"][:, t, own], b["act"][:, t, own], b["weight_now"][:, t, h, :], ALU.mult).then_inc(weighted, 1)
                if ahead:
                    weights(per - 1)


def rope_tables():
    import numpy as np
    f = np.float32
    half = np.arange(0, WIDE, 2, dtype=f)
    inv_freq = (f(1.0) / f(10000.0) ** (half / f(WIDE))).astype(f)
    t = np.arange(SEQ, dtype=f)
    freqs = (t[:, None] * inv_freq[None, :]).astype(f)
    base = ((half + f(0.4 * WIDE)) / f(1.4 * WIDE)).astype(f)
    power = ((t - SEQ // 2) / f(P // 2)).astype(f)
    scale = (base[None, :] ** power[:, None]).astype(f)
    twice = lambda v: np.concatenate([v, v], axis=-1)
    sign = np.where(np.arange(WIDE) < WIDE // 2, f(-1), f(1))
    out = np.zeros((2, SEQ, 2, WIDE), f)
    cos, sin, scale = twice(np.cos(freqs)), twice(np.sin(freqs)) * sign, twice(scale)
    out[0, :, 0], out[0, :, 1] = cos * scale, cos / scale
    out[1, :, 0], out[1, :, 1] = sin * scale, sin / scale
    return np.ascontiguousarray(out.reshape(2, TILES, P, 2, WIDE).transpose(2, 0, 1, 3, 4))


def layout_more(a, io, cols):
    import numpy as np
    f = np.float32
    io["L0_ffn_wg"] = a["L0_ffn_wg"]
    io["L0_ffn_w1"] = a["L0_ffn_w_gate"].reshape(EXPERTS * DIM, EXPERT_INNER)
    io["L0_ffn_w2"] = a["L0_ffn_w_down"].reshape(EXPERTS * EXPERT_INNER, DIM)
    io["rope"] = rope_tables()
    io["L1_ffn_wqkv"] = a["L1_ffn_wqkv"].reshape(DEPTH * DIM, 3 * INNER)
    io["L1_ffn_wo"] = a["L1_ffn_wo"].reshape(DEPTH * INNER, DIM)
    io["L1_ffn_scales"] = np.concatenate([a["L1_ffn_q_scale"], a["L1_ffn_k_scale"]], axis=1)
    w1, b1 = np.zeros((DEPTH, DIM, 2, HC * P), f), np.zeros((DEPTH, 2, HC * P), f)
    w1[..., :HIDDEN] = a["L1_ffn_w1"].reshape(DEPTH, DIM, 2, HIDDEN)
    b1[..., :HIDDEN] = a["L1_ffn_b1"].reshape(DEPTH, 2, HIDDEN)
    w2 = np.zeros((DEPTH, HC * P, DIM), f)
    w2[:, :HIDDEN] = a["L1_ffn_w2"]
    io["L1_ffn_w1"], io["L1_ffn_w2"] = w1.reshape(DEPTH * DIM, 2 * HC * P), w2.reshape(DEPTH * HC * P, DIM)
    io["L1_ffn_b1"] = np.concatenate([cols(b1[n].ravel()) for n in range(DEPTH)])
    io["L1_ffn_b2"] = np.concatenate([cols(a["L1_ffn_b2"][n]) for n in range(DEPTH)])
    io["L1_ffn_ln"] = np.concatenate([np.concatenate([cols(a["L1_ffn_ln_g"][n]), cols(a["L1_ffn_ln_b"][n])], axis=1) for n in range(DEPTH)])
    io["L2_attn_win"] = np.ascontiguousarray(a["L2_attn_in_proj_w"].T)
    io["L2_attn_wout"] = np.ascontiguousarray(a["L2_attn_out_proj_w"].T)
    io["L2_attn_wx"] = np.ascontiguousarray(a["L2_attn_x_proj_w"].T)
    io["L2_attn_wdt"] = np.ascontiguousarray(a["L2_attn_dt_proj_w"].T)
    io["L2_attn_conv"] = a["L2_attn_conv_w"].reshape(-1, TAPS)
    io["L2_attn_vec"] = np.ascontiguousarray(np.stack([cols(a["L2_attn_" + n]) for n in ("conv_b", "dt_proj_b", "D")], axis=1))
    io["L2_attn_norm"] = cols(a["L2_attn_norm_w"])
    io["L2_attn_alog"] = a["L2_attn_A_log"]
    pick = np.zeros((2 * STATES, 2 * STATES, P), f)
    pick[np.arange(2 * STATES), np.arange(2 * STATES)] = 1.0
    io["pick"] = pick.reshape(2 * STATES, -1)
    io["L3_ffn_wq"] = np.ascontiguousarray(a["L3_ffn_w_queries"].T)
    keys = np.zeros((RHEADS, RDIM, SIDES, RHEADS, KEYS), f)
    for h in range(RHEADS):
        keys[h, :, :, h, :] = a["L3_ffn_keys"][h].transpose(2, 1, 0)
    io["L3_ffn_keys"] = keys.reshape(P, SIDES, RHEADS * KEYS)
    io["L3_ffn_tables"] = np.concatenate([a["L3_ffn_down_embed"], a["L3_ffn_up_embed"]], axis=1)
    io["L3_ffn_wg"], io["L3_ffn_wu"], io["L3_ffn_wd"] = (np.ascontiguousarray(a["L3_ffn_w_" + n].T) for n in ("gate", "up", "down"))


LAYERS = [quantised_attention, cross_attention, expert_ffn, normed_attention, context_mlp, local_transformer,
          state_space, concat_context, spiking_ffn, linear_attention, causal_attention, retrieval_ffn]


def decoder(nc, io, out, layers):
    with ExitStack() as ctx:
        chip = Chip(nc, ctx, io)
        chip.ctx_t = ctx.enter_context(sbuf(nc, "context", [P, FC, BATCH * CTX], F32))
        load(nc, [(chip.xt[:, :, :], io["x"].rearrange("(c p) t -> p c t", p=P)), (chip.const[:, :], io["constants"]),
                  (chip.ctx_t[:, :, :], io["ctx_t"].rearrange("(c p) t -> p c t", p=P)), (chip.eps[:, :], io["epsilons"])])
        with step(nc, "copied") as (block, copied):
            @block.vector
            def _(dve):
                for dst, src in ((chip.id_bf, C_ID), (chip.far_t, C_FART), (chip.far_n, C_FARN)):
                    nc.vector.tensor_copy(dst[:, :], chip.c(src)).then_inc(copied, 1)
                dve.wait_ge(copied, 3)
        for layer in layers:
            layer(chip)
        with step(nc, "stored") as (block, stored):
            @block.sync
            def _(sp):
                sp.dma_start(out.rearrange("(c p) t -> p c t", p=P), chip.xt[:, :, :]).then_inc(stored, 16)
                sp.wait_ge(stored, 16)


def constants():
    import numpy as np
    row, col = np.arange(P)[:, None], np.arange(P)[None, :]
    c = np.zeros((P, C_END), np.float32)
    c[:, C_ID:C_ID + P] = row == col
    c[:, C_MEAN:C_MEAN + P] = 1.0 / DIM
    c[:, C_ONES:C_ONES + P] = 1.0
    c[:, C_HEADMEAN:C_HEADMEAN + P] = (row // HEAD == col // HEAD) / HEAD
    c[:, C_DEN:C_DEN + P] = (row // SLOT == col // SLOT) & (row % SLOT == HEAD)
    c[:, C_FART:C_FART + P] = np.where(row > col, FAR, 0.0)
    c[:, C_FARN:C_FARN + P] = np.where(col > row, FAR, 0.0)
    c[:, C_KEEPT:C_KEEPT + P] = row <= col
    c[:, C_BEFORE:C_BEFORE + P] = row < col
    c[:, C_BAND:C_BAND + P] = np.where(col < row, FAR, 0.0)
    c[:, C_SELF:C_SELF + P] = np.where(col > row, FAR, 0.0)
    c[:, C_IOTA:C_IOTA + P] = col
    c[:, C_SLOTS:C_SLOTS + P] = row // SLOT == col // SLOT
    c[:, C_ROWS] = np.arange(P) % SLOT < HEAD
    c[STACK:STACK + PARTS, C_PARTROW:C_PARTROW + PARTS] = np.eye(PARTS)
    return c


def layout(a):
    import numpy as np
    f = np.float32
    cols = lambda v: np.ascontiguousarray(v.reshape(-1, P).T)

    def pad_rows(w):
        out = np.zeros((HEADS, SLOT, w.shape[1]), f)
        out[:, :HEAD] = w.reshape(HEADS, HEAD, w.shape[1])
        return out.reshape(PADDED, w.shape[1])

    none = np.zeros(DIM, f)
    io = {"x": np.ascontiguousarray(a["x"].reshape(TOKENS, DIM).T), "constants": constants(),
          "ctx_t": np.ascontiguousarray(a["ctx_1024"].reshape(-1, DIM).T), "ctx": a["ctx_1024"].reshape(-1, DIM),
          "epsilons": np.tile(np.array([1e-5, 1e-6, 1.0, 0.0], f), (P, 1))}
    qk = lambda bq, bk: np.ascontiguousarray(np.stack([cols(bq), cols(bk)], axis=1))
    io["L0_attn_w"] = np.ascontiguousarray(a["L0_attn_W_qkv"].reshape(3, DIM, DIM).transpose(0, 2, 1))
    bqkv = a["L0_attn_b_qkv"].reshape(3, DIM)
    io["L0_attn_b"], io["L0_attn_vb"] = qk(bqkv[0], bqkv[1]), bqkv[2:3]
    io["L0_attn_wo"] = pad_rows(a["L0_attn_W_proj"].T)
    io["L0_attn_bo"] = cols(a["L0_attn_b_proj"])
    io["L0_attn_ws"] = np.stack([a["L0_attn_s_w_qkv"], a["L0_attn_zp_w_qkv"]])
    io["L0_attn_ps"] = np.stack([a["L0_attn_s_w_proj"], a["L0_attn_zp_w_proj"]])
    io["L0_attn_scalars"] = np.stack([a["L0_attn_" + n] for n in (
        "s_act_qkv", "zp_act_qkv", "s_attn", "zp_attn", "s_act_proj", "zp_act_proj")]).reshape(1, 6)
    io["L0_xattn_w"] = np.stack([a["L0_xattn_W" + n].T for n in "qkv"])
    io["L0_xattn_b"] = qk(none, none)
    io["L0_xattn_wo"] = pad_rows(a["L0_xattn_Wo"].T)
    io["L0_xattn_bo"] = cols(none)
    io["key_bias"] = a["fside_BxS2_0"].reshape(1, -1)
    io["L1_attn_w"] = np.stack([a["L1_attn_W" + n] for n in "qkv"])
    io["L1_attn_b"], io["L1_attn_vb"] = qk(a["L1_attn_bq"], a["L1_attn_bk"]), a["L1_attn_bv"].reshape(1, DIM)
    norm = np.stack([np.stack([np.tile(a[f"L1_attn_{n}_{s}"], HALF_HEADS) for s in ("scale", "bias")], axis=1) for n in "qk"], axis=1)
    io["L1_attn_norm"] = np.ascontiguousarray(norm)
    io["L1_attn_norm_v"] = np.concatenate([a["L1_attn_v_scale"], a["L1_attn_v_bias"]]).reshape(1, -1)
    io["L1_attn_wo"] = pad_rows(a["L1_attn_Wo"])
    io["L1_attn_bo"] = cols(a["L1_attn_bo"])
    io["L2_xattn_w"] = np.ascontiguousarray(a["L2_xattn_W"].T)
    io["L2_xattn_b"] = cols(a["L2_xattn_b"])
    io["L2_ffn_w1"] = np.ascontiguousarray(a["L2_ffn_W_fc"].T)
    io["L2_ffn_w2"] = np.ascontiguousarray(a["L2_ffn_W_proj"].T)
    half = DIM // 4
    wkv = np.concatenate([a["L3_attn_Wk"], a["L3_attn_Wv"]], axis=1)
    io["L3_attn_wkv"] = np.ascontiguousarray(wkv)
    io["L3_attn_bkv"] = np.concatenate([a["L3_attn_bk"], a["L3_attn_bv"]]).reshape(P, 1)
    wc = np.zeros((P, P), f)
    wc[:half, :half] = wc[half:, half:] = a["L3_attn_Wc"]
    io["L3_attn_wc"] = wc
    def by_kv(w):
        out = np.zeros(w.shape[:-1] + (REPEAT, KV_HEADS, SLOT), f)
        out[..., :HEAD] = np.swapaxes(w.reshape(w.shape[:-1] + (KV_HEADS, REPEAT, HEAD)), -3, -2)
        return out.reshape(w.shape[:-1] + (REPEAT, P))

    io["L3_attn_wq"] = by_kv(a["L3_attn_Wq"])
    io["L3_attn_bq"] = np.ascontiguousarray(by_kv(a["L3_attn_bq"]).T)
    up = np.zeros((P, KV_HEADS, SLOT), f)
    up[:half, :, :HEAD] = a["L3_attn_We"].reshape(half, KV_HEADS, HEAD)
    io["L3_attn_wk"] = up.reshape(P, P)
    both = np.zeros((P, P), f)
    both[:half, :half] = both[half:, half:] = a["L3_attn_We"]
    io["L3_attn_wkv_up"] = both
    io["L3_attn_wo"] = np.ascontiguousarray(by_kv(np.ascontiguousarray(a["L3_attn_Wo"].T)).reshape(DIM, REPEAT * P).T)
    io["L3_attn_bo"] = cols(a["L3_attn_bo"])
    io["L3_attn_affine"] = np.ascontiguousarray(np.stack([cols(a["L3_attn_gamma"]), cols(a["L3_attn_beta"])], axis=1))
    wkv = a["L3_xattn_Wkv"]
    io["L3_xattn_w"] = np.stack([a["L3_xattn_Wq"], wkv[:, :DIM], wkv[:, DIM:]])
    io["L3_xattn_b"] = qk(none, none)
    io["L3_xattn_wo"] = pad_rows(a["L3_xattn_Wout"])
    io["L3_xattn_bo"] = cols(a["L3_xattn_bout"])
    layout_more(a, io, cols)
    return io


def kernel(**inputs):
    import numpy as np
    import concourse.bacc as bacc
    from concourse.bass_utils import run_bass_kernel_spmd

    arrays = layout({k: np.asarray(v) for k, v in inputs.items()})
    nc = bacc.Bacc("TRN2", target_bir_lowering=False, num_devices=1)
    io = {k: nc.dram_tensor("in_" + k, v.shape, mybir.dt.from_np(v.dtype), kind="ExternalInput").ap() for k, v in arrays.items()}
    out = nc.dram_tensor("out_t", (DIM, TOKENS), F32, kind="ExternalOutput").ap()
    decoder(nc, io, out, LAYERS)
    result = run_bass_kernel_spmd(nc, [{"in_" + k: v for k, v in arrays.items()}], core_ids=[0])
    return np.ascontiguousarray(result.results[0]["out_t"].T).reshape(BATCH, SEQ, DIM)
```

```python
from contextlib import ExitStack, contextmanager

import concourse.bass as bass
from concourse import mybir

F32 = mybir.dt.float32
BF16 = mybir.dt.bfloat16
U32 = mybir.dt.uint32
ALU = mybir.AluOpType
ACT = mybir.ActivationFunctionType
AX = mybir.AxisListType

P = 128
BATCH, SEQ, DIM = 4, 1024, 256
TOKENS = BATCH * SEQ
CTX = 77
FC = DIM // P
GROUP = 512
GROUPS = TOKENS // GROUP
HEADS, HEAD = 16, 16
SLOT = 32
PACK = P // SLOT
HGS = HEADS // PACK
PADDED = HEADS * SLOT
TILES = SEQ // P
FAR = -float(2 ** 60)
ROUND = float(1.5 * 2 ** 23)
QMAX = 255.0
C_ID, C_MEAN, C_ONES, C_HEADMEAN, C_DEN, C_FART, C_FARN, C_KEEPT, C_BEFORE = (P * n for n in range(9))
C_IOTA = 9 * P
C_SLOTS = C_IOTA + P
C_ROWS = C_SLOTS + P
C_PARTROW = C_ROWS + 1
C_END = C_PARTROW + 3


def sbuf(nc, name, shape, dtype):
    return nc.sbuf_tensor(name, shape, dtype, allow_name_mangling=True)


def banks(nc, name, shape, dtype):
    return nc.psum_tensor(name, shape, dtype, allow_name_mangling=True)


@contextmanager
def step(nc, names):
    with ExitStack() as ctx:
        sems = [ctx.enter_context(nc.semaphore(n)) for n in names.split()]
        with nc.Block() as block:
            yield (block, *sems)
        nums = sorted(s.num for s in sems)
        start = 0
        for n in range(len(nums)):
            if n + 1 == len(nums) or nums[n + 1] != nums[n] + 1:
                nc.sync.sem_clear(range(nums[start], nums[n] + 1))
                start = n + 1
        nc.all_engine_barrier(sem_only=True)


def in_order(eng, sem):
    count = [0]

    def then(instruction):
        count[0] += 1
        instruction.then_inc(sem, 1)
        eng.wait_ge(sem, count[0])

    return then


def load(nc, pairs):
    with step(nc, "loaded") as (block, loaded):
        @block.sync
        def _(sp):
            for dst, src in pairs:
                sp.dma_start(dst, src).then_inc(loaded, 16)
            sp.wait_ge(loaded, 16 * len(pairs))


class Chip:

    def __init__(self, nc, ctx, io):
        self.nc, self.io, self.ctx = nc, io, ctx
        self.xt = ctx.enter_context(sbuf(nc, "residual", [P, FC, TOKENS], F32))
        self.const = ctx.enter_context(sbuf(nc, "constants", [P, C_END], F32))
        self.id_bf, self.far_t, self.far_n = (ctx.enter_context(sbuf(nc, n, [P, P], BF16)) for n in ("identity_bf16", "far_t_bf16", "far_n_bf16"))
        self.eps = ctx.enter_context(sbuf(nc, "epsilons", [P, 4], F32))
        self.z = ctx.enter_context(sbuf(nc, "norm_sum", [P, 2, FC, GROUP], F32))
        self.sq = ctx.enter_context(sbuf(nc, "norm_squares", [P, 2, FC, GROUP], F32))
        self.root = ctx.enter_context(sbuf(nc, "norm_root", [P, 2, GROUP // P], F32))

    def keep_semaphore(self, name):
        return self.ctx.enter_context(self.nc.semaphore(name))

    def c(self, start, n=P):
        return self.const[:, start:start + n]


def add_norm(chip, toks, psum, product=None, ready=None, bias=None, affine=None, keeps=1.0, beside=None):
    nc, z, sq, root = chip.nc, chip.z, chip.sq, chip.root
    n, per = len(toks), GROUP // P
    y_ps = lambda g, c: psum[:, 4 * g + c, :]
    mean_ps = lambda g: psum[:, 4 * g + 2, :]
    rstd_ps = lambda g: psum[:, 4 * g + 3, :]
    rounds = 2 if affine else 1
    x = lambda g, c: chip.xt[:, c, toks[g]]
    with step(nc, "y_ready sum_ready mean_ready centred squares_ready var_ready root_ready inverse_ready rstd_ready dve_step beside_step") as (
            block, y_ready, sum_ready, mean_ready, centred, squares_ready, var_ready, root_ready, inverse_ready, rstd_ready, dve_step, beside_step):
        if beside:
            beside(block, beside_step)

        @block.tensor
        def _(pe):
            if product:
                weights, inputs = product
                chunks = weights.shape[1]
                for g in range(n):
                    for c in range(FC):
                        for k in range(chunks):
                            last = nc.tensor.matmul(y_ps(g, c), weights[:, k, c * P:(c + 1) * P], inputs(g, k),
                                                    start=(k == 0), stop=(k == chunks - 1))
                        last.then_inc(y_ready, 1)
            for r in range(rounds):
                for g in range(n):
                    pe.wait_ge(sum_ready, FC * (r * n + g + 1))
                    for c in range(FC):
                        last = nc.tensor.matmul(mean_ps(g), chip.c(C_MEAN), z[:, g, c, :], start=(c == 0), stop=(c == FC - 1))
                    last.then_inc(mean_ready, 1)
                for g in range(n):
                    pe.wait_ge(squares_ready, FC * (r * n + g + 1))
                    for t in range(per):
                        for c in range(FC):
                            last = nc.tensor.matmul(rstd_ps(g)[:, t:t + 1], sq[:, g, c, t * P:(t + 1) * P], chip.c(C_MEAN, 1),
                                                    start=(c == 0), stop=(c == FC - 1))
                    last.then_inc(var_ready, 1)
                for g in range(n):
                    pe.wait_ge(inverse_ready, r * n + g + 1)
                    for t in range(per):
                        last = nc.tensor.matmul(rstd_ps(g)[:, t * P:(t + 1) * P], root[:, g, t:t + 1].to_broadcast((P, P)),
                                                chip.c(C_ID), start=True, stop=True)
                    last.then_inc(rstd_ready, 1)

        @block.scalar
        def _(act):
            for r in range(rounds):
                for g in range(n):
                    for c in range(FC):
                        act.wait_ge(centred, FC * (r * n + g) + c + 1)
                        nc.scalar.activation(sq[:, g, c, :], z[:, g, c, :], ACT.Square).then_inc(squares_ready, 1)
                for g in range(n):
                    act.wait_ge(var_ready, r * n + g + 1)
                    nc.scalar.activation(root[:, g, :], rstd_ps(g)[:, 0:per], ACT.Sqrt, bias=chip.eps[:, 0:1]).then_inc(root_ready, 1)

        @block.vector
        def _(dve):
            then = in_order(dve, dve_step)
            for g in range(n):
                for c in range(FC):
                    if product:
                        dve.wait_ge(y_ready, FC * g + c + 1)
                    y = y_ps(g, c) if product else ready(g, c)
                    if keeps != 1.0:
                        nc.vector.scalar_tensor_tensor(out=z[:, g, c, :], in0=x(g, c), scalar=keeps, in1=y,
                                                       op0=ALU.mult, op1=ALU.add).then_inc(sum_ready, 1)
                    elif bias is None:
                        nc.vector.tensor_tensor(z[:, g, c, :], y, x(g, c), ALU.add).then_inc(sum_ready, 1)
                    else:
                        nc.vector.scalar_tensor_tensor(out=z[:, g, c, :], in0=y, scalar=bias[:, c:c + 1], in1=x(g, c),
                                                       op0=ALU.add, op1=ALU.add).then_inc(sum_ready, 1)
            for r in range(rounds):
                for g in range(n):
                    dve.wait_ge(mean_ready, r * n + g + 1)
                    for c in range(FC):
                        nc.vector.tensor_tensor(z[:, g, c, :], z[:, g, c, :], mean_ps(g), ALU.subtract).then_inc(centred, 1)
                for g in range(n):
                    dve.wait_ge(root_ready, r * n + g + 1)
                    nc.vector.reciprocal(root[:, g, :], root[:, g, :]).then_inc(inverse_ready, 1)
                for g in range(n):
                    dve.wait_ge(rstd_ready, r * n + g + 1)
                    for c in range(FC):
                        if r == rounds - 1:
                            nc.vector.tensor_tensor(x(g, c), z[:, g, c, :], rstd_ps(g), ALU.mult)
                        else:
                            scale, shift = affine
                            then(nc.vector.tensor_tensor(z[:, g, c, :], z[:, g, c, :], rstd_ps(g), ALU.mult))
                            then(nc.vector.tensor_scalar(z[:, g, c, :], z[:, g, c, :], scale[:, c:c + 1], shift[:, c:c + 1],
                                                         ALU.mult, ALU.add))
                            nc.vector.tensor_tensor(z[:, g, c, :], z[:, g, c, :], x(g, c), ALU.add).then_inc(sum_ready, 1)


def group_slice(g):
    return bass.ds(g * GROUP, GROUP)


def fake_quant(nc, then, tmp, src, scalars, out):
    inv, zero, scale = (scalars[:, n:n + 1] for n in range(3))
    then(nc.vector.tensor_scalar(tmp, src, inv, zero, ALU.mult, ALU.add))
    then(nc.vector.tensor_scalar(tmp, tmp, 0.0, QMAX, ALU.max, ALU.min))
    then(nc.vector.tensor_scalar(tmp, tmp, ROUND, ROUND, ALU.add, ALU.subtract))
    return nc.vector.tensor_scalar(out, tmp, zero, scale, ALU.subtract, ALU.mult)


PARTS = 3
PAIRS = [(0, 0), (0, 1), (0, 2), (1, 0), (1, 1), (2, 0)]
STACK = len(PAIRS) * HEAD
HALF_HEADS = P // HEAD
HALVES = SEQ // GROUP
PER_HALF = GROUP // P


def stack_parts(nc, sp, scratch, parts, stack, tokens, which, m, written, stacked, at):
    for p in range(PARTS):
        sp.dma_start(scratch[p, m * P:(m + 1) * P, 0:tokens], parts[:, p, :]).then_inc(written, 16)
    sp.wait_ge(written, at + 16 * PARTS)
    for n, pair in enumerate(PAIRS):
        sp.dma_start(stack[n * HEAD:(n + 1) * HEAD, m * HALF_HEADS:(m + 1) * HALF_HEADS, 0:tokens],
                     scratch[pair[which], m * P:(m + 1) * P, 0:tokens].rearrange("(h r) t -> r h t", r=HEAD)).then_inc(stacked, 16)


def split_attention(chip, mode, params, key_bias=None, norm=None, quant=None):
    nc, io = chip.nc, chip.io
    w, wo, b_qk, v_bias, bo = params
    quantised, normed, causal, cross = (mode == m for m in ("quant", "normed", "causal", "cross"))
    own, context, maxed = not cross, cross or causal, not quantised
    extra = PARTS if cross or quantised else 0
    max_row = STACK + extra
    rows = max_row + (PARTS if maxed else 0)
    scale = quant[:, 3:4] if quantised else HEAD ** -0.5
    sides = 2 if own else 1
    blocks = [(t, m) for m in range(2) for t in range(sides)]
    kinds = (1 if context else 0) + (HALVES if own else 0)

    def items(half):
        out = [(None, 0)] if context else []
        if own:
            tiles = PER_HALF * (half + 1) if causal else TILES
            out += [(kt, max(0, kt - PER_HALF * half) * P if causal else 0) for kt in range(tiles)]
        return out

    slots = [(g, half, kt, off) for g in range(HGS) for half in range(HALVES) for kt, off in items(half)]
    last_slot = {(g, half): n for n, (g, half, _, _) in enumerate(slots)}
    diagonal = lambda half, kt: causal and kt is not None and kt >= PER_HALF * half

    def first_pass(g):
        out = []
        for qt in range(TILES):
            if context:
                out.append((qt, None, None))
            if own:
                out += [(qt, i, j) for i in range(PACK) for j in range(1 + qt // PER_HALF if causal else HALVES)]
        return out

    ring_kinds = ("project", "vproj", "vars", "spread", "max", "turn", "sums", "normal")
    per_group = len(slots) // HGS

    def prepare(m, nx):
        out = [("stage", m, nx)] + ([("contexts", m, nx)] if context else [])
        for t in range(sides):
            out += [("project", m, nx, t, j) for j in range(HALVES)]
            out += [("squares", m, nx, t)] if normed else [("split", m, nx, t)]
        out += [("vproj", m, nx, j) for j in range(HALVES)] if own else []
        if normed:
            out += [("vars", m, nx, t) for t in range(sides)]
            out += [(kind, m, nx) for kind in ("vsquares", "vsum", "roots", "inverse", "wide")]
            for t in range(sides):
                out += [("spread", m, nx, t, j) for j in range(HALVES)] + [("split", m, nx, t)]
            out.append(("vaffine", m, nx))
        return out

    def maxima(g, nx, jobs):
        return [("max", g, nx) + job for job in jobs]

    def main_order(has_next):
        order, due = [], {}
        sums_after, normal_after, at_once = (2, 4, 2 if maxed else 1) if own else (1, 2, len(prepare(0, 0)))
        for n, (g, half, kt, off) in enumerate(slots):
            s = n % per_group
            if s == 0:
                ahead = prepare(1, 0) if g == 0 else prepare(0, 1) if has_next and g == HGS // 2 else []
            target, nx = ((g + 1) % HGS, (g + 1) // HGS)
            jobs = first_pass(target) if maxed and (not nx or has_next) else []
            spread = max(1, per_group - 3)
            share = jobs[len(jobs) * s // spread:len(jobs) * (s + 1) // spread] if s < spread else []
            take = lambda: [ahead.pop(0) for _ in range(min(at_once, len(ahead))) if s or cross]
            order += due.pop(n, [])
            order.append(("scores", n, 0))
            cuts = [len(share) // 5, 3 * len(share) // 5]
            order += take() + maxima(target, nx, share[:cuts[0]])
            order.append(("scores", n, 1))
            order += maxima(target, nx, share[cuts[0]:cuts[1]])
            if n:
                order.append(("values", n - 1))
                if last_slot[slots[n - 1][:2]] == n - 1:
                    order.append(("raw",) + slots[n - 1][:2])
                    due.setdefault(n + sums_after, []).append(("sums",) + slots[n - 1][:2])
                    due.setdefault(n + normal_after, []).append(("normal",) + slots[n - 1][:2])
            order += take() + maxima(target, nx, share[cuts[1]:])
            if jobs and s == min(spread, per_group - 1):
                order.append(("turn", target, nx))
        for n in sorted(due):
            order += due[n]
        return order + [("values", len(slots) - 1), ("raw",) + slots[-1][:2], ("sums",) + slots[-1][:2], ("normal",) + slots[-1][:2]]

    first_order = prepare(0, 1) + (maxima(0, 1, first_pass(0)) + [("turn", 0, 1)] if maxed else [])

    with ExitStack() as ctx:
        sb = lambda name, shape, dt=F32: ctx.enter_context(sbuf(nc, name, shape, dt))
        q_stack = sb("query_stack", [rows, HEADS, SEQ], BF16)
        ot = sb("heads_out", [P, HGS, SEQ])
        probs = sb("probs", [P, 2, 2, 2, GROUP])
        parts = sb("parts", [P, PARTS, SEQ], BF16)
        raws = HALVES if cross else 1
        raw_out = sb("raw_out", [P, raws, GROUP])
        inverse = sb("inverse", [P, raws, PER_HALF * PACK])
        wide_inverse = sb("wide_inverse", [P, raws, PER_HALF * PACK, SLOT])
        stage = chip.z
        room = chip.sq[:, :, :, :].rearrange("p n c t -> p n (c t)")
        features = sb("features", [P, sides, SEQ])[:, :, :] if normed else room
        squares = wide_root = room
        scratch = [nc.dram_tensor(f"{mode}_parts_{t}", (PARTS, DIM, SEQ), BF16).ap() for t in range(2)]
        if own:
            k_stack = sb("key_stack", [rows, HEADS, SEQ], BF16)
            v = sb("head_values", [P, TILES, HEADS, SLOT])
        if maxed:
            row_max = sb("row_max", [P, PACK, TILES, kinds])
            top = sb("top", [P, PACK, TILES])
            top_parts = sb("top_parts", [P, PARTS, PACK, TILES], BF16)
            top_rows = sb("top_rows", [PARTS * PACK * TILES, P], BF16)
            top_dram = nc.dram_tensor(f"{mode}_top", (PARTS, PACK, SEQ), BF16).ap()
        if context:
            keys_c = sb("context_keys", [rows, HEADS, BATCH * CTX], BF16) if cross else None
            context_parts = nc.dram_tensor(f"{mode}_context_parts", (PARTS, DIM, BATCH * CTX), BF16).ap()
            keys_now = sb("context_keys_now", [rows, HEADS, CTX], BF16)
            values_c = sb("context_values", [CTX, BATCH, HEADS, HEAD])
            values_now = sb("context_values_now", [CTX, HEADS, SLOT])
        if normed:
            head_root = sb("head_root", [P, sides, TILES, HALF_HEADS])
            value_root = sb("value_root", [P, TILES, HALF_HEADS])

        with step(nc, "set set_by_pool dve_step") as (block, set_, set_by_pool, dve_step):
            fills = [(q_stack[STACK:rows, :, :], 1.0)] if extra else []
            fills += [(k_stack[STACK:rows, :, :], 1.0), (v[:, :, :, HEAD + 1:], 0.0), (v[:, :, :, HEAD:HEAD + 1], 1.0)] if own else []
            fills += [((keys_c if cross else keys_now)[STACK:rows, :, :], 1.0), (values_now[:, :, HEAD + 1:], 0.0),
                      (values_now[:, :, HEAD:HEAD + 1], 1.0)] if context else []
            fills += [(row_max[:, :, :, :], FAR)] if maxed else []

            @block.gpsimd
            def _(pool):
                for n, (buffer, value) in enumerate(fills[0::2]):
                    if n:
                        pool.wait_ge(set_by_pool, n)
                    nc.gpsimd.memset(buffer, value).then_inc(set_by_pool, 1)

            @block.vector
            def _(dve):
                for buffer, value in fills[1::2]:
                    nc.vector.memset(buffer, value).then_inc(set_, 1)
                if fills[1::2]:
                    dve.wait_ge(set_, len(fills[1::2]))
                dve.wait_ge(set_by_pool, len(fills[0::2]))
                if quantised:
                    then = in_order(dve, dve_step)
                    zero, zero_bf, row = inverse[:, 0, 0:1], parts[:, 0, 0:1], inverse[:, 0, 1:2]
                    then(nc.vector.tensor_copy(zero, quant[:, 2:3]))
                    then(nc.vector.memset(row, 0.0))
                    for p in range(PARTS):
                        then(nc.vector.tensor_copy(zero_bf, zero))
                        then(nc.vector.tensor_tensor(zero, zero, zero_bf, ALU.subtract))
                        then(nc.vector.scalar_tensor_tensor(out=row, in0=zero_bf, scalar=chip.c(C_PARTROW + p, 1), in1=row,
                                                            op0=ALU.mult, op1=ALU.add))
                    then(nc.vector.tensor_scalar(k_stack[STACK:rows, :, :], k_stack[STACK:rows, :, :], row[STACK:rows, :], None, ALU.mult))
        if context:
            context_stacks(chip, mode, params, key_bias, ot, parts, context_parts, keys_c, values_c)

        def attend(order, b, b_next, s_ps, r_ps, o_ps):
            place = {}
            for step_ in order:
                place[step_] = sum(1 for other in place if other[0] == step_[0])
            ring = {step_: r for r, step_ in enumerate(s for s in order if s[0] in ring_kinds)}
            turns = place
            prepared = [(s[1], s[2]) for s in order if s[0] == "project" and s[3:] == (0, 0)]
            batch_of = lambda nx: b_next if nx else b
            quick = b is None or cross
            raw_index = lambda step_: HALVES * step_[1] + step_[2]
            heads_of = lambda m: slice(m * HALF_HEADS, (m + 1) * HALF_HEADS)
            old_slots = HGS // 2 * per_group
            with step(nc, "staged now_ready keys_loaded squares_ready v_squares v_summed roots_ready inverse_ready root_wide affine_ready v_scaled v_done "
                          "parts_ready written stacked_0 stacked_1 ring_ready ring_read top_ready top_written top_loaded scores_ready scores_raw "
                          "scores_read probs_ready outputs_added raw_ready wide_ready dve_step pool_step") as (
                    block, staged, now_ready, keys_loaded, squares_ready, v_squares, v_summed, roots_ready, inverse_ready, root_wide, affine_ready, v_scaled, v_done,
                    parts_ready, written, stacked_0, stacked_1, ring_ready, ring_read, top_ready, top_written, top_loaded, scores_ready, scores_raw,
                    scores_read, probs_ready, outputs_added, raw_ready, wide_ready, dve_step, pool_step):
                stacked = (stacked_0, stacked_1)
                x = lambda c, j: stage[:, j, c, :]
                k_of = lambda step_: prepared.index((step_[1], step_[2]))
                last_read = [max(r for s, r in ring.items() if s[0] in ("project", "vproj") and (s[1], s[2]) == which) for which in prepared]

                def split(eng, ops, then, step_):
                    _, m, nx, t = step_
                    count = sides * k_of(step_) + t
                    if normed:
                        eng.wait_ge(affine_ready, HALVES * (count + 1))
                    else:
                        eng.wait_ge(ring_read, ring[("project", m, nx, t, HALVES - 1)] + 1)
                    if count:
                        eng.wait_ge(written, 16 * PARTS * count)
                    own_f = features[:, t, :]
                    then(ops.tensor_copy(parts[:, 0, :], own_f))
                    then(ops.tensor_tensor(own_f, own_f, parts[:, 0, :], ALU.subtract))
                    then(ops.tensor_copy(parts[:, 1, :], own_f))
                    ops.tensor_tensor(parts[:, 2, :], own_f, parts[:, 1, :], ALU.subtract).then_inc(parts_ready, 1)

                def stage_free(eng, step_):
                    if k_of(step_):
                        eng.wait_ge(ring_ready, last_read[k_of(step_) - 1] + 1)

                @block.tensor
                def _(pe):
                    def ring_bank(step_):
                        r = ring[step_]
                        if r >= 2:
                            pe.wait_ge(ring_read, r - 1)
                        return r_ps[:, r % 2, :]

                    def stacks_ready(g, nx):
                        m = g * PACK // HALF_HEADS
                        if (m, nx) in prepared:
                            pe.wait_ge(stacked[m], 16 * len(PAIRS) * sides)
                            if context:
                                k = prepared.index((m, nx)) + 1
                                pe.wait_ge(now_ready, (2 if cross else 1) * k)
                                if not cross:
                                    pe.wait_ge(keys_loaded, 16 * len(PAIRS) * k)

                    for step_ in order:
                        kind = step_[0]
                        if kind == "project":
                            _, m, nx, t, j = step_
                            out = ring_bank(step_)
                            pe.wait_ge(staged, k_of(step_) + 1)
                            for c in range(FC):
                                last = nc.tensor.matmul(out, w[:, t, c, m * P:(m + 1) * P], x(c, j), start=(c == 0), stop=(c == FC - 1))
                            last.then_inc(ring_ready, 1)
                        elif kind == "vproj":
                            _, m, nx, j = step_
                            out = ring_bank(step_)
                            for i in range(PER_HALF):
                                for c in range(FC):
                                    last = nc.tensor.matmul(out[:, i * P:(i + 1) * P], x(c, j)[:, i * P:(i + 1) * P], w[:, 2, c, m * P:(m + 1) * P],
                                                            start=(c == 0), stop=(c == FC - 1))
                            last.then_inc(ring_ready, 1)
                        elif kind == "vars":
                            _, m, nx, t = step_
                            out = ring_bank(step_)
                            pe.wait_ge(squares_ready, place[("squares", m, nx, t)] + 1)
                            for kt in range(TILES):
                                last = nc.tensor.matmul(out[:, kt * HALF_HEADS:(kt + 1) * HALF_HEADS], squares[:, t, kt * P:(kt + 1) * P],
                                                        chip.c(C_HEADMEAN)[:, 0:P:HEAD], start=True, stop=True)
                            last.then_inc(ring_ready, 1)
                        elif kind == "spread":
                            _, m, nx, t, j = step_
                            out = ring_bank(step_)
                            pe.wait_ge(root_wide, sides * k_of(step_) + t + 1)
                            for i in range(PER_HALF):
                                last = nc.tensor.matmul(out[:, i * P:(i + 1) * P], wide_root[:, t, (j * PER_HALF + i) * P:(j * PER_HALF + i + 1) * P], chip.c(C_ID), start=True, stop=True)
                            last.then_inc(ring_ready, 1)
                        elif kind == "max":
                            _, g, nx, qt, i, j = step_
                            if step_[3:] == first_pass(g)[0]:
                                stacks_ready(g, nx)
                            out = ring_bank(step_)
                            heads = range(PACK) if i is None else [i]
                            for i_ in heads:
                                h = PACK * g + i_
                                lhs = q_stack[0:max_row, h, qt * P:(qt + 1) * P]
                                if i is None:
                                    last = nc.tensor.matmul(out[:, i_ * CTX:(i_ + 1) * CTX], lhs, keys_now[0:max_row, h, :], start=True, stop=True)
                                else:
                                    cols = min(GROUP, (qt + 1) * P - j * GROUP) if causal else GROUP
                                    edge = causal and j == qt // PER_HALF
                                    last = nc.tensor.matmul(out[:, 0:cols], lhs, k_stack[0:max_row, h, j * GROUP:j * GROUP + cols],
                                                            start=True, stop=not edge)
                                    if edge:
                                        last = nc.tensor.matmul(out[:, cols - P:cols], chip.id_bf[:, :], chip.far_n[:, :], start=False, stop=True)
                            last.then_inc(ring_ready, 1)
                        elif kind == "turn":
                            out = ring_bank(step_)
                            pe.wait_ge(top_ready, turns[step_] + 1)
                            nc.tensor.matmul(out[0:PARTS * PACK * TILES, 0:P], top_parts[:, :, :, :].rearrange("p a i q -> p (a i q)"),
                                             chip.id_bf[:, :], start=True, stop=True).then_inc(ring_ready, 1)
                        elif kind == "scores":
                            _, n, pair = step_
                            g, half, kt, off = slots[n]
                            e = 2 * n + pair
                            if n % per_group == 0 and pair == 0:
                                stacks_ready(g, 0)
                                if ("turn", g, 0) in turns:
                                    pe.wait_ge(top_loaded, 16 * (turns[("turn", g, 0)] + 1))
                            if e >= 2:
                                pe.wait_ge(scores_raw if quantised else probs_ready, e - 1)
                            for i in range(2):
                                h = PACK * g + 2 * pair + i
                                k_rows = CTX if kt is None else P
                                keys = keys_now[0:rows, h, :] if kt is None else k_stack[0:rows, h, kt * P:(kt + 1) * P]
                                out = s_ps[0:k_rows, 2 * (e % 2) + i, :]
                                edge = diagonal(half, kt)
                                last = nc.tensor.matmul(out[:, off:GROUP], keys, q_stack[0:rows, h, half * GROUP + off:(half + 1) * GROUP],
                                                        start=True, stop=not edge)
                                if edge:
                                    last = nc.tensor.matmul(out[:, off:off + P], chip.id_bf[:, :], chip.far_t[:, :], start=False, stop=True)
                            last.then_inc(scores_ready, 1)
                        elif kind == "values":
                            n = step_[1]
                            g, half, kt, off = slots[n]
                            k_rows = CTX if kt is None else P
                            first, final = (kt, off) == items(half)[0], (kt, off) == items(half)[-1]
                            pe.wait_ge(probs_ready, 2 * n + 2)
                            if own and n == old_slots:
                                pe.wait_ge(ring_read, ring[("vproj", 1, 0, HALVES - 1)] + 1)
                                if normed:
                                    pe.wait_ge(v_done, place[("vaffine", 1, 0)] + 1)
                            if first and g:
                                pe.wait_ge(raw_ready, HALVES * (g - 1) + half + 1)
                            for i in range(PACK):
                                h = PACK * g + i
                                vals = values_now[:, h, :] if kt is None else v[:, kt, h, :]
                                last = nc.tensor.matmul(o_ps[SLOT * i:SLOT * (i + 1), half, off:GROUP], vals,
                                                        probs[0:k_rows, n % 2, i // 2, i % 2, off:GROUP], start=first, stop=final)
                            last.then_inc(outputs_added, 1)
                        elif kind == "sums":
                            _, g, half = step_
                            out = ring_bank(step_)
                            pe.wait_ge(raw_ready, HALVES * g + half + 1)
                            for t in range(PER_HALF):
                                last = nc.tensor.matmul(out[:, t * PACK:(t + 1) * PACK], raw_out[:, half % raws, t * P:(t + 1) * P],
                                                        chip.c(C_DEN)[:, 0:P:SLOT], start=True, stop=True)
                            last.then_inc(ring_ready, 1)
                        elif kind == "normal":
                            _, g, half = step_
                            out = ring_bank(step_)
                            pe.wait_ge(wide_ready, HALVES * g + half + 1)
                            for t in range(PER_HALF):
                                spread = wide_inverse[:, half % raws, t * PACK:(t + 1) * PACK, :].rearrange("p h r -> p (h r)")
                                last = nc.tensor.matmul(out[:, t * P:(t + 1) * P], spread, chip.c(C_ID), start=True, stop=True)
                            last.then_inc(ring_ready, 1)

                @block.scalar
                def _(act):
                    for step_ in order:
                        kind = step_[0]
                        if kind == "stage" and not quantised:
                            _, m, nx = step_
                            stage_free(act, step_)
                            now = chip.xt[:, :, bass.ds(batch_of(nx) * SEQ, SEQ)].rearrange("p c (j t) -> p j c t", j=HALVES)
                            nc.scalar.activation(stage[:, :, :, :], now, ACT.Copy).then_inc(staged, 1)
                        elif kind == "squares":
                            _, m, nx, t = step_
                            act.wait_ge(ring_read, ring[("project", m, nx, t, HALVES - 1)] + 1)
                            if k_of(step_):
                                before = prepared[k_of(step_) - 1]
                                act.wait_ge(ring_ready, ring[("spread",) + before + (sides - 1, HALVES - 1)] + 1)
                            nc.scalar.activation(squares[:, t, :], features[:, t, :], ACT.Square).then_inc(squares_ready, 1)
                        elif kind == "vsquares":
                            _, m, nx = step_
                            act.wait_ge(ring_read, ring[("vproj", m, nx, HALVES - 1)] + 1)
                            act.wait_ge(ring_ready, ring[("vars", m, nx, 0)] + 1)
                            nc.scalar.activation(squares[:, 0, :].rearrange("p (t h d) -> p t h d", t=TILES, d=HEAD), v[:, :, heads_of(m), 0:HEAD],
                                                 ACT.Square).then_inc(v_squares, 1)
                        elif kind == "roots":
                            _, m, nx = step_
                            act.wait_ge(ring_read, ring[("vars", m, nx, sides - 1)] + 1)
                            act.wait_ge(v_summed, k_of(step_) + 1)
                            nc.scalar.activation(head_root[:, :, :, :], head_root[:, :, :, :], ACT.Sqrt, bias=chip.eps[:, 1:2]).then_inc(roots_ready, 1)
                            nc.scalar.activation(value_root[:, :, :], value_root[:, :, :], ACT.Sqrt, bias=chip.eps[:, 1:2], scale=1.0 / HEAD).then_inc(roots_ready, 1)
                        elif kind == "wide":
                            _, m, nx = step_
                            act.wait_ge(inverse_ready, 2 * k_of(step_) + 2)
                            act.wait_ge(ring_ready, ring[("vars", m, nx, sides - 1)] + 1)
                            for t in range(sides):
                                nc.scalar.activation(wide_root[:, t, :].rearrange("p (n d) -> p n d", d=HEAD),
                                                     head_root[:, t, :, :].rearrange("p t (h o) -> p (t h) o", o=1).to_broadcast((P, TILES * HALF_HEADS, HEAD)),
                                                     ACT.Copy).then_inc(root_wide, 1)
                        elif kind == "scores":
                            _, n, pair = step_
                            g, half, kt, off = slots[n]
                            e = 2 * n + pair
                            k_rows = CTX if kt is None else P
                            if n >= 2:
                                act.wait_ge(outputs_added, n - 1)
                            dst = probs[0:k_rows, n % 2, pair, :, off:GROUP]
                            if quantised:
                                act.wait_ge(scores_read, e + 1)
                                nc.scalar.activation(dst, dst, ACT.Exp, bias=quant[:, 4:5], scale=scale).then_inc(probs_ready, 1)
                            else:
                                act.wait_ge(scores_ready, e + 1)
                                nc.scalar.activation(dst, s_ps[0:k_rows, 2 * (e % 2):2 * (e % 2) + 2, off:GROUP], ACT.Exp,
                                                     scale=scale).then_inc(probs_ready, 1)
                        elif kind == "raw":
                            _, g, half = step_
                            act.wait_ge(outputs_added, last_slot[(g, half)] + 1)
                            before = raw_index(step_) - raws
                            if before >= 0:
                                act.wait_ge(ring_read, ring[("normal", before // HALVES, before % HALVES)] + 1)
                            nc.scalar.activation(raw_out[:, half % raws, :], o_ps[:, half, :], ACT.Copy).then_inc(raw_ready, 1)
                        elif kind == "normal":
                            _, g, half = step_
                            act.wait_ge(ring_read, ring[("sums", g, half)] + 1)
                            nc.scalar.activation(wide_inverse[:, half % raws, :, :], inverse[:, half % raws, :].rearrange("p (n o) -> p n o", o=1)
                                                 .to_broadcast((P, PER_HALF * PACK, SLOT)), ACT.Copy).then_inc(wide_ready, 1)

                @block.vector
                def _(dve):
                    then = in_order(dve, dve_step)
                    tt, ts, copy = nc.vector.tensor_tensor, nc.vector.tensor_scalar, nc.vector.tensor_copy
                    for step_ in order:
                        kind = step_[0]
                        if step_ in ring:
                            r = ring[step_]
                            src = r_ps[:, r % 2, :]
                            if kind != "turn":
                                dve.wait_ge(ring_ready, r + 1)
                        if kind == "stage" and quantised:
                            _, m, nx = step_
                            stage_free(dve, step_)
                            now = chip.xt[:, :, bass.ds(batch_of(nx) * SEQ, SEQ)].rearrange("p c (j t) -> p j c t", j=HALVES)
                            fake_quant(nc, then, stage[:, :, :, :], now, quant[:, 8:11], stage[:, :, :, :]).then_inc(staged, 1)
                        elif kind == "project":
                            _, m, nx, t, j = step_
                            if k_of(step_):
                                dve.wait_ge(parts_ready, sides * k_of(step_))
                            factor = quant[:, 1:2] if quantised and t == 0 else 1.0
                            ts(features[:, t, j * GROUP:(j + 1) * GROUP], src, factor, b_qk[:, t, m:m + 1], ALU.mult, ALU.add).then_inc(ring_read, 1)
                        elif kind == "split" and quick:
                            split(dve, nc.vector, then, step_)
                        elif kind == "vproj":
                            _, m, nx, j = step_
                            if nx and b is not None:
                                dve.wait_ge(outputs_added, old_slots)
                            out = v[:, j * PER_HALF:(j + 1) * PER_HALF, heads_of(m), 0:HEAD]
                            rows_ = src.rearrange("p (t h d) -> p t h d", t=PER_HALF, d=HEAD)
                            if v_bias is None:
                                copy(out, rows_).then_inc(ring_read, 1)
                            else:
                                bias = v_bias[:, m * P:(m + 1) * P].rearrange("p (o h d) -> p o h d", o=1, d=HEAD).to_broadcast((P, PER_HALF, HALF_HEADS, HEAD))
                                tt(out, rows_, bias, ALU.add).then_inc(ring_read, 1)
                        elif kind == "vars":
                            t = step_[3]
                            copy(head_root[:, t, :, :], src[:, 0:TILES * HALF_HEADS].rearrange("p (t h) -> p t h", t=TILES)).then_inc(ring_read, 1)
                        elif kind == "vsum":
                            dve.wait_ge(v_squares, k_of(step_) + 1)
                            nc.vector.reduce_sum(value_root[:, :, :], squares[:, 0, :].rearrange("p (t h d) -> p t h d", t=TILES, d=HEAD), AX.X).then_inc(v_summed, 1)
                        elif kind == "inverse":
                            _, m, nx = step_
                            dve.wait_ge(roots_ready, 2 * k_of(step_) + 2)
                            nc.vector.reciprocal(head_root[:, :, :, :], head_root[:, :, :, :]).then_inc(inverse_ready, 1)
                            nc.vector.reciprocal(value_root[:, :, :], value_root[:, :, :]).then_inc(inverse_ready, 1)
                            dve.wait_ge(inverse_ready, 2 * k_of(step_) + 2)
                            every = v[:, :, heads_of(m), 0:HEAD]
                            tt(every, every, value_root[:, :, :].rearrange("p t (h o) -> p t h o", o=1).to_broadcast((P, TILES, HALF_HEADS, HEAD)),
                               ALU.mult).then_inc(v_scaled, 1)
                        elif kind == "spread":
                            _, m, nx, t, j = step_
                            part = features[:, t, j * GROUP:(j + 1) * GROUP]
                            tt(part, part, src, ALU.mult).then_inc(ring_read, 1)
                            dve.wait_ge(ring_read, r + 1)
                            ts(part, part, norm[0][:, t, 0:1], norm[0][:, t, 1:2], ALU.mult, ALU.add).then_inc(affine_ready, 1)
                        elif kind == "max":
                            _, g, nx, qt, i, j = step_
                            if i is None:
                                nc.vector.reduce_max(row_max[:, :, qt, 0], src[:, 0:PACK * CTX].rearrange("p (i n) -> p i n", i=PACK),
                                                     AX.X).then_inc(ring_read, 1)
                            else:
                                cols = min(GROUP, (qt + 1) * P - j * GROUP) if causal else GROUP
                                at = j + kinds - HALVES
                                nc.vector.reduce_max(row_max[:, i, qt, at:at + 1], src[:, 0:cols], AX.X).then_inc(ring_read, 1)
                        elif kind == "turn":
                            if r:
                                dve.wait_ge(ring_read, r)
                            then(nc.vector.reduce_max(top[:, :, :], row_max[:, :, :, :], AX.X))
                            then(ts(top[:, :, :], top[:, :, :], -1.0, None, ALU.mult))
                            for p in range(PARTS):
                                last = copy(top_parts[:, p, :, :], top[:, :, :])
                                if p < PARTS - 1:
                                    then(last)
                                    then(tt(top[:, :, :], top[:, :, :], top_parts[:, p, :, :], ALU.subtract))
                            last.then_inc(top_ready, 1)
                            dve.wait_ge(ring_ready, r + 1)
                            if turns[step_]:
                                dve.wait_ge(top_written, 16 * turns[step_])
                            copy(top_rows[:, :], src[0:PARTS * PACK * TILES, 0:P]).then_inc(ring_read, 1)
                        elif kind == "scores" and quantised:
                            _, n, pair = step_
                            e = 2 * n + pair
                            lv = probs[:, n % 2, pair, :, :]
                            dve.wait_ge(scores_ready, e + 1)
                            if n >= 2:
                                dve.wait_ge(outputs_added, n - 1)
                            ts(lv, s_ps[:, 2 * (e % 2):2 * (e % 2) + 2, :], ROUND, ROUND, ALU.add, ALU.max).then_inc(scores_raw, 1)
                            dve.wait_ge(scores_raw, e + 1)
                            ts(lv, lv, ROUND + QMAX, ROUND, ALU.min, ALU.subtract).then_inc(scores_read, 1)
                        elif kind == "sums":
                            _, g, half = step_
                            nc.vector.reciprocal(inverse[:, half % raws, :], src[:, 0:PER_HALF * PACK]).then_inc(ring_read, 1)
                        elif kind == "normal":
                            _, g, half = step_
                            out = ot[:, g, half * GROUP:(half + 1) * GROUP]
                            tt(out, raw_out[:, half % raws, :], src, ALU.mult).then_inc(ring_read, 1)
                            if quantised:
                                dve.wait_ge(ring_read, r + 1)
                                then(fake_quant(nc, then, out, out, quant[:, 5:8], out))

                @block.gpsimd
                def _(pool):
                    then = in_order(pool, pool_step)
                    tt, copy = nc.gpsimd.tensor_tensor, nc.gpsimd.tensor_copy
                    for step_ in order:
                        kind = step_[0]
                        if kind == "contexts":
                            _, m, nx = step_
                            if nx and b is not None:
                                pool.wait_ge(scores_ready, 2 * old_slots)
                                pool.wait_ge(outputs_added, old_slots)
                            own_heads = heads_of(m)
                            if cross:
                                copy(keys_now[:, own_heads, :], keys_c[:, own_heads, bass.ds(batch_of(nx) * CTX, CTX)]).then_inc(now_ready, 1)
                            copy(values_now[:, own_heads, 0:HEAD], values_c[:, bass.ds(batch_of(nx), 1), own_heads, :].rearrange("p o h d -> p (o h) d")).then_inc(now_ready, 1)
                        elif kind == "split" and not quick:
                            split(pool, nc.gpsimd, then, step_)
                        elif kind == "vaffine":
                            _, m, nx = step_
                            pool.wait_ge(v_scaled, k_of(step_) + 1)
                            every = v[:, :, heads_of(m), 0:HEAD]
                            wide = lambda n: norm[1][:, n, :].rearrange("p (o u d) -> p o u d", o=1, u=1).to_broadcast((P, TILES, HALF_HEADS, HEAD))
                            then(tt(every, every, wide(0), ALU.mult))
                            tt(every, every, wide(1), ALU.add).then_inc(v_done, 1)

                @block.sync
                def _(sp):
                    for step_ in order:
                        kind = step_[0]
                        if kind == "contexts" and not cross:
                            _, m, nx = step_
                            if nx and b is not None:
                                sp.wait_ge(scores_ready, 2 * old_slots)
                            for n, pair in enumerate(PAIRS):
                                source = context_parts[pair[1], m * P:(m + 1) * P, bass.ds(batch_of(nx) * CTX, CTX)]
                                sp.dma_start(keys_now[n * HEAD:(n + 1) * HEAD, heads_of(m), :], source.rearrange("(h r) t -> r h t", r=HEAD)).then_inc(keys_loaded, 16)
                        elif kind == "split":
                            _, m, nx, t = step_
                            count = sides * k_of(step_) + t
                            if nx and b is not None:
                                sp.wait_ge(scores_ready, 2 * old_slots)
                            sp.wait_ge(parts_ready, count + 1)
                            stack_parts(nc, sp, scratch[t], parts[:, :, :], k_stack if t else q_stack, SEQ, t, m, written, stacked[m], 16 * PARTS * count)
                        elif kind == "turn":
                            g = step_[1]
                            sp.wait_ge(ring_read, ring[step_] + 1)
                            sp.dma_start(top_dram.rearrange("p i (q n) -> (p i q) n", n=P), top_rows[:, :]).then_inc(top_written, 16)
                            sp.wait_ge(top_written, 16 * (turns[step_] + 1))
                            sp.dma_start(q_stack[max_row:rows, PACK * g:PACK * (g + 1), :], top_dram).then_inc(top_loaded, 16)
                    for m, nx in prepared:
                        sp.wait_ge(stacked[m], 16 * len(PAIRS) * sides)
                    if context and not cross:
                        sp.wait_ge(keys_loaded, 16 * len(PAIRS) * len(prepared))
                    made = sum(1 for s in order if s[0] == "turn")
                    if made:
                        sp.wait_ge(top_loaded, 16 * made)

        def batch(order, b, b_next):
            with banks(nc, "scores", [P, 4, GROUP], F32) as s_ps, banks(nc, "ring", [P, 2, GROUP], F32) as r_ps, \
                    banks(nc, "outputs", [P, 2, GROUP], F32) as o_ps:
                attend(order, b, b_next, s_ps, r_ps, o_ps)
            if b is not None:
                with banks(nc, "norm_psum", [P, 8, GROUP], F32) as norm_ps:
                    add_norm(chip, [bass.ds(b * SEQ + j * GROUP, GROUP) for j in range(HALVES)], norm_ps,
                             product=(wo, lambda j, k: ot[:, k, j * GROUP:(j + 1) * GROUP]), bias=bo)

        batch(first_order, None, 0)
        with nc.Fori(0, BATCH - 1) as b:
            batch(main_order(True), b, b + 1)
        batch(main_order(False), BATCH - 1, None)


def context_stacks(chip, mode, params, key_bias, f, parts, scratch, keys_c, values_c):
    nc = chip.nc
    w = params[0]
    width = BATCH * CTX
    with banks(nc, "context_psum", [P, 2 + BATCH, GROUP], F32) as ps, step(
            nc, "projected features_ready parts_ready bias_parts written bias_written stacked values_ready dve_step") as (
            block, projected, features_ready, parts_ready, bias_parts, written, bias_written, stacked, values_ready, dve_step):
        bias_at = 2 * width
        @block.tensor
        def _(pe):
            for m in range(FC):
                for c in range(FC):
                    last = nc.tensor.matmul(ps[:, m, 0:width], w[:, 1, c, m * P:(m + 1) * P], chip.ctx_t[:, c, :], start=(c == 0), stop=(c == FC - 1))
                last.then_inc(projected, 1)
            for b in range(BATCH):
                for c in range(FC):
                    last = nc.tensor.matmul(ps[0:CTX, 2 + b, 0:DIM], chip.ctx_t[:, c, b * CTX:(b + 1) * CTX], w[:, 2, c, :], start=(c == 0), stop=(c == FC - 1))
                last.then_inc(projected, 1)

        @block.scalar
        def _(act):
            for m in range(FC):
                act.wait_ge(projected, m + 1)
                nc.scalar.activation(f[:, m, 0:width], ps[:, m, 0:width], ACT.Copy).then_inc(features_ready, 1)
            for b in range(BATCH):
                act.wait_ge(projected, FC + b + 1)
                nc.scalar.activation(values_c[:, b, :, :], ps[0:CTX, 2 + b, 0:DIM].rearrange("p (h d) -> p h d", d=HEAD), ACT.Copy).then_inc(values_ready, 1)
            act.wait_ge(values_ready, BATCH)

        @block.vector
        def _(dve):
            then = in_order(dve, dve_step)
            jobs = []
            if key_bias is not None:
                then(nc.vector.tensor_scalar(key_bias, key_bias, HEAD ** 0.5, None, ALU.mult))
                jobs.append((key_bias, parts[0:1, :, bias_at:bias_at + width], bias_parts))
            jobs += [(f[:, m, 0:width], parts[:, :, m * width:(m + 1) * width], parts_ready) for m in range(FC)]
            for n, (src, dst, ready) in enumerate(jobs):
                m = n - len(jobs) + FC
                if m >= 0:
                    dve.wait_ge(features_ready, m + 1)
                for p in range(PARTS):
                    last = nc.vector.tensor_copy(dst[:, p, :], src)
                    if p < PARTS - 1:
                        then(last)
                        then(nc.vector.tensor_tensor(src, src, dst[:, p, :], ALU.subtract))
                last.then_inc(ready, 1)

        @block.sync
        def _(sp):
            if key_bias is not None:
                sp.wait_ge(bias_parts, 1)
                at = nc.dram_tensor(f"{mode}_bias_parts", (PARTS, width), BF16).ap()
                sp.dma_start(at.rearrange("(o p) t -> o p t", o=1), parts[0:1, :, bias_at:bias_at + width]).then_inc(bias_written, 16)
                sp.wait_ge(bias_written, 16)
                for h in range(HEADS):
                    sp.dma_start(keys_c[STACK:STACK + PARTS, h, :], at).then_inc(stacked, 16)
            for m in range(FC):
                sp.wait_ge(parts_ready, m + 1)
                own_parts = parts[:, :, m * width:(m + 1) * width]
                if keys_c is not None:
                    stack_parts(nc, sp, scratch, own_parts, keys_c, width, 1, m, written, stacked, 16 * PARTS * m)
                else:
                    for p in range(PARTS):
                        sp.dma_start(scratch[p, m * P:(m + 1) * P, :], own_parts[:, p, :]).then_inc(written, 16)
            sp.wait_ge(written, 16 * PARTS * FC)
            if keys_c is not None:
                sp.wait_ge(stacked, 16 * (len(PAIRS) * FC + (HEADS if key_bias is not None else 0)))


def load_split(chip, ctx, layer, v_bias=True):
    nc, io = chip.nc, chip.io
    sb = lambda name, shape: ctx.enter_context(sbuf(nc, name, shape, F32))
    w = sb("split_w", [P, 3, FC, DIM])
    wo = sb("split_wo", [P, HGS, DIM])
    b_qk = sb("split_b", [P, 2, FC])
    bo = sb("split_bo", [P, FC])
    vb = sb("split_vb", [P, DIM]) if v_bias else None
    load(nc, [(w[:, t, :, :], io[layer + "_w"][t].rearrange("(c p) m -> p c m", p=P)) for t in range(3)] + [
        (wo[:, :, :], io[layer + "_wo"].rearrange("(g p) n -> p g n", p=P)),
        (b_qk[:, :, :], io[layer + "_b"]), (bo[:, :], io[layer + "_bo"])]
        + ([(vb[:, :], io[layer + "_vb"].partition_broadcast(P))] if v_bias else []))
    return w, wo, b_qk, vb, bo


def quantised_attention(chip):
    nc, io = chip.nc, chip.io
    with ExitStack() as ctx:
        sb = lambda name, shape: ctx.enter_context(sbuf(nc, name, shape, F32))
        params = load_split(chip, ctx, "L0_attn")
        w, wo, b_qk, _, _ = params
        ten = sb("scalars", [P, 8])
        quant = sb("quant", [P, 11])
        quant_x = quant[:, 8:11]
        with ExitStack() as early:
            eb = lambda name, shape: early.enter_context(sbuf(nc, name, shape, F32))
            sw = eb("weight_scales", [P, 2, 3, DIM])
            sp_ = eb("proj_scales", [P, 2, DIM])
            inv = eb("weight_inverse", [P, 3, DIM])
            inv_p = eb("proj_inverse", [P, DIM])
            load(nc, [(sw[:, n, :, :].rearrange("p t m -> p (t m)"), io["L0_attn_ws"][n:n + 1, :].partition_broadcast(P))
                      for n in range(2)]
                 + [(sp_[:, n, :], io["L0_attn_ps"][n:n + 1, :].partition_broadcast(P)) for n in range(2)]
                 + [(ten[:, 0:6], io["L0_attn_scalars"].partition_broadcast(P))])
            with step(nc, "dve_step") as (block, dve_step):
                @block.vector
                def _(dve):
                    then = in_order(dve, dve_step)
                    one = lambda t, n: t[:, n:n + 1]
                    then(nc.vector.reciprocal(one(quant_x, 0), one(ten, 0)))
                    then(nc.vector.tensor_copy(one(quant_x, 1), one(ten, 1)))
                    then(nc.vector.tensor_copy(one(quant_x, 2), one(ten, 0)))
                    then(nc.vector.tensor_scalar(one(quant, 0), one(ten, 2), HEAD ** 0.5, None, ALU.mult))
                    then(nc.vector.reciprocal(one(quant, 1), one(quant, 0)))
                    then(nc.vector.tensor_copy(one(quant, 2), one(ten, 3)))
                    then(nc.vector.tensor_copy(one(quant, 3), one(ten, 2)))
                    then(nc.vector.tensor_scalar(one(quant, 4), one(ten, 2), -QMAX, None, ALU.mult))
                    then(nc.vector.reciprocal(one(quant, 5), one(ten, 4)))
                    then(nc.vector.tensor_copy(one(quant, 6), one(ten, 5)))
                    then(nc.vector.tensor_copy(one(quant, 7), one(ten, 4)))
                    then(nc.vector.reciprocal(inv[:, :, :], sw[:, 0, :, :]))
                    then(nc.vector.reciprocal(inv_p[:, :], sp_[:, 0, :]))
                    jobs = [(w[:, t, c, :], inv[:, t, :], sw[:, 1, t, :], sw[:, 0, t, :]) for t in range(3) for c in range(FC)]
                    jobs += [(wo[:, g, :], inv_p[:, :], sp_[:, 1, :], sp_[:, 0, :]) for g in range(HGS)]
                    for weight, inverse, zero, scale in jobs:
                        then(nc.vector.tensor_tensor(weight, weight, inverse, ALU.mult))
                        then(nc.vector.tensor_tensor(weight, weight, zero, ALU.add))
                        then(nc.vector.tensor_scalar(weight, weight, 0.0, QMAX, ALU.max, ALU.min))
                        then(nc.vector.tensor_scalar(weight, weight, ROUND, ROUND, ALU.add, ALU.subtract))
                        then(nc.vector.tensor_tensor(weight, weight, zero, ALU.subtract))
                        then(nc.vector.tensor_tensor(weight, weight, scale, ALU.mult))
                    then(nc.vector.tensor_scalar(b_qk[:, 0, :], b_qk[:, 0, :], one(quant, 1), None, ALU.mult))
                    for g in range(HGS):
                        then(nc.vector.tensor_scalar(wo[:, g, :], wo[:, g, :], chip.c(C_ROWS, 1), None, ALU.mult))
        split_attention(chip, "quant", params, quant=quant)


def cross_attention(chip):
    nc, io = chip.nc, chip.io
    with ExitStack() as ctx:
        params = load_split(chip, ctx, "L0_xattn", v_bias=False)
        key_bias = ctx.enter_context(sbuf(nc, "key_bias", [1, BATCH * CTX], F32))
        load(nc, [(key_bias[:, :], io["key_bias"])])
        split_attention(chip, "cross", params, key_bias=key_bias[:, :])


def normed_attention(chip):
    nc, io = chip.nc, chip.io
    with ExitStack() as ctx:
        sb = lambda name, shape: ctx.enter_context(sbuf(nc, name, shape, F32))
        params = load_split(chip, ctx, "L1_attn")
        w, _, b_qk, v_bias, _ = params
        norm = sb("head_norm", [P, 2, 2])
        norm_v = sb("value_norm", [P, 2, HEAD])
        means = sb("head_means", [P, (3 * FC + 1) * HEADS])
        load(nc, [(norm[:, :, :], io["L1_attn_norm"]), (norm_v[:, :, :].rearrange("p n d -> p (n d)"), io["L1_attn_norm_v"].partition_broadcast(P))])
        with banks(nc, "bias_means", [P, 2 * FC], F32) as mean_ps, step(nc, "means_ready dve_step") as (block, means_ready, dve_step):
            @block.tensor
            def _(pe):
                nc.tensor.matmul(mean_ps[:, :], chip.c(C_HEADMEAN), b_qk[:, :, :].rearrange("p t m -> p (t m)"),
                                 start=True, stop=True).then_inc(means_ready, 1)

            @block.vector
            def _(dve):
                then = in_order(dve, dve_step)
                heads = [w[:, :, :, :].rearrange("p t c (h d) -> p (t c h) d", d=HEAD), v_bias[:, :].rearrange("p (h d) -> p h d", d=HEAD)]
                at = 0
                for part in heads:
                    n = part.shape[1]
                    mean = means[:, at:at + n]
                    then(nc.vector.reduce_sum(mean, part, AX.X))
                    then(nc.vector.tensor_scalar(mean, mean, 1.0 / HEAD, None, ALU.mult))
                    then(nc.vector.tensor_tensor(part, part, mean.rearrange("p (h o) -> p h o", o=1).to_broadcast((P, n, HEAD)), ALU.subtract))
                    at += n
                dve.wait_ge(means_ready, 1)
                every = b_qk[:, :, :].rearrange("p t m -> p (t m)")
                then(nc.vector.tensor_tensor(every, every, mean_ps[:, :], ALU.subtract))
        split_attention(chip, "normed", params, norm=(norm, norm_v))


def causal_attention(chip):
    with ExitStack() as ctx:
        params = load_split(chip, ctx, "L3_xattn", v_bias=False)
        split_attention(chip, "causal", params)


KV_HEADS = 4
REPEAT = HEADS // KV_HEADS


def linear_attention(chip):
    nc, io = chip.nc, chip.io
    with ExitStack() as ctx:
        sb = lambda name, shape: ctx.enter_context(sbuf(nc, name, shape, F32))
        wq, bq = sb("linear_wq", [P, FC, REPEAT, P]), sb("linear_bq", [P, 2, REPEAT])
        wkv, bkv = sb("kv_down", [P, FC, P]), sb("kv_bias", [P, 1])
        wc, wk, wkv_up = sb("kv_compress", [P, P]), sb("k_up", [P, P]), sb("kv_up", [P, P])
        wo, bo = sb("linear_wo", [P, REPEAT, DIM]), sb("linear_bo", [P, FC])
        affine = sb("affine", [P, 2, FC])
        load(nc, [(wq[:, c, :, :], io["L3_attn_wq"][c * P:(c + 1) * P]) for c in range(FC)]
             + [(bq[:, 0, :], io["L3_attn_bq"]), (wkv[:, :, :], io["L3_attn_wkv"].rearrange("(c p) m -> p c m", p=P)),
                (bkv[:, :], io["L3_attn_bkv"]), (wc[:, :], io["L3_attn_wc"]), (wk[:, :], io["L3_attn_wk"]), (wkv_up[:, :], io["L3_attn_wkv_up"]),
                (wo[:, :, :], io["L3_attn_wo"].rearrange("(r p) n -> p r n", p=P)), (bo[:, :], io["L3_attn_bo"]), (affine[:, :, :], io["L3_attn_affine"])])
        q_f, k_f = sb("query_features", [P, REPEAT, SEQ]), sb("key_features", [P, SEQ])
        k_rows, v_rows = sb("key_rows", [P, TILES, KV_HEADS, SLOT]), sb("value_rows", [P, TILES, KV_HEADS, SLOT])
        ot = sb("linear_out", [P, REPEAT, SEQ])
        with step(nc, "set_") as (block, set_):
            @block.vector
            def _(dve):
                nc.vector.tensor_scalar(bq[:, 1, :], bq[:, 0, :], 1.0, None, ALU.add).then_inc(set_, 1)
                nc.vector.memset(k_rows[:, :, :, :], 0.0).then_inc(set_, 1)
                nc.vector.memset(v_rows[:, :, :, HEAD + 1:], 0.0).then_inc(set_, 1)
                nc.vector.memset(v_rows[:, :, :, HEAD:HEAD + 1], 1.0).then_inc(set_, 1)
                dve.wait_ge(set_, 4)
        with nc.Fori(0, BATCH) as b:
            linear_features(chip, b, wq, bq, wkv, bkv, wc, wk, wkv_up, q_f, k_f, k_rows, v_rows)
            linear_chunks(chip, q_f, k_f, k_rows, v_rows, ot)
            with banks(nc, "norm_psum", [P, 8, GROUP], F32) as norm_ps:
                add_norm(chip, [bass.ds(b * SEQ + j * GROUP, GROUP) for j in range(HALVES)], norm_ps, bias=bo,
                         product=(wo, lambda j, r: ot[:, r, j * GROUP:(j + 1) * GROUP]), affine=(affine[:, 0, :], affine[:, 1, :]))


def linear_features(chip, b, wq, bq, wkv, bkv, wc, wk, wkv_up, q_f, k_f, k_rows, v_rows):
    nc = chip.nc
    part = lambda j: slice(j * GROUP, (j + 1) * GROUP)
    queries = [(4 + n % 4, q_f[:, n // HALVES, part(n % HALVES)], bq[:, 0, n // HALVES:n // HALVES + 1], bq[:, 1, n // HALVES:n // HALVES + 1])
               for n in range(REPEAT * HALVES)]
    keys = [(j, k_f[:, part(j)], 0.0, 1.0) for j in range(HALVES)]
    rows = [(2 + j, k_rows[:, PER_HALF * j:PER_HALF * (j + 1), :, 0:HEAD], 0.0, 1.0) for j in range(HALVES)]
    jobs = queries[:4] + keys + rows + queries[4:]
    with ExitStack() as ctx:
        kv = ctx.enter_context(sbuf(nc, "kv", [P, SEQ], F32))
        latent = ctx.enter_context(sbuf(nc, "latent", [P, SEQ], F32))
        low = ctx.enter_context(sbuf(nc, "feature_low", [P, 3, GROUP], F32))
        ps = ctx.enter_context(banks(nc, "linear_psum", [P, 8, GROUP], F32))

        def source(n):
            bank = ps[:, jobs[n][0], :]
            if jobs[n] in rows:
                return bank.rearrange("p (t s h d) -> p t s h d", t=PER_HALF, s=2, h=KV_HEADS)[:, :, 0, :, :]
            return bank

        def lower(n):
            buf = low[:, n % 3, :]
            if jobs[n] in rows:
                return buf[:, 0:GROUP // 2].rearrange("p (t h d) -> p t h d", t=PER_HALF, h=KV_HEADS)
            return buf

        with step(nc, "down_ready kv_ready latents_ready latents_copied projected rows_copied low_ready exps_ready features_ready") as (
                block, down_ready, kv_ready, latents_ready, latents_copied, projected, rows_copied, low_ready, exps_ready, features_ready):
            @block.tensor
            def _(pe):
                tok = lambda j: bass.ds(b * SEQ + j * GROUP, GROUP)

                def query(n):
                    for c in range(FC):
                        last = nc.tensor.matmul(ps[:, queries[n][0], :], wq[:, c, n // HALVES, :], chip.xt[:, c, tok(n % HALVES)], start=(c == 0), stop=(c == FC - 1))
                    last.then_inc(projected, 1)

                for j in range(HALVES):
                    for c in range(FC):
                        last = nc.tensor.matmul(ps[:, j, :], wkv[:, c, :], chip.xt[:, c, tok(j)], start=(c == 0), stop=(c == FC - 1))
                    last.then_inc(down_ready, 1)
                for n in range(4):
                    query(n)
                for j in range(HALVES):
                    pe.wait_ge(kv_ready, j + 1)
                    nc.tensor.matmul(ps[:, 2 + j, :], wc[:, :], kv[:, part(j)], start=True, stop=True).then_inc(latents_ready, 1)
                for j in range(HALVES):
                    pe.wait_ge(latents_copied, j + 1)
                    nc.tensor.matmul(ps[:, j, :], wk[:, :], latent[:, part(j)], start=True, stop=True).then_inc(projected, 1)
                for j in range(HALVES):
                    for t in range(PER_HALF):
                        last = nc.tensor.matmul(ps[:, 2 + j, t * P:(t + 1) * P], latent[:, (PER_HALF * j + t) * P:(PER_HALF * j + t + 1) * P], wkv_up[:, :],
                                                start=True, stop=True)
                    last.then_inc(projected, 1)
                for n in range(4, len(queries)):
                    pe.wait_ge(features_ready, n - 3)
                    query(n)

            @block.scalar
            def _(act):
                for j in range(HALVES):
                    act.wait_ge(down_ready, j + 1)
                    nc.scalar.activation(kv[:, part(j)], ps[:, j, :], ACT.Identity, bias=bkv[:, 0:1]).then_inc(kv_ready, 1)
                for j in range(HALVES):
                    act.wait_ge(latents_ready, j + 1)
                    nc.scalar.activation(latent[:, part(j)], ps[:, 2 + j, :], ACT.Copy).then_inc(latents_copied, 1)
                for n in range(len(jobs)):
                    act.wait_ge(low_ready, n + 1)
                    nc.scalar.activation(lower(n), lower(n), ACT.Exp).then_inc(exps_ready, 1)
                for j in range(HALVES):
                    act.wait_ge(features_ready, jobs.index(rows[j]) + 1)
                    nc.scalar.activation(v_rows[:, PER_HALF * j:PER_HALF * (j + 1), :, 0:HEAD],
                                         ps[:, 2 + j, :].rearrange("p (t s h d) -> p t s h d", t=PER_HALF, s=2, h=KV_HEADS)[:, :, 1, :, :],
                                         ACT.Copy).then_inc(rows_copied, 1)

            @block.vector
            def _(dve):
                def low_part(n):
                    dve.wait_ge(projected, n + 1)
                    if n >= 3:
                        dve.wait_ge(features_ready, n - 2)
                    nc.vector.tensor_scalar(lower(n), source(n), jobs[n][2], 0.0, ALU.add, ALU.min).then_inc(low_ready, 1)

                low_part(0)
                for n in range(len(jobs)):
                    if n + 1 < len(jobs):
                        low_part(n + 1)
                    dve.wait_ge(exps_ready, n + 1)
                    nc.vector.scalar_tensor_tensor(out=jobs[n][1], in0=source(n), scalar=jobs[n][3], in1=lower(n),
                                                   op0=ALU.add, op1=ALU.max).then_inc(features_ready, 1)


def linear_chunks(chip, q_f, k_f, k_rows, v_rows, ot):
    nc = chip.nc
    with ExitStack() as ctx:
        sb = lambda name, shape: ctx.enter_context(sbuf(nc, name, shape, F32))
        masked = sb("masked_products", [P, 2, KV_HEADS, GROUP])
        state = sb("linear_state", [P, 2, P])
        raw = sb("linear_raw", [P, 2, GROUP])
        inverse, wide = sb("linear_inverse", [P, 2, KV_HEADS * REPEAT]), sb("linear_inverse_wide", [P, 2, KV_HEADS * REPEAT, SLOT])
        product_ps = ctx.enter_context(banks(nc, "linear_products", [P, 3, GROUP], F32))
        out_ps = ctx.enter_context(banks(nc, "linear_outputs", [P, 2, GROUP], F32))
        state_ps = ctx.enter_context(banks(nc, "linear_sum", [P, P], F32))
        spread_ps = ctx.enter_context(banks(nc, "linear_spread", [P, 2, GROUP], F32))
        chunk = lambda c: slice(c * P, (c + 1) * P)
        own = lambda g: slice(SLOT * g, SLOT * g + HEAD)
        with step(nc, "products_ready masked_ready state_summed state_ready out_ready raw_ready sums_ready inverse_ready wide_ready spread_ready out_done dve_step") as (
                block, products_ready, masked_ready, state_summed, state_ready, out_ready, raw_ready, sums_ready, inverse_ready, wide_ready, spread_ready,
                out_done, dve_step):
            @block.tensor
            def _(pe):
                def products(c):
                    for g in range(KV_HEADS):
                        n = KV_HEADS * c + g
                        if n >= 3:
                            pe.wait_ge(masked_ready, n - 2)
                        nc.tensor.matmul(product_ps[:, n % 3, :].rearrange("p (r t) -> p r t", r=REPEAT), k_f[own(g), chunk(c)], q_f[own(g), :, chunk(c)],
                                         start=True, stop=True).then_inc(products_ready, 1)

                def outputs(c):
                    if c >= 2:
                        pe.wait_ge(raw_ready, c - 1)
                    out = out_ps[:, c % 2, :].rearrange("p (r t) -> p r t", r=REPEAT)
                    if c:
                        pe.wait_ge(state_ready, c)
                        nc.tensor.matmul(out, state[:, c % 2, :], q_f[:, :, chunk(c)], start=True, stop=False)
                    pe.wait_ge(masked_ready, KV_HEADS * (c + 1))
                    for g in range(KV_HEADS):
                        last = nc.tensor.matmul(out_ps[SLOT * g:SLOT * (g + 1), c % 2, :], v_rows[:, c, g, :], masked[:, c % 2, g, :], start=(c == 0), stop=True)
                    last.then_inc(out_ready, 1)

                def add_state(c):
                    if c:
                        pe.wait_ge(state_ready, c)
                    nc.tensor.matmul(state_ps[:, :], k_rows[:, c, :, :].rearrange("p h r -> p (h r)"), v_rows[:, c, :, :].rearrange("p h r -> p (h r)"),
                                     start=True, stop=True).then_inc(state_summed, 1)

                def sums(c):
                    pe.wait_ge(raw_ready, c + 1)
                    if c >= 2:
                        pe.wait_ge(out_done, c - 1)
                    for r in range(REPEAT):
                        last = nc.tensor.matmul(spread_ps[:, c % 2, r * KV_HEADS:(r + 1) * KV_HEADS], raw[:, c % 2, r * P:(r + 1) * P],
                                                chip.c(C_DEN)[:, 0:P:SLOT], start=True, stop=True)
                    last.then_inc(sums_ready, 1)

                def spread(c):
                    pe.wait_ge(wide_ready, c + 1)
                    for r in range(REPEAT):
                        last = nc.tensor.matmul(spread_ps[:, c % 2, r * P:(r + 1) * P],
                                                wide[:, c % 2, r * KV_HEADS:(r + 1) * KV_HEADS, :].rearrange("p h r -> p (h r)"), chip.c(C_ID), start=True, stop=True)
                    last.then_inc(spread_ready, 1)

                for c in range(TILES + 3):
                    if c < TILES:
                        products(c)
                        if c < TILES - 1:
                            add_state(c)
                    if 1 <= c <= TILES:
                        outputs(c - 1)
                    if 2 <= c <= TILES + 1:
                        sums(c - 2)
                    if c >= 3:
                        spread(c - 3)

            @block.vector
            def _(dve):
                then = in_order(dve, dve_step)
                keep = chip.c(C_KEEPT).rearrange("p (o n) -> p o n", o=1).to_broadcast((P, REPEAT, P))
                for c in range(TILES + 3):
                    if c < TILES:
                        for g in range(KV_HEADS):
                            n = KV_HEADS * c + g
                            dve.wait_ge(products_ready, n + 1)
                            if c >= 2:
                                dve.wait_ge(out_ready, c - 1)
                            nc.vector.tensor_tensor(masked[:, c % 2, g, :].rearrange("p (r t) -> p r t", r=REPEAT),
                                                    product_ps[:, n % 3, :].rearrange("p (r t) -> p r t", r=REPEAT), keep, ALU.mult).then_inc(masked_ready, 1)
                        if c < TILES - 1:
                            dve.wait_ge(state_summed, c + 1)
                            if c >= 1:
                                dve.wait_ge(out_ready, c)
                            last = nc.vector.tensor_tensor(state[:, (c + 1) % 2, :], state_ps[:, :], chip.c(C_SLOTS), ALU.mult)
                            if c:
                                then(last)
                                dve.wait_ge(state_ready, c)
                                last = nc.vector.tensor_tensor(state[:, (c + 1) % 2, :], state[:, (c + 1) % 2, :], state[:, c % 2, :], ALU.add)
                            last.then_inc(state_ready, 1)
                    if 2 <= c <= TILES + 1:
                        i = c - 2
                        dve.wait_ge(sums_ready, i + 1)
                        if i >= 2:
                            dve.wait_ge(wide_ready, i - 1)
                        then(nc.vector.tensor_scalar(inverse[:, i % 2, :], spread_ps[:, i % 2, 0:KV_HEADS * REPEAT], 1e-6, None, ALU.add))
                        nc.vector.reciprocal(inverse[:, i % 2, :], inverse[:, i % 2, :]).then_inc(inverse_ready, 1)
                    if c >= 3:
                        i = c - 3
                        dve.wait_ge(spread_ready, i + 1)
                        nc.vector.tensor_tensor(ot[:, :, chunk(i)], raw[:, i % 2, :].rearrange("p (r t) -> p r t", r=REPEAT),
                                                spread_ps[:, i % 2, :].rearrange("p (r t) -> p r t", r=REPEAT), ALU.mult).then_inc(out_done, 1)

            @block.scalar
            def _(act):
                for c in range(TILES + 2):
                    if c < TILES:
                        act.wait_ge(out_ready, c + 1)
                        if c >= 2:
                            act.wait_ge(out_done, c - 1)
                        nc.scalar.activation(raw[:, c % 2, :], out_ps[:, c % 2, :], ACT.Copy).then_inc(raw_ready, 1)
                    if 1 <= c <= TILES:
                        i = c - 1
                        act.wait_ge(inverse_ready, i + 1)
                        nc.scalar.activation(wide[:, i % 2, :, :], inverse[:, i % 2, :].rearrange("p (n o) -> p n o", o=1)
                                             .to_broadcast((P, KV_HEADS * REPEAT, SLOT)), ACT.Copy).then_inc(wide_ready, 1)


def context_mlp(chip):
    nc, io = chip.nc, chip.io
    with ExitStack() as ctx:
        rows = ctx.enter_context(sbuf(nc, "context_rows", [CTX, BATCH, DIM], F32))
        stage = ctx.enter_context(sbuf(nc, "context_stage", [P, FC, CTX], F32))
        stage_rows = ctx.enter_context(sbuf(nc, "context_stage_rows", [CTX, 1, DIM], F32))
        h = ctx.enter_context(sbuf(nc, "hidden", [CTX, 2, GROUP], F32))
        load(nc, [(rows[:, :, :], io["ctx"].rearrange("(b s) d -> s b d", b=BATCH))])
        halves = SEQ // GROUP
        with nc.Fori(0, BATCH) as b:
            tok = lambda j: bass.ds(b * SEQ + j * GROUP, GROUP)
            with banks(nc, "hidden_psum", [P, 2, GROUP], F32) as ps, step(nc, "staged products_ready hidden_ready") as (
                    block, staged, products_ready, hidden_ready):
                @block.vector
                def _(dve):
                    nc.vector.tensor_copy(stage[:, :, :], chip.ctx_t[:, :, bass.ds(b * CTX, CTX)]).then_inc(staged, 1)
                    nc.vector.tensor_copy(stage_rows[:, 0, :], rows[:, bass.ds(b, 1), :].rearrange("p o d -> p (o d)")).then_inc(staged, 1)
                    dve.wait_ge(staged, 2)

                @block.tensor
                def _(pe):
                    pe.wait_ge(staged, 2)
                    for j in range(halves):
                        for c in range(FC):
                            last = nc.tensor.matmul(ps[0:CTX, j, :], stage[:, c, :], chip.xt[:, c, tok(j)], start=(c == 0), stop=(c == FC - 1))
                        last.then_inc(products_ready, 1)

                @block.scalar
                def _(act):
                    for j in range(halves):
                        act.wait_ge(products_ready, j + 1)
                        nc.scalar.activation(h[:, j, :], ps[0:CTX, j, :], ACT.Gelu_apprx_tanh).then_inc(hidden_ready, 1)
            with banks(nc, "norm_psum", [P, 8, GROUP], F32) as norm_ps:
                add_norm(chip, [tok(j) for j in range(halves)], norm_ps, product=(stage_rows, lambda j, k: h[:, j, :]))


def concat_context(chip):
    nc, io = chip.nc, chip.io
    with ExitStack() as ctx:
        sb = lambda name, shape: ctx.enter_context(sbuf(nc, name, shape, F32))
        w = sb("concat_w", [P, 2 * FC, DIM])
        bias = sb("concat_b", [P, FC])
        sums = sb("context_sums", [P, FC, BATCH])
        shift = sb("context_shift", [P, BATCH, FC])
        shift_b = sb("context_shift_now", [P, FC])
        load(nc, [(w[:, :, :], io["L2_xattn_w"].rearrange("(c p) n -> p c n", p=P)), (bias[:, :], io["L2_xattn_b"])])
        with banks(nc, "shift_psum", [P, FC, BATCH], F32) as ps, step(nc, "sums_ready shift_ready dve_step") as (block, sums_ready, shift_ready, dve_step):
            @block.vector
            def _(dve):
                nc.vector.reduce_sum(sums[:, :, :], chip.ctx_t[:, :, :].rearrange("p c (b s) -> p c b s", b=BATCH), AX.X).then_inc(sums_ready, 1)
                dve.wait_ge(shift_ready, FC)
                then = in_order(dve, dve_step)
                for c in range(FC):
                    then(nc.vector.tensor_scalar(shift[:, :, c], ps[:, c, :], 1.0 / CTX, bias[:, c:c + 1], ALU.mult, ALU.add))

            @block.tensor
            def _(pe):
                pe.wait_ge(sums_ready, 1)
                for c in range(FC):
                    for k in range(FC):
                        last = nc.tensor.matmul(ps[:, c, :], w[:, FC + k, c * P:(c + 1) * P], sums[:, k, :], start=(k == 0), stop=(k == FC - 1))
                    last.then_inc(shift_ready, 1)
        with nc.Fori(0, BATCH) as b:
            with step(nc, "staged") as (block, staged):
                @block.vector
                def _(dve):
                    nc.vector.tensor_copy(shift_b[:, :], shift[:, bass.ds(b, 1), :].rearrange("p o c -> p (o c)")).then_inc(staged, 1)
                    dve.wait_ge(staged, 1)
            tok = lambda j: bass.ds(b * SEQ + j * GROUP, GROUP)
            with banks(nc, "norm_psum", [P, 8, GROUP], F32) as norm_ps:
                add_norm(chip, [tok(0), tok(1)], norm_ps, product=(w[:, 0:FC, :], lambda j, k: chip.xt[:, k, tok(j)]), bias=shift_b)


def spiking_ffn(chip):
    nc, io = chip.nc, chip.io
    inner = 4 * DIM
    ic = inner // P
    steps, beta, threshold = 5, 0.9, 1.0
    with ExitStack() as ctx:
        sb = lambda name, shape: ctx.enter_context(sbuf(nc, name, shape, F32))
        w1, w2 = sb("fc_w", [P, FC, inner]), sb("proj_w", [P, ic, DIM])
        h = sb("hidden", [P, ic, GROUP])
        y, mem, spike, total = (sb(n, [P, FC, GROUP]) for n in ("drive", "membrane", "spike", "spikes"))
        load(nc, [(w1[:, :, :], io["L2_ffn_w1"].rearrange("(c p) n -> p c n", p=P)), (w2[:, :, :], io["L2_ffn_w2"].rearrange("(c p) n -> p c n", p=P))])
        h_ps = ctx.enter_context(banks(nc, "hidden_psum", [P, 2, GROUP], F32))
        y_ps = ctx.enter_context(banks(nc, "drive_psum", [P, FC, GROUP], F32))
        norm_ps = ctx.enter_context(banks(nc, "norm_psum", [P, 4, GROUP], F32))

        def group(now, following):
            with step(nc, "h_ready relu_ready squared y_ready y_taken dve_step") as (block, h_ready, relu_ready, squared, y_ready, y_taken, dve_step):
                if following is not None:
                    @block.tensor
                    def _(pe):
                        for n in range(ic):
                            if n >= 2:
                                pe.wait_ge(relu_ready, n - 1)
                            for c in range(FC):
                                last = nc.tensor.matmul(h_ps[:, n % 2, :], w1[:, c, n * P:(n + 1) * P], chip.xt[:, c, group_slice(following)],
                                                        start=(c == 0), stop=(c == FC - 1))
                            last.then_inc(h_ready, 1)
                        if now is not None:
                            pe.wait_ge(y_taken, 1)
                        for c in range(FC):
                            for n in range(ic):
                                pe.wait_ge(squared, n + 1)
                                last = nc.tensor.matmul(y_ps[:, c, :], w2[:, n, c * P:(c + 1) * P], h[:, n, :], start=(n == 0), stop=(n == ic - 1))
                        last.then_inc(y_ready, 1)

                    @block.scalar
                    def _(act):
                        for n in range(ic):
                            act.wait_ge(h_ready, n + 1)
                            nc.scalar.activation(h[:, n, :], h_ps[:, n % 2, :], ACT.Relu).then_inc(relu_ready, 1)
                            act.wait_ge(relu_ready, n + 1)
                            nc.scalar.activation(h[:, n, :], h[:, n, :], ACT.Square).then_inc(squared, 1)

                if now is not None:
                    @block.vector
                    def _(dve):
                        then = in_order(dve, dve_step)
                        nc.vector.tensor_copy(y[:, :, :], y_ps[:, :, :]).then_inc(y_taken, 1)
                        dve.wait_ge(y_taken, 1)
                        then(nc.vector.tensor_scalar(spike[:, :, :], y[:, :, :], threshold, None, ALU.is_gt))
                        then(nc.vector.tensor_copy(total[:, :, :], spike[:, :, :]))
                        for s in range(1, steps):
                            before = y if s == 1 else mem
                            then(nc.vector.scalar_tensor_tensor(out=mem[:, :, :], in0=before[:, :, :], scalar=beta, in1=y[:, :, :], op0=ALU.mult, op1=ALU.add))
                            then(nc.vector.tensor_tensor(mem[:, :, :], mem[:, :, :], spike[:, :, :], ALU.subtract))
                            then(nc.vector.tensor_scalar(spike[:, :, :], mem[:, :, :], threshold, None, ALU.is_gt))
                            then(nc.vector.tensor_tensor(total[:, :, :], total[:, :, :], spike[:, :, :], ALU.add))
                        then(nc.vector.tensor_scalar(total[:, :, :], total[:, :, :], 1.0 / steps, None, ALU.mult))
            if now is not None:
                add_norm(chip, [group_slice(now)], norm_ps, ready=lambda _, c: total[:, c, :])

        group(None, 0)
        with nc.Fori(0, GROUPS - 1) as g:
            group(g, g + 1)
        group(GROUPS - 1, None)




EXPERTS, EXPERT_INNER = 8, 1024
CAPACITY = 2 * TOKENS // EXPERTS
TOKEN_TILES = TOKENS // P
ROUND_EXPERTS = 4


def token_rows(chip, rows, logits=None, gate_w=None):
    nc = chip.nc
    per = GROUP // P
    with ExitStack() as ctx:
        stage = ctx.enter_context(sbuf(nc, "token_stage", [P, FC, GROUP], F32))
        turn_ps = ctx.enter_context(banks(nc, "rows_psum", [P, per, DIM], F32))
        logit_ps = ctx.enter_context(banks(nc, "logits_psum", [P, per, EXPERTS], F32))
        with nc.Fori(0, GROUPS) as g, step(nc, "staged turned logits_ready copied") as (block, staged, turned, logits_ready, copied):
            @block.vector
            def _(dve):
                nc.vector.tensor_copy(stage[:, :, :], chip.xt[:, :, group_slice(g)]).then_inc(staged, 1)
                if logits is not None:
                    dve.wait_ge(logits_ready, 1)
                    nc.vector.tensor_copy(logits[:, bass.ds(g * per, per), :], logit_ps[:, :, :]).then_inc(copied, 1)

            @block.tensor
            def _(pe):
                pe.wait_ge(staged, 1)
                for t in range(per):
                    for c in range(FC):
                        last = nc.tensor.transpose(turn_ps[:, t, c * P:(c + 1) * P], stage[:, c, t * P:(t + 1) * P], chip.c(C_ID))
                last.then_inc(turned, 1)
                if logits is not None:
                    for t in range(per):
                        for c in range(FC):
                            last = nc.tensor.matmul(logit_ps[:, t, :], stage[:, c, t * P:(t + 1) * P], gate_w[:, c, :],
                                                    start=(c == 0), stop=(c == FC - 1))
                    last.then_inc(logits_ready, 1)

            @block.scalar
            def _(act):
                act.wait_ge(turned, 1)
                nc.scalar.activation(rows[:, bass.ds(g * per, per), :], turn_ps[:, :, :], ACT.Copy).then_inc(copied, 1)


def route(chip, logits, place, scatter_to, gates):
    nc = chip.nc
    E, N = EXPERTS, TOKEN_TILES
    with ExitStack() as ctx:
        sb = lambda name, shape: ctx.enter_context(sbuf(nc, name, shape, F32))
        best = sb("best", [P, 2, N])
        index = sb("expert_index", [P, 2, N])
        hot = sb("one_hot", [P, 2, N, E])
        work = sb("route_work", [P, N, E])
        rest = sb("route_rest", [P, N, E])
        total = sb("tile_totals", [P, 2, 2, N, E])
        slot = sb("slots", [P, 2, N])
        keep = sb("keep", [P, 2, N])
        ex = sb("gate_exps", [P, N, E])
        small = sb("gate_sums", [P, 4, N])
        ps = ctx.enter_context(banks(nc, "route_psum", [P, 2, 2, N, E], F32))
        wide = lambda t: t.rearrange("p (n o) -> p n o", o=1).to_broadcast((P, N, E))
        iota = chip.c(C_IOTA, E).rearrange("p (o e) -> p o e", o=1).to_broadcast((P, N, E))
        with step(nc, "hot_ready counts_ready shifted exps_ready dve_step") as (block, hot_ready, counts_ready, shifted, exps_ready, dve_step):
            @block.vector
            def _(dve):
                then = in_order(dve, dve_step)
                tt, ts = nc.vector.tensor_tensor, nc.vector.tensor_scalar
                for k in range(2):
                    src = logits[:, :, :] if k == 0 else rest[:, :, :]
                    then(nc.vector.reduce_max(best[:, k, :], src, AX.X))
                    then(tt(work[:, :, :], src, wide(best[:, k, :]), ALU.is_lt))
                    then(ts(work[:, :, :], work[:, :, :], float(E), None, ALU.mult))
                    then(tt(work[:, :, :], work[:, :, :], iota, ALU.add))
                    then(nc.vector.tensor_reduce(index[:, k, :], work[:, :, :], AX.X, ALU.min))
                    nc.vector.tensor_tensor(hot[:, k, :, :], wide(index[:, k, :]), iota, ALU.is_equal).then_inc(hot_ready, 1)
                    dve.wait_ge(hot_ready, k + 1)
                    if k == 0:
                        then(ts(rest[:, :, :], hot[:, 0, :, :], FAR, None, ALU.mult))
                        then(tt(rest[:, :, :], logits[:, :, :], rest[:, :, :], ALU.add))
                nc.vector.tensor_tensor(work[:, :, :], logits[:, :, :], wide(best[:, 0, :]), ALU.subtract).then_inc(shifted, 1)
                nc.vector.tensor_tensor(small[:, 1, :], best[:, 1, :], best[:, 0, :], ALU.subtract).then_inc(shifted, 1)
                dve.wait_ge(exps_ready, 2)
                then(nc.vector.reduce_sum(small[:, 0, :], ex[:, :, :], AX.X))
                then(nc.vector.reciprocal(small[:, 0, :], small[:, 0, :]))
                then(tt(small[:, 1, :], small[:, 2, :], small[:, 0, :], ALU.mult))
                then(tt(small[:, 3, :], small[:, 0, :], small[:, 1, :], ALU.add))
                then(ts(small[:, 3, :], small[:, 3, :], 1e-9, None, ALU.max))
                then(nc.vector.reciprocal(small[:, 3, :], small[:, 3, :]))
                dve.wait_ge(counts_ready, 1)
                for k in range(2):
                    then(nc.vector.memset(total[:, 0, k, 0, :], 0.0))
                    then(nc.vector.tensor_copy(total[:, 0, k, 1:N, :], ps[:, 1, k, 0:N - 1, :]))
                at = 0
                for shift in (1, 2, 4, 8, 16):
                    for k in range(2):
                        then(nc.vector.tensor_copy(total[:, 1 - at, k, 0:shift, :], total[:, at, k, 0:shift, :]))
                        then(tt(total[:, 1 - at, k, shift:N, :], total[:, at, k, shift:N, :], total[:, at, k, 0:N - shift, :], ALU.add))
                    at = 1 - at
                for k in range(2):
                    then(tt(work[:, :, :], ps[:, 0, k, :, :], total[:, at, k, :, :], ALU.add))
                    if k == 1:
                        then(tt(rest[:, 0, :], total[:, at, 0, N - 1, :], ps[:, 1, 0, N - 1, :], ALU.add))
                        then(tt(work[:, :, :], work[:, :, :], rest[:, 0:1, :].to_broadcast((P, N, E)), ALU.add))
                    then(tt(work[:, :, :], work[:, :, :], hot[:, k, :, :], ALU.mult))
                    then(nc.vector.reduce_sum(slot[:, k, :], work[:, :, :], AX.X))
                then(ts(keep[:, :, :], slot[:, :, :], float(CAPACITY), None, ALU.is_lt))
                then(ts(slot[:, :, :], slot[:, :, :], float(CAPACITY - 1), None, ALU.min))
                then(ts(index[:, :, :], index[:, :, :], float(CAPACITY), None, ALU.mult))
                then(tt(slot[:, :, :], slot[:, :, :], index[:, :, :], ALU.add))
                then(nc.vector.tensor_copy(place[:, :, :], slot[:, :, :]))
                then(ts(index[:, :, :], keep[:, :, :], -float(2 * EXPERTS * CAPACITY), float(2 * EXPERTS * CAPACITY), ALU.mult, ALU.add))
                then(tt(slot[:, :, :], slot[:, :, :], index[:, :, :], ALU.add))
                then(nc.vector.tensor_copy(scatter_to[:, :, :], slot[:, :, :]))
                for k in range(2):
                    then(tt(gates[:, k, :], small[:, k, :], small[:, 3, :], ALU.mult))
                    then(tt(gates[:, k, :], gates[:, k, :], keep[:, k, :], ALU.mult))

            @block.scalar
            def _(act):
                act.wait_ge(shifted, 2)
                nc.scalar.activation(ex[:, :, :], work[:, :, :], ACT.Exp).then_inc(exps_ready, 1)
                nc.scalar.activation(small[:, 2, :], small[:, 1, :], ACT.Exp).then_inc(exps_ready, 1)

            @block.tensor
            def _(pe):
                for k in range(2):
                    pe.wait_ge(hot_ready, k + 1)
                    nc.tensor.matmul(ps[:, 0, k, :, :], chip.c(C_BEFORE), hot[:, k, :, :], start=True, stop=True)
                    last = nc.tensor.matmul(ps[:, 1, k, :, :], chip.c(C_ONES), hot[:, k, :, :], start=True, stop=True)
                last.then_inc(counts_ready, 1)


def expert_ffn(chip):
    nc, io = chip.nc, chip.io
    slots = EXPERTS * CAPACITY
    ic, tiles = EXPERT_INNER // P, CAPACITY // P
    dispatched = nc.dram_tensor("dispatched", (slots, DIM), F32).ap()
    produced = nc.dram_tensor("produced", (slots, DIM), F32).ap()
    with ExitStack() as ctx:
        sb = lambda name, shape, dt=F32: ctx.enter_context(sbuf(nc, name, shape, dt))
        place, scatter_to = sb("place", [P, 2, TOKEN_TILES], U32), sb("scatter_to", [P, 2, TOKEN_TILES], U32)
        gates = sb("gates", [P, 2, TOKEN_TILES])
        with ExitStack() as early:
            rows = early.enter_context(sbuf(nc, "rows", [P, TOKEN_TILES, DIM], F32))
            logits = early.enter_context(sbuf(nc, "logits", [P, TOKEN_TILES, EXPERTS], F32))
            gate_w = early.enter_context(sbuf(nc, "gate_w", [P, FC, EXPERTS], F32))
            zeros = early.enter_context(sbuf(nc, "zeros", [P, 16 * DIM], F32))
            load(nc, [(gate_w[:, :, :], io["L0_ffn_wg"].rearrange("(c p) e -> p c e", p=P))])
            zeroed = chip.keep_semaphore("zeroed")
            whole = dispatched.rearrange("(n p r) d -> n p (r d)", p=P, r=16)
            with step(nc, "cleared") as (block, cleared):
                @block.gpsimd
                def _(pool):
                    nc.gpsimd.memset(zeros[:, :], 0.0).then_inc(cleared, 1)

                @block.sync
                def _(sp):
                    sp.wait_ge(cleared, 1)
                    for n in range(whole.shape[0]):
                        sp.dma_start(whole[n], zeros[:, :]).then_inc(zeroed, 16)
            token_rows(chip, rows, logits, gate_w)
            route(chip, logits, place, scatter_to, gates)
            scattered = chip.keep_semaphore("scattered")
            with nc.Block() as block:
                @block.gpsimd
                def _(pool):
                    pool.wait_ge(zeroed, 16 * whole.shape[0])
                    for t in range(TOKEN_TILES):
                        for k in range(2):
                            nc.gpsimd.indirect_dma_start(
                                out=dispatched, out_offset=bass.IndirectOffsetOnAxis(ap=scatter_to[:, k, t:t + 1], axis=0),
                                in_=rows[:, t, :], in_offset=None, bounds_check=slots - 1, oob_is_err=False).then_inc(scattered, 16)
                    pool.wait_ge(scattered, 16 * 2 * TOKEN_TILES)
        with ExitStack() as mid:
            eb = lambda name, shape: mid.enter_context(sbuf(nc, name, shape, F32))
            w1, w2 = eb("expert_w1", [P, 2, FC, EXPERT_INNER]), eb("expert_w2", [P, 2, ic, DIM])
            taken = eb("taken", [P, 2, tiles, DIM])
            taken_t = eb("taken_t", [P, FC, CAPACITY])
            h = eb("expert_hidden", [P, ic, GROUP])
            made = eb("made", [P, 2, tiles, DIM])
            turn_ps = mid.enter_context(banks(nc, "taken_psum", [P, 2, GROUP], F32))
            h_ps = mid.enter_context(banks(nc, "expert_psum", [P, 4, GROUP], F32))
            y_ps = mid.enter_context(banks(nc, "made_psum", [P, 2, GROUP], F32))
            per, parts = GROUP // P, CAPACITY // GROUP
            with nc.Fori(0, EXPERTS // ROUND_EXPERTS) as round_, step(
                    nc, "weights_loaded_0 weights_loaded_1 taken_loaded_0 taken_loaded_1 turned turned_copied h_ready hidden_ready y_ready made_ready stored_0 stored_1") as (
                    block, weights_loaded_0, weights_loaded_1, taken_loaded_0, taken_loaded_1, turned, turned_copied, h_ready, hidden_ready, y_ready, made_ready,
                    stored_0, stored_1):
                weights_loaded, taken_loaded, stored = (weights_loaded_0, weights_loaded_1), (taken_loaded_0, taken_loaded_1), (stored_0, stored_1)
                every, first = range(ROUND_EXPERTS), round_ * ROUND_EXPERTS

                @block.sync
                def _(sp):
                    def fetch(e):
                        i = e % 2
                        if e >= 2:
                            sp.wait_ge(turned, FC * parts * (e - 1))
                            sp.wait_ge(y_ready, tiles * (e - 1))
                        sp.dma_start(taken[:, i, :, :], dispatched[bass.ds((first + e) * CAPACITY, CAPACITY), :].rearrange("(t p) d -> p t d", p=P)).then_inc(taken_loaded[i], 16)
                        sp.dma_start(w1[:, i, :, :], io["L0_ffn_w1"][bass.ds((first + e) * DIM, DIM), :].rearrange("(c p) f -> p c f", p=P)).then_inc(weights_loaded[i], 16)
                        sp.dma_start(w2[:, i, :, :], io["L0_ffn_w2"][bass.ds((first + e) * EXPERT_INNER, EXPERT_INNER), :].rearrange("(c p) d -> p c d", p=P)).then_inc(weights_loaded[i], 16)

                    fetch(0)
                    fetch(1)
                    for e in every:
                        sp.wait_ge(made_ready, tiles * (e + 1))
                        sp.dma_start(produced[bass.ds((first + e) * CAPACITY, CAPACITY), :].rearrange("(t p) d -> p t d", p=P), made[:, e % 2, :, :]).then_inc(stored[e % 2], 16)
                        if e + 2 < ROUND_EXPERTS:
                            fetch(e + 2)
                    for i in range(2):
                        sp.wait_ge(stored[i], 16 * ROUND_EXPERTS // 2)

                @block.tensor
                def _(pe):
                    for e in every:
                        i = e % 2
                        pe.wait_ge(taken_loaded[i], 16 * (e // 2 + 1))
                        for c in range(FC):
                            for j in range(parts):
                                n = (e * FC + c) * parts + j
                                if n >= 2:
                                    pe.wait_ge(turned_copied, n - 1)
                                for t in range(per):
                                    last = nc.tensor.transpose(turn_ps[:, n % 2, t * P:(t + 1) * P], taken[:, i, j * per + t, c * P:(c + 1) * P], chip.c(C_ID))
                                last.then_inc(turned, 1)
                        pe.wait_ge(turned_copied, FC * parts * (e + 1))
                        pe.wait_ge(weights_loaded[i], 32 * (e // 2 + 1))
                        for j in range(parts):
                            for n in range(ic):
                                m = (e * parts + j) * ic + n
                                if m >= 4:
                                    pe.wait_ge(hidden_ready, m - 3)
                                for c in range(FC):
                                    last = nc.tensor.matmul(h_ps[:, m % 4, :], w1[:, i, c, n * P:(n + 1) * P], taken_t[:, c, j * GROUP:(j + 1) * GROUP],
                                                            start=(c == 0), stop=(c == FC - 1))
                                last.then_inc(h_ready, 1)
                            pe.wait_ge(hidden_ready, (e * parts + j + 1) * ic)
                            for t in range(per):
                                m = (e * parts + j) * per + t
                                if m >= 2:
                                    pe.wait_ge(made_ready, m - 1)
                                for n in range(ic):
                                    last = nc.tensor.matmul(y_ps[:, m % 2, 0:DIM], h[:, n, t * P:(t + 1) * P], w2[:, i, n, :], start=(n == 0), stop=(n == ic - 1))
                                last.then_inc(y_ready, 1)

                @block.scalar
                def _(act):
                    for m in range(ROUND_EXPERTS * parts * ic):
                        if m >= ic and m % ic == 0:
                            act.wait_ge(y_ready, m // ic * per)
                        act.wait_ge(h_ready, m + 1)
                        nc.scalar.activation(h[:, m % ic, :], h_ps[:, m % 4, :], ACT.Gelu).then_inc(hidden_ready, 1)

                @block.vector
                def _(dve):
                    for e in every:
                        if e:
                            dve.wait_ge(h_ready, e * parts * ic)
                        for c in range(FC):
                            for j in range(parts):
                                n = (e * FC + c) * parts + j
                                dve.wait_ge(turned, n + 1)
                                nc.vector.tensor_copy(taken_t[:, c, j * GROUP:(j + 1) * GROUP], turn_ps[:, n % 2, :]).then_inc(turned_copied, 1)
                        if e >= 2:
                            dve.wait_ge(stored[e % 2], 16 * (e // 2))
                        for m in range(e * tiles, (e + 1) * tiles):
                            dve.wait_ge(y_ready, m + 1)
                            nc.vector.tensor_copy(made[:, e % 2, m % tiles, :], y_ps[:, m % 2, 0:DIM]).then_inc(made_ready, 1)
        combine(chip, ctx, produced, place, gates)


def combine(chip, ctx, produced, place, gates):
    nc = chip.nc
    tiles, rounds = 2 * (GROUP // P), GROUPS // 2
    sb = lambda name, shape, dt=F32: ctx.enter_context(sbuf(nc, name, shape, dt))
    gathered = [chip.keep_semaphore(f"gathered_{t}") for t in range(tiles)]
    got = sb("got", [P, tiles, 2, DIM])
    at = sb("place_now", [P, tiles, 2], U32)
    gate = sb("gate_now", [P, 2, tiles])
    mixed = sb("mixed", [P, tiles, DIM])
    ps = ctx.enter_context(banks(nc, "norm_psum", [P, 8, GROUP], F32))

    def gather(g):
        def program(block, staged):
            @block.gpsimd
            def _(pool):
                nc.gpsimd.tensor_copy(at[:, :, :].rearrange("p t k -> p k t"), place[:, :, bass.ds(g * tiles, tiles)]).then_inc(staged, 1)
                pool.wait_ge(staged, 1)
                for t in range(tiles):
                    for k in range(2):
                        nc.gpsimd.indirect_dma_start(out=got[:, t, k, :], out_offset=None, in_=produced,
                                                     in_offset=bass.IndirectOffsetOnAxis(ap=at[:, t, k:k + 1], axis=0)).then_inc(gathered[t], 16)
        return program

    def mix(g, more):
        with step(nc, "mixed_ready turned dve_step") as (block, mixed_ready, turned, dve_step):
            @block.vector
            def _(dve):
                then = in_order(dve, dve_step)
                then(nc.vector.tensor_copy(gate[:, :, :], gates[:, :, bass.ds(g * tiles, tiles)]))
                for t in range(tiles):
                    dve.wait_ge(gathered[t], 32 * g + 32)
                    then(nc.vector.tensor_scalar(mixed[:, t, :], got[:, t, 0, :], gate[:, 0, t:t + 1], None, ALU.mult))
                    nc.vector.scalar_tensor_tensor(out=mixed[:, t, :], in0=got[:, t, 1, :], scalar=gate[:, 1, t:t + 1], in1=mixed[:, t, :],
                                                   op0=ALU.mult, op1=ALU.add).then_inc(mixed_ready, 1)

            @block.tensor
            def _(pe):
                per = tiles // 2
                for t in range(tiles):
                    pe.wait_ge(mixed_ready, t + 1)
                    for c in range(FC):
                        last = nc.tensor.transpose(ps[:, 4 * (t // per) + c, (t % per) * P:(t % per + 1) * P], mixed[:, t, c * P:(c + 1) * P], chip.c(C_ID))
                last.then_inc(turned, 1)
        add_norm(chip, [bass.ds((g * 2 + i) * GROUP, GROUP) for i in range(2)], ps, ready=lambda i, c: ps[:, 4 * i + c, :], beside=gather(g + 1) if more else None)

    with step(nc, "staged") as (block, staged):
        gather(0)(block, staged)
    with nc.Fori(0, rounds - 1) as g:
        mix(g, True)
    mix(rounds - 1, False)


WIDE_HEADS, WIDE = 8, 64
INNER = WIDE_HEADS * WIDE
DEPTH = 2
HIDDEN = DIM * 4 * 2 // 3
HC = -(-HIDDEN // P)


def local_transformer(chip):
    nc, io = chip.nc, chip.io
    with ExitStack() as ctx:
        sb = lambda name, shape: ctx.enter_context(sbuf(nc, name, shape, F32))
        inner = sb("inner", [P, FC, TOKENS])
        with step(nc, "copied") as (block, copied):
            @block.scalar
            def _(act):
                nc.scalar.activation(inner[:, :, :], chip.xt[:, :, :], ACT.Copy).then_inc(copied, 1)
                act.wait_ge(copied, 1)
        with nc.Fori(0, DEPTH) as layer:
            window_attention(chip, layer, inner)
            gated_ffn(chip, layer, inner)
        with banks(nc, "norm_psum", [P, 8, GROUP], F32) as ps, nc.Fori(0, GROUPS // 2) as pair:
            tok = lambda g: bass.ds((pair * 2 + g) * GROUP, GROUP)
            add_norm(chip, [tok(0), tok(1)], ps, ready=lambda g, c: inner[:, c, tok(g)])


class Tile:

    def __init__(self, b, c):
        self.b, self.c = b, c
        self.first = c % TILES == 0
        self.token = b * SEQ + c * P

    def count(self, per, offset=0):
        return self.b * (TILES * per) + (self.c * per + offset)

    def at_least(self, n):
        return not isinstance(self.b, int) or self.count(1) >= n

    def followed(self, n=1):
        return not isinstance(self.b, int) or self.count(1) + n < BATCH * TILES


def through_tiles(eng, late, iteration):
    def tile_of(b, k):
        def tile(lag):
            if isinstance(b, int) and not (b * TILES + k - lag >= 0 and k - lag < TILES):
                return None
            return Tile(b, k - lag)
        return tile

    for k in range(TILES):
        iteration(tile_of(0, k))
    with eng.Fori(1, BATCH) as b:
        for k in range(TILES):
            iteration(tile_of(b, k))
    for k in range(TILES, TILES + late):
        iteration(tile_of(BATCH - 1, k))


def window_attention(chip, layer, inner):
    nc, io = chip.nc, chip.io
    H2, HP, half, late = 2 * WIDE_HEADS, WIDE_HEADS // 2, WIDE // 2, 4
    oc = INNER // P
    with ExitStack() as ctx:
        sb = lambda name, shape, dt=F32: ctx.enter_context(sbuf(nc, name, shape, dt))
        wqkv = sb("wide_w", [P, FC, 3 * INNER])
        wo = sb("wide_wo", [P, oc, DIM])
        scales = sb("wide_scales", [P, 2, WIDE])
        tables = sb("rope", [P, 2, TILES, 2, WIDE])
        load(nc, [(tables[:, :, :, :, :], io["rope"]), (wqkv[:, :, :], io["L1_ffn_wqkv"][bass.ds(layer * DIM, DIM), :].rearrange("(c p) n -> p c n", p=P)),
                  (wo[:, :, :], io["L1_ffn_wo"][bass.ds(layer * INNER, INNER), :].rearrange("(c p) n -> p c n", p=P)),
                  (scales[:, :, :].rearrange("p a d -> p (a d)"), io["L1_ffn_scales"][bass.ds(layer, 1), :].partition_broadcast(P))])
        shifted = sb("shifted", [P, 2, FC, P])
        root = sb("qk_root", [P, 2, H2])
        qk, qk_cos = (sb(n, [P, 2, H2, WIDE]) for n in ("qk", "qk_cos"))
        squares, qk_sin = (t[:, :, :, :].rearrange("p n c t -> p n (c t)").rearrange("p n (h d) -> p n h d", d=WIDE) for t in (chip.z, chip.sq))
        qk_t = sb("qk_t", [P, 4, 2, HP, P])
        values = sb("wide_values", [P, 4, INNER])
        probs = sb("wide_probs", [P, 2, WIDE_HEADS, 2 * P])
        probs_t = sb("wide_probs_t", [P, 2, WIDE_HEADS, 2, P])
        top, den = sb("wide_max", [P, 2, WIDE_HEADS]), sb("wide_den", [P, 2, WIDE_HEADS])
        out = sb("wide_out", [P, 2, INNER])
        out_t = sb("wide_out_t", [P, 2, oc, P])
        masks = sb("window_masks", [P, 2, 2, P], BF16)
        product_ps = ctx.enter_context(banks(nc, "window_products", [P, 3, GROUP], F32))
        score_ps = ctx.enter_context(banks(nc, "window_scores", [P, 2, GROUP], F32))
        turn_ps = ctx.enter_context(banks(nc, "window_turned", [P, 2, GROUP], F32))
        out_ps = ctx.enter_context(banks(nc, "window_out", [P, GROUP], F32))
        with step(nc, "set_") as (block, set_):
            @block.vector
            def _(dve):
                for i in range(2):
                    nc.vector.tensor_copy(masks[:, i, 0, :], chip.c(C_FARN)).then_inc(set_, 1)
                    nc.vector.tensor_copy(masks[:, i, 1, :], chip.c(C_FART)).then_inc(set_, 1)
                wide = lambda t, d0: scales[:, t, d0:d0 + half].rearrange("p (o d) -> p o d", o=1).to_broadcast((P, TILES, half))
                for t in range(2):
                    for a in range(2):
                        for d0 in (0, half):
                            nc.vector.tensor_tensor(tables[:, a, :, t, d0:d0 + half], tables[:, a, :, t, d0:d0 + half], wide(t, d0 if a == 0 else half - d0),
                                                    ALU.mult).then_inc(set_, 1)
                dve.wait_ge(set_, 12)

        span = lambda i: P if i.first else 2 * P
        windows = lambda i: span(i) // P
        heads = lambda part: [HP * part + h for h in (0, 2, 1, 3)]
        both = lambda bank: bank.rearrange("p (h n) -> p h n", h=2)
        turned_bank = lambda bank, i: bank.rearrange("p (h s n) -> p h s n", h=2, s=2)[:, :, 0:windows(i), :]
        with step(nc, "shift_ready products_ready squares_ready sums_ready root_ready values_ready normed sin_ready qk_ready turned q_copied k_copied "
                      "scores_ready top_ready exps_ready probs_turned probs_copied_0 probs_copied_1 out_ready out_scaled out_turned out_copied "
                      "y_ready y_added max_ready clipped inverse_ready cos_ready den_ready") as (
                block, shift_ready, products_ready, squares_ready, sums_ready, root_ready, values_ready, normed, sin_ready, qk_ready, turned, q_copied, k_copied,
                scores_ready, top_ready, exps_ready, probs_turned, probs_copied_0, probs_copied_1, out_ready, out_scaled, out_turned, out_copied,
                y_ready, y_added, max_ready, clipped, inverse_ready, cos_ready, den_ready):

            @block.tensor
            def _(pe):
                def project(i):
                    pe.wait_ge(shift_ready, i.count(3, 3))
                    if i.at_least(1):
                        pe.wait_ge(normed, i.count(1))
                        pe.wait_ge(values_ready, i.count(1))
                    for n in range(3):
                        for c in range(FC):
                            last = nc.tensor.matmul(product_ps[:, n, :], shifted[:, i.c % 2, c, :], wqkv[:, c, n * INNER:(n + 1) * INNER], start=(c == 0), stop=(c == FC - 1))
                        last.then_inc(products_ready, 1)

                def turn_qk(i):
                    pe.wait_ge(qk_ready, i.count(1, 1))
                    if i.at_least(1):
                        pe.wait_ge(probs_copied_0, i.count(2, -1))
                        pe.wait_ge(probs_copied_1, i.count(2, -1))
                    for t in range(2):
                        for p in range(HP):
                            pair = t * WIDE_HEADS + 2 * p
                            last = nc.tensor.transpose(turn_ps[:, t, p * P:(p + 1) * P], qk[:, i.c % 2, pair:pair + 2, :].rearrange("p h d -> p (h d)"), chip.c(C_ID))
                        last.then_inc(turned, 1)

                def score(i, part):
                    if part == 0:
                        pe.wait_ge(q_copied, i.count(1, 1))
                        pe.wait_ge(k_copied, i.count(1, 1))
                    if part or i.at_least(1):
                        pe.wait_ge(exps_ready, i.count(WIDE_HEADS, HP * part))
                    for n in range(2):
                        nc.tensor.matmul(both(score_ps[:, n, :])[:, :, 0:span(i)], chip.id_bf[:, :],
                                         masks[:, :, :, :].rearrange("p h s n -> p h (s n)")[:, :, 0:span(i)], start=True, stop=False)
                    for m in range(2):
                        for which in range(windows(i)):
                            for n in range(2):
                                h = heads(part)[2 * n + m]
                                rows = slice(WIDE * (h % 2), WIDE * (h % 2) + WIDE)
                                last = nc.tensor.matmul(both(score_ps[:, n, :])[:, m, which * P:(which + 1) * P], qk_t[rows, i.c % 4, 0, h // 2, :],
                                                        qk_t[rows, (i.c - which) % 4, 1, h // 2, :], start=False, stop=(m == 1 and which == windows(i) - 1))
                    last.then_inc(scores_ready, 1)

                def turn_probs(i, part):
                    if part == 0:
                        if i.at_least(1):
                            pe.wait_ge(probs_copied_0, i.count(2))
                            pe.wait_ge(probs_copied_1, i.count(2))
                    else:
                        if i.followed():
                            pe.wait_ge(q_copied, i.count(1, 2))
                            pe.wait_ge(k_copied, i.count(1, 2))
                        else:
                            pe.wait_ge(probs_copied_0, i.count(2, 1))
                            pe.wait_ge(probs_copied_1, i.count(2, 1))
                        if i.at_least(1):
                            pe.wait_ge(out_copied, i.count(1))
                    pe.wait_ge(exps_ready, i.count(WIDE_HEADS, HP * (part + 1)))
                    for n in range(2):
                        for m in range(2):
                            h = HP * part + 2 * n + m
                            place = HP * part + heads(part).index(h)
                            for which in range(windows(i)):
                                at = (m * 2 + which) * P
                                last = nc.tensor.transpose(turn_ps[:, n, at:at + P], probs[:, i.c % 2, place, which * P:(which + 1) * P], chip.c(C_ID))
                        last.then_inc(probs_turned, 1)

                def weigh(i, part):
                    pe.wait_ge(probs_copied_0, i.count(2, part + 1))
                    pe.wait_ge(probs_copied_1, i.count(2, part + 1))
                    if part == 0:
                        pe.wait_ge(values_ready, i.count(1, 1))
                        if i.at_least(1):
                            pe.wait_ge(out_scaled, i.count(2))
                        if i.at_least(2):
                            pe.wait_ge(y_added, i.count(1, -1))
                    for h in range(HP * part, HP * (part + 1)):
                        for which in range(windows(i)):
                            last = nc.tensor.matmul(out_ps[:, h * WIDE:(h + 1) * WIDE], probs_t[:, i.c % 2, h, which, :],
                                                    values[:, (i.c - which) % 4, h * WIDE:(h + 1) * WIDE], start=(which == 0), stop=(which == windows(i) - 1))
                    if part:
                        last.then_inc(out_ready, 1)

                def turn_out(i):
                    pe.wait_ge(out_scaled, i.count(2, 2))
                    if i.followed(2):
                        pe.wait_ge(k_copied, i.count(1, 3))
                    elif i.followed():
                        pe.wait_ge(probs_copied_1, i.count(2, 3))
                    else:
                        pe.wait_ge(probs_copied_1, i.count(2, 2))
                    for c in range(oc):
                        last = nc.tensor.transpose(turn_ps[:, 1, c * P:(c + 1) * P], out[:, i.c % 2, c * P:(c + 1) * P], chip.c(C_ID))
                    last.then_inc(out_turned, 1)

                def multiply_out(i):
                    pe.wait_ge(out_copied, i.count(1, 1))
                    pe.wait_ge(out_scaled, i.count(2, 4 if i.followed() else 2))
                    if not i.followed():
                        pe.wait_ge(y_added, i.count(1))
                    for c in range(FC):
                        for k in range(oc):
                            last = nc.tensor.matmul(out_ps[:, c * P:(c + 1) * P], wo[:, k, c * P:(c + 1) * P], out_t[:, i.c % 2, k, :],
                                                    start=(k == 0), stop=(k == oc - 1))
                    last.then_inc(y_ready, 1)

                def iteration(tile):
                    now, one, two, three, four = (tile(lag) for lag in range(5))
                    if now:
                        project(now)
                    if two:
                        turn_probs(two, 0)
                        score(two, 1)
                    if four:
                        multiply_out(four)
                    if one:
                        turn_qk(one)
                    if two:
                        weigh(two, 0)
                    if three:
                        turn_out(three)
                    if two:
                        turn_probs(two, 1)
                    if one:
                        score(one, 0)
                    if two:
                        weigh(two, 1)

                through_tiles(pe, late, iteration)

            @block.scalar
            def _(act):
                def exps(i, part):
                    act.wait_ge(top_ready, i.count(2, part + 1))
                    if part == 0 and i.at_least(2):
                        act.wait_ge(probs_turned, i.count(4, -4))
                        act.wait_ge(out_scaled, i.count(2, -2))
                    for n in range(HP):
                        at = HP * part + n
                        nc.scalar.activation(probs[:, i.c % 2, at, 0:span(i)], both(score_ps[:, n // 2, :])[:, n % 2, 0:span(i)], ACT.Exp, scale=WIDE ** 0.5,
                                             bias=top[:, i.c % 2, at:at + 1], accum_out=den[:, i.c % 2, at:at + 1]).then_inc(exps_ready, 1)

                def copy_probs(i, part):
                    act.wait_ge(probs_turned, i.count(4, 2 * part + 1))
                    if part == 0 and i.at_least(2):
                        act.wait_ge(out_ready, i.count(1, -1))
                    at = HP * part
                    nc.scalar.activation(probs_t[:, i.c % 2, at:at + 2, 0:windows(i), :], turned_bank(turn_ps[:, 0, :], i), ACT.Copy).then_inc(probs_copied_0, 1)

                def iteration(tile):
                    now, one, two = (tile(lag) for lag in range(3))
                    if two:
                        exps(two, 0)
                    if now:
                        i = now
                        act.wait_ge(products_ready, i.count(3, 2))
                        if i.at_least(2):
                            act.wait_ge(sums_ready, i.count(1, -1))
                        nc.scalar.activation(squares[:, i.c % 2, :, :].rearrange("p h d -> p (h d)"), product_ps[:, 0:2, :].rearrange("p b n -> p (b n)"),
                                             ACT.Square).then_inc(squares_ready, 1)
                        act.wait_ge(products_ready, i.count(3, 3))
                        if i.at_least(3):
                            act.wait_ge(out_ready, i.count(1, -2))
                        nc.scalar.activation(values[:, i.c % 4, :], product_ps[:, 2, :], ACT.Copy).then_inc(values_ready, 1)
                        act.wait_ge(sums_ready, i.count(1, 1))
                        nc.scalar.activation(root[:, i.c % 2, :], root[:, i.c % 2, :], ACT.Sqrt).then_inc(root_ready, 1)
                    if two:
                        copy_probs(two, 0)
                        exps(two, 1)
                    if one:
                        act.wait_ge(turned, one.count(2, 1))
                        if one.at_least(3):
                            act.wait_ge(scores_ready, one.count(2, -4))
                        nc.scalar.activation(qk_t[:, one.c % 4, 0, :, :].rearrange("p h n -> p (h n)"), turn_ps[:, 0, :], ACT.Copy).then_inc(q_copied, 1)
                    if two:
                        copy_probs(two, 1)

                through_tiles(act, late, iteration)

            @block.vector
            def _(dve):
                tt, ts, copy = nc.vector.tensor_tensor, nc.vector.tensor_scalar, nc.vector.tensor_copy

                def shift(i):
                    if i.at_least(2):
                        dve.wait_ge(products_ready, i.count(3, -3))
                    copy(shifted[:, i.c % 2, 0, :], inner[:, 0, bass.ds(i.token, P)]).then_inc(shift_ready, 1)
                    copy(shifted[:, i.c % 2, 1, 1:P], inner[:, 1, bass.ds(i.token, P - 1)]).then_inc(shift_ready, 1)
                    before = shifted[:, i.c % 2, 1, 0:1]
                    if i.first:
                        nc.vector.memset(before, 0.0).then_inc(shift_ready, 1)
                    else:
                        copy(before, inner[:, 1, bass.ds(i.token - 1, 1)]).then_inc(shift_ready, 1)

                def maxima(i, part):
                    dve.wait_ge(scores_ready, i.count(2, part + 1))
                    if part == 0 and i.at_least(2):
                        dve.wait_ge(exps_ready, i.count(WIDE_HEADS, -WIDE_HEADS))
                    own = top[:, i.c % 2, HP * part:HP * (part + 1)]
                    nc.vector.reduce_max(own, score_ps[:, :, :].rearrange("p b (h n) -> p (b h) n", h=2)[:, :, 0:span(i)], AX.X).then_inc(max_ready, 1)
                    dve.wait_ge(max_ready, i.count(2, part + 1))
                    ts(own, own, -WIDE ** 0.5, None, ALU.mult).then_inc(top_ready, 1)

                def normalise(i):
                    own = root[:, i.c % 2, :]
                    dve.wait_ge(root_ready, i.count(1, 1))
                    ts(own, own, 1e-12, None, ALU.max).then_inc(clipped, 1)
                    dve.wait_ge(clipped, i.count(1, 1))
                    nc.vector.reciprocal(own, own).then_inc(inverse_ready, 1)
                    dve.wait_ge(inverse_ready, i.count(1, 1))
                    if i.at_least(2):
                        dve.wait_ge(turned, i.count(2, -2))
                    tt(qk[:, i.c % 2, :, :], product_ps[:, 0:2, :].rearrange("p b (h d) -> p (b h) d", d=WIDE),
                       own.rearrange("p (h o) -> p h o", o=1).to_broadcast((P, H2, WIDE)), ALU.mult).then_inc(normed, 1)

                def cosines(i):
                    dve.wait_ge(normed, i.count(1, 1))
                    for t in range(2):
                        own = slice(t * WIDE_HEADS, (t + 1) * WIDE_HEADS)
                        table = tables[:, 0, i.c % TILES, t, :].rearrange("p (o d) -> p o d", o=1).to_broadcast((P, WIDE_HEADS, WIDE))
                        tt(qk_cos[:, i.c % 2, own, :], qk[:, i.c % 2, own, :], table, ALU.mult).then_inc(cos_ready, 1)

                def rotated(i):
                    dve.wait_ge(cos_ready, i.count(2, 2))
                    dve.wait_ge(sin_ready, i.count(4, 4))
                    tt(qk[:, i.c % 2, :, :], qk_cos[:, i.c % 2, :, :], qk_sin[:, i.c % 2, :, :], ALU.add).then_inc(qk_ready, 1)

                def copy_probs(i, part):
                    dve.wait_ge(probs_turned, i.count(4, 2 * part + 2))
                    if part == 0 and i.at_least(2):
                        dve.wait_ge(out_ready, i.count(1, -1))
                    at = HP * part + 2
                    copy(probs_t[:, i.c % 2, at:at + 2, 0:windows(i), :], turned_bank(turn_ps[:, 1, :], i)).then_inc(probs_copied_1, 1)

                def scale_out(i):
                    own = den[:, i.c % 2, :]
                    dve.wait_ge(out_ready, i.count(1, 1))
                    nc.vector.reciprocal(own, own).then_inc(den_ready, 1)
                    dve.wait_ge(den_ready, i.count(1, 1))
                    if i.at_least(2):
                        dve.wait_ge(out_turned, i.count(1, -1))
                    for part in range(2):
                        inv = den[:, i.c % 2, HP * part:HP * (part + 1)].rearrange("p (a c o) -> p c a o", a=2, o=1).to_broadcast((P, 2, 2, WIDE))
                        side = lambda t: t[:, part * HP * WIDE:(part + 1) * HP * WIDE].rearrange("p (c a d) -> p c a d", a=2, d=WIDE)
                        tt(side(out[:, i.c % 2, :]), side(out_ps[:, :]), inv, ALU.mult).then_inc(out_scaled, 1)

                def iteration(tile):
                    now, one, two, three, four = (tile(lag) for lag in range(5))
                    if now:
                        shift(now)
                    if two:
                        maxima(two, 0)
                    if three:
                        scale_out(three)
                    if now:
                        dve.wait_ge(squares_ready, now.count(1, 1))
                        nc.vector.reduce_sum(root[:, now.c % 2, :], squares[:, now.c % 2, :, :], AX.X).then_inc(sums_ready, 1)
                    if two:
                        copy_probs(two, 0)
                    if now:
                        normalise(now)
                    if two:
                        maxima(two, 1)
                    if now:
                        cosines(now)
                    if four:
                        dve.wait_ge(y_ready, four.count(1, 1))
                        at = inner[:, :, bass.ds(four.token, P)]
                        tt(at, out_ps[:, 0:DIM].rearrange("p (c n) -> p c n", c=FC), at, ALU.add).then_inc(y_added, 1)
                    if one:
                        dve.wait_ge(turned, one.count(2, 2))
                        if one.at_least(3):
                            dve.wait_ge(scores_ready, one.count(2, -4))
                        copy(qk_t[:, one.c % 4, 1, :, :].rearrange("p h n -> p (h n)"), turn_ps[:, 1, :]).then_inc(k_copied, 1)
                    if now:
                        rotated(now)
                    if three:
                        dve.wait_ge(out_turned, three.count(1, 1))
                        if three.at_least(2):
                            dve.wait_ge(y_ready, three.count(1, -1))
                        copy(out_t[:, three.c % 2, :, :].rearrange("p c n -> p (c n)"), turn_ps[:, 1, :]).then_inc(out_copied, 1)
                    if two:
                        copy_probs(two, 1)

                through_tiles(dve, late, iteration)

            @block.gpsimd
            def _(pool):
                def iteration(tile):
                    i = tile(0)
                    if i:
                        pool.wait_ge(normed, i.count(1, 1))
                        for t in range(2):
                            own = slice(t * WIDE_HEADS, (t + 1) * WIDE_HEADS)
                            for d0 in (0, half):
                                table = tables[:, 1, i.c % TILES, t, d0:d0 + half].rearrange("p (o d) -> p o d", o=1).to_broadcast((P, WIDE_HEADS, half))
                                nc.gpsimd.tensor_tensor(qk_sin[:, i.c % 2, own, d0:d0 + half], qk[:, i.c % 2, own, half - d0:WIDE - d0], table, ALU.mult).then_inc(sin_ready, 1)

                through_tiles(pool, late, iteration)


def gated_ffn(chip, layer, inner):
    nc, io = chip.nc, chip.io
    with ExitStack() as ctx:
        sb = lambda name, shape: ctx.enter_context(sbuf(nc, name, shape, F32))
        w1, w2 = sb("gated_w1", [P, FC, 2 * HC * P]), sb("gated_w2", [P, HC, DIM])
        b1, b2, affine = sb("gated_b1", [P, 2 * HC]), sb("gated_b2", [P, FC]), sb("gated_norm", [P, 2 * FC])
        load(nc, [(w1[:, :, :], io["L1_ffn_w1"][bass.ds(layer * DIM, DIM), :].rearrange("(c p) n -> p c n", p=P)),
                  (w2[:, :, :], io["L1_ffn_w2"][bass.ds(layer * HC * P, HC * P), :].rearrange("(c p) n -> p c n", p=P)),
                  (b1[:, :], io["L1_ffn_b1"][bass.ds(layer * P, P), :]), (b2[:, :], io["L1_ffn_b2"][bass.ds(layer * P, P), :]),
                  (affine[:, :], io["L1_ffn_ln"][bass.ds(layer * P, P), :])])
        h, sq, root = chip.z, chip.sq, chip.root
        gate = sb("gate", [P, 2, GROUP])
        hidden = sb("gated_hidden", [P, 2, HC, GROUP])
        after = sb("gated_after", [P, FC, TOKENS])
        st_ps = ctx.enter_context(banks(nc, "gated_stats", [P, 2, GROUP], F32))
        h_ps = ctx.enter_context(banks(nc, "gated_psum", [P, 4, GROUP], F32))
        y_ps = ctx.enter_context(banks(nc, "gated_out", [P, 2, GROUP], F32))
        with nc.Fori(0, BATCH) as b, step(
                nc, "shift_ready mean_ready centred squares_ready var_ready root_ready inverse_ready rstd_ready normed pair_ready gate_ready hidden_ready y_ready y_added dve_step") as (
                block, shift_ready, mean_ready, centred, squares_ready, var_ready, root_ready, inverse_ready, rstd_ready, normed, pair_ready, gate_ready, hidden_ready,
                y_ready, y_added, dve_step):
            at = lambda j: b * SEQ + j * GROUP
            pairs = [(j, n) for j in range(HALVES) for n in range(HC)]

            @block.tensor
            def _(pe):
                for j in range(HALVES):
                    pe.wait_ge(shift_ready, FC * (j + 1))
                    for c in range(FC):
                        last = nc.tensor.matmul(st_ps[:, j, :], chip.c(C_MEAN), h[:, j, c, :], start=(c == 0), stop=(c == FC - 1))
                    last.then_inc(mean_ready, 1)
                for j in range(HALVES):
                    pe.wait_ge(squares_ready, FC * (j + 1))
                    for t in range(PER_HALF):
                        for c in range(FC):
                            last = nc.tensor.matmul(st_ps[:, j, t:t + 1], sq[:, j, c, t * P:(t + 1) * P], chip.c(C_MEAN, 1), start=(c == 0), stop=(c == FC - 1))
                    last.then_inc(var_ready, 1)
                for j in range(HALVES):
                    pe.wait_ge(inverse_ready, j + 1)
                    for t in range(PER_HALF):
                        last = nc.tensor.matmul(st_ps[:, j, t * P:(t + 1) * P], root[:, j, t:t + 1].to_broadcast((P, P)), chip.c(C_ID), start=True, stop=True)
                    last.then_inc(rstd_ready, 1)
                for k, (j, n) in enumerate(pairs):
                    pe.wait_ge(normed, FC * (j + 1))
                    if k >= 2:
                        pe.wait_ge(hidden_ready, k - 1)
                    for part in range(2):
                        for c in range(FC):
                            m = part * HC + n
                            last = nc.tensor.matmul(h_ps[:, 2 * (k % 2) + part, :], w1[:, c, m * P:(m + 1) * P], h[:, j, c, :], start=(c == 0), stop=(c == FC - 1))
                    last.then_inc(pair_ready, 1)
                for j in range(HALVES):
                    for c in range(FC):
                        if j:
                            pe.wait_ge(y_added, c + 1)
                        for n in range(HC):
                            pe.wait_ge(hidden_ready, HC * j + n + 1)
                            last = nc.tensor.matmul(y_ps[:, c, :], w2[:, n, c * P:(c + 1) * P], hidden[:, j, n, :], start=(n == 0), stop=(n == HC - 1))
                        last.then_inc(y_ready, 1)

            @block.scalar
            def _(act):
                for j in range(HALVES):
                    for c in range(FC):
                        act.wait_ge(centred, FC * j + c + 1)
                        nc.scalar.activation(sq[:, j, c, :], h[:, j, c, :], ACT.Square).then_inc(squares_ready, 1)
                for j in range(HALVES):
                    act.wait_ge(var_ready, j + 1)
                    nc.scalar.activation(root[:, j, :], st_ps[:, j, 0:PER_HALF], ACT.Sqrt, bias=chip.eps[:, 0:1]).then_inc(root_ready, 1)
                for k, (j, n) in enumerate(pairs):
                    act.wait_ge(pair_ready, k + 1)
                    if k >= 2:
                        act.wait_ge(hidden_ready, k - 1)
                    nc.scalar.activation(gate[:, k % 2, :], h_ps[:, 2 * (k % 2) + 1, :], ACT.Gelu, bias=b1[:, HC + n:HC + n + 1]).then_inc(gate_ready, 1)

            @block.vector
            def _(dve):
                then = in_order(dve, dve_step)
                for j in range(HALVES):
                    nc.vector.tensor_copy(h[:, j, 0, :], inner[:, 0, bass.ds(at(j), GROUP)]).then_inc(shift_ready, 1)
                    if j == 0:
                        then(nc.vector.memset(h[:, 0, 1, 0:1], 0.0))
                        nc.vector.tensor_copy(h[:, 0, 1, 1:GROUP], inner[:, 1, bass.ds(at(0), GROUP - 1)]).then_inc(shift_ready, 1)
                    else:
                        nc.vector.tensor_copy(h[:, j, 1, :], inner[:, 1, bass.ds(at(j) - 1, GROUP)]).then_inc(shift_ready, 1)
                for j in range(HALVES):
                    dve.wait_ge(mean_ready, j + 1)
                    for c in range(FC):
                        nc.vector.tensor_tensor(h[:, j, c, :], h[:, j, c, :], st_ps[:, j, :], ALU.subtract).then_inc(centred, 1)
                for j in range(HALVES):
                    dve.wait_ge(root_ready, j + 1)
                    nc.vector.reciprocal(root[:, j, :], root[:, j, :]).then_inc(inverse_ready, 1)
                for j in range(HALVES):
                    dve.wait_ge(rstd_ready, j + 1)
                    for c in range(FC):
                        then(nc.vector.tensor_tensor(h[:, j, c, :], h[:, j, c, :], st_ps[:, j, :], ALU.mult))
                        nc.vector.tensor_scalar(h[:, j, c, :], h[:, j, c, :], affine[:, c:c + 1], affine[:, FC + c:FC + c + 1], ALU.mult, ALU.add).then_inc(normed, 1)
                for k, (j, n) in enumerate(pairs):
                    dve.wait_ge(gate_ready, k + 1)
                    nc.vector.scalar_tensor_tensor(out=hidden[:, j, n, :], in0=h_ps[:, 2 * (k % 2), :], scalar=b1[:, n:n + 1], in1=gate[:, k % 2, :],
                                                   op0=ALU.add, op1=ALU.mult).then_inc(hidden_ready, 1)
                for j in range(HALVES):
                    for c in range(FC):
                        dve.wait_ge(y_ready, FC * j + c + 1)
                        nc.vector.scalar_tensor_tensor(out=after[:, c, bass.ds(at(j), GROUP)], in0=y_ps[:, c, :], scalar=b2[:, c:c + 1],
                                                       in1=inner[:, c, bass.ds(at(j), GROUP)], op0=ALU.add, op1=ALU.add).then_inc(y_added, 1)
        with step(nc, "copied") as (block, copied):
            @block.scalar
            def _(act):
                nc.scalar.activation(inner[:, 0, :], after[:, 0, :], ACT.Copy).then_inc(copied, 1)

            @block.vector
            def _(dve):
                nc.vector.tensor_copy(inner[:, 1, :], after[:, 1, :]).then_inc(copied, 1)


STATES, TAPS, RANK = 16, 4, 64
SC = 2 * DIM // P


def state_space(chip):
    nc, io = chip.nc, chip.io
    halves = SEQ // GROUP
    width = SC * P
    with ExitStack() as ctx:
        sb = lambda name, shape: ctx.enter_context(sbuf(nc, name, shape, F32))
        w_in, w_out = sb("in_w", [P, FC, 2 * width]), sb("out_w", [P, SC, DIM])
        w_x, w_dt = sb("x_w", [P, SC, RANK + 2 * STATES]), sb("dt_w", [RANK, width])
        conv = sb("conv_w", [P, SC, TAPS])
        per_feature = sb("ssm_vectors", [P, 3, SC])
        norm_w = sb("ssm_norm", [P, FC])
        a_log = sb("a_log", [P, SC, STATES])
        w_states = sb("states_w", [P, SC, PARTS * 2 * STATES])
        pick = ctx.enter_context(sbuf(nc, "pick", [PARTS * 2 * STATES, 2 * STATES * P], BF16))
        load(nc, [(w_in[:, :, :], io["L2_attn_win"].rearrange("(c p) n -> p c n", p=P)),
                  (w_out[:, :, :], io["L2_attn_wout"].rearrange("(c p) n -> p c n", p=P)),
                  (w_x[:, :, :], io["L2_attn_wx"].rearrange("(c p) n -> p c n", p=P)), (w_dt[:, :], io["L2_attn_wdt"]),
                  (conv[:, :, :], io["L2_attn_conv"].rearrange("(c p) k -> p c k", p=P)), (per_feature[:, :, :], io["L2_attn_vec"]),
                  (norm_w[:, :], io["L2_attn_norm"]), (a_log[:, :, :], io["L2_attn_alog"].rearrange("(c p) n -> p c n", p=P)),
                  ])
        xs = sb("ssm_x", [P, SC, TAPS - 1 + SEQ])
        gate = sb("ssm_gate", [P, SC, SEQ])
        states = ctx.enter_context(sbuf(nc, "ssm_states", [PARTS * 2 * STATES, SEQ], BF16))
        u, dt, du = sb("ssm_u", [P, SC, SEQ]), sb("ssm_dt", [P, SC, SEQ]), sb("ssm_du", [P, SC, SEQ])
        whole_pick = u[0:PARTS * 2 * STATES, :, :].rearrange("p c t -> p (c t)")
        load(nc, [(whole_pick, io["pick"])])
        with step(nc, "exp_ready dve_step") as (block, exp_ready, dve_step):
            @block.scalar
            def _(act):
                nc.scalar.activation(a_log[:, :, :], a_log[:, :, :], ACT.Exp).then_inc(exp_ready, 1)

            @block.vector
            def _(dve):
                dve.wait_ge(exp_ready, 1)
                then = in_order(dve, dve_step)
                then(nc.vector.tensor_scalar(a_log[:, :, :], a_log[:, :, :], -1.0, None, ALU.mult))
                then(nc.vector.memset(xs[:, :, 0:TAPS - 1], 0.0))
                then(nc.vector.tensor_copy(pick[:, :], whole_pick))
                for part in range(PARTS):
                    then(nc.vector.tensor_copy(w_states[:, :, part * 2 * STATES:(part + 1) * 2 * STATES], w_x[:, :, RANK:RANK + 2 * STATES]))
        with nc.Fori(0, BATCH) as b:
            ssm_inputs(chip, b, w_in, norm_w, xs, gate)
            ssm_steps(chip, conv, per_feature, w_x, w_states, w_dt, xs, states, u, dt, du)
            ssm_scan(chip, a_log, pick, states, u, dt, du, gate, per_feature)
            with banks(nc, "norm_psum", [P, 8, GROUP], F32) as norm_ps:
                add_norm(chip, [bass.ds(b * SEQ + j * GROUP, GROUP) for j in range(halves)], norm_ps, keeps=2.0,
                         product=(w_out, lambda j, k: u[:, k, j * GROUP:(j + 1) * GROUP]))


def ssm_inputs(chip, b, w_in, norm_w, xs, gate):
    nc = chip.nc
    halves = SEQ // GROUP
    with ExitStack() as ctx:
        h = ctx.enter_context(sbuf(nc, "ssm_in", [P, FC, SEQ], F32))
        sq, rms = chip.sq[:, 0, :, :], chip.z[:, 0, 0, :]
        mean_ps = ctx.enter_context(banks(nc, "ssm_mean", [P, 2, GROUP], F32))
        in_ps = ctx.enter_context(banks(nc, "ssm_in_psum", [P, 4, GROUP], F32))
        with step(nc, "squares_ready mean_ready rms_ready h_ready in_ready in_copied dve_step") as (
                block, squares_ready, mean_ready, rms_ready, h_ready, in_ready, in_copied, dve_step):
            jobs = [(m, j) for m in range(2 * SC) for j in range(halves)]
            x = lambda c, j: chip.xt[:, c, bass.ds(b * SEQ + j * GROUP, GROUP)]

            @block.scalar
            def _(act):
                for j in range(halves):
                    if j:
                        act.wait_ge(mean_ready, j)
                    for c in range(FC):
                        nc.scalar.activation(sq[:, c, :], x(c, j), ACT.Square).then_inc(squares_ready, 1)
                    act.wait_ge(mean_ready, j + 1)
                    if j:
                        act.wait_ge(h_ready, j)
                    nc.scalar.activation(rms[:, :], mean_ps[:, j, :], ACT.Sqrt, bias=chip.eps[:, 0:1]).then_inc(rms_ready, 1)
                for n, (m, j) in enumerate(jobs):
                    act.wait_ge(in_ready, n + 1)
                    part = slice(j * GROUP, (j + 1) * GROUP)
                    if m < SC:
                        dst = xs[:, m, TAPS - 1 + j * GROUP:TAPS - 1 + (j + 1) * GROUP]
                        nc.scalar.activation(dst, in_ps[:, n % 4, :], ACT.Copy).then_inc(in_copied, 1)
                    else:
                        nc.scalar.activation(gate[:, m - SC, part], in_ps[:, n % 4, :], ACT.Silu).then_inc(in_copied, 1)

            @block.tensor
            def _(pe):
                for j in range(halves):
                    pe.wait_ge(squares_ready, FC * (j + 1))
                    for c in range(FC):
                        last = nc.tensor.matmul(mean_ps[:, j, :], chip.c(C_MEAN), sq[:, c, :], start=(c == 0), stop=(c == FC - 1))
                    last.then_inc(mean_ready, 1)
                pe.wait_ge(h_ready, halves)
                for n, (m, j) in enumerate(jobs):
                    if n >= 4:
                        pe.wait_ge(in_copied, n - 3)
                    for c in range(FC):
                        last = nc.tensor.matmul(in_ps[:, n % 4, :], w_in[:, c, m * P:(m + 1) * P], h[:, c, j * GROUP:(j + 1) * GROUP],
                                                start=(c == 0), stop=(c == FC - 1))
                    last.then_inc(in_ready, 1)

            @block.vector
            def _(dve):
                then = in_order(dve, dve_step)
                for j in range(halves):
                    dve.wait_ge(rms_ready, j + 1)
                    then(nc.vector.reciprocal(rms[:, :], rms[:, :]))
                    for c in range(FC):
                        last = nc.vector.scalar_tensor_tensor(out=h[:, c, j * GROUP:(j + 1) * GROUP], in0=x(c, j), scalar=norm_w[:, c:c + 1],
                                                              in1=rms[:, :], op0=ALU.mult, op1=ALU.mult)
                    last.then_inc(h_ready, 1)


def ssm_steps(chip, conv, per_feature, w_x, w_states, w_dt, xs, states, u, dt, du):
    nc = chip.nc
    halves, rows = SEQ // GROUP, PARTS * 2 * STATES
    with ExitStack() as ctx:
        sb = lambda name, shape: ctx.enter_context(sbuf(nc, name, shape, F32))
        pre = sb("ssm_pre", [P, SC, SEQ])
        logs = sb("ssm_logs", [P, SC, SEQ])
        series = sb("ssm_series", [P, SEQ])
        low, rest = sb("ssm_low", [RANK, SEQ]), series[0:rows, :]
        low_ps = ctx.enter_context(banks(nc, "ssm_low_psum", [P, 2, GROUP], F32))
        dt_ps = ctx.enter_context(banks(nc, "ssm_dt_psum", [P, 2, 2, GROUP], F32))
        st_ps = ctx.enter_context(banks(nc, "ssm_states_psum", [P, 2, GROUP], F32))
        with step(nc, "conv_ready u_ready low_ready low_copied rest_ready dt_ready shifted_ready size_ready exp_ready log_ready dt_done dve_step") as (
                block, conv_ready, u_ready, low_ready, low_copied, rest_ready, dt_ready, shifted_ready, size_ready, exp_ready, log_ready, dt_done, dve_step):
            flat = lambda t: t.rearrange("p b n -> p (b n)")
            z = lambda c: flat(dt_ps[:, c % 2, :, :])

            @block.vector
            def _(dve):
                then = in_order(dve, dve_step)
                stt, tt, copy = nc.vector.scalar_tensor_tensor, nc.vector.tensor_tensor, nc.vector.tensor_copy
                for c in range(SC):
                    acc = pre[:, c, :]
                    for k in range(TAPS):
                        tap = xs[:, c, k:k + SEQ]
                        if k == 0:
                            then(nc.vector.tensor_scalar(acc, tap, conv[:, c, 0:1], per_feature[:, 0, c:c + 1], ALU.mult, ALU.add))
                        else:
                            last = stt(out=acc, in0=tap, scalar=conv[:, c, k:k + 1], in1=acc, op0=ALU.mult, op1=ALU.add)
                            if k < TAPS - 1:
                                then(last)
                    last.then_inc(conv_ready, 1)

                def shift(c):
                    dve.wait_ge(dt_ready, c + 1)
                    nc.vector.tensor_scalar(dt[:, c, :], z(c), per_feature[:, 1, c:c + 1], 0.0, ALU.add, ALU.max).then_inc(shifted_ready, 1)

                shift(0)
                shift(1)
                dve.wait_ge(rest_ready, 1)
                third = lambda t, n: t[n * 2 * STATES:(n + 1) * 2 * STATES, :]
                then(copy(states[:, :], rest))
                then(tt(rest, rest, states[:, :], ALU.subtract))
                then(copy(third(states, 1), third(rest, 1)))
                then(copy(third(states, 2), third(rest, 2)))
                then(tt(third(rest, 2), third(rest, 2), third(states, 2), ALU.subtract))
                then(copy(third(states, 2), third(rest, 2)))
                shift(2)
                shift(3)
                edge = 2.0 ** -6
                for c in range(SC):
                    dve.wait_ge(exp_ready, c + 1)
                    e, log = pre[:, c, :], logs[:, c, :]
                    then(nc.vector.tensor_scalar(series[:, :], e, -1 / 4, 1 / 3, ALU.mult, ALU.add))
                    then(tt(series[:, :], series[:, :], e, ALU.mult))
                    then(stt(out=series[:, :], in0=series[:, :], scalar=-0.5, in1=e, op0=ALU.add, op1=ALU.mult))
                    then(stt(out=series[:, :], in0=series[:, :], scalar=1.0, in1=e, op0=ALU.add, op1=ALU.mult))
                    dve.wait_ge(log_ready, c + 1)
                    then(stt(out=log, in0=e, scalar=edge, in1=log, op0=ALU.is_lt, op1=ALU.subtract))
                    then(stt(out=series[:, :], in0=log, scalar=-1.0, in1=series[:, :], op0=ALU.mult, op1=ALU.max))
                    dve.wait_ge(shifted_ready, c + 1)
                    tt(dt[:, c, :], dt[:, c, :], series[:, :], ALU.add).then_inc(dt_done, 1)
                    dve.wait_ge(dt_done, c + 1)

            @block.gpsimd
            def _(pool):
                for c in range(SC):
                    pool.wait_ge(dt_done, c + 1)
                    nc.gpsimd.tensor_tensor(du[:, c, :], dt[:, c, :], u[:, c, :], ALU.mult)

            @block.scalar
            def _(act):
                for c in range(SC):
                    act.wait_ge(conv_ready, c + 1)
                    nc.scalar.activation(u[:, c, :], pre[:, c, :], ACT.Silu).then_inc(u_ready, 1)
                act.wait_ge(low_ready, 1)
                nc.scalar.activation(low[:, :], flat(low_ps[:, :, :])[0:RANK, :], ACT.Copy).then_inc(low_copied, 1)
                nc.scalar.activation(rest, flat(st_ps[:, :, :])[0:rows, :], ACT.Copy).then_inc(rest_ready, 1)
                for c in range(SC):
                    act.wait_ge(shifted_ready, c + 1)
                    act.wait_ge(u_ready, c + 1)
                    nc.scalar.activation(pre[:, c, :], z(c), ACT.Abs, bias=per_feature[:, 1, c:c + 1]).then_inc(size_ready, 1)
                for c in range(SC):
                    act.wait_ge(size_ready, c + 1)
                    nc.scalar.activation(pre[:, c, :], pre[:, c, :], ACT.Exp, scale=-1.0).then_inc(exp_ready, 1)
                for c in range(SC):
                    act.wait_ge(exp_ready, c + 1)
                    nc.scalar.activation(logs[:, c, :], pre[:, c, :], ACT.Ln, bias=chip.eps[:, 2:3]).then_inc(log_ready, 1)

            @block.tensor
            def _(pe):
                for c in range(SC):
                    pe.wait_ge(u_ready, c + 1)
                    for j in range(halves):
                        own = u[:, c, j * GROUP:(j + 1) * GROUP]
                        nc.tensor.matmul(low_ps[0:RANK, j, :], w_x[:, c, 0:RANK], own, start=(c == 0), stop=(c == SC - 1))
                        last = nc.tensor.matmul(st_ps[0:rows, j, :], w_states[:, c, :], own, start=(c == 0), stop=(c == SC - 1))
                last.then_inc(low_ready, 1)
                pe.wait_ge(low_copied, 1)
                for c in range(SC):
                    if c >= 2:
                        pe.wait_ge(shifted_ready, c - 1)
                        pe.wait_ge(size_ready, c - 1)
                    for j in range(halves):
                        last = nc.tensor.matmul(dt_ps[:, c % 2, j, :], w_dt[:, c * P:(c + 1) * P], low[:, j * GROUP:(j + 1) * GROUP], start=True, stop=True)
                    last.then_inc(dt_ready, 1)


def ssm_scan(chip, a, pick, states, u, dt, du, gate, per_feature):
    nc = chip.nc
    halves = SEQ // GROUP
    with ExitStack() as ctx:
        sb = lambda name, shape: ctx.enter_context(sbuf(nc, name, shape, F32))
        state_in, decay, added, state, term = (sb(n, [P, 2, SEQ]) for n in ("state_in_rows", "decay", "added", "state", "term"))
        b_ps = ctx.enter_context(banks(nc, "state_in", [P, 2, SEQ], F32))
        c_ps = ctx.enter_context(banks(nc, "state_out", [P, SEQ], F32))
        sum_ps = ctx.enter_context(banks(nc, "state_sums", [P, SEQ], F32))
        total = STATES * SC
        half = lambda j: slice(j * GROUP, (j + 1) * GROUP)
        with step(nc, "in_spread in_copied out_spread decay_ready added_ready state_ready term_ready summed sums_read dve_step") as (
                block, in_spread, in_copied, out_spread, decay_ready, added_ready, state_ready, term_ready, summed, sums_read, dve_step):
            @block.tensor
            def _(pe):
                def spread(out, row, done):
                    for j in range(halves):
                        last = nc.tensor.matmul(out[:, half(j)], pick[:, row * P:(row + 1) * P], states[:, half(j)], start=True, stop=True)
                    last.then_inc(done, 1)

                def spread_in(i):
                    if i < total:
                        if i >= 2:
                            pe.wait_ge(in_copied, i - 1)
                        spread(b_ps[:, i % 2, :], i % STATES, in_spread)

                def add(i):
                    c, n = divmod(i, STATES)
                    pe.wait_ge(term_ready, i + 1)
                    if n == 0 and c:
                        pe.wait_ge(sums_read, c)
                    for j in range(halves):
                        last = nc.tensor.matmul(sum_ps[:, half(j)], chip.c(C_ID), term[:, i % 2, half(j)], start=(n == 0), stop=(n == STATES - 1))
                    last.then_inc(summed, 1)

                spread_in(0)
                spread_in(1)
                for i in range(total):
                    spread_in(i + 2)
                    if i:
                        pe.wait_ge(term_ready, i)
                    spread(c_ps[:, :], STATES + i % STATES, out_spread)
                    if i:
                        add(i - 1)
                add(total - 1)

            @block.scalar
            def _(act):
                for i in range(total):
                    c, n = divmod(i, STATES)
                    act.wait_ge(in_spread, i + 1)
                    if i >= 2:
                        act.wait_ge(added_ready, i - 1)
                    nc.scalar.activation(state_in[:, i % 2, :], b_ps[:, i % 2, :], ACT.Copy).then_inc(in_copied, 1)
                    if i >= 2:
                        act.wait_ge(state_ready, i - 1)
                    nc.scalar.activation(decay[:, i % 2, :], dt[:, c, :], ACT.Exp, scale=a[:, c, n:n + 1]).then_inc(decay_ready, 1)

            @block.gpsimd
            def _(pool):
                for i in range(total):
                    pool.wait_ge(in_copied, i + 1)
                    if i >= 2:
                        pool.wait_ge(state_ready, i - 1)
                    nc.gpsimd.tensor_tensor(added[:, i % 2, :], du[:, i // STATES, :], state_in[:, i % 2, :], ALU.mult).then_inc(added_ready, 1)

            @block.vector
            def _(dve):
                then = in_order(dve, dve_step)

                def finish(c):
                    dve.wait_ge(summed, STATES * (c + 1))
                    nc.vector.scalar_tensor_tensor(out=u[:, c, :], in0=u[:, c, :], scalar=per_feature[:, 2, c:c + 1], in1=sum_ps[:, :],
                                                   op0=ALU.mult, op1=ALU.add).then_inc(sums_read, 1)
                    dve.wait_ge(sums_read, c + 1)
                    then(nc.vector.tensor_tensor(u[:, c, :], u[:, c, :], gate[:, c, :], ALU.mult))

                for i in range(total):
                    c, n = divmod(i, STATES)
                    dve.wait_ge(added_ready, i + 1)
                    dve.wait_ge(decay_ready, i + 1)
                    nc.vector.tensor_tensor_scan(state[:, i % 2, :], decay[:, i % 2, :], added[:, i % 2, :], 0.0, ALU.mult, ALU.add).then_inc(state_ready, 1)
                    dve.wait_ge(state_ready, i + 1)
                    dve.wait_ge(out_spread, i + 1)
                    if i >= 2:
                        dve.wait_ge(summed, i - 1)
                    nc.vector.tensor_tensor(term[:, i % 2, :], state[:, i % 2, :], c_ps[:, :], ALU.mult).then_inc(term_ready, 1)
                    if n == 0 and c:
                        finish(c - 1)
                finish(SC - 1)


KEYS, TOP, SIDES, RHEADS, RDIM = 128, 8, 2, 4, 32
EMBEDS, RINNER = 4096, 512
PICKS = RHEADS * TOP


def retrieval_ffn(chip):
    nc, io = chip.nc, chip.io
    rc = RINNER // P
    with ExitStack() as ctx:
        sb = lambda name, shape, dt=F32: ctx.enter_context(sbuf(nc, name, shape, dt))
        b = {"tables": io["L3_ffn_tables"]}
        b["wq"], b["keys"] = sb("query_w", [P, FC, SIDES * P]), sb("product_keys", [P, SIDES, RHEADS * KEYS])
        b["wg"], b["wu"], b["wd"] = sb("r_gate_w", [P, FC, RINNER]), sb("r_up_w", [P, FC, RINNER]), sb("r_down_w", [P, rc, DIM])
        load(nc, [(b["wq"][:, :, :], io["L3_ffn_wq"].rearrange("(c p) n -> p c n", p=P)), (b["keys"][:, :, :], io["L3_ffn_keys"]),
                  (b["wg"][:, :, :], io["L3_ffn_wg"].rearrange("(c p) n -> p c n", p=P)), (b["wu"][:, :, :], io["L3_ffn_wu"].rearrange("(c p) n -> p c n", p=P)),
                  (b["wd"][:, :, :], io["L3_ffn_wd"].rearrange("(c p) n -> p c n", p=P))])
        for when in ("now", "next"):
            b["rows_" + when] = sb("r_rows_" + when, [P, PER_HALF, DIM])
            b["pick_" + when] = sb("r_pick_" + when, [P, PER_HALF, PICKS], U32)
            b["weight_" + when] = sb("r_weight_" + when, [P, PER_HALF, RHEADS, TOP])
        b["stage"], b["q_t"] = sb("r_stage", [P, FC, GROUP]), sb("r_queries", [P, SIDES, GROUP])
        b["sims"] = sb("r_sims", [P, SIDES, RHEADS * KEYS])
        b["best"], b["at_f"] = sb("r_best", [P, SIDES, RHEADS, TOP]), sb("r_at", [P, SIDES, RHEADS, TOP])
        b["best_at"] = sb("r_best_at", [P, SIDES, RHEADS, TOP], U32)
        b["sums"] = sb("r_sums", [P, RHEADS, TOP, TOP])
        b["score"], b["pos"], b["pos_f"] = sb("r_score", [P, RHEADS, TOP]), sb("r_pos", [P, RHEADS, TOP], U32), sb("r_pos_f", [P, SIDES, RHEADS, TOP])
        b["hot"], b["code"], b["total"] = sb("r_hot", [P, SIDES, RHEADS, TOP, TOP]), sb("r_code", [P, SIDES, RHEADS, TOP]), sb("r_total", [P, RHEADS])
        b["got"] = sb("r_got", [P, PICKS, 2 * DIM])
        b["scratch"] = sb("r_scratch", [P, 2, DIM])
        b["dots"], b["act"] = sb("r_dots", [P, PER_HALF, PICKS]), sb("r_act", [P, PER_HALF, PICKS])
        b["diagonal"] = sb("r_diagonal", [P, 2, TOP, P])
        b["hidden"], b["gate"] = sb("r_hidden", [P, 2, GROUP]), sb("r_gate", [P, 2, GROUP])
        arrived = [chip.keep_semaphore(f"row_arrived_{n}") for n in range(PICKS)]
        y_ps = ctx.enter_context(banks(nc, "r_psum_y", [P, FC, GROUP], F32))

        def fetch_first(block, taken):
            @block.gpsimd
            def _(pool):
                nc.gpsimd.tensor_copy(b["pick_now"][:, :, :], b["pick_next"][:, :, :]).then_inc(taken, 1)
                pool.wait_ge(taken, 1)
                for n in range(FETCHED):
                    fetch_row(nc, b, arrived, 0, n)

        def group(now, following):
            retrieval_step(chip, b, arrived, y_ps, now, following)
            if now is not None:
                with banks(nc, "norm_psum", [P, 4, GROUP], F32) as norm_ps:
                    add_norm(chip, [group_slice(now)], norm_ps, ready=lambda _, c: y_ps[:, c, :], beside=fetch_first if following is not None else None)
            else:
                with step(nc, "taken") as (block, taken):
                    fetch_first(block, taken)

        group(None, 0)
        with nc.Fori(0, GROUPS - 1) as g:
            group(g, g + 1)
        group(GROUPS - 1, None)


FETCHED = 8


def fetch_row(nc, b, arrived, t, n):
    nc.gpsimd.indirect_dma_start(out=b["got"][:, n, :], out_offset=None, in_=b["tables"],
                                 in_offset=bass.IndirectOffsetOnAxis(ap=b["pick_now"][:, t, n:n + 1], axis=0)).then_inc(arrived[n], 16)


def retrieval_step(chip, b, arrived, y_ps, now, following):
    nc, io = chip.nc, chip.io
    per, rc = PER_HALF, RINNER // P
    current, ahead = now is not None, following is not None
    gated = list(range(1, rc))
    gate = lambda: [("gate", gated[0], 0)] if gated else []
    hide = lambda: [("hide", gated.pop(0), 0)] if gated else []
    pieces = [("search", t, h) for t in range(per) for h in range(RHEADS + 1)]

    def search(n):
        return [pieces.pop(0) for _ in range(min(n, len(pieces)))]

    order = [("gate", 0, 0), ("hide", 0, 0), ("project", 0, 0)] + search(0)
    for t in range(per):
        order += gate() + [("dots", t, 0)] + search(1) + [("dots", t, 1)] + hide() + [("mix", t, 0)] + search(1) + [("dots", t, 2), ("mix", t, 1)] + gate()
        order += search(1) + [("dots", t, 3)] + hide() + [("mix", t, 2), ("mix", t, 3)] + search(2)
    order += pieces
    order = [s for s in order if (ahead if s[0] in ("search", "project") else current)]
    with ExitStack() as ctx:
        pair_ps = ctx.enter_context(banks(nc, "r_psum_pair", [P, 2, 2, GROUP], F32))
        q_ps = ctx.enter_context(banks(nc, "r_psum_q", [P, SIDES, GROUP], F32))
        rows_ps = q_ps
        with step(nc, "taken pair_ready gate_ready hidden_ready staged q_ready q_copied turned rows_ready sims_ready sims_copied sims_used "
                      "shifted exps_ready dot_ready dots_active weighted diagonal_ready summed y_added dve_step") as (
                block, taken, pair_ready, gate_ready, hidden_ready, staged, q_ready, q_copied, turned, rows_ready, sims_ready, sims_copied, sims_used,
                shifted, exps_ready, dot_ready, dots_active, weighted, diagonal_ready, summed, y_added, dve_step):
            if current:
                @block.gpsimd
                def _(pool):
                    for t in range(per):
                        for n in range(FETCHED if t == 0 else 0, PICKS):
                            if t and n % TOP == 0:
                                pool.wait_ge(summed, RHEADS * (t - 1) + n // TOP + 1)
                            fetch_row(nc, b, arrived, t, n)

            @block.tensor
            def _(pe):
                def project():
                    for s in range(SIDES):
                        for c in range(FC):
                            last = nc.tensor.matmul(q_ps[:, s, :], b["wq"][:, c, s * P:(s + 1) * P], chip.xt[:, c, group_slice(following)],
                                                    start=(c == 0), stop=(c == FC - 1))
                        last.then_inc(q_ready, 1)
                    pe.wait_ge(staged, 1)
                    pe.wait_ge(q_copied, SIDES)
                    for t in range(per):
                        for c in range(FC):
                            at = (t % 2) * DIM + c * P
                            last = nc.tensor.transpose(rows_ps[:, t // 2, at:at + P], b["stage"][:, c, t * P:(t + 1) * P], chip.c(C_ID))
                    last.then_inc(turned, 1)

                for kind, t, h in order:
                    if kind == "project":
                        project()
                    elif kind == "gate":
                        n = t
                        if n >= 1:
                            pe.wait_ge(hidden_ready, n)
                        for k, w in enumerate((b["wg"], b["wu"])):
                            for c in range(FC):
                                last = nc.tensor.matmul(pair_ps[:, 0, k, :], w[:, c, n * P:(n + 1) * P], chip.xt[:, c, group_slice(now)],
                                                        start=(c == 0), stop=(c == FC - 1))
                        last.then_inc(pair_ready, 1)
                    elif kind == "hide":
                        n = t
                        pe.wait_ge(hidden_ready, n + 1)
                        for c in range(FC):
                            nc.tensor.matmul(y_ps[:, c, :], b["wd"][:, n, c * P:(c + 1) * P], b["hidden"][:, n % 2, :], start=(n == 0), stop=False).then_inc(y_added, 1)
                    elif kind == "search" and h == 0:
                        pe.wait_ge(q_copied, SIDES)
                        if t:
                            pe.wait_ge(sims_copied, t)
                        for s in range(SIDES):
                            last = nc.tensor.matmul(pair_ps[:, 1, s, :], b["q_t"][:, s, t * P:(t + 1) * P], b["keys"][:, s, :], start=True, stop=True)
                        last.then_inc(sims_ready, 1)
                    elif kind == "mix":
                        k = RHEADS * t + h
                        pe.wait_ge(diagonal_ready, TOP * (k + 1))
                        for n in range(TOP):
                            for c in range(FC):
                                row = b["got"][:, TOP * h + n, DIM + c * P:DIM + (c + 1) * P]
                                last = nc.tensor.matmul(y_ps[:, c, t * P:(t + 1) * P], row, b["diagonal"][:, k % 2, n, :],
                                                        start=False, stop=(k == RHEADS * per - 1 and n == TOP - 1))
                        last.then_inc(summed, 1)

            @block.scalar
            def _(act):
                if current:
                    nc.scalar.activation(b["rows_now"][:, :, :], b["rows_next"][:, :, :], ACT.Copy).then_inc(taken, 1)
                if ahead:
                    nc.scalar.activation(b["stage"][:, :, :], chip.xt[:, :, group_slice(following)], ACT.Copy).then_inc(staged, 1)
                def project():
                    for s in range(SIDES):
                        act.wait_ge(q_ready, s + 1)
                        nc.scalar.activation(b["q_t"][:, s, :], q_ps[:, s, :], ACT.Copy).then_inc(q_copied, 1)
                    act.wait_ge(turned, 1)
                    if current:
                        act.wait_ge(taken, 2)
                    nc.scalar.activation(b["rows_next"][:, :, :], rows_ps[:, :, :].rearrange("p b (t n) -> p (b t) n", n=DIM), ACT.Copy).then_inc(rows_ready, 1)

                for kind, t, h in order:
                    if kind == "project":
                        project()
                    elif kind == "gate":
                        n = t
                        act.wait_ge(pair_ready, n + 1)
                        if n >= 2:
                            act.wait_ge(hidden_ready, n - 1)
                        nc.scalar.activation(b["gate"][:, n % 2, :], pair_ps[:, 0, 0, :], ACT.Silu).then_inc(gate_ready, 1)
                    elif kind == "search" and h == 0:
                        act.wait_ge(sims_ready, t + 1)
                        if t:
                            act.wait_ge(sims_used, t)
                        nc.scalar.activation(b["sims"][:, :, :], pair_ps[:, 1, :, :], ACT.Copy).then_inc(sims_copied, 1)
                    elif kind == "search" and h == RHEADS:
                        weight = b["weight_next"][:, t, :, :]
                        act.wait_ge(shifted, t + 1)
                        nc.scalar.activation(weight, weight, ACT.Exp).then_inc(exps_ready, 1)
                    elif kind == "dots":
                        act.wait_ge(dot_ready, PICKS * t + TOP * (h + 1))
                        own = slice(TOP * h, TOP * (h + 1))
                        nc.scalar.activation(b["act"][:, t, own], b["dots"][:, t, own], ACT.Silu).then_inc(dots_active, 1)
                    elif kind == "mix":
                        k = RHEADS * t + h
                        act.wait_ge(weighted, k + 1)
                        if k >= 2:
                            act.wait_ge(summed, k - 1)
                        for n in range(TOP):
                            nc.scalar.activation(b["diagonal"][:, k % 2, n, :], chip.c(C_ID), ACT.Copy,
                                                 scale=b["act"][:, t, TOP * h + n:TOP * h + n + 1]).then_inc(diagonal_ready, 1)

            @block.vector
            def _(dve):
                then = in_order(dve, dve_step)
                tt, ts, copy = nc.vector.tensor_tensor, nc.vector.tensor_scalar, nc.vector.tensor_copy
                if current:
                    copy(b["weight_now"][:, :, :, :], b["weight_next"][:, :, :, :]).then_inc(taken, 1)
                    dve.wait_ge(taken, 2)

                def best_keys(t, s):
                    dve.wait_ge(sims_copied, t + 1)
                    for h in range(RHEADS):
                        own = b["sims"][:, s, h * KEYS:(h + 1) * KEYS]
                        then(nc.vector.max(b["best"][:, s, h, :], own))
                        last = nc.vector.max_index(b["best_at"][:, s, h, :], b["best"][:, s, h, :], own)
                        if (s, h) != (SIDES - 1, RHEADS - 1):
                            then(last)
                    if s == SIDES - 1:
                        last.then_inc(sims_used, 1)
                        dve.wait_ge(sims_used, t + 1)

                def best_pairs():
                    best = b["best"]
                    then(copy(b["at_f"][:, :, :, :], b["best_at"][:, :, :, :]))
                    second = best[:, 1, :, :].rearrange("p h (o k) -> p h o k", o=1).to_broadcast((P, RHEADS, TOP, TOP))
                    mine = best[:, 0, :, :].rearrange("p h (k o) -> p h k o", o=1).to_broadcast((P, RHEADS, TOP, TOP))
                    then(tt(b["sums"][:, :, :, :], mine, second, ALU.add))
                    for h in range(RHEADS):
                        flat = b["sums"][:, h, :, :].rearrange("p a b -> p (a b)")
                        then(nc.vector.max(b["score"][:, h, :], flat))
                        then(nc.vector.max_index(b["pos"][:, h, :], b["score"][:, h, :], flat))
                    then(copy(b["pos_f"][:, SIDES - 1, :, :], b["pos"][:, :, :]))

                def picked(t):
                    first, second = b["pos_f"][:, 0, :, :], b["pos_f"][:, 1, :, :]
                    then(ts(first, second, 1.0 / TOP, 0.5 / TOP - 0.5, ALU.mult, ALU.add))
                    then(ts(first, first, ROUND, ROUND, ALU.add, ALU.subtract))
                    then(nc.vector.scalar_tensor_tensor(out=second, in0=first, scalar=-float(TOP), in1=second, op0=ALU.mult, op1=ALU.add))
                    for s in range(SIDES):
                        hot = b["hot"][:, s, :, :, :]
                        rank = b["pos_f"][:, s, :, :].rearrange("p h (k o) -> p h k o", o=1).to_broadcast((P, RHEADS, TOP, TOP))
                        iota = chip.c(C_IOTA, TOP).rearrange("p (o u n) -> p o u n", o=1, u=1).to_broadcast((P, RHEADS, TOP, TOP))
                        index = b["at_f"][:, s, :, :].rearrange("p h (o n) -> p h o n", o=1).to_broadcast((P, RHEADS, TOP, TOP))
                        then(tt(hot, rank, iota, ALU.is_equal))
                        then(tt(hot, hot, index, ALU.mult))
                        then(nc.vector.reduce_sum(b["code"][:, s, :, :], hot, AX.X))
                    code = b["code"][:, 0, :, :]
                    then(nc.vector.scalar_tensor_tensor(out=code, in0=code, scalar=float(KEYS), in1=b["code"][:, 1, :, :], op0=ALU.mult, op1=ALU.add))
                    then(ts(code, code, float(EMBEDS - 1), None, ALU.min))
                    then(copy(b["pick_next"][:, t, :], code.rearrange("p h k -> p (h k)")))
                    top = b["score"][:, :, 0:1].to_broadcast((P, RHEADS, TOP))
                    tt(b["weight_next"][:, t, :, :], b["score"][:, :, :], top, ALU.subtract).then_inc(shifted, 1)
                    dve.wait_ge(shifted, t + 1)

                def weights(t):
                    weight, total = b["weight_next"][:, t, :, :], b["total"][:, :]
                    dve.wait_ge(exps_ready, t + 1)
                    then(nc.vector.reduce_sum(total, weight, AX.X))
                    then(nc.vector.reciprocal(total, total))
                    then(tt(weight, weight, total.rearrange("p (h o) -> p h o", o=1).to_broadcast((P, RHEADS, TOP)), ALU.mult))

                for kind, t, h in order:
                    if kind == "hide":
                        n = t
                        dve.wait_ge(gate_ready, n + 1)
                        if n >= 2:
                            dve.wait_ge(y_added, FC * (n - 1))
                        tt(b["hidden"][:, n % 2, :], b["gate"][:, n % 2, :], pair_ps[:, 0, 1, :], ALU.mult).then_inc(hidden_ready, 1)
                    elif kind == "search":
                        if h < SIDES:
                            if h == 1 and t:
                                weights(t - 1)
                            best_keys(t, h)
                        elif h == 2:
                            best_pairs()
                        elif h == 3:
                            picked(t)
                    elif kind == "dots":
                        for n in range(TOP * h, TOP * (h + 1)):
                            k = PICKS * t + n
                            dve.wait_ge(arrived[n], 16 * per * now + 16 * (t + 1))
                            if k >= 2:
                                dve.wait_ge(dot_ready, k - 1)
                            nc.vector.tensor_tensor_reduce(b["scratch"][:, k % 2, :], b["got"][:, n, 0:DIM], b["rows_now"][:, t, :], 1.0, 0.0, ALU.mult, ALU.add,
                                                           b["dots"][:, t, n:n + 1]).then_inc(dot_ready, 1)
                    elif kind == "mix":
                        own = slice(TOP * h, TOP * (h + 1))
                        dve.wait_ge(dots_active, RHEADS * t + h + 1)
                        tt(b["act"][:, t, own], b["act"][:, t, own], b["weight_now"][:, t, h, :], ALU.mult).then_inc(weighted, 1)
                if ahead:
                    weights(per - 1)


def rope_tables():
    import numpy as np
    f = np.float32
    half = np.arange(0, WIDE, 2, dtype=f)
    inv_freq = (f(1.0) / f(10000.0) ** (half / f(WIDE))).astype(f)
    t = np.arange(SEQ, dtype=f)
    freqs = (t[:, None] * inv_freq[None, :]).astype(f)
    base = ((half + f(0.4 * WIDE)) / f(1.4 * WIDE)).astype(f)
    power = ((t - SEQ // 2) / f(P // 2)).astype(f)
    scale = (base[None, :] ** power[:, None]).astype(f)
    twice = lambda v: np.concatenate([v, v], axis=-1)
    sign = np.where(np.arange(WIDE) < WIDE // 2, f(-1), f(1))
    out = np.zeros((2, SEQ, 2, WIDE), f)
    cos, sin, scale = twice(np.cos(freqs)), twice(np.sin(freqs)) * sign, twice(scale)
    out[0, :, 0], out[0, :, 1] = cos * scale, cos / scale
    out[1, :, 0], out[1, :, 1] = sin * scale, sin / scale
    return np.ascontiguousarray(out.reshape(2, TILES, P, 2, WIDE).transpose(2, 0, 1, 3, 4))


def layout_more(a, io, cols):
    import numpy as np
    f = np.float32
    io["L0_ffn_wg"] = a["L0_ffn_wg"]
    io["L0_ffn_w1"] = a["L0_ffn_w_gate"].reshape(EXPERTS * DIM, EXPERT_INNER)
    io["L0_ffn_w2"] = a["L0_ffn_w_down"].reshape(EXPERTS * EXPERT_INNER, DIM)
    io["rope"] = rope_tables()
    io["L1_ffn_wqkv"] = a["L1_ffn_wqkv"].reshape(DEPTH * DIM, 3 * INNER)
    io["L1_ffn_wo"] = a["L1_ffn_wo"].reshape(DEPTH * INNER, DIM)
    io["L1_ffn_scales"] = np.concatenate([a["L1_ffn_q_scale"], a["L1_ffn_k_scale"]], axis=1)
    w1, b1 = np.zeros((DEPTH, DIM, 2, HC * P), f), np.zeros((DEPTH, 2, HC * P), f)
    w1[..., :HIDDEN] = a["L1_ffn_w1"].reshape(DEPTH, DIM, 2, HIDDEN)
    b1[..., :HIDDEN] = a["L1_ffn_b1"].reshape(DEPTH, 2, HIDDEN)
    w2 = np.zeros((DEPTH, HC * P, DIM), f)
    w2[:, :HIDDEN] = a["L1_ffn_w2"]
    io["L1_ffn_w1"], io["L1_ffn_w2"] = w1.reshape(DEPTH * DIM, 2 * HC * P), w2.reshape(DEPTH * HC * P, DIM)
    io["L1_ffn_b1"] = np.concatenate([cols(b1[n].ravel()) for n in range(DEPTH)])
    io["L1_ffn_b2"] = np.concatenate([cols(a["L1_ffn_b2"][n]) for n in range(DEPTH)])
    io["L1_ffn_ln"] = np.concatenate([np.concatenate([cols(a["L1_ffn_ln_g"][n]), cols(a["L1_ffn_ln_b"][n])], axis=1) for n in range(DEPTH)])
    io["L2_attn_win"] = np.ascontiguousarray(a["L2_attn_in_proj_w"].T)
    io["L2_attn_wout"] = np.ascontiguousarray(a["L2_attn_out_proj_w"].T)
    io["L2_attn_wx"] = np.ascontiguousarray(a["L2_attn_x_proj_w"].T)
    io["L2_attn_wdt"] = np.ascontiguousarray(a["L2_attn_dt_proj_w"].T)
    io["L2_attn_conv"] = a["L2_attn_conv_w"].reshape(-1, TAPS)
    io["L2_attn_vec"] = np.ascontiguousarray(np.stack([cols(a["L2_attn_" + n]) for n in ("conv_b", "dt_proj_b", "D")], axis=1))
    io["L2_attn_norm"] = cols(a["L2_attn_norm_w"])
    io["L2_attn_alog"] = a["L2_attn_A_log"]
    pick = np.zeros((PARTS, 2 * STATES, 2 * STATES, P), f)
    pick[:, np.arange(2 * STATES), np.arange(2 * STATES)] = 1.0
    io["pick"] = pick.reshape(PARTS * 2 * STATES, -1)
    io["L3_ffn_wq"] = np.ascontiguousarray(a["L3_ffn_w_queries"].T)
    keys = np.zeros((RHEADS, RDIM, SIDES, RHEADS, KEYS), f)
    for h in range(RHEADS):
        keys[h, :, :, h, :] = a["L3_ffn_keys"][h].transpose(2, 1, 0)
    io["L3_ffn_keys"] = keys.reshape(P, SIDES, RHEADS * KEYS)
    io["L3_ffn_tables"] = np.concatenate([a["L3_ffn_down_embed"], a["L3_ffn_up_embed"]], axis=1)
    io["L3_ffn_wg"], io["L3_ffn_wu"], io["L3_ffn_wd"] = (np.ascontiguousarray(a["L3_ffn_w_" + n].T) for n in ("gate", "up", "down"))


LAYERS = [quantised_attention, cross_attention, expert_ffn, normed_attention, context_mlp, local_transformer,
          state_space, concat_context, spiking_ffn, linear_attention, causal_attention, retrieval_ffn]


def decoder(nc, io, out, layers):
    with ExitStack() as ctx:
        chip = Chip(nc, ctx, io)
        chip.ctx_t = ctx.enter_context(sbuf(nc, "context", [P, FC, BATCH * CTX], F32))
        load(nc, [(chip.xt[:, :, :], io["x"].rearrange("(c p) t -> p c t", p=P)), (chip.const[:, :], io["constants"]),
                  (chip.ctx_t[:, :, :], io["ctx_t"].rearrange("(c p) t -> p c t", p=P)), (chip.eps[:, :], io["epsilons"])])
        with step(nc, "copied") as (block, copied):
            @block.vector
            def _(dve):
                for dst, src in ((chip.id_bf, C_ID), (chip.far_t, C_FART), (chip.far_n, C_FARN)):
                    nc.vector.tensor_copy(dst[:, :], chip.c(src)).then_inc(copied, 1)
                dve.wait_ge(copied, 3)
        for layer in layers:
            layer(chip)
        with step(nc, "stored") as (block, stored):
            @block.sync
            def _(sp):
                sp.dma_start(out.rearrange("(c p) t -> p c t", p=P), chip.xt[:, :, :]).then_inc(stored, 16)
                sp.wait_ge(stored, 16)


def constants():
    import numpy as np
    row, col = np.arange(P)[:, None], np.arange(P)[None, :]
    c = np.zeros((P, C_END), np.float32)
    c[:, C_ID:C_ID + P] = row == col
    c[:, C_MEAN:C_MEAN + P] = 1.0 / DIM
    c[:, C_ONES:C_ONES + P] = 1.0
    c[:, C_HEADMEAN:C_HEADMEAN + P] = (row // HEAD == col // HEAD) / HEAD
    c[:, C_DEN:C_DEN + P] = (row // SLOT == col // SLOT) & (row % SLOT == HEAD)
    c[:, C_FART:C_FART + P] = np.where(row > col, FAR, 0.0)
    c[:, C_FARN:C_FARN + P] = np.where(col > row, FAR, 0.0)
    c[:, C_KEEPT:C_KEEPT + P] = row <= col
    c[:, C_BEFORE:C_BEFORE + P] = row < col
    c[:, C_IOTA:C_IOTA + P] = col
    c[:, C_SLOTS:C_SLOTS + P] = row // SLOT == col // SLOT
    c[:, C_ROWS] = np.arange(P) % SLOT < HEAD
    c[STACK:STACK + PARTS, C_PARTROW:C_PARTROW + PARTS] = np.eye(PARTS)
    return c


def layout(a):
    import numpy as np
    f = np.float32
    cols = lambda v: np.ascontiguousarray(v.reshape(-1, P).T)

    def pad_rows(w):
        out = np.zeros((HEADS, SLOT, w.shape[1]), f)
        out[:, :HEAD] = w.reshape(HEADS, HEAD, w.shape[1])
        return out.reshape(PADDED, w.shape[1])

    none = np.zeros(DIM, f)
    io = {"x": np.ascontiguousarray(a["x"].reshape(TOKENS, DIM).T), "constants": constants(),
          "ctx_t": np.ascontiguousarray(a["ctx_1024"].reshape(-1, DIM).T), "ctx": a["ctx_1024"].reshape(-1, DIM),
          "epsilons": np.tile(np.array([1e-5, 1e-6, 1.0, 0.0], f), (P, 1))}
    qk = lambda bq, bk: np.ascontiguousarray(np.stack([cols(bq), cols(bk)], axis=1))
    io["L0_attn_w"] = np.ascontiguousarray(a["L0_attn_W_qkv"].reshape(3, DIM, DIM).transpose(0, 2, 1))
    bqkv = a["L0_attn_b_qkv"].reshape(3, DIM)
    io["L0_attn_b"], io["L0_attn_vb"] = qk(bqkv[0], bqkv[1]), bqkv[2:3]
    io["L0_attn_wo"] = pad_rows(a["L0_attn_W_proj"].T)
    io["L0_attn_bo"] = cols(a["L0_attn_b_proj"])
    io["L0_attn_ws"] = np.stack([a["L0_attn_s_w_qkv"], a["L0_attn_zp_w_qkv"]])
    io["L0_attn_ps"] = np.stack([a["L0_attn_s_w_proj"], a["L0_attn_zp_w_proj"]])
    io["L0_attn_scalars"] = np.stack([a["L0_attn_" + n] for n in (
        "s_act_qkv", "zp_act_qkv", "s_attn", "zp_attn", "s_act_proj", "zp_act_proj")]).reshape(1, 6)
    io["L0_xattn_w"] = np.stack([a["L0_xattn_W" + n].T for n in "qkv"])
    io["L0_xattn_b"] = qk(none, none)
    io["L0_xattn_wo"] = pad_rows(a["L0_xattn_Wo"].T)
    io["L0_xattn_bo"] = cols(none)
    io["key_bias"] = a["fside_BxS2_0"].reshape(1, -1)
    io["L1_attn_w"] = np.stack([a["L1_attn_W" + n] for n in "qkv"])
    io["L1_attn_b"], io["L1_attn_vb"] = qk(a["L1_attn_bq"], a["L1_attn_bk"]), a["L1_attn_bv"].reshape(1, DIM)
    norm = np.stack([np.stack([np.tile(a[f"L1_attn_{n}_{s}"], HALF_HEADS) for s in ("scale", "bias")], axis=1) for n in "qk"], axis=1)
    io["L1_attn_norm"] = np.ascontiguousarray(norm)
    io["L1_attn_norm_v"] = np.concatenate([a["L1_attn_v_scale"], a["L1_attn_v_bias"]]).reshape(1, -1)
    io["L1_attn_wo"] = pad_rows(a["L1_attn_Wo"])
    io["L1_attn_bo"] = cols(a["L1_attn_bo"])
    io["L2_xattn_w"] = np.ascontiguousarray(a["L2_xattn_W"].T)
    io["L2_xattn_b"] = cols(a["L2_xattn_b"])
    io["L2_ffn_w1"] = np.ascontiguousarray(a["L2_ffn_W_fc"].T)
    io["L2_ffn_w2"] = np.ascontiguousarray(a["L2_ffn_W_proj"].T)
    half = DIM // 4
    wkv = np.concatenate([a["L3_attn_Wk"], a["L3_attn_Wv"]], axis=1)
    io["L3_attn_wkv"] = np.ascontiguousarray(wkv)
    io["L3_attn_bkv"] = np.concatenate([a["L3_attn_bk"], a["L3_attn_bv"]]).reshape(P, 1)
    wc = np.zeros((P, P), f)
    wc[:half, :half] = wc[half:, half:] = a["L3_attn_Wc"]
    io["L3_attn_wc"] = wc
    def by_kv(w):
        out = np.zeros(w.shape[:-1] + (REPEAT, KV_HEADS, SLOT), f)
        out[..., :HEAD] = np.swapaxes(w.reshape(w.shape[:-1] + (KV_HEADS, REPEAT, HEAD)), -3, -2)
        return out.reshape(w.shape[:-1] + (REPEAT, P))

    io["L3_attn_wq"] = by_kv(a["L3_attn_Wq"])
    io["L3_attn_bq"] = np.ascontiguousarray(by_kv(a["L3_attn_bq"]).T)
    up = np.zeros((P, KV_HEADS, SLOT), f)
    up[:half, :, :HEAD] = a["L3_attn_We"].reshape(half, KV_HEADS, HEAD)
    io["L3_attn_wk"] = up.reshape(P, P)
    both = np.zeros((P, P), f)
    both[:half, :half] = both[half:, half:] = a["L3_attn_We"]
    io["L3_attn_wkv_up"] = both
    io["L3_attn_wo"] = np.ascontiguousarray(by_kv(np.ascontiguousarray(a["L3_attn_Wo"].T)).reshape(DIM, REPEAT * P).T)
    io["L3_attn_bo"] = cols(a["L3_attn_bo"])
    io["L3_attn_affine"] = np.ascontiguousarray(np.stack([cols(a["L3_attn_gamma"]), cols(a["L3_attn_beta"])], axis=1))
    wkv = a["L3_xattn_Wkv"]
    io["L3_xattn_w"] = np.stack([a["L3_xattn_Wq"], wkv[:, :DIM], wkv[:, DIM:]])
    io["L3_xattn_b"] = qk(none, none)
    io["L3_xattn_wo"] = pad_rows(a["L3_xattn_Wout"])
    io["L3_xattn_bo"] = cols(a["L3_xattn_bout"])
    layout_more(a, io, cols)
    return io


def kernel(**inputs):
    import numpy as np
    import concourse.bacc as bacc
    from concourse.bass_utils import run_bass_kernel_spmd

    arrays = layout({k: np.asarray(v) for k, v in inputs.items()})
    nc = bacc.Bacc("TRN2", target_bir_lowering=False, num_devices=1)
    io = {k: nc.dram_tensor("in_" + k, v.shape, mybir.dt.from_np(v.dtype), kind="ExternalInput").ap() for k, v in arrays.items()}
    out = nc.dram_tensor("out_t", (DIM, TOKENS), F32, kind="ExternalOutput").ap()
    decoder(nc, io, out, LAYERS)
    result = run_bass_kernel_spmd(nc, [{"in_" + k: v for k, v in arrays.items()}], core_ids=[0])
    return np.ascontiguousarray(result.results[0]["out_t"].T).reshape(BATCH, SEQ, DIM)
```
